# Optimizing a Trainium2 kernel written in Bass

```python
import numpy as np
import jax
import jax.numpy as jnp

def _softmax(x, axis=-1):
    return jax.nn.softmax(x, axis=axis)

def _gelu(x):
    return jax.nn.gelu(x, approximate=True)

def _silu(x):
    return jax.nn.silu(x)

def _sigmoid(x):
    return jax.nn.sigmoid(x)

def _layernorm(x, axis=-1, eps=1e-05):
    m = jnp.mean(x, axis=axis, keepdims=True)
    v = jnp.var(x, axis=axis, keepdims=True)
    return (x - m) / jnp.sqrt(v + eps)

def _scatter_add(tgt, idx, src, axis=0):
    return tgt.at[idx].add(src)

def _segment_sum(src, seg, n):
    return jax.ops.segment_sum(src, seg, n)
kernel_name = 'mk_perceiver_d4_seqx_r8_05fcd3'

def setup_inputs(seed: int=0):
    np.random.seed(seed)
    _w = jnp.asarray

    def _rec_inputs():
        import jax
        import jax.numpy as jnp
        _rk = jax.random.key(seed)
        x = 0.002226 + 0.9996 * jax.random.normal(jax.random.fold_in(_rk, 1), (16, 64, 128), jnp.float32)
        _lenS = 64 - jax.random.randint(jax.random.fold_in(_rk, 7), (16,), 0, max(1, 64 // 4) + 1, jnp.int32)
        _lenS2 = 1601 - jax.random.randint(jax.random.fold_in(_rk, 8), (16,), 0, max(1, 1601 // 4) + 1, jnp.int32)
        _ctx_1024P = jax.random.normal(jax.random.fold_in(_rk, 11), (16, 16, 128), jnp.float32)
        _ctx_1024c = jax.random.dirichlet(jax.random.fold_in(_rk, 511), 0.3 * jnp.ones((16,), jnp.float32), (16, 1601))
        _ctx_1024t = jnp.einsum('bsk,bkd->bsd', _ctx_1024c, _ctx_1024P)
        _ctx_1024t = _ctx_1024t * jax.lax.rsqrt(jnp.mean(jnp.square(_ctx_1024t)) + 1e-12) * 0.953939
        ctx_1024 = -0.000125008 + 0.999885 * (_ctx_1024t + 0.3 * jax.random.normal(jax.random.fold_in(_rk, 611), (16, 1601, 128), jnp.float32))
        _validS = jnp.arange(64)[None, :] < _lenS[:, None]
        _validS2 = jnp.arange(1601)[None, :] < _lenS2[:, None]
        _causal = jnp.tril(jnp.ones((64, 64), dtype=bool))
        mask_BxS2_bk1 = jnp.broadcast_to(_validS2[:, :], (16, 1601))
        return (x, ctx_1024, mask_BxS2_bk1)
    x, ctx_1024, mask_BxS2_bk1 = _rec_inputs()

    def _L0_xattn_setup():
        import jax, jax.numpy as jnp
        import numpy as np
        DIM = 128
        DIM_HEAD = 64
        HEADS = 8
        INNER = DIM_HEAD * HEADS
        EPS = 1e-05

        def layernorm(x, g, b):
            mu = jnp.mean(x, axis=-1, keepdims=True)
            var = jnp.var(x, axis=-1, keepdims=True)
            return (x - mu) * jax.lax.rsqrt(var + EPS) * g + b
        key = jax.random.key(seed)
        ks = jax.random.split(key, 8)
        b, n, m = (8, 512, 64)
        x = jax.random.normal(ks[0], (b, n, DIM), dtype=jnp.float32)
        latents = jax.random.normal(ks[1], (b, m, DIM), dtype=jnp.float32)
        mask = jax.random.bernoulli(ks[2], 0.9, (b, n))
        s = DIM ** (-0.5)
        Wq = jax.random.normal(ks[3], (DIM, INNER), dtype=jnp.float32) * s
        Wkv = jax.random.normal(ks[4], (DIM, 2 * INNER), dtype=jnp.float32) * s
        Wo = jax.random.normal(ks[5], (INNER, DIM), dtype=jnp.float32) * INNER ** (-0.5)
        ln_x_g = jnp.ones((DIM,), jnp.float32)
        ln_x_b = jnp.zeros((DIM,), jnp.float32)
        ln_l_g = jnp.ones((DIM,), jnp.float32)
        ln_l_b = jnp.zeros((DIM,), jnp.float32)
        ln_o_g = jnp.ones((DIM,), jnp.float32)
        ln_o_b = jnp.zeros((DIM,), jnp.float32)
        return {'x': x, 'latents': latents, 'mask': mask, 'Wq': Wq, 'Wkv': Wkv, 'Wo': Wo, 'ln_x_g': ln_x_g, 'ln_x_b': ln_x_b, 'ln_l_g': ln_l_g, 'ln_l_b': ln_l_b, 'ln_o_g': ln_o_g, 'ln_o_b': ln_o_b}
    _L0_xattn_all = _L0_xattn_setup()
    _L0_xattn_in = {k: v for k, v in _L0_xattn_all.items() if k in ('Wq', 'Wkv', 'Wo', 'ln_x_g', 'ln_x_b', 'ln_l_g', 'ln_l_b', 'ln_o_g', 'ln_o_b')}
    del _L0_xattn_all

    def _L0_attn_setup():
        import jax, jax.numpy as jnp
        import numpy as np
        B, S, D = (2, 128, 128)
        NH = 8
        QK = D // 2
        V = D
        DQK = QK // NH
        DV = V // NH
        CAP = 15.0
        EPS = 1e-06

        def soft_cap(t, cap=CAP):
            return cap * jnp.tanh(t / cap)

        def _mlstm_forward(x, Wq, Wk, Wv, Wog, Wi, bi, Wf, bf, ln_w, ln_b, Wout):
            Bx, Sx, _ = x.shape
            q = (x @ Wq.T).reshape(Bx, Sx, NH, DQK)
            k = (x @ Wk.T).reshape(Bx, Sx, NH, DQK)
            v = (x @ Wv.T).reshape(Bx, Sx, NH, DV)
            o_preact = x @ Wog.T
            i_pre = soft_cap(x @ Wi.T + bi)
            f_pre = soft_cap(x @ Wf.T + bf)
            qT = jnp.moveaxis(q, 1, 0)
            kT = jnp.moveaxis(k, 1, 0)
            vT = jnp.moveaxis(v, 1, 0)
            iT = jnp.moveaxis(i_pre, 1, 0)
            fT = jnp.moveaxis(f_pre, 1, 0)
            qk_scale = DQK ** (-0.5)

            def step(carry, inp):
                C, n, m = carry
                q_t, k_t, v_t, i_t, f_t = inp
                m_new = jnp.maximum(f_t + m, i_t)
                f_act = jnp.exp(f_t + m - m_new)
                i_act = jnp.exp(i_t - m_new)
                C = f_act[..., None, None] * C + i_act[..., None, None] * (k_t[..., :, None] * v_t[..., None, :])
                n = f_act[..., None] * n + i_act[..., None] * k_t
                qs = q_t * qk_scale
                num = jnp.einsum('bhk,bhkv->bhv', qs, C)
                qn = jnp.einsum('bhk,bhk->bh', qs, n)
                denom = jnp.maximum(jnp.abs(qn), jnp.exp(-m_new)) + 1e-06
                h_t = num / denom[..., None]
                return ((C, n, m_new), h_t)
            C0 = jnp.zeros((Bx, NH, DQK, DV), x.dtype)
            n0 = jnp.zeros((Bx, NH, DQK), x.dtype)
            m0 = jnp.zeros((Bx, NH), x.dtype)
            _, hs = jax.lax.scan(step, (C0, n0, m0), (qT, kT, vT, iT, fT))
            h = jnp.moveaxis(hs, 0, 1).reshape(Bx, Sx, NH * DV)
            mu = jnp.mean(h, axis=-1, keepdims=True)
            var = jnp.mean((h - mu) ** 2, axis=-1, keepdims=True)
            h_norm = (h - mu) * jax.lax.rsqrt(var + EPS) * ln_w + ln_b
            h_out = jax.nn.sigmoid(o_preact) * h_norm
            y = h_out @ Wout.T
            return y
        key = jax.random.key(seed)
        ks = jax.random.split(key, 12)
        sc = 0.02
        return {'x': jax.random.normal(ks[0], (B, S, D), jnp.float32), 'Wq': jax.random.normal(ks[1], (QK, D), jnp.float32) * sc, 'Wk': jax.random.normal(ks[2], (QK, D), jnp.float32) * sc, 'Wv': jax.random.normal(ks[3], (V, D), jnp.float32) * sc, 'Wog': jax.random.normal(ks[4], (V, D), jnp.float32) * sc, 'Wi': jax.random.normal(ks[5], (NH, D), jnp.float32) * sc, 'bi': jax.random.normal(ks[6], (NH,), jnp.float32) * sc, 'Wf': jax.random.normal(ks[7], (NH, D), jnp.float32) * sc, 'bf': jax.random.normal(ks[8], (NH,), jnp.float32) * sc + 3.0, 'ln_w': jnp.ones((NH * DV,), jnp.float32), 'ln_b': jnp.zeros((NH * DV,), jnp.float32), 'Wout': jax.random.normal(ks[9], (D, V), jnp.float32) * sc}
    _L0_attn_all = _L0_attn_setup()
    _L0_attn_in = {k: v for k, v in _L0_attn_all.items() if k in ('Wq', 'Wk', 'Wv', 'Wog', 'Wi', 'bi', 'Wf', 'bf', 'ln_w', 'ln_b', 'Wout')}
    del _L0_attn_all

    def _L0_ffn_setup():
        import jax, jax.numpy as jnp
        import numpy as np
        NUM_EXPERTS = 8
        TOP_K = 2
        key = jax.random.key(seed)
        ks = jax.random.split(key, 6)
        B, S, D, H, E = (4, 128, 128, 256, NUM_EXPERTS)
        x = jax.random.normal(ks[0], (B, S, D), dtype=jnp.float32)
        Wg = jax.random.normal(ks[1], (D, E), dtype=jnp.float32) * 0.02
        W1 = jax.random.normal(ks[2], (E, D, H), dtype=jnp.float32) * 0.02
        b1 = jax.random.normal(ks[3], (E, H), dtype=jnp.float32) * 0.02
        W2 = jax.random.normal(ks[4], (E, H, D), dtype=jnp.float32) * 0.02
        b2 = jax.random.normal(ks[5], (E, D), dtype=jnp.float32) * 0.02
        return {'x': x, 'Wg': Wg, 'W1': W1, 'b1': b1, 'W2': W2, 'b2': b2}
    _L0_ffn_all = _L0_ffn_setup()
    _L0_ffn_in = {k: v for k, v in _L0_ffn_all.items() if k in ('Wg', 'W1', 'b1', 'W2', 'b2')}
    del _L0_ffn_all

    def _L1_xattn_setup():
        import jax, jax.numpy as jnp
        import numpy as np
        DIM = 128
        HEADS = 16
        DIM_HEAD = 64
        INNER = HEADS * DIM_HEAD
        CTX_DIM = 128
        key = jax.random.key(seed)
        ks = jax.random.split(key, 7)
        b, n, m = (4, 256, 256)
        x = jax.random.normal(ks[0], (b, n, DIM), dtype=jnp.float32)
        context = jax.random.normal(ks[1], (b, m, CTX_DIM), dtype=jnp.float32)
        s = 0.02
        W_q = jax.random.normal(ks[2], (DIM, INNER), dtype=jnp.float32) * s
        W_k = jax.random.normal(ks[3], (CTX_DIM, INNER), dtype=jnp.float32) * s
        W_v = jax.random.normal(ks[4], (CTX_DIM, INNER), dtype=jnp.float32) * s
        W_o = jax.random.normal(ks[5], (INNER, DIM), dtype=jnp.float32) * s
        b_o = jax.random.normal(ks[6], (DIM,), dtype=jnp.float32) * s
        return {'x': x, 'context': context, 'W_q': W_q, 'W_k': W_k, 'W_v': W_v, 'W_o': W_o, 'b_o': b_o}
    _L1_xattn_all = _L1_xattn_setup()
    _L1_xattn_in = {k: v for k, v in _L1_xattn_all.items() if k in ('W_q', 'W_k', 'W_v', 'W_o', 'b_o')}
    del _L1_xattn_all

    def _L1_attn_setup():
        import jax, jax.numpy as jnp
        import numpy as np
        DIM = 128
        HEADS = 1
        HDIM = DIM // HEADS
        INNER = 16
        B, L = (2, 512)
        ROPE_BASE = 32.0

        def _apply_rope(x, pos, base):
            d = x.shape[-1]
            inv_freq = base ** (-jnp.arange(0, d, 2, dtype=jnp.float32) / d)
            ang = pos[:, None].astype(jnp.float32) * inv_freq
            emb = jnp.concatenate([ang, ang], axis=-1)
            cos = jnp.cos(emb)[None, :, None, :].astype(x.dtype)
            sin = jnp.sin(emb)[None, :, None, :].astype(x.dtype)
            x1, x2 = (x[..., :d // 2], x[..., d // 2:])
            rot = jnp.concatenate([-x2, x1], axis=-1)
            return x * cos + rot * sin
        key = jax.random.key(seed)
        ks = jax.random.split(key, 7)
        hidden_states = jax.random.normal(ks[0], (B, L, DIM), dtype=jnp.float32)
        Wq = jax.random.normal(ks[1], (DIM, DIM), dtype=jnp.float32) * 0.02
        Wk = jax.random.normal(ks[2], (DIM, DIM), dtype=jnp.float32) * 0.02
        fc1_w = jax.random.normal(ks[3], (INNER, 1), dtype=jnp.float32) * 0.1
        fc1_b = jax.random.normal(ks[4], (INNER,), dtype=jnp.float32) * 0.1
        fc2_w = jax.random.normal(ks[5], (DIM, INNER), dtype=jnp.float32) * 0.1
        fc2_b = jax.random.normal(ks[6], (DIM,), dtype=jnp.float32) * 0.1
        return {'hidden_states': hidden_states, 'Wq': Wq, 'Wk': Wk, 'fc1_w': fc1_w, 'fc1_b': fc1_b, 'fc2_w': fc2_w, 'fc2_b': fc2_b}
    _L1_attn_all = _L1_attn_setup()
    _L1_attn_in = {k: v for k, v in _L1_attn_all.items() if k in ('Wq', 'Wk', 'fc1_w', 'fc1_b', 'fc2_w', 'fc2_b')}
    del _L1_attn_all

    def _L1_ffn_setup():
        import jax, jax.numpy as jnp
        import numpy as np
        TOP_K = 2
        key = jax.random.key(seed)
        k1, k2, k3, k4 = jax.random.split(key, 4)
        B, T, D, H, E = (2, 256, 128, 256, 8)
        x = jax.random.normal(k1, (B, T, D), dtype=jnp.float32)
        w12 = jax.random.normal(k2, (E, 2 * H, D), dtype=jnp.float32) * D ** (-0.5)
        w3 = jax.random.normal(k3, (E, D, H), dtype=jnp.float32) * H ** (-0.5)
        gate_w = jax.random.normal(k4, (E, D), dtype=jnp.float32) * D ** (-0.5)
        return {'x': x, 'w12': w12, 'w3': w3, 'gate_w': gate_w}
    _L1_ffn_all = _L1_ffn_setup()
    _L1_ffn_in = {k: v for k, v in _L1_ffn_all.items() if k in ('w12', 'w3', 'gate_w')}
    del _L1_ffn_all

    def _L2_xattn_setup():
        import jax, jax.numpy as jnp
        import numpy as np
        B, S, E = (4, 256, 128)
        key = jax.random.key(seed)
        ks = jax.random.split(key, 9)
        lim = 1.0 / np.sqrt(E)
        inp = {'query': jax.random.normal(ks[0], (B, S, E), dtype=jnp.float32), 'key': jax.random.normal(ks[1], (B, S, E), dtype=jnp.float32), 'value': jax.random.normal(ks[2], (B, S, E), dtype=jnp.float32), 'Wq': jax.random.uniform(ks[3], (E, E), jnp.float32, -lim, lim), 'bq': jax.random.uniform(ks[4], (E,), jnp.float32, -lim, lim), 'Wk': jax.random.uniform(ks[5], (E, E), jnp.float32, -lim, lim), 'bk': jax.random.uniform(ks[6], (E,), jnp.float32, -lim, lim), 'Wv': jax.random.uniform(ks[7], (E, E), jnp.float32, -lim, lim), 'bv': jax.random.uniform(ks[8], (E,), jnp.float32, -lim, lim)}
        return inp
    _L2_xattn_all = _L2_xattn_setup()
    _L2_xattn_in = {k: v for k, v in _L2_xattn_all.items() if k in ('Wq', 'bq', 'Wk', 'bk', 'Wv', 'bv')}
    del _L2_xattn_all

    def _L2_attn_setup():
        import jax, jax.numpy as jnp
        import numpy as np
        EPS = 1e-05

        def _ln(x, g, b):
            mu = jnp.mean(x, axis=-1, keepdims=True)
            var = jnp.var(x, axis=-1, keepdims=True)
            return (x - mu) * jax.lax.rsqrt(var + EPS) * g + b

        def _talking_head_attn(y, qkv_w, proj_w, proj_b, pre_w, pre_b, post_w, post_b, num_heads):
            B, N, C = y.shape
            H = num_heads
            d = C // H
            qkv = (y @ qkv_w.T).reshape(B, N, 3, H, d)
            q, k, v = (qkv[:, :, 0], qkv[:, :, 1], qkv[:, :, 2])
            q = q * d ** (-0.5)
            attn = jnp.einsum('bnhd,bmhd->bhnm', q, k)
            attn = jnp.einsum('bhnm,gh->bgnm', attn, pre_w) + pre_b[None, :, None, None]
            attn = jax.nn.softmax(attn, axis=-1)
            attn = jnp.einsum('bhnm,gh->bgnm', attn, post_w) + post_b[None, :, None, None]
            _x_attn_unused = jnp.einsum('bhnm,bmhd->bnhd', attn, v).reshape(B, N, C)
            return y @ proj_w.T + proj_b
        B, N, C, H = (16, 128, 128, 16)
        hidden = 4 * C
        key = jax.random.key(seed)
        ks = jax.random.split(key, 12)
        s = 0.02
        return {'x': jax.random.normal(ks[0], (B, N, C), jnp.float32), 'ln1_g': jnp.ones((C,), jnp.float32), 'ln1_b': jnp.zeros((C,), jnp.float32), 'qkv_w': jax.random.normal(ks[1], (3 * C, C), jnp.float32) * s, 'proj_w': jax.random.normal(ks[2], (C, C), jnp.float32) * s, 'proj_b': jnp.zeros((C,), jnp.float32), 'pre_w': jax.random.normal(ks[3], (H, H), jnp.float32) * s, 'pre_b': jnp.zeros((H,), jnp.float32), 'post_w': jax.random.normal(ks[4], (H, H), jnp.float32) * s, 'post_b': jnp.zeros((H,), jnp.float32), 'ln2_g': jnp.ones((C,), jnp.float32), 'ln2_b': jnp.zeros((C,), jnp.float32), 'fc1_w': jax.random.normal(ks[5], (hidden, C), jnp.float32) * s, 'fc1_b': jnp.zeros((hidden,), jnp.float32), 'lnh_g': jnp.ones((hidden,), jnp.float32), 'lnh_b': jnp.zeros((hidden,), jnp.float32), 'fc2_w': jax.random.normal(ks[6], (C, hidden), jnp.float32) * s, 'fc2_b': jnp.zeros((C,), jnp.float32), 'gamma1': 0.0001 * jnp.ones((C,), jnp.float32), 'gamma2': 0.0001 * jnp.ones((C,), jnp.float32)}
    _L2_attn_all = _L2_attn_setup()
    _L2_attn_in = {k: v for k, v in _L2_attn_all.items() if k in ('ln1_g', 'ln1_b', 'qkv_w', 'proj_w', 'proj_b', 'pre_w', 'pre_b', 'post_w', 'post_b', 'ln2_g', 'ln2_b', 'fc1_w', 'fc1_b', 'lnh_g', 'lnh_b', 'fc2_w', 'fc2_b', 'gamma1', 'gamma2')}
    del _L2_attn_all

    def _L2_ffn_setup():
        import jax, jax.numpy as jnp
        import numpy as np
        B, T, D, H, E, K = (2, 256, 128, 512, 8, 2)
        EPS = 1e-12

        def moe_forward(x, Wg, bg, W1, b1, W2, b2):
            gates = jax.nn.softmax(x @ Wg + bg, axis=-1)
            _, top_idx = jax.lax.top_k(gates, K)
            mask = jax.nn.one_hot(top_idx, E, dtype=gates.dtype).sum(axis=-2)
            g = gates * mask
            g = g / jnp.maximum(jnp.sum(jnp.abs(g), axis=-1, keepdims=True), EPS)
            h = jnp.einsum('btd,edh->bteh', x, W1) + b1[None, None]
            h = jax.nn.gelu(h, approximate=False)
            eo = jnp.einsum('bteh,ehd->bted', h, W2) + b2[None, None]
            return jnp.einsum('bte,bted->btd', g, eo)
        key = jax.random.key(seed)
        ks = jax.random.split(key, 8)
        s_d = 1.0 / np.sqrt(D)
        s_h = 1.0 / np.sqrt(H)
        return {'x': jax.random.normal(ks[0], (B, T, D), dtype=jnp.float32), 'Wg': jax.random.uniform(ks[1], (D, E), jnp.float32, -s_d, s_d), 'bg': jax.random.uniform(ks[2], (E,), jnp.float32, -s_d, s_d), 'W1': jax.random.uniform(ks[3], (E, D, H), jnp.float32, -s_d, s_d), 'b1': jax.random.uniform(ks[4], (E, H), jnp.float32, -s_d, s_d), 'W2': jax.random.uniform(ks[5], (E, H, D), jnp.float32, -s_h, s_h), 'b2': jax.random.uniform(ks[6], (E, D), jnp.float32, -s_h, s_h)}
    _L2_ffn_all = _L2_ffn_setup()
    _L2_ffn_in = {k: v for k, v in _L2_ffn_all.items() if k in ('Wg', 'bg', 'W1', 'b1', 'W2', 'b2')}
    del _L2_ffn_all

    def _L3_xattn_setup():
        import jax, jax.numpy as jnp
        import numpy as np
        DIM = 128
        HEAD_DIM = 64
        NUM_HEADS = 8
        INNER = HEAD_DIM * NUM_HEADS
        ROT_DIM = HEAD_DIM
        ROPE_BASE = 10000.0
        EPS = 1e-05

        def layer_norm(x, g, b):
            mu = jnp.mean(x, axis=-1, keepdims=True)
            var = jnp.var(x, axis=-1, keepdims=True)
            return (x - mu) * jax.lax.rsqrt(var + EPS) * g + b

        def rope_rotate_k(k):
            n = k.shape[1]
            half = ROT_DIM // 2
            inv_freq = 1.0 / ROPE_BASE ** (jnp.arange(0, ROT_DIM, 2, dtype=jnp.float32) / ROT_DIM)
            theta = jnp.arange(n, dtype=jnp.float32)[:, None] * inv_freq[None, :]
            angles = jnp.concatenate([theta, theta], axis=-1)
            cos = jnp.cos(angles)[None, :, None, :].astype(k.dtype)
            sin = jnp.sin(angles)[None, :, None, :].astype(k.dtype)
            k_rope, k_pass = (k[..., :ROT_DIM], k[..., ROT_DIM:])
            neg_half = jnp.concatenate([-k_rope[..., half:], k_rope[..., :half]], axis=-1)
            k_rope = k_rope * cos + neg_half * sin
            return jnp.concatenate([k_rope, k_pass], axis=-1)
        key = jax.random.key(seed)
        ks = jax.random.split(key, 5)
        b, n, m = (8, 1024, 64)
        s = 1.0 / np.sqrt(DIM)
        return {'x': jax.random.normal(ks[0], (b, n, DIM), jnp.float32), 'latents': jax.random.normal(ks[1], (b, m, DIM), jnp.float32), 'gamma_x': jnp.ones((DIM,), jnp.float32), 'beta_x': jnp.zeros((DIM,), jnp.float32), 'gamma_l': jnp.ones((DIM,), jnp.float32), 'beta_l': jnp.zeros((DIM,), jnp.float32), 'Wq': jax.random.normal(ks[2], (DIM, INNER), jnp.float32) * s, 'Wkv': jax.random.normal(ks[3], (DIM, 2 * INNER), jnp.float32) * s, 'Wo': jax.random.normal(ks[4], (INNER, DIM), jnp.float32) * (1.0 / np.sqrt(INNER))}
    _L3_xattn_all = _L3_xattn_setup()
    _L3_xattn_in = {k: v for k, v in _L3_xattn_all.items() if k in ('gamma_x', 'beta_x', 'gamma_l', 'beta_l', 'Wq', 'Wkv', 'Wo')}
    del _L3_xattn_all

    def _L3_attn_setup():
        import jax, jax.numpy as jnp
        import numpy as np
        import math
        B, T, C = (2, 256, 128)
        H, L = (16, 64)
        DH = C // H
        DHE = DH // 2
        THETA = 10000.0

        def _rope_cache(t, dim):
            inv_freq = 1.0 / THETA ** (jnp.arange(0, dim, 2, dtype=jnp.float32) / dim)
            freqs = jnp.arange(t, dtype=jnp.float32)[:, None] * inv_freq[None, :]
            emb = jnp.concatenate((freqs, freqs), axis=-1)
            return (jnp.cos(emb), jnp.sin(emb))

        def _apply_rope(x, cos, sin):
            x1 = x[..., 0::2]
            x2 = x[..., 1::2]
            rot = jnp.stack((-x2, x1), axis=-1).reshape(x.shape)
            return x * cos[None, None] + rot * sin[None, None]
        key = jax.random.key(seed)
        ks = jax.random.split(key, 10)
        s = 0.02
        return {'x': jax.random.normal(ks[0], (B, T, C), jnp.float32), 'Wq_down': jax.random.normal(ks[1], (C, H * L), jnp.float32) * s, 'Wk_down': jax.random.normal(ks[2], (C, H * L), jnp.float32) * s, 'Wv_down': jax.random.normal(ks[3], (C, H * L), jnp.float32) * s, 'Wq_up_c': jax.random.normal(ks[4], (L, DHE), jnp.float32) * s, 'Wq_up_e': jax.random.normal(ks[5], (L, DHE), jnp.float32) * s, 'Wk_up_c': jax.random.normal(ks[6], (L, DHE), jnp.float32) * s, 'Wk_up_e': jax.random.normal(ks[7], (L, DHE), jnp.float32) * s, 'Wv_up': jax.random.normal(ks[8], (L, DH), jnp.float32) * s, 'Wc': jax.random.normal(ks[9], (C, C), jnp.float32) * s}
    _L3_attn_all = _L3_attn_setup()
    _L3_attn_in = {k: v for k, v in _L3_attn_all.items() if k in ('Wq_down', 'Wk_down', 'Wv_down', 'Wq_up_c', 'Wq_up_e', 'Wk_up_c', 'Wk_up_e', 'Wv_up', 'Wc')}
    del _L3_attn_all

    def _L3_ffn_setup():
        import jax, jax.numpy as jnp
        import numpy as np
        from jax import lax
        T, B, I, M, O = (32, 64, 128, 128, 128)

        def _xavier(key, shape):
            fan_out, fan_in = shape
            limit = float(np.sqrt(6.0 / (fan_in + fan_out)))
            return jax.random.uniform(key, shape, jnp.float32, -limit, limit)
        key = jax.random.key(seed)
        ks = jax.random.split(key, 9)
        x = jax.random.normal(ks[0], (T, B, I), jnp.float32)
        return {'x': x, 'wf': _xavier(ks[1], (M, I)), 'uf': _xavier(ks[2], (M, M)), 'bf': jnp.zeros((M,), jnp.float32), 'wi': _xavier(ks[3], (M, I)), 'ui': _xavier(ks[4], (M, M)), 'bi': jnp.zeros((M,), jnp.float32), 'wc': _xavier(ks[5], (M, I)), 'uc': _xavier(ks[6], (M, M)), 'bc': jnp.zeros((M,), jnp.float32), 'wo': _xavier(ks[7], (O, I)), 'uo': _xavier(ks[8], (O, M)), 'bo': jnp.zeros((O,), jnp.float32), 'in_c': jnp.zeros((M,), jnp.float32)}
    _L3_ffn_all = _L3_ffn_setup()
    _L3_ffn_in = {k: v for k, v in _L3_ffn_all.items() if k in ('wf', 'uf', 'bf', 'wi', 'ui', 'bi', 'wc', 'uc', 'bc', 'wo', 'uo', 'bo', 'in_c')}
    del _L3_ffn_all
    return {'x': x, 'ctx_1024': ctx_1024, 'mask_BxS2_bk1': mask_BxS2_bk1, 'L0_xattn_Wq': _L0_xattn_in['Wq'], 'L0_xattn_Wkv': _L0_xattn_in['Wkv'], 'L0_xattn_Wo': _L0_xattn_in['Wo'], 'L0_xattn_ln_x_g': _L0_xattn_in['ln_x_g'], 'L0_xattn_ln_x_b': _L0_xattn_in['ln_x_b'], 'L0_xattn_ln_l_g': _L0_xattn_in['ln_l_g'], 'L0_xattn_ln_l_b': _L0_xattn_in['ln_l_b'], 'L0_xattn_ln_o_g': _L0_xattn_in['ln_o_g'], 'L0_xattn_ln_o_b': _L0_xattn_in['ln_o_b'], 'L0_attn_Wq': _L0_attn_in['Wq'], 'L0_attn_Wk': _L0_attn_in['Wk'], 'L0_attn_Wv': _L0_attn_in['Wv'], 'L0_attn_Wog': _L0_attn_in['Wog'], 'L0_attn_Wi': _L0_attn_in['Wi'], 'L0_attn_bi': _L0_attn_in['bi'], 'L0_attn_Wf': _L0_attn_in['Wf'], 'L0_attn_bf': _L0_attn_in['bf'], 'L0_attn_ln_w': _L0_attn_in['ln_w'], 'L0_attn_ln_b': _L0_attn_in['ln_b'], 'L0_attn_Wout': _L0_attn_in['Wout'], 'L0_ffn_Wg': _L0_ffn_in['Wg'], 'L0_ffn_W1': _L0_ffn_in['W1'], 'L0_ffn_b1': _L0_ffn_in['b1'], 'L0_ffn_W2': _L0_ffn_in['W2'], 'L0_ffn_b2': _L0_ffn_in['b2'], 'L1_xattn_W_q': _L1_xattn_in['W_q'], 'L1_xattn_W_k': _L1_xattn_in['W_k'], 'L1_xattn_W_v': _L1_xattn_in['W_v'], 'L1_xattn_W_o': _L1_xattn_in['W_o'], 'L1_xattn_b_o': _L1_xattn_in['b_o'], 'L1_attn_Wq': _L1_attn_in['Wq'], 'L1_attn_Wk': _L1_attn_in['Wk'], 'L1_attn_fc1_w': _L1_attn_in['fc1_w'], 'L1_attn_fc1_b': _L1_attn_in['fc1_b'], 'L1_attn_fc2_w': _L1_attn_in['fc2_w'], 'L1_attn_fc2_b': _L1_attn_in['fc2_b'], 'L1_ffn_w12': _L1_ffn_in['w12'], 'L1_ffn_w3': _L1_ffn_in['w3'], 'L1_ffn_gate_w': _L1_ffn_in['gate_w'], 'L2_xattn_Wq': _L2_xattn_in['Wq'], 'L2_xattn_bq': _L2_xattn_in['bq'], 'L2_xattn_Wk': _L2_xattn_in['Wk'], 'L2_xattn_bk': _L2_xattn_in['bk'], 'L2_xattn_Wv': _L2_xattn_in['Wv'], 'L2_xattn_bv': _L2_xattn_in['bv'], 'L2_attn_ln1_g': _L2_attn_in['ln1_g'], 'L2_attn_ln1_b': _L2_attn_in['ln1_b'], 'L2_attn_qkv_w': _L2_attn_in['qkv_w'], 'L2_attn_proj_w': _L2_attn_in['proj_w'], 'L2_attn_proj_b': _L2_attn_in['proj_b'], 'L2_attn_pre_w': _L2_attn_in['pre_w'], 'L2_attn_pre_b': _L2_attn_in['pre_b'], 'L2_attn_post_w': _L2_attn_in['post_w'], 'L2_attn_post_b': _L2_attn_in['post_b'], 'L2_attn_ln2_g': _L2_attn_in['ln2_g'], 'L2_attn_ln2_b': _L2_attn_in['ln2_b'], 'L2_attn_fc1_w': _L2_attn_in['fc1_w'], 'L2_attn_fc1_b': _L2_attn_in['fc1_b'], 'L2_attn_lnh_g': _L2_attn_in['lnh_g'], 'L2_attn_lnh_b': _L2_attn_in['lnh_b'], 'L2_attn_fc2_w': _L2_attn_in['fc2_w'], 'L2_attn_fc2_b': _L2_attn_in['fc2_b'], 'L2_attn_gamma1': _L2_attn_in['gamma1'], 'L2_attn_gamma2': _L2_attn_in['gamma2'], 'L2_ffn_Wg': _L2_ffn_in['Wg'], 'L2_ffn_bg': _L2_ffn_in['bg'], 'L2_ffn_W1': _L2_ffn_in['W1'], 'L2_ffn_b1': _L2_ffn_in['b1'], 'L2_ffn_W2': _L2_ffn_in['W2'], 'L2_ffn_b2': _L2_ffn_in['b2'], 'L3_xattn_gamma_x': _L3_xattn_in['gamma_x'], 'L3_xattn_beta_x': _L3_xattn_in['beta_x'], 'L3_xattn_gamma_l': _L3_xattn_in['gamma_l'], 'L3_xattn_beta_l': _L3_xattn_in['beta_l'], 'L3_xattn_Wq': _L3_xattn_in['Wq'], 'L3_xattn_Wkv': _L3_xattn_in['Wkv'], 'L3_xattn_Wo': _L3_xattn_in['Wo'], 'L3_attn_Wq_down': _L3_attn_in['Wq_down'], 'L3_attn_Wk_down': _L3_attn_in['Wk_down'], 'L3_attn_Wv_down': _L3_attn_in['Wv_down'], 'L3_attn_Wq_up_c': _L3_attn_in['Wq_up_c'], 'L3_attn_Wq_up_e': _L3_attn_in['Wq_up_e'], 'L3_attn_Wk_up_c': _L3_attn_in['Wk_up_c'], 'L3_attn_Wk_up_e': _L3_attn_in['Wk_up_e'], 'L3_attn_Wv_up': _L3_attn_in['Wv_up'], 'L3_attn_Wc': _L3_attn_in['Wc'], 'L3_ffn_wf': _L3_ffn_in['wf'], 'L3_ffn_uf': _L3_ffn_in['uf'], 'L3_ffn_bf': _L3_ffn_in['bf'], 'L3_ffn_wi': _L3_ffn_in['wi'], 'L3_ffn_ui': _L3_ffn_in['ui'], 'L3_ffn_bi': _L3_ffn_in['bi'], 'L3_ffn_wc': _L3_ffn_in['wc'], 'L3_ffn_uc': _L3_ffn_in['uc'], 'L3_ffn_bc': _L3_ffn_in['bc'], 'L3_ffn_wo': _L3_ffn_in['wo'], 'L3_ffn_uo': _L3_ffn_in['uo'], 'L3_ffn_bo': _L3_ffn_in['bo'], 'L3_ffn_in_c': _L3_ffn_in['in_c']}

def reference(x, ctx_1024, mask_BxS2_bk1, L0_xattn_Wq, L0_xattn_Wkv, L0_xattn_Wo, L0_xattn_ln_x_g, L0_xattn_ln_x_b, L0_xattn_ln_l_g, L0_xattn_ln_l_b, L0_xattn_ln_o_g, L0_xattn_ln_o_b, L0_attn_Wq, L0_attn_Wk, L0_attn_Wv, L0_attn_Wog, L0_attn_Wi, L0_attn_bi, L0_attn_Wf, L0_attn_bf, L0_attn_ln_w, L0_attn_ln_b, L0_attn_Wout, L0_ffn_Wg, L0_ffn_W1, L0_ffn_b1, L0_ffn_W2, L0_ffn_b2, L1_xattn_W_q, L1_xattn_W_k, L1_xattn_W_v, L1_xattn_W_o, L1_xattn_b_o, L1_attn_Wq, L1_attn_Wk, L1_attn_fc1_w, L1_attn_fc1_b, L1_attn_fc2_w, L1_attn_fc2_b, L1_ffn_w12, L1_ffn_w3, L1_ffn_gate_w, L2_xattn_Wq, L2_xattn_bq, L2_xattn_Wk, L2_xattn_bk, L2_xattn_Wv, L2_xattn_bv, L2_attn_ln1_g, L2_attn_ln1_b, L2_attn_qkv_w, L2_attn_proj_w, L2_attn_proj_b, L2_attn_pre_w, L2_attn_pre_b, L2_attn_post_w, L2_attn_post_b, L2_attn_ln2_g, L2_attn_ln2_b, L2_attn_fc1_w, L2_attn_fc1_b, L2_attn_lnh_g, L2_attn_lnh_b, L2_attn_fc2_w, L2_attn_fc2_b, L2_attn_gamma1, L2_attn_gamma2, L2_ffn_Wg, L2_ffn_bg, L2_ffn_W1, L2_ffn_b1, L2_ffn_W2, L2_ffn_b2, L3_xattn_gamma_x, L3_xattn_beta_x, L3_xattn_gamma_l, L3_xattn_beta_l, L3_xattn_Wq, L3_xattn_Wkv, L3_xattn_Wo, L3_attn_Wq_down, L3_attn_Wk_down, L3_attn_Wv_down, L3_attn_Wq_up_c, L3_attn_Wq_up_e, L3_attn_Wk_up_c, L3_attn_Wk_up_e, L3_attn_Wv_up, L3_attn_Wc, L3_ffn_wf, L3_ffn_uf, L3_ffn_bf, L3_ffn_wi, L3_ffn_ui, L3_ffn_bi, L3_ffn_wc, L3_ffn_uc, L3_ffn_bc, L3_ffn_wo, L3_ffn_uo, L3_ffn_bo, L3_ffn_in_c):
    import jax
    import jax.numpy as jnp

    def _L0_xattn_ref(x, latents, mask, Wq, Wkv, Wo, ln_x_g, ln_x_b, ln_l_g, ln_l_b, ln_o_g, ln_o_b):
        import jax, jax.numpy as jnp
        import numpy as np
        DIM = 128
        DIM_HEAD = 64
        HEADS = 8
        INNER = DIM_HEAD * HEADS
        EPS = 1e-05

        def layernorm(x, g, b):
            mu = jnp.mean(x, axis=-1, keepdims=True)
            var = jnp.var(x, axis=-1, keepdims=True)
            return (x - mu) * jax.lax.rsqrt(var + EPS) * g + b
        scale = DIM_HEAD ** (-0.5)
        b, m = (latents.shape[0], latents.shape[1])
        xn = layernorm(x, ln_x_g, ln_x_b)
        ln = layernorm(latents, ln_l_g, ln_l_b)
        q = ln @ Wq
        kv_in = jnp.concatenate([xn, ln], axis=1)
        kv = kv_in @ Wkv
        k, v = jnp.split(kv, 2, axis=-1)
        q = q.reshape(b, m, HEADS, DIM_HEAD).transpose(0, 2, 1, 3)
        k = k.reshape(b, k.shape[1], HEADS, DIM_HEAD).transpose(0, 2, 1, 3)
        v = v.reshape(b, v.shape[1], HEADS, DIM_HEAD).transpose(0, 2, 1, 3)
        sim = jnp.einsum('bhid,bhjd->bhij', q * scale, k) * scale
        full_mask = jnp.concatenate([mask, jnp.ones((b, m), dtype=bool)], axis=1)
        max_neg = -jnp.finfo(sim.dtype).max
        sim = jnp.where(full_mask[:, None, None, :], sim, max_neg)
        attn = jax.nn.softmax(sim.astype(jnp.float32), axis=-1).astype(sim.dtype)
        out = jnp.einsum('bhij,bhjd->bhid', attn, v)
        out = out.transpose(0, 2, 1, 3).reshape(b, m, INNER)
        out = out @ Wo
        return layernorm(out, ln_o_g, ln_o_b)

    def _L0_attn_ref(x, Wq, Wk, Wv, Wog, Wi, bi, Wf, bf, ln_w, ln_b, Wout):
        import jax, jax.numpy as jnp
        import numpy as np
        B, S, D = (2, 128, 128)
        NH = 8
        QK = D // 2
        V = D
        DQK = QK // NH
        DV = V // NH
        CAP = 15.0
        EPS = 1e-06

        def soft_cap(t, cap=CAP):
            return cap * jnp.tanh(t / cap)

        def _mlstm_forward(x, Wq, Wk, Wv, Wog, Wi, bi, Wf, bf, ln_w, ln_b, Wout):
            Bx, Sx, _ = x.shape
            q = (x @ Wq.T).reshape(Bx, Sx, NH, DQK)
            k = (x @ Wk.T).reshape(Bx, Sx, NH, DQK)
            v = (x @ Wv.T).reshape(Bx, Sx, NH, DV)
            o_preact = x @ Wog.T
            i_pre = soft_cap(x @ Wi.T + bi)
            f_pre = soft_cap(x @ Wf.T + bf)
            qT = jnp.moveaxis(q, 1, 0)
            kT = jnp.moveaxis(k, 1, 0)
            vT = jnp.moveaxis(v, 1, 0)
            iT = jnp.moveaxis(i_pre, 1, 0)
            fT = jnp.moveaxis(f_pre, 1, 0)
            qk_scale = DQK ** (-0.5)

            def step(carry, inp):
                C, n, m = carry
                q_t, k_t, v_t, i_t, f_t = inp
                m_new = jnp.maximum(f_t + m, i_t)
                f_act = jnp.exp(f_t + m - m_new)
                i_act = jnp.exp(i_t - m_new)
                C = f_act[..., None, None] * C + i_act[..., None, None] * (k_t[..., :, None] * v_t[..., None, :])
                n = f_act[..., None] * n + i_act[..., None] * k_t
                qs = q_t * qk_scale
                num = jnp.einsum('bhk,bhkv->bhv', qs, C)
                qn = jnp.einsum('bhk,bhk->bh', qs, n)
                denom = jnp.maximum(jnp.abs(qn), jnp.exp(-m_new)) + 1e-06
                h_t = num / denom[..., None]
                return ((C, n, m_new), h_t)
            C0 = jnp.zeros((Bx, NH, DQK, DV), x.dtype)
            n0 = jnp.zeros((Bx, NH, DQK), x.dtype)
            m0 = jnp.zeros((Bx, NH), x.dtype)
            _, hs = jax.lax.scan(step, (C0, n0, m0), (qT, kT, vT, iT, fT))
            h = jnp.moveaxis(hs, 0, 1).reshape(Bx, Sx, NH * DV)
            mu = jnp.mean(h, axis=-1, keepdims=True)
            var = jnp.mean((h - mu) ** 2, axis=-1, keepdims=True)
            h_norm = (h - mu) * jax.lax.rsqrt(var + EPS) * ln_w + ln_b
            h_out = jax.nn.sigmoid(o_preact) * h_norm
            y = h_out @ Wout.T
            return y
        return _mlstm_forward(x, Wq, Wk, Wv, Wog, Wi, bi, Wf, bf, ln_w, ln_b, Wout)

    def _L0_ffn_ref(x, Wg, W1, b1, W2, b2):
        import jax, jax.numpy as jnp
        import numpy as np
        NUM_EXPERTS = 8
        TOP_K = 2
        B, S, D = x.shape
        E, _, H = W1.shape
        OUT = W2.shape[2]
        xm = x.reshape(-1, D)
        logits = xm @ Wg
        probs = jax.nn.softmax(logits, axis=-1)
        topk_p, topk_i = jax.lax.top_k(probs, TOP_K)
        flat_e = topk_i.reshape(-1)
        flat_p = topk_p.reshape(-1)
        order = jnp.argsort(flat_e)
        tok_idx = order // TOP_K
        e_sorted = flat_e[order]
        p_sorted = flat_p[order]
        xs = xm[tok_idx]
        y = jnp.zeros((xs.shape[0], OUT), dtype=xs.dtype)
        for e in range(E):
            h = jax.nn.relu(xs @ W1[e] + b1[e])
            ye = h @ W2[e] + b2[e]
            m = (e_sorted == e)[:, None].astype(xs.dtype)
            y = y + m * ye
        y = y * p_sorted[:, None]
        out = jnp.zeros((B * S, OUT), dtype=y.dtype).at[tok_idx].add(y)
        return out.reshape(B, S, OUT)

    def _L1_xattn_ref(x, context, W_q, W_k, W_v, W_o, b_o):
        import jax, jax.numpy as jnp
        import numpy as np
        DIM = 128
        HEADS = 16
        DIM_HEAD = 64
        INNER = HEADS * DIM_HEAD
        CTX_DIM = 128
        b, n, _ = x.shape
        m = context.shape[1]
        h, d = (HEADS, DIM_HEAD)
        q = (x @ W_q).reshape(b, n, h, d).transpose(0, 2, 1, 3)
        k = (context @ W_k).reshape(b, m, h, d).transpose(0, 2, 1, 3)
        v = (context @ W_v).reshape(b, m, h, d).transpose(0, 2, 1, 3)
        sim = jnp.einsum('bhnd,bhmd->bhnm', q, k) * d ** (-0.5)
        attn = jax.nn.softmax(sim, axis=-1)
        out = jnp.einsum('bhnm,bhmd->bhnd', attn, v)
        out = out.transpose(0, 2, 1, 3).reshape(b, n, h * d)
        return out @ W_o + b_o

    def _L1_attn_ref(hidden_states, Wq, Wk, fc1_w, fc1_b, fc2_w, fc2_b):
        import jax, jax.numpy as jnp
        import numpy as np
        DIM = 128
        HEADS = 1
        HDIM = DIM // HEADS
        INNER = 16
        B, L = (2, 512)
        ROPE_BASE = 32.0

        def _apply_rope(x, pos, base):
            d = x.shape[-1]
            inv_freq = base ** (-jnp.arange(0, d, 2, dtype=jnp.float32) / d)
            ang = pos[:, None].astype(jnp.float32) * inv_freq
            emb = jnp.concatenate([ang, ang], axis=-1)
            cos = jnp.cos(emb)[None, :, None, :].astype(x.dtype)
            sin = jnp.sin(emb)[None, :, None, :].astype(x.dtype)
            x1, x2 = (x[..., :d // 2], x[..., d // 2:])
            rot = jnp.concatenate([-x2, x1], axis=-1)
            return x * cos + rot * sin
        b, l, _ = hidden_states.shape
        q = (hidden_states @ Wq.T).reshape(b, l, HEADS, HDIM).astype(jnp.bfloat16)
        k = (hidden_states @ Wk.T).reshape(b, l, HEADS, HDIM).astype(jnp.bfloat16)
        pos = jnp.arange(l)
        q = _apply_rope(q, pos, ROPE_BASE)
        k = _apply_rope(k, pos, ROPE_BASE)
        scores = jnp.einsum('bqhd,bkhd->bhqk', q.astype(jnp.float32), k.astype(jnp.float32)) / HDIM ** 0.5
        causal = jnp.tril(jnp.ones((l, l), dtype=bool))
        exp_qk = jnp.where(causal[None, None], jnp.exp(scores), 0.0)
        o = jnp.swapaxes(exp_qk.sum(axis=-1), 1, 2)
        o = jax.nn.relu(o @ fc1_w.T + fc1_b)
        return o @ fc2_w.T + fc2_b

    def _L1_ffn_ref(x, w12, w3, gate_w):
        import jax, jax.numpy as jnp
        import numpy as np
        TOP_K = 2
        E = gate_w.shape[0]
        H = w3.shape[-1]
        scores = jnp.einsum('btd,ed->bte', x, gate_w)
        topk_scores, topk_idx = jax.lax.top_k(scores, TOP_K)
        topk_probs = jax.nn.softmax(topk_scores, axis=-1)
        total_probs = jnp.sum(jax.nn.one_hot(topk_idx, E, dtype=topk_probs.dtype) * topk_probs[..., None], axis=-2)
        h12 = jnp.einsum('btd,ehd->bteh', x, w12)
        h1, h2 = (h12[..., :H], h12[..., H:])
        hidden = jax.nn.silu(h1) * h2
        expert_out = jnp.einsum('bteh,edh->bted', hidden, w3)
        y = jnp.sum(total_probs[..., None] * expert_out, axis=-2)
        return y

    def _L2_xattn_ref(query, key, value, Wq, bq, Wk, bk, Wv, bv):
        import jax, jax.numpy as jnp
        import numpy as np
        B, S, E = (4, 256, 128)
        q = query @ Wq + bq
        k = key @ Wk + bk
        v = value @ Wv + bv
        inv_scale = jnp.asarray(E, q.dtype) ** 0.5
        scores = jnp.einsum('bse,bte->bst', q, k) / inv_scale
        attn = jax.nn.softmax(scores, axis=-1)
        out = jnp.einsum('bst,bte->bse', attn, v)
        return out

    def _L2_attn_ref(x, ln1_g, ln1_b, qkv_w, proj_w, proj_b, pre_w, pre_b, post_w, post_b, ln2_g, ln2_b, fc1_w, fc1_b, lnh_g, lnh_b, fc2_w, fc2_b, gamma1, gamma2):
        import jax, jax.numpy as jnp
        import numpy as np
        EPS = 1e-05

        def _ln(x, g, b):
            mu = jnp.mean(x, axis=-1, keepdims=True)
            var = jnp.var(x, axis=-1, keepdims=True)
            return (x - mu) * jax.lax.rsqrt(var + EPS) * g + b

        def _talking_head_attn(y, qkv_w, proj_w, proj_b, pre_w, pre_b, post_w, post_b, num_heads):
            B, N, C = y.shape
            H = num_heads
            d = C // H
            qkv = (y @ qkv_w.T).reshape(B, N, 3, H, d)
            q, k, v = (qkv[:, :, 0], qkv[:, :, 1], qkv[:, :, 2])
            q = q * d ** (-0.5)
            attn = jnp.einsum('bnhd,bmhd->bhnm', q, k)
            attn = jnp.einsum('bhnm,gh->bgnm', attn, pre_w) + pre_b[None, :, None, None]
            attn = jax.nn.softmax(attn, axis=-1)
            attn = jnp.einsum('bhnm,gh->bgnm', attn, post_w) + post_b[None, :, None, None]
            _x_attn_unused = jnp.einsum('bhnm,bmhd->bnhd', attn, v).reshape(B, N, C)
            return y @ proj_w.T + proj_b
        H = pre_w.shape[0]
        y = _ln(x, ln1_g, ln1_b)
        x = x + gamma1 * _talking_head_attn(y, qkv_w, proj_w, proj_b, pre_w, pre_b, post_w, post_b, H)
        z = _ln(x, ln2_g, ln2_b)
        h = jax.nn.gelu(z @ fc1_w.T + fc1_b, approximate=False)
        h = _ln(h, lnh_g, lnh_b)
        m = h @ fc2_w.T + fc2_b
        return x + gamma2 * m

    def _L2_ffn_ref(x, Wg, bg, W1, b1, W2, b2):
        import jax, jax.numpy as jnp
        import numpy as np
        B, T, D, H, E, K = (2, 256, 128, 512, 8, 2)
        EPS = 1e-12

        def moe_forward(x, Wg, bg, W1, b1, W2, b2):
            gates = jax.nn.softmax(x @ Wg + bg, axis=-1)
            _, top_idx = jax.lax.top_k(gates, K)
            mask = jax.nn.one_hot(top_idx, E, dtype=gates.dtype).sum(axis=-2)
            g = gates * mask
            g = g / jnp.maximum(jnp.sum(jnp.abs(g), axis=-1, keepdims=True), EPS)
            h = jnp.einsum('btd,edh->bteh', x, W1) + b1[None, None]
            h = jax.nn.gelu(h, approximate=False)
            eo = jnp.einsum('bteh,ehd->bted', h, W2) + b2[None, None]
            return jnp.einsum('bte,bted->btd', g, eo)
        return moe_forward(x, Wg, bg, W1, b1, W2, b2)

    def _L3_xattn_ref(x, latents, gamma_x, beta_x, gamma_l, beta_l, Wq, Wkv, Wo):
        import jax, jax.numpy as jnp
        import numpy as np
        DIM = 128
        HEAD_DIM = 64
        NUM_HEADS = 8
        INNER = HEAD_DIM * NUM_HEADS
        ROT_DIM = HEAD_DIM
        ROPE_BASE = 10000.0
        EPS = 1e-05

        def layer_norm(x, g, b):
            mu = jnp.mean(x, axis=-1, keepdims=True)
            var = jnp.var(x, axis=-1, keepdims=True)
            return (x - mu) * jax.lax.rsqrt(var + EPS) * g + b

        def rope_rotate_k(k):
            n = k.shape[1]
            half = ROT_DIM // 2
            inv_freq = 1.0 / ROPE_BASE ** (jnp.arange(0, ROT_DIM, 2, dtype=jnp.float32) / ROT_DIM)
            theta = jnp.arange(n, dtype=jnp.float32)[:, None] * inv_freq[None, :]
            angles = jnp.concatenate([theta, theta], axis=-1)
            cos = jnp.cos(angles)[None, :, None, :].astype(k.dtype)
            sin = jnp.sin(angles)[None, :, None, :].astype(k.dtype)
            k_rope, k_pass = (k[..., :ROT_DIM], k[..., ROT_DIM:])
            neg_half = jnp.concatenate([-k_rope[..., half:], k_rope[..., :half]], axis=-1)
            k_rope = k_rope * cos + neg_half * sin
            return jnp.concatenate([k_rope, k_pass], axis=-1)
        b, n, _ = x.shape
        m = latents.shape[1]
        h, d = (NUM_HEADS, HEAD_DIM)
        scale = d ** (-0.5)
        xn = layer_norm(x, gamma_x, beta_x)
        ln = layer_norm(latents, gamma_l, beta_l)
        q = (ln @ Wq).reshape(b, m, h, d)
        kv_x = xn @ Wkv
        k_x, v_x = (kv_x[..., :INNER], kv_x[..., INNER:])
        kv_l = ln @ Wkv
        k_l, v_l = (kv_l[..., :INNER], kv_l[..., INNER:])
        k_x = k_x.reshape(b, n, h, d)
        v_x = v_x.reshape(b, n, h, d)
        k_x = rope_rotate_k(k_x)
        q = jnp.transpose(q, (0, 2, 1, 3)) * scale
        k_x = jnp.transpose(k_x, (0, 2, 1, 3))
        v_x = jnp.transpose(v_x, (0, 2, 1, 3))
        k_l = jnp.transpose(k_l.reshape(b, m, h, d), (0, 2, 1, 3))
        v_l = jnp.transpose(v_l.reshape(b, m, h, d), (0, 2, 1, 3))
        k = jnp.concatenate([k_x, k_l], axis=2)
        v = jnp.concatenate([v_x, v_l], axis=2)
        sim = jnp.einsum('bhid,bhjd->bhij', q, k)
        attn = jax.nn.softmax(sim, axis=-1)
        out = jnp.einsum('bhij,bhjd->bhid', attn, v)
        out = jnp.transpose(out, (0, 2, 1, 3)).reshape(b, m, INNER)
        return out @ Wo

    def _L3_attn_ref(x, Wq_down, Wk_down, Wv_down, Wq_up_c, Wq_up_e, Wk_up_c, Wk_up_e, Wv_up, Wc):
        import jax, jax.numpy as jnp
        import numpy as np
        import math
        B, T, C = (2, 256, 128)
        H, L = (16, 64)
        DH = C // H
        DHE = DH // 2
        THETA = 10000.0

        def _rope_cache(t, dim):
            inv_freq = 1.0 / THETA ** (jnp.arange(0, dim, 2, dtype=jnp.float32) / dim)
            freqs = jnp.arange(t, dtype=jnp.float32)[:, None] * inv_freq[None, :]
            emb = jnp.concatenate((freqs, freqs), axis=-1)
            return (jnp.cos(emb), jnp.sin(emb))

        def _apply_rope(x, cos, sin):
            x1 = x[..., 0::2]
            x2 = x[..., 1::2]
            rot = jnp.stack((-x2, x1), axis=-1).reshape(x.shape)
            return x * cos[None, None] + rot * sin[None, None]
        b, t, c = x.shape
        q_lat = (x @ Wq_down).reshape(b, t, H, L)
        k_lat = (x @ Wk_down).reshape(b, t, H, L)
        v_lat = (x @ Wv_down).reshape(b, t, H, L)
        q_c = jnp.einsum('bthl,ld->bhtd', q_lat, Wq_up_c)
        q_e = jnp.einsum('bthl,ld->bhtd', q_lat, Wq_up_e)
        k_c = jnp.einsum('bthl,ld->bhtd', k_lat, Wk_up_c)
        k_e = jnp.einsum('bthl,ld->bhtd', k_lat, Wk_up_e)
        v = jnp.einsum('bthl,ld->bhtd', v_lat, Wv_up)
        cos, sin = _rope_cache(t, DHE)
        q = jnp.concatenate([q_c, _apply_rope(q_e, cos, sin)], axis=-1)
        k = jnp.concatenate([k_c, _apply_rope(k_e, cos, sin)], axis=-1)
        scale = 1.0 / math.sqrt(DH)
        scores = jnp.einsum('bhqd,bhkd->bhqk', q, k) * scale
        causal = jnp.tril(jnp.ones((t, t), dtype=bool))
        scores = jnp.where(causal[None, None], scores, -jnp.inf)
        att = jax.nn.softmax(scores, axis=-1)
        y = jnp.einsum('bhqk,bhkd->bhqd', att, v)
        y = y.transpose(0, 2, 1, 3).reshape(b, t, c)
        return y @ Wc

    def _L3_ffn_ref(x, wf, uf, bf, wi, ui, bi, wc, uc, bc, wo, uo, bo, in_c):
        import jax, jax.numpy as jnp
        import numpy as np
        from jax import lax
        T, B, I, M, O = (32, 64, 128, 128, 128)

        def _xavier(key, shape):
            fan_out, fan_in = shape
            limit = float(np.sqrt(6.0 / (fan_in + fan_out)))
            return jax.random.uniform(key, shape, jnp.float32, -limit, limit)
        batch = x.shape[1]
        c0 = jnp.broadcast_to(in_c, (batch, in_c.shape[0]))

        def step(c, xt):
            ft = jax.nn.sigmoid(xt @ wf.T + c @ uf.T + bf)
            it = jax.nn.sigmoid(xt @ wi.T + c @ ui.T + bi)
            gt = jnp.tanh(xt @ wc.T + c @ uc.T + bc)
            c = ft * c + it * gt
            return (c, None)
        c_final, _ = lax.scan(step, c0, x)
        h = jnp.tanh(jnp.einsum('tbi,oi->tbo', x, wo) + c_final @ uo.T + bo)
        return h
    x = x + _L0_xattn_ref(ctx_1024, _layernorm(x, axis=-1), mask_BxS2_bk1, L0_xattn_Wq, L0_xattn_Wkv, L0_xattn_Wo, L0_xattn_ln_x_g, L0_xattn_ln_x_b, L0_xattn_ln_l_g, L0_xattn_ln_l_b, L0_xattn_ln_o_g, L0_xattn_ln_o_b)
    x = x + _L0_attn_ref(_layernorm(x, axis=-1), L0_attn_Wq, L0_attn_Wk, L0_attn_Wv, L0_attn_Wog, L0_attn_Wi, L0_attn_bi, L0_attn_Wf, L0_attn_bf, L0_attn_ln_w, L0_attn_ln_b, L0_attn_Wout)
    x = x + _L0_ffn_ref(_layernorm(x, axis=-1), L0_ffn_Wg, L0_ffn_W1, L0_ffn_b1, L0_ffn_W2, L0_ffn_b2)
    x = x + _L1_xattn_ref(_layernorm(x, axis=-1), ctx_1024, L1_xattn_W_q, L1_xattn_W_k, L1_xattn_W_v, L1_xattn_W_o, L1_xattn_b_o)
    x = x + _L1_attn_ref(_layernorm(x, axis=-1), L1_attn_Wq, L1_attn_Wk, L1_attn_fc1_w, L1_attn_fc1_b, L1_attn_fc2_w, L1_attn_fc2_b)
    x = x + _L1_ffn_ref(_layernorm(x, axis=-1), L1_ffn_w12, L1_ffn_w3, L1_ffn_gate_w)
    x = x + _L2_xattn_ref(_layernorm(x, axis=-1), ctx_1024, ctx_1024, L2_xattn_Wq, L2_xattn_bq, L2_xattn_Wk, L2_xattn_bk, L2_xattn_Wv, L2_xattn_bv)
    x = x + _L2_attn_ref(_layernorm(x, axis=-1), L2_attn_ln1_g, L2_attn_ln1_b, L2_attn_qkv_w, L2_attn_proj_w, L2_attn_proj_b, L2_attn_pre_w, L2_attn_pre_b, L2_attn_post_w, L2_attn_post_b, L2_attn_ln2_g, L2_attn_ln2_b, L2_attn_fc1_w, L2_attn_fc1_b, L2_attn_lnh_g, L2_attn_lnh_b, L2_attn_fc2_w, L2_attn_fc2_b, L2_attn_gamma1, L2_attn_gamma2)
    x = x + _L2_ffn_ref(_layernorm(x, axis=-1), L2_ffn_Wg, L2_ffn_bg, L2_ffn_W1, L2_ffn_b1, L2_ffn_W2, L2_ffn_b2)
    x = x + _L3_xattn_ref(ctx_1024, _layernorm(x, axis=-1), L3_xattn_gamma_x, L3_xattn_beta_x, L3_xattn_gamma_l, L3_xattn_beta_l, L3_xattn_Wq, L3_xattn_Wkv, L3_xattn_Wo)
    x = x + _L3_attn_ref(_layernorm(x, axis=-1), L3_attn_Wq_down, L3_attn_Wk_down, L3_attn_Wv_down, L3_attn_Wq_up_c, L3_attn_Wq_up_e, L3_attn_Wk_up_c, L3_attn_Wk_up_e, L3_attn_Wv_up, L3_attn_Wc)
    x = x + _L3_ffn_ref(_layernorm(x, axis=-1), L3_ffn_wf, L3_ffn_uf, L3_ffn_bf, L3_ffn_wi, L3_ffn_ui, L3_ffn_bi, L3_ffn_wc, L3_ffn_uc, L3_ffn_bc, L3_ffn_wo, L3_ffn_uo, L3_ffn_bo, L3_ffn_in_c)
    return x

_drawn_inputs = setup_inputs


def setup_inputs(seed=0):
    import zlib

    import numpy as np

    out = dict(_drawn_inputs(seed))
    spreads = {'L0_xattn_ln_x_g': (1.0, 0.2),
     'L0_xattn_ln_x_b': (0.0, 0.1),
     'L0_xattn_ln_l_g': (1.0, 0.6),
     'L0_xattn_ln_l_b': (0.0, 0.45),
     'L0_xattn_ln_o_g': (1.0, 0.2),
     'L0_xattn_ln_o_b': (0.0, 0.1),
     'L0_attn_ln_w': (1.0, 0.6),
     'L0_attn_ln_b': (0.0, 0.62),
     'L2_attn_ln1_g': (1.0, 0.6),
     'L2_attn_ln1_b': (0.0, 2.0),
     'L2_attn_proj_b': (0.0, 2.0),
     'L2_attn_pre_b': (0.0, 0.1),
     'L2_attn_post_b': (0.0, 0.1),
     'L2_attn_ln2_g': (1.0, 0.6),
     'L2_attn_ln2_b': (0.0, 2.0),
     'L2_attn_fc1_b': (0.0, 2.0),
     'L2_attn_lnh_g': (1.0, 0.6),
     'L2_attn_lnh_b': (0.0, 2.0),
     'L2_attn_fc2_b': (0.0, 2.0),
     'L2_attn_gamma1': (9.999999747378752e-05, 0.6),
     'L2_attn_gamma2': (9.999999747378752e-05, 0.6),
     'L3_xattn_gamma_x': (1.0, 0.2),
     'L3_xattn_beta_x': (0.0, 0.1),
     'L3_xattn_gamma_l': (1.0, 0.6),
     'L3_xattn_beta_l': (0.0, 0.8),
     'L3_ffn_bf': (0.0, 0.8),
     'L3_ffn_bi': (0.0, 0.8),
     'L3_ffn_bc': (0.0, 0.285),
     'L3_ffn_bo': (0.0, 0.356),
     'L3_ffn_in_c': (0.0, 0.8)}
    factors = {'L0_attn_Wog': 4.386,
     'L0_attn_Wi': 5.324,
     'L0_attn_bi': 8.0,
     'L0_attn_Wf': 7.28,
     'L0_attn_bf': 46.599,
     'L0_ffn_Wg': 5.374,
     'L0_ffn_W1': 5.733,
     'L0_ffn_b1': 8.0,
     'L0_ffn_W2': 4.779,
     'L0_ffn_b2': 8.0,
     'L1_xattn_W_q': 8.0,
     'L1_xattn_W_k': 8.0,
     'L1_xattn_b_o': 3.214,
     'L1_attn_Wq': 5.361,
     'L1_attn_Wk': 3.75,
     'L2_xattn_Wq': 3.006,
     'L2_xattn_bq': 8.0,
     'L2_xattn_Wk': 2.873,
     'L2_xattn_bk': 64.0,
     'L2_attn_proj_w': 64.0,
     'L2_attn_fc1_w': 64.0,
     'L2_attn_fc2_w': 64.0,
     'L2_ffn_bg': 5.37,
     'L2_ffn_b1': 8.0,
     'L2_ffn_b2': 8.0,
     'L3_attn_Wq_down': 8.0,
     'L3_attn_Wk_down': 8.0,
     'L3_attn_Wv_down': 8.0,
     'L3_attn_Wq_up_c': 8.0,
     'L3_attn_Wq_up_e': 8.0,
     'L3_attn_Wk_up_c': 8.0,
     'L3_attn_Wk_up_e': 8.0,
     'L3_attn_Wv_up': 8.0,
     'L3_attn_Wc': 8.0}
    for name, (base, spread) in spreads.items():
        noise = np.random.default_rng([zlib.crc32(name.encode()), seed]).standard_normal(out[name].shape)
        drawn = base * np.exp(spread * noise) if base else spread * noise
        out[name] = jnp.asarray(drawn.astype(out[name].dtype))
    for name, factor in factors.items():
        out[name] = (out[name] * factor).astype(out[name].dtype)
    return out
```

```python
from contextlib import ExitStack

import numpy as np

import concourse.bass as bass
from concourse import mybir

ALU = mybir.AluOpType
ACT = mybir.ActivationFunctionType
AX = mybir.AxisListType.X
F32 = mybir.dt.float32
BF16 = mybir.dt.bfloat16
U8 = mybir.dt.uint8

P = 128
D = 128
BATCHES = 16
SEQ = 64
TILES = BATCHES * SEQ // P
TOKENS = BATCHES * SEQ
CTX = 1601
BANK = 512
EPS_5, EPS_6 = 0, 1


class Stage:

    def __init__(self, nc, ctx, name):
        self.nc, self.ctx, self.name, self.sems = nc, ctx, name, []
        ctx.callback(self.clear)

    def sb(self, name, shape, dtype=F32):
        return self.ctx.enter_context(self.nc.sbuf_tensor(f"{self.name}_{name}", shape, dtype))

    def ps(self, name, shape, dtype=F32):
        return self.ctx.enter_context(self.nc.psum_tensor(f"{self.name}_{name}", shape, dtype))

    def sem(self, name):
        handle = self.nc.alloc_semaphore(name=f"{self.name}_{name}")
        self.sems.append(handle)
        return handle

    def clear(self):
        self.nc.clear_and_free_semaphores(self.sems)
        self.nc.all_engine_barrier()

    def block(self):
        return self.ctx.enter_context(self.nc.Block())


def over_last(ap, width):
    return ap.unsqueeze(2).to_broadcast([ap.shape[0], ap.shape[1], width])


def over_tiles(ap, tiles):
    return ap.unsqueeze(1).to_broadcast([ap.shape[0], tiles, ap.shape[1]])


def normalize_dve(nc, dve, out, src, square, stats, var_ready, std_ready, use):
    n, width = src.shape[1], src.shape[2]
    mean, var, std, rstd = (stats[:, k, 0:n] for k in range(4))
    nc.vector.tensor_reduce(mean, src, AX, ALU.add)
    dve.drain()
    nc.vector.tensor_scalar(mean, mean, 1.0 / width, None, ALU.mult)
    dve.drain()
    nc.vector.tensor_tensor(out, src, over_last(mean, width), ALU.subtract)
    dve.drain()
    nc.vector.tensor_tensor(square, out, out, ALU.mult)
    dve.drain()
    nc.vector.tensor_reduce(var, square, AX, ALU.add).then_inc(var_ready, 1)
    dve.wait_ge(std_ready, use)
    nc.vector.reciprocal(rstd, std)
    dve.drain()
    return nc.vector.tensor_tensor(out, out, over_last(rstd, width), ALU.mult)


def normalize_act(nc, act, eps, n, width, stats, var_ready, std_ready, use):
    act.wait_ge(var_ready, use)
    nc.scalar.activation(stats[:, 2, 0:n], stats[:, 1, 0:n], ACT.Sqrt, bias=eps, scale=1.0 / width)\
        .then_inc(std_ready, 1)


class Lane:

    def __init__(self, banks, full, free):
        self.banks, self.full, self.free = banks, full, free
        self.at, self.n, self.turn = 0, 0, 0

    def go_to(self, at, turn):
        self.at, self.n, self.turn = at, 0, turn

    def count(self):
        return self.at + self.n

    def bank(self):
        return self.banks[self.turn % len(self.banks)]

    def next(self):
        self.n += 1
        self.turn += 1


def full_tiles(tiles):
    if tiles[0] < CTX // P:
        return [(tiles[0], len(tiles), P)]
    return [(tiles[0], 1, CTX % P)] + [(k, 1, SEQ) for k in tiles[1:]]


def cross_attention_stage(core, name, w, heads, scale, normed=False, masked=False, rotary=False, single=False,
                          out_norm=False):
    nc, lat = core.nc, core.lat
    absorbed = not (rotary or single)
    NH, HD = heads, D if single else 64
    PAIRS = max(NH // 2, 1)
    ROWS = SEQ if single else P
    R = 1 if single else PAIRS
    TPG = min(R, 4)
    GROUPS = R // TPG
    GROWS = TPG * ROWS
    CT = -(-CTX // P)
    TAIL = CTX - (CT - 1) * P
    KEYS = CTX + (SEQ if normed else 0)
    tile_of_keys = [(k * P, min(P, CTX - k * P)) for k in range(CT)] + ([(CTX, SEQ)] if normed else [])
    KT = len(tile_of_keys)
    CHUNKS = [(c * BANK, min(BANK, KEYS - c * BANK)) for c in range(-(-KEYS // BANK))]
    CTX_CHUNKS = [(c * BANK, min(BANK, CTX - c * BANK)) for c in range(-(-CTX // BANK))]
    QUADS = [list(range(q, min(q + 4, KT))) for q in range(0, KT, 4)]
    T_LANES = "AAAA" if rotary else "ADAD"
    PV_PARTS = [range(0, 5), range(5, 10), range(10, KT)]
    QJOBS = max(NH // 8, 1)
    FOLDS = PAIRS if not single else 0

    with ExitStack() as ctx:
        s = Stage(nc, ctx, name)
        y, square, yT = s.sb("y", [P, TILES, D]), s.sb("square", [P, TILES, D]), s.sb("yT", [P, TOKENS])
        stats = s.sb("stats", [P, 4, TILES])
        staged = s.sb("staged", [P, CT, D]) if normed or single else None
        rows = s.sb("rows", [P, 2, KT, D])
        keysT = s.sb("keysT", [P, 2, KEYS])
        prob = s.sb("prob", [P, 2, KEYS])
        probT = s.sb("probT", [P, 2, KT, GROWS])
        queries = s.sb("queries", [P, 2, R * ROWS])
        peak, neg_peak = s.sb("peak", [P, 2]), s.sb("neg_peak", [P, 2])
        rsum, rinv = s.sb("rsum", [P, 2]), s.sb("rinv", [P, 2])
        mixed = s.sb("mixed", [P, 2, GROWS])
        outT = s.sb("outT", [P, TOKENS])
        if normed:
            raw = s.sb("raw", [P, CT, D])
            csq = s.sb("csq", [P, CT, D])
            cstats = s.sb("cstats", [P, 4, CT])
            gains = s.sb("gains", [P, 4, D])
            cols = s.sb("cols", [P, 2])
        if out_norm:
            out_gains = s.sb("out_gains", [P, 2, D])
            out_rows = s.sb("out_rows", [P, TILES, D])
        if masked:
            pick16 = s.sb("pick16", [P, P], BF16)
            mask16 = s.sb("mask16", [P, 2, KEYS], BF16)
            mask_u8, mask_all = s.sb("mask_u8", [BATCHES, CTX], U8), s.sb("mask_all", [BATCHES, KEYS], BF16)
            mask_dram = nc.dram_tensor(f"{name}_mask_rows", (BATCHES, KEYS), BF16, kind="Internal").ap()
        if single:
            wq, wk, wv, bias = s.sb("wq", [P, D]), s.sb("wk", [P, D]), s.sb("wv", [P, D]), s.sb("bias", [P, 3])
            projected = s.sb("projected", [P, 2, KEYS])
        else:
            wv_rows, wo_rows = s.sb("wv_rows", [P, NH * HD]), s.sb("wo_rows", [P, PAIRS, D])
            wvT = s.sb("wvT", [P, PAIRS, D])
            fold_vo = s.sb("fold_vo", [P, NH, D])
            if absorbed:
                wq_rows, wk_rows = s.sb("wq_rows", [P, NH * HD]), s.sb("wk_rows", [P, NH * HD])
                wqT, wkT = s.sb("wqT", [P, PAIRS, D]), s.sb("wkT", [P, PAIRS, D])
                fold_qk = s.sb("fold_qk", [P, NH, D])
            else:
                wq, wk = s.sb("wq", [P, PAIRS, P]), s.sb("wk", [P, PAIRS, P])
                rot_cos, rot_sin = s.sb("rot_cos", [P, CTX]), s.sb("rot_sin", [P, CTX])
                projected = s.sb("projected", [P, 2, KEYS])
                crossed = s.sb("crossed", [P, 2, BANK])
        if not single and "b_o" in w:
            out_bias = s.sb("out_bias", [P, 1])

        score = s.ps("score", [P, 4 * BANK])
        lane_bank = [s.ps(f"lane{i}", [P, BANK]) for i in range(3)]
        sums = s.ps("sums", [P, BANK])

        w_loaded, var_ready, std_ready = s.sem("w_loaded"), s.sem("var_ready"), s.sem("std_ready")
        y_ready, y_turned, yT_kept = s.sem("y_ready"), s.sem("y_turned"), s.sem("yT_kept")
        w_turned, w_kept = s.sem("w_turned"), s.sem("w_kept")
        mask_ready, mask_stored = s.sem("mask_ready"), s.sem("mask_stored")
        mask_loaded = [s.sem(f"mask_loaded{i}") for i in range(2)]
        cleared = s.sem("cleared")
        ctx_loaded, centred, cvar_ready, cstd_ready, c_ready = (s.sem("ctx_loaded"), s.sem("centred"),
                                                                s.sem("cvar_ready"), s.sem("cstd_ready"), s.sem("c_ready"))
        own_loaded = [s.sem(f"own_loaded{i}") for i in range(2)]
        rows_ready = s.sem("rows_ready")
        rows_loaded = [s.sem(f"rows_loaded{i}") for i in range(2)]
        score_half, peak_ready, exp_done, prob_ready = (s.sem("score_half"), s.sem("peak_ready"), s.sem("exp_done"),
                                                        s.sem("prob_ready"))
        sums_done, sums_kept = s.sem("sums_done"), s.sem("sums_kept")
        crossed_ready, keys_turned = s.sem("crossed_ready"), s.sem("keys_turned")
        act_full, act_free, dve_full, dve_free = s.sem("act_full"), s.sem("act_free"), s.sem("dve_full"), s.sem("dve_free")
        out_turned = s.sem("out_turned")

        ACT_FIRST = 2 + QJOBS + (len(CTX_CHUNKS) if single else 0)
        DVE_FIRST = 2 + (2 * len(CHUNKS) if rotary else 0)
        ACT_BATCH = T_LANES.count("A") * R + ACT_FIRST + 1
        DVE_BATCH = T_LANES.count("D") * R + 2 + (len(CHUNKS) * R if rotary else 0)

        def lanes():
            return {"A": Lane(lane_bank[0:2], act_full, act_free), "D": Lane(lane_bank[2:3], dve_full, dve_free)}

        def go_to_batch(lane, b, parity, first):
            if first:
                lane["A"].go_to(ACT_FIRST, ACT_FIRST)
                lane["D"].go_to(DVE_FIRST, 0)
            else:
                lane["A"].go_to(ACT_FIRST - 1 + ACT_BATCH * b, ACT_FIRST - 1 + ACT_BATCH * parity)
                lane["D"].go_to(DVE_FIRST + DVE_BATCH * b, 0)

        out_slot = 4 if GROUPS > 1 else 0

        def sums_of_slot(t):
            if R == 1:
                return []
            if GROUPS == 1:
                return [(1, 0, t - 1)]
            return [(1, GROUPS - 1, t - 1)] if t <= 3 else [(0, 0, t - 5)] if t >= 5 else []

        loads = [0]
        block = s.block()

        @block.sync
        def _(sp):
            def load(dst, src):
                sp.dma_start(dst, src).then_inc(w_loaded, 16)
                loads[0] += 1

            lane = lanes()

            def load_context(pair, parity, dst, done):
                src = core.w["ctx_1024"][bass.ds(pair * 2 + parity, 1)].rearrange("a n d -> (a n) d")
                sp.dma_start(dst[:, 0:CT - 1, :], src[0:(CT - 1) * P].rearrange("(k p) d -> p k d", p=P)).then_inc(done, 16)
                sp.dma_start(dst[0:TAIL, CT - 1, :], src[(CT - 1) * P:CTX]).then_inc(done, 16)

            def load_staged(pair, parity):
                load_context(pair, parity, raw if normed else staged, ctx_loaded)

            def load_rows(pair, parity):
                load_context(pair, parity, rows[:, parity], rows_loaded[parity])

            def load_own(pair, parity, used=None):
                if used is not None and normed:
                    sp.wait_ge(sums_done, used)
                if normed:
                    sp.dma_start(rows[0:SEQ, parity, CT, :], y[parity * SEQ:(parity + 1) * SEQ, bass.ds(pair, 1), :]
                                 .rearrange("p a d -> p (a d)")).then_inc(own_loaded[parity], 16)
                if masked:
                    sp.dma_start(mask16[0:1, parity, :], mask_dram[bass.ds(pair * 2 + parity, 1)]).then_inc(mask_loaded[parity], 16)

            def during(pair, parity, first=False, last=False):
                b = pair * 2 + parity
                if normed:
                    load_own(pair + parity, 1 - parity, None if first else GROUPS * b)
                    if not last:
                        sp.wait_ge(centred, b + 2)
                        load_staged(pair + 1, parity)
                    return
                if not first:
                    sp.wait_ge(sums_done, GROUPS * b)
                load_rows(pair + parity, 1 - parity)
                if single and not last:
                    go_to_batch(lane, b, parity, first)
                    sp.wait_ge(act_full, lane["A"].count() + 2)
                    sp.wait_ge(dve_full, lane["D"].count() + 2)
                    load_staged(pair + 1, parity)

            sp.wait_ge(cleared, 1)
            if normed or single:
                load_staged(0, 0)
            if not normed:
                load_rows(0, 0)
            if masked:
                load(mask_u8[:], core.w["mask_BxS2_bk1"])
            if normed:
                names = ("ln_x_g", "ln_x_b", "ln_l_g", "ln_l_b") if "ln_x_g" in w else ("gamma_x", "beta_x", "gamma_l", "beta_l")
                for n, src in enumerate(names):
                    load(gains[:, n, :], w[src].partition_broadcast(P))
                with nc.allow_non_contiguous_dma("gain columns"):
                    for n in range(2):
                        load(cols[:, n:n + 1], column(w[names[n]]))
            if "Wkv" in w:
                wk_src, wv_src, wo_src = w["Wkv"][:, 0:NH * HD], w["Wkv"][:, NH * HD:2 * NH * HD], w["Wo"]
            elif not single:
                wk_src, wv_src, wo_src = w["W_k"], w["W_v"], w["W_o"]
            if absorbed:
                load(wq_rows[:], w["Wq"] if "Wq" in w else w["W_q"])
                load(wk_rows[:], wk_src)
            if rotary:
                with nc.allow_non_contiguous_dma("head halves"):
                    for dst, src in ((wq, w["Wq"]), (wk, wk_src)):
                        for t in range(PAIRS):
                            for half in range(2):
                                load(dst[:, t, half * SEQ:(half + 1) * SEQ].rearrange("p (h d) -> p h d", h=2),
                                     src[:, t * P:(t + 1) * P].rearrange("p (h a d) -> p a h d", h=2, a=2)[:, half])
                load(rot_cos[:], core.w["c_rope64"][0])
                load(rot_sin[:], core.w["c_rope64"][1])
            if single:
                for dst, src in ((wq, "Wq"), (wk, "Wk"), (wv, "Wv")):
                    load(dst[:], w[src])
                with nc.allow_non_contiguous_dma("bias columns"):
                    for n, src in enumerate(("bq", "bk", "bv")):
                        load(bias[:, n:n + 1], column(w[src]))
            else:
                load(wv_rows[:], wv_src)
                load(wo_rows[:], wo_src.rearrange("(t p) d -> p t d", p=P))
            if out_norm:
                load(out_gains[:, 0, :], w["ln_o_g"].partition_broadcast(P))
                load(out_gains[:, 1, :], w["ln_o_b"].partition_broadcast(P))
            if "b_o" in w:
                with nc.allow_non_contiguous_dma("bias column"):
                    load(out_bias[:], column(w["b_o"]))
            if masked:
                sp.wait_ge(mask_ready, 1)
                sp.dma_start(mask_dram, mask_all[:]).then_inc(mask_stored, 16)
                sp.wait_ge(mask_stored, 16)
                sp.wait_ge(cleared, 2)
            if normed:
                sp.wait_ge(y_ready, 1)
                sp.wait_ge(centred, 1)
                load_own(0, 0)
                load_staged(0, 1)
            elif single:
                sp.wait_ge(act_full, 2)
                sp.wait_ge(dve_full, 2)
                load_staged(0, 1)
            during(0, 0, first=True)
            during(0, 1)
            with sp.Fori(1, BATCHES // 2 - 1) as pair:
                during(pair, 0)
                during(pair, 1)
            during(BATCHES // 2 - 1, 0, last=True)

        LOADS = loads[0]
        QUAD_TURNS = [n for n in (("wq", "wk", "wv") if absorbed else ("wv",)) for _ in range(PAIRS // 4)] if not single else []
        TURNS = len(QUAD_TURNS)

        @block.tensor
        def _(pe):
            lane = lanes()
            pe.wait_ge(cleared, 2)
            pe.wait_ge(w_loaded, 16 * LOADS)
            if not single:
                todo = ((wq_rows, wk_rows, wv_rows) if absorbed else (wv_rows,))
                for j in range(TURNS):
                    source, quad = todo[j // (PAIRS // 4)], j % (PAIRS // 4)
                    if j >= 4:
                        pe.wait_ge(w_kept, j - 3)
                    for i in range(4):
                        turn = nc.tensor.transpose(score[:, (j % 4) * BANK + i * P:(j % 4) * BANK + (i + 1) * P],
                                                   source[:, (4 * quad + i) * P:(4 * quad + i + 1) * P], core.ident[:])
                    turn.then_inc(w_turned, 1)
                pe.wait_ge(w_kept, TURNS)
                for f, (left, right) in enumerate(([(wqT, wkT)] if absorbed else []) * (PAIRS // 4) + [(wvT, wo_rows)] * (PAIRS // 4)):
                    quad = f % (PAIRS // 4)
                    if f >= 2:
                        pe.wait_ge(w_kept, TURNS + f - 1)
                    for odd in range(2):
                        part = slice(odd * SEQ, (odd + 1) * SEQ)
                        bank = score[:, (2 * (f % 2) + odd) * BANK:(2 * (f % 2) + odd + 1) * BANK]
                        for i in range(4):
                            mm = nc.tensor.matmul(bank[:, i * P:(i + 1) * P], left[part, 4 * quad + i, :],
                                                  right[part, 4 * quad + i, :], start=True, stop=True)
                    mm.then_inc(w_turned, 1)
            turn_tiles_pe(nc, pe, core.ident[:], y[:], lane_bank[0:2], y_ready, 1, y_turned)
            pe.wait_ge(yT_kept, 2)
            if not single:
                pe.wait_ge(w_kept, TURNS + (2 if absorbed else 1) * (PAIRS // 4))

            def fill(name):
                ln = lane[name]
                count = ln.count() - len(ln.banks) + 1
                if not isinstance(count, int) or count > 0:
                    pe.wait_ge(ln.free, count)
                return ln.bank()

            def filled(name, ins):
                ins.then_inc(lane[name].full, 1)
                lane[name].next()

            def emptied(name):
                pe.wait_ge(lane[name].free, lane[name].count())

            def context_turns(pair, parity):
                b = pair * 2 + parity
                if normed:
                    pe.wait_ge(c_ready, b + 1)
                elif single:
                    pe.wait_ge(ctx_loaded, 32 * (b + 1))
                else:
                    pe.wait_ge(rows_loaded[parity], 32 * (pair + 1))
                for c, (c0, n) in enumerate(CTX_CHUNKS):
                    bank = fill("AD"[c % 2])
                    for k in range(c0 // P, -(-(c0 + n) // P)):
                        size = tile_of_keys[k][1]
                        source = rows[0:size, parity, k, :] if staged is None else staged[0:size, k, :]
                        turn = nc.tensor.transpose(bank[:, k * P - c0:k * P - c0 + size], source,
                                                   core.ident[0:size, 0:size])
                    filled("AD"[c % 2], turn)

            def make_queries(pair, parity):
                own = yT[:, bass.ds((pair * 2 + parity) * SEQ, SEQ)]
                if single:
                    filled("A", nc.tensor.matmul(fill("A")[:, 0:SEQ], wq[:], own, start=True, stop=True))
                    return
                for job in range(QJOBS):
                    bank = fill("A")
                    for i in range(8 if absorbed else PAIRS):
                        left = fold_qk[:, 8 * job + i, :] if absorbed else wq[:, i, :]
                        mm = nc.tensor.matmul(bank[:, i * SEQ:(i + 1) * SEQ], left, own, start=True, stop=True)
                    filled("A", mm)

            def project_keys(parity):
                emptied("A")
                emptied("D")
                for c0, n in CHUNKS:
                    filled("A", nc.tensor.matmul(fill("A")[:, 0:n], wk[:], keysT[:, parity, c0:c0 + n], start=True, stop=True))

            def rotary_chunk(pair, parity, t, c):
                if c == 0 and t == 0:
                    emptied("A")
                    emptied("D")
                c0, n = CTX_CHUNKS[c]
                bank = fill("D")
                mm = nc.tensor.matmul(bank[:, 0:n], wk[:, t, :], keysT[:, parity, c0:c0 + n], start=True, stop=True)
                if c == len(CTX_CHUNKS) - 1:
                    mm = nc.tensor.matmul(bank[:, P:P + SEQ], wk[:, t, :], yT[:, bass.ds((pair * 2 + parity) * SEQ, SEQ)],
                                          start=True, stop=True)
                filled("D", mm)

            def scores(pair, parity, t, first=False):
                b = pair * 2 + parity
                tile = b * R + t
                if t == 0 and not rotary:
                    emptied("A")
                    emptied("D")
                if masked and t == 0:
                    pe.wait_ge(mask_loaded[parity], 16 * (pair + 1))
                if rotary:
                    pe.wait_ge(keys_turned, (tile + 1) * len(CTX_CHUNKS))
                if not first:
                    pe.wait_ge(exp_done, tile)
                keys = keysT[:, parity] if absorbed else projected[:, parity] if single else projected[:, t % 2]
                for c, (c0, n) in enumerate(CHUNKS):
                    mm = nc.tensor.matmul(score[0:ROWS, c0:c0 + n], queries[:, parity, t * ROWS:(t + 1) * ROWS],
                                          keys[:, c0:c0 + n], start=True, stop=not masked)
                    if masked:
                        mm = nc.tensor.matmul(score[0:ROWS, c0:c0 + n], pick16[:], mask16[:, parity, c0:c0 + n],
                                              start=False, stop=True)
                    if c in (1, len(CHUNKS) - 1):
                        mm.then_inc(score_half, 1)

            def turn_probs(pair, parity, t, quads):
                if 0 in quads:
                    pe.wait_ge(prob_ready, (pair * 2 + parity) * R + t + 1)
                which = t % 2 if R > 1 else parity
                for j in quads:
                    bank = fill(T_LANES[j])
                    for i, k in enumerate(QUADS[j]):
                        c0, n = tile_of_keys[k]
                        turn = nc.tensor.transpose(bank[0:n, i * P:(i + 1) * P], prob[:, which, c0:c0 + n], core.ident[:])
                    filled(T_LANES[j], turn)

            def sum_context(pair, parity, group, part, turned):
                b = pair * 2 + parity
                if part == 0:
                    for name, count in turned.items():
                        pe.wait_ge(lane[name].free, count)
                    if single:
                        pe.wait_ge(rows_loaded[parity], 32 * (pair + 1))
                    if normed:
                        pe.wait_ge(rows_ready, b + 1)
                        pe.wait_ge(own_loaded[parity], 16 * (pair + 1))
                    if not (isinstance(b, int) and b == 0 and group == 0):
                        pe.wait_ge(sums_kept, b * GROUPS + group)
                which = group if GROUPS > 1 else parity
                for k in PV_PARTS[part]:
                    n = tile_of_keys[k][1]
                    mm = nc.tensor.matmul(sums[:, 0:GROWS], rows[0:n, parity, k, :], probT[0:n, which, k, :],
                                          start=(k == 0), stop=(k == KT - 1))
                if part == len(PV_PARTS) - 1:
                    mm.then_inc(sums_done, 1)

            def output(pair, parity):
                b = pair * 2 + parity
                pe.wait_ge(sums_kept, GROUPS * (b + 1))
                bank = fill("A")
                for h in range(NH):
                    which = h // 8 if GROUPS > 1 else parity
                    col = (h % (2 * TPG)) * SEQ
                    mm = nc.tensor.matmul(bank[:, 0:SEQ], wv[:] if single else fold_vo[:, h, :], mixed[:, which, col:col + SEQ],
                                          start=(h == 0), stop=(h == NH - 1))
                filled("A", mm)

            def prepare(pair, parity, first=False, before=None):
                context_turns(pair, parity)
                make_queries(pair, parity)
                if before is not None:
                    output(*before)
                if single:
                    project_keys(parity)
                if rotary:
                    for c in range(len(CTX_CHUNKS)):
                        rotary_chunk(pair, parity, 0, c)
                scores(pair, parity, 0, first)

            def batch(pair, parity, first=False, last=False):
                b = pair * 2 + parity
                go_to_batch(lane, b, parity, first)
                previous = (pair - (1 - parity), 1 - parity)
                start = {name: lane[name].at for name in "AD"}
                group_turned = start
                for t in range(1, R):
                    scores(pair, parity, t)
                    parts = [(pair, parity, g, p, group_turned) if back == 0 else (*previous, g, p, start)
                             for back, g, p in sums_of_slot(t) if back == 0 or not first]
                    if rotary:
                        chunks = range(len(CTX_CHUNKS)) if t + 1 < R else ()
                        for c in range(4):
                            if c in chunks:
                                rotary_chunk(pair, parity, t + 1, c)
                            if c < 2:
                                turn_probs(pair, parity, t - 1, (2 * c, 2 * c + 1))
                            if c == 2:
                                for part in parts:
                                    sum_context(*part)
                    else:
                        turn_probs(pair, parity, t - 1, (0, 1, 2))
                        for part in parts:
                            sum_context(*part)
                        turn_probs(pair, parity, t - 1, (3,))
                    if t % 4 == 0:
                        group_turned = {name: lane[name].count() for name in "AD"}
                    if t == out_slot and not first:
                        output(*previous)
                if R == 1 and not first:
                    for p in range(len(PV_PARTS)):
                        sum_context(*previous, 0, p, start)
                due = previous if out_slot == 0 and not first else None
                if last:
                    if due is not None:
                        output(*due)
                else:
                    prepare(pair + parity, 1 - parity, before=due)
                    if rotary:
                        for c in range(len(CTX_CHUNKS)):
                            rotary_chunk(pair + parity, 1 - parity, 1, c)
                turn_probs(pair, parity, R - 1, range(len(QUADS)))

            prepare(0, 0, first=True)
            if rotary:
                for c in range(len(CTX_CHUNKS)):
                    rotary_chunk(0, 0, 1, c)
            batch(0, 0, first=True)
            batch(0, 1)
            with pe.Fori(1, BATCHES // 2 - 1) as pair:
                batch(pair, 0)
                batch(pair, 1)
            batch(BATCHES // 2 - 1, 0)
            batch(BATCHES // 2 - 1, 1, last=True)
            for p in range(len(PV_PARTS)):
                sum_context(BATCHES // 2 - 1, 1, GROUPS - 1, p, {name: lane[name].count() for name in "AD"})
            output(BATCHES // 2 - 1, 1)
            emptied("A")
            pe.wait_ge(exp_done, BATCHES * R)
            for t in range(TILES):
                turn = nc.tensor.transpose(score[:, t * P:(t + 1) * P], outT[:, t * P:(t + 1) * P], core.ident[:])
            turn.then_inc(out_turned, 1)

        @block.scalar
        def _(act):
            lane = lanes()
            act.wait_ge(cleared, 2)
            act.wait_ge(w_loaded, 16 * LOADS)
            if not single:
                turned = {"wq": wqT, "wk": wkT, "wv": wvT} if absorbed else {"wv": wvT}
                for j, n in enumerate(QUAD_TURNS):
                    quad = j % (PAIRS // 4)
                    act.wait_ge(w_turned, j + 1)
                    nc.scalar.copy(turned[n][:, 4 * quad:4 * quad + 4, :].rearrange("p i d -> p (i d)"),
                                   score[:, (j % 4) * BANK:(j % 4 + 1) * BANK]).then_inc(w_kept, 1)
                for f, dst in enumerate(([fold_qk] if absorbed else []) * (PAIRS // 4) + [fold_vo] * (PAIRS // 4)):
                    quad = f % (PAIRS // 4)
                    act.wait_ge(w_turned, TURNS + f + 1)
                    for odd in range(2):
                        bank = score[:, (2 * (f % 2) + odd) * BANK:(2 * (f % 2) + odd + 1) * BANK]
                        kept = nc.scalar.copy(dst[:].rearrange("p (i r) d -> p r i d", r=2)[:, odd, 4 * quad:4 * quad + 4, :],
                                              bank.rearrange("p (i d) -> p i d", d=D))
                    kept.then_inc(w_kept, 1)
            normalize_act(nc, act, core.eps(EPS_5), TILES, D, stats, var_ready, std_ready, 1)
            if normed:
                normalize_act(nc, act, core.eps(EPS_5), TILES, D, stats, var_ready, std_ready, 2)
            keep_turned_act(nc, act, yT, lane_bank[0:2], y_turned, 1, yT_kept)

            def take():
                act.wait_ge(lane["A"].full, lane["A"].count() + 1)
                return lane["A"].bank()

            def emptied(ins):
                ins.then_inc(lane["A"].free, 1)
                lane["A"].next()

            def keep_context(pair, parity):
                for c in range(0, len(CTX_CHUNKS), 2):
                    c0, n = CTX_CHUNKS[c]
                    bank = take()
                    if normed:
                        if c == 0:
                            nc.scalar.copy(keysT[:, parity, CTX:KEYS], yT[:, bass.ds((pair * 2 + parity) * SEQ, SEQ)])
                        emptied(nc.scalar.activation(keysT[:, parity, c0:c0 + n], bank[:, 0:n], ACT.Identity,
                                                     bias=cols[:, 1:2], scale=cols[:, 0:1]))
                    else:
                        emptied(nc.scalar.copy(keysT[:, parity, c0:c0 + n], bank[:, 0:n]))

            def keep_queries(parity):
                for job in range(QJOBS):
                    bank = take()
                    if single:
                        emptied(nc.scalar.activation(queries[:, parity, :], bank[:, 0:SEQ], ACT.Identity, bias=bias[:, 0:1]))
                    elif absorbed:
                        emptied(nc.scalar.copy(queries[:, parity, job * BANK:(job + 1) * BANK], bank[:]))
                    else:
                        for q in range(4):
                            part = slice(32 * q, 32 * q + 32)
                            last = nc.scalar.copy(queries[part, parity, :].rearrange("p (t h i) -> p t h i", h=2, i=SEQ)[:, :, q % 2, :],
                                                  bank[part, 0:PAIRS * SEQ].rearrange("p (t i) -> p t i", i=SEQ))
                        emptied(last)

            def exps(pair, parity, t):
                tile = (pair * 2 + parity) * R + t
                which = t % 2 if R > 1 else parity
                act.wait_ge(peak_ready, tile + 1)
                nc.scalar.activation(prob[0:ROWS, which, :], score[0:ROWS, 0:KEYS], ACT.Exp,
                                     bias=neg_peak[0:ROWS, which:which + 1], scale=scale,
                                     accum_out=rsum[0:ROWS, which:which + 1]).then_inc(exp_done, 1)

            def keep_probs(parity, t, quads):
                which, col = (t // TPG if GROUPS > 1 else parity), (t % TPG) * ROWS
                for j in quads:
                    if T_LANES[j] == "A":
                        bank = take()
                        for k0, n, size in full_tiles(QUADS[j]):
                            last = nc.scalar.copy(probT[0:size, which, k0:k0 + n, col:col + ROWS],
                                                  bank[0:size, (k0 % 4) * P:(k0 % 4 + n) * P]
                                                  .rearrange("p (i r) -> p i r", r=P)[:, :, 0:ROWS])
                        emptied(last)

            def keep_sums(pair, parity, group):
                act.wait_ge(sums_done, (pair * 2 + parity) * GROUPS + group + 1)
                which = group if GROUPS > 1 else parity
                nc.scalar.copy(mixed[:, which, :], sums[:, 0:GROWS]).then_inc(sums_kept, 1)

            def keep_output(pair, parity):
                bank = take()
                dst = outT[:, bass.ds((pair * 2 + parity) * SEQ, SEQ)]
                if single:
                    emptied(nc.scalar.activation(dst, bank[:, 0:SEQ], ACT.Identity, bias=bias[:, 2:3]))
                elif "b_o" in w:
                    emptied(nc.scalar.activation(dst, bank[:, 0:SEQ], ACT.Identity, bias=out_bias[:]))
                else:
                    emptied(nc.scalar.copy(dst, bank[:, 0:SEQ]))

            def context_root(b):
                act.wait_ge(cvar_ready, b + 1)
                nc.scalar.activation(cstats[:, 2, :], cstats[:, 1, :], ACT.Sqrt, bias=core.eps(EPS_5), scale=1.0 / D)\
                    .then_inc(cstd_ready, 1)

            def prepare(pair, parity, before=None):
                keep_context(pair, parity)
                keep_queries(parity)
                if before is not None:
                    keep_output(*before)
                if single:
                    for c0, n in CHUNKS:
                        emptied(nc.scalar.activation(projected[:, parity, c0:c0 + n], take()[:, 0:n], ACT.Identity,
                                                     bias=bias[:, 1:2]))

            def batch(pair, parity, first=False, last=False):
                b = pair * 2 + parity
                go_to_batch(lane, b, parity, first)
                previous = (pair - (1 - parity), 1 - parity)
                for t in range(1, R):
                    if GROUPS > 1 and t == 4 and not first:
                        keep_sums(*previous, GROUPS - 1)
                    keep_probs(parity, t - 1, range(len(QUADS)))
                    if t == out_slot and not first:
                        keep_output(*previous)
                    exps(pair, parity, t)
                    if normed and t == 2 and not last:
                        context_root(b + 1)
                if GROUPS > 1:
                    keep_sums(pair, parity, 0)
                elif not first:
                    keep_sums(*previous, 0)
                due = previous if out_slot == 0 and not first else None
                if last:
                    if due is not None:
                        keep_output(*due)
                else:
                    prepare(pair + parity, 1 - parity, due)
                if not last and R == 1:
                    keep_probs(parity, R - 1, range(len(QUADS)))
                    exps(pair + parity, 1 - parity, 0)
                elif not last:
                    keep_probs(parity, R - 1, range(len(QUADS)))
                    exps(pair + parity, 1 - parity, 0)
                else:
                    keep_probs(parity, R - 1, range(len(QUADS)))

            if normed:
                context_root(0)
            prepare(0, 0)
            exps(0, 0, 0)
            batch(0, 0, first=True)
            batch(0, 1)
            with act.Fori(1, BATCHES // 2 - 1) as pair:
                batch(pair, 0)
                batch(pair, 1)
            batch(BATCHES // 2 - 1, 0)
            batch(BATCHES // 2 - 1, 1, last=True)
            keep_sums(BATCHES // 2 - 1, 1, GROUPS - 1)
            keep_output(BATCHES // 2 - 1, 1)
            if out_norm:
                normalize_act(nc, act, core.eps(EPS_5), TILES, D, stats, var_ready, std_ready, 3)

        @block.gpsimd
        def _(pool):
            if normed:
                nc.gpsimd.memset(raw[:], 0.0)
            if single:
                nc.gpsimd.memset(prob[:], 0.0)
            pool.drain()
            nc.gpsimd.memset(neg_peak[:], 0.0).then_inc(cleared, 1)
            if masked:
                nc.gpsimd.memset(pick16[:], 0.0)
                nc.gpsimd.memset(mask16[:], 0.0)
                pool.drain()
                nc.gpsimd.memset(pick16[0:1, :], 1.0)
            if rotary:
                nc.gpsimd.memset(queries[:], 0.0)
            pool.drain()
            nc.gpsimd.memset(peak[:], 0.0).then_inc(cleared, 1)
            pool.wait_ge(w_loaded, 16 * LOADS)

            def add_crossed(tile, t):
                for c, (c0, n) in enumerate(CTX_CHUNKS):
                    pool.wait_ge(crossed_ready, tile * len(CTX_CHUNKS) + c + 1)
                    nc.gpsimd.tensor_tensor(projected[:, t % 2, c0:c0 + n], projected[:, t % 2, c0:c0 + n],
                                            crossed[:, c % 2, 0:n], ALU.add).then_inc(keys_turned, 1)

            def make_rows(pair, parity, free=None):
                b = pair * 2 + parity
                if free is not None:
                    pool.wait_ge(sums_done, free)
                dst = rows[:, parity, 0:CT, :]
                pool.wait_ge(c_ready, b + 1)
                nc.gpsimd.tensor_tensor(dst, staged[:], over_tiles(gains[:, 0, :], CT), ALU.mult)
                pool.drain()
                nc.gpsimd.tensor_tensor(dst, dst, over_tiles(gains[:, 1, :], CT), ALU.add).then_inc(rows_ready, 1)

            def batch(pair, parity, first=False, last=False):
                b = pair * 2 + parity
                for t in range(1, R - 1):
                    if rotary:
                        add_crossed(b * R + t + 1, t + 1)
                if not last:
                    make_rows(pair + parity, 1 - parity, None if first else GROUPS * b)
                    if rotary:
                        add_crossed(b * R + R, 0)
                        add_crossed(b * R + R + 1, 1)

            if normed:
                make_rows(0, 0)
                if rotary:
                    add_crossed(0, 0)
                    add_crossed(1, 1)
                batch(0, 0, first=True)
                batch(0, 1)
                with pool.Fori(1, BATCHES // 2 - 1) as pair:
                    batch(pair, 0)
                    batch(pair, 1)
                batch(BATCHES // 2 - 1, 0)
                batch(BATCHES // 2 - 1, 1, last=True)

        @block.vector
        def _(dve):
            lane = lanes()
            normalize_dve(nc, dve, y[:], lat[:], square[:], stats, var_ready, std_ready, 1)
            dve.drain()
            dve.wait_ge(w_loaded, 16 * LOADS)
            if normed:
                normalize_dve(nc, dve, y[:], y[:], square[:], stats, var_ready, std_ready, 2)
                dve.drain()
                nc.vector.tensor_tensor(y[:], y[:], over_tiles(gains[:, 2, :], TILES), ALU.mult)
                dve.drain()
                nc.vector.tensor_tensor(y[:], y[:], over_tiles(gains[:, 3, :], TILES), ALU.add).then_inc(y_ready, 1)
            else:
                nc.vector.tensor_copy(square[:, 0, 0:1], y[:, 0, 0:1]).then_inc(y_ready, 1)
            if masked:
                nc.vector.memset(mask_all[:, CTX:KEYS], 0.0)
                nc.vector.tensor_scalar(mask_all[:, 0:CTX], mask_u8[:], -1.0, 1e30, ALU.add, ALU.mult).then_inc(mask_ready, 1)
            dve.wait_ge(cleared, 2)

            def take():
                dve.wait_ge(lane["D"].full, lane["D"].count() + 1)
                return lane["D"].bank()

            def emptied(ins):
                ins.then_inc(lane["D"].free, 1)
                lane["D"].next()

            def centre(b, first=False):
                dve.wait_ge(ctx_loaded, 32 * (b + 1))
                nc.vector.tensor_reduce(cstats[:, 0, :], raw[:], AX, ALU.add)
                dve.drain()
                nc.vector.tensor_scalar(cstats[:, 0, :], cstats[:, 0, :], 1.0 / D, None, ALU.mult)
                dve.drain()
                if not first:
                    dve.wait_ge(rows_ready, b)
                nc.vector.tensor_tensor(staged[:], raw[:], over_last(cstats[:, 0, :], D), ALU.subtract).then_inc(centred, 1)
                dve.drain()

            def spread(b):
                nc.vector.tensor_tensor(csq[:], staged[:], staged[:], ALU.mult)
                dve.drain()
                nc.vector.tensor_reduce(cstats[:, 1, :], csq[:], AX, ALU.add).then_inc(cvar_ready, 1)

            def rescale(b):
                dve.wait_ge(cstd_ready, b + 1)
                nc.vector.reciprocal(cstats[:, 3, :], cstats[:, 2, :])
                dve.drain()
                nc.vector.tensor_tensor(staged[:], staged[:], over_last(cstats[:, 3, :], D), ALU.mult).then_inc(c_ready, 1)
                dve.drain()

            def keep_context(parity):
                for c in range(1, len(CTX_CHUNKS), 2):
                    c0, n = CTX_CHUNKS[c]
                    bank = take()
                    if normed:
                        emptied(nc.vector.tensor_scalar(keysT[:, parity, c0:c0 + n], bank[:, 0:n], cols[:, 0:1], cols[:, 1:2],
                                                        ALU.mult, ALU.add))
                    else:
                        emptied(nc.vector.tensor_copy(keysT[:, parity, c0:c0 + n], bank[:, 0:n]))

            def turn_keys(tile, t, start=False):
                for c, (c0, n) in enumerate(CTX_CHUNKS):
                    bank = take()
                    if not (start and c < 2):
                        dve.wait_ge(keys_turned, tile * len(CTX_CHUNKS) + c - 1)
                    if c == len(CTX_CHUNKS) - 1:
                        nc.vector.tensor_copy(projected[:, t % 2, CTX:KEYS], bank[:, P:P + SEQ])
                    nc.vector.tensor_tensor(projected[:, t % 2, c0:c0 + n], bank[:, 0:n], rot_cos[:, c0:c0 + n], ALU.mult)
                    nc.vector.tensor_tensor(crossed[SEQ:P, c % 2, 0:n], bank[0:SEQ, 0:n], rot_sin[0:SEQ, c0:c0 + n], ALU.mult)
                    nc.vector.tensor_tensor(crossed[0:SEQ, c % 2, 0:n], bank[SEQ:P, 0:n], rot_sin[SEQ:P, c0:c0 + n], ALU.mult)\
                        .then_inc(crossed_ready, 1)
                    emptied(dve.drain())

            def maximum(pair, parity, t):
                tile = (pair * 2 + parity) * R + t
                which = t % 2 if R > 1 else parity
                dve.wait_ge(score_half, 2 * tile + 1)
                nc.vector.tensor_reduce(peak[0:ROWS, 0:1], score[0:ROWS, 0:2 * BANK], AX, ALU.max)
                dve.wait_ge(score_half, 2 * tile + 2)
                nc.vector.tensor_reduce(peak[0:ROWS, 1:2], score[0:ROWS, 2 * BANK:KEYS], AX, ALU.max)
                dve.drain()
                nc.vector.tensor_scalar(neg_peak[0:ROWS, which:which + 1], peak[0:ROWS, 0:1], peak[0:ROWS, 1:2], -scale,
                                        ALU.max, ALU.mult).then_inc(peak_ready, 1)

            def normalise(pair, parity, t):
                tile = (pair * 2 + parity) * R + t
                which = t % 2 if R > 1 else parity
                dve.wait_ge(exp_done, tile + 1)
                nc.vector.reciprocal(rinv[0:ROWS, which:which + 1], rsum[0:ROWS, which:which + 1])
                dve.drain()
                nc.vector.tensor_scalar(prob[0:ROWS, which, :], prob[0:ROWS, which, :], rinv[0:ROWS, which:which + 1], None,
                                        ALU.mult).then_inc(prob_ready, 1)

            def keep_probs(parity, t, quads):
                which, col = (t // TPG if GROUPS > 1 else parity), (t % TPG) * ROWS
                for j in quads:
                    if T_LANES[j] == "D":
                        bank = take()
                        for k0, n, size in full_tiles(QUADS[j]):
                            last = nc.vector.tensor_copy(probT[0:size, which, k0:k0 + n, col:col + ROWS],
                                                         bank[0:size, (k0 % 4) * P:(k0 % 4 + n) * P]
                                                         .rearrange("p (i r) -> p i r", r=P)[:, :, 0:ROWS])
                        emptied(last)

            def batch(pair, parity, first=False, last=False):
                b = pair * 2 + parity
                go_to_batch(lane, b, parity, first)
                for t in range(1, R):
                    normalise(pair, parity, t - 1)
                    maximum(pair, parity, t)
                    if rotary and t + 1 < R:
                        turn_keys(b * R + t + 1, t + 1)
                    keep_probs(parity, t - 1, range(len(QUADS)))
                    if normed and not last:
                        if t == 1:
                            centre(b + 1)
                        if t == 2:
                            spread(b + 1)
                        if t == 3:
                            rescale(b + 1)
                normalise(pair, parity, R - 1)
                if not last:
                    keep_context(1 - parity)
                    if rotary:
                        turn_keys(b * R + R, 0)
                    maximum(pair + parity, 1 - parity, 0)
                    if rotary:
                        turn_keys(b * R + R + 1, 1)
                keep_probs(parity, R - 1, range(len(QUADS)))

            if normed:
                centre(0, first=True)
                spread(0)
                rescale(0)
            keep_context(0)
            if rotary:
                turn_keys(0, 0, start=True)
            maximum(0, 0, 0)
            if rotary:
                turn_keys(1, 1)
            batch(0, 0, first=True)
            batch(0, 1)
            with dve.Fori(1, BATCHES // 2 - 1) as pair:
                batch(pair, 0)
                batch(pair, 1)
            batch(BATCHES // 2 - 1, 0)
            batch(BATCHES // 2 - 1, 1, last=True)
            dve.wait_ge(out_turned, 1)
            turned = score[:, 0:TOKENS].rearrange("p (t d) -> p t d", d=D)
            if out_norm:
                nc.vector.tensor_copy(out_rows[:], turned)
                dve.drain()
                normalize_dve(nc, dve, out_rows[:], out_rows[:], square[:], stats, var_ready, std_ready, 3)
                dve.drain()
                nc.vector.tensor_tensor(out_rows[:], out_rows[:], over_tiles(out_gains[:, 0, :], TILES), ALU.mult)
                dve.drain()
                nc.vector.tensor_tensor(out_rows[:], out_rows[:], over_tiles(out_gains[:, 1, :], TILES), ALU.add)
                dve.drain()
                nc.vector.tensor_tensor(lat[:], lat[:], out_rows[:], ALU.add)
            else:
                nc.vector.tensor_tensor(lat[:], lat[:], turned, ALU.add)


def top2_mask_dve(nc, dve, prob, rank, low, mask, work):
    n, experts = prob.shape[1], prob.shape[2]
    first, rest, cand, top = work[:, 0], work[:, 1], work[:, 2], work[:, 3]
    peak = top[:, :, 0]
    for source, chosen in ((prob, first), (rest, mask)):
        nc.vector.tensor_reduce(peak, source, AX, ALU.max)
        dve.drain()
        nc.vector.tensor_tensor(cand, source, over_last(peak, experts), ALU.is_ge)
        dve.drain()
        nc.vector.tensor_tensor(cand, cand, over_tiles(rank, n), ALU.mult)
        dve.drain()
        nc.vector.tensor_reduce(peak, cand, AX, ALU.max)
        dve.drain()
        nc.vector.tensor_tensor(chosen, cand, over_last(peak, experts), ALU.is_equal)
        dve.drain()
        if chosen is first:
            nc.vector.scalar_tensor_tensor(rest, first, low, prob, ALU.mult, ALU.add)
            dve.drain()
    nc.vector.tensor_tensor(mask, mask, first, ALU.add)
    dve.drain()


def moe_stage(core, name, kind, wg, w1, b1, w2, b2, bg=None):
    nc, lat = core.nc, core.lat
    E = 8
    swiglu = kind == "swiglu"
    H = w2.shape[2] if swiglu else w1.shape[2]
    C = H // P
    with ExitStack() as ctx:
        s = Stage(nc, ctx, name)
        y = s.sb("y", [P, TILES, D])
        square = s.sb("square", [P, TILES, D])
        yT = s.sb("yT", [P, TOKENS])
        stats = s.sb("stats", [P, 4, TILES])
        wg_sb = s.sb("wg", [P, E])
        w1_sb = s.sb("w1", [P, E, (2 if swiglu else 1) * H])
        w2_sb = s.sb("w2", [P, E, C, D])
        hT = s.sb("hT", [P, 2, C, TOKENS])
        prob = s.sb("prob", [P, TILES, E])
        gate = s.sb("gate", [P, TILES, E])
        mask = s.sb("mask", [P, TILES, E])
        work = s.sb("work", [P, 4, TILES, E])
        norm = s.sb("norm", [P, 2, TILES])
        gated = s.sb("gated", [P, TILES, D])
        acc = s.sb("acc", [P, TILES, D])
        if swiglu:
            w1_rows = s.sb("w1_rows", [P, E, 2 * H // P, D])
            w2_rows = s.sb("w2_rows", [P, E, H])
            wg_rows = s.sb("wg_rows", [E, D])
            silu = s.sb("silu", [P, TOKENS])
        else:
            b1_sb = s.sb("b1", [P, E, C])
            b2_sb = s.sb("b2", [E, D])
            gateT = s.sb("gateT", [E, TOKENS])
            if bg is not None:
                bg_sb = s.sb("bg", [P, E])
        hid = [s.ps(f"hid{i}", [P, TOKENS]) for i in range(2)]
        mix = s.ps("mix", [P, TILES, D])
        aux = [s.ps(f"aux{i}", [P, BANK]) for i in range(2)]

        gate_loaded, w1_loaded, w2_loaded = s.sem("gate_loaded"), s.sem("w1_loaded"), s.sem("w2_loaded")
        var_ready, std_ready = s.sem("var_ready"), s.sem("std_ready")
        y_ready, y_turned, yT_ready = s.sem("y_ready"), s.sem("y_turned"), s.sem("yT_ready")
        w_turned, w_copied = s.sem("w_turned"), s.sem("w_copied")
        logits_done, shifted, exp_done = s.sem("logits_done"), s.sem("shifted"), s.sem("exp_done")
        gate_ready, gate_turned, gateT_ready = s.sem("gate_ready"), s.sem("gate_turned"), s.sem("gateT_ready")
        hid_done, h_ready, silu_done = s.sem("hid_done"), s.sem("h_ready"), s.sem("silu_done")
        mix_done, mix_used = s.sem("mix_done"), s.sem("mix_used")
        TURNS = E * (2 * H // P) // 4 + E * C // 4
        block = s.block()

        @block.sync
        def _(sp):
            if swiglu:
                sp.dma_start(wg_rows[:], wg).then_inc(gate_loaded, 16)
                sp.dma_start(w1_rows[:], w1.rearrange("e (c p) d -> p e c d", p=P)).then_inc(w1_loaded, 16)
                sp.dma_start(w2_rows[:], w2.rearrange("e d h -> d e h")).then_inc(w2_loaded, 16)
            else:
                sp.dma_start(wg_sb[:], wg).then_inc(gate_loaded, 16)
                if bg is not None:
                    sp.dma_start(bg_sb[:], bg.partition_broadcast(P)).then_inc(gate_loaded, 16)
                sp.dma_start(w1_sb[:], w1.rearrange("e d h -> d e h")).then_inc(w1_loaded, 16)
                with nc.allow_non_contiguous_dma("bias columns"):
                    for e in range(E):
                        sp.dma_start(b1_sb[:, e, :], b1[e].rearrange("(c p) -> p c", p=P)).then_inc(w1_loaded, 16)
                sp.dma_start(b2_sb[:], b2).then_inc(w2_loaded, 16)
                sp.dma_start(w2_sb[:], w2.rearrange("e (c p) d -> p e c d", p=P)).then_inc(w2_loaded, 16)
        gate_loads = 2 if bg is not None else 1
        w1_loads = 1 if swiglu else 1 + E
        w2_loads = 1 if swiglu else 2

        @block.tensor
        def _(pe):
            pe.wait_ge(y_ready, 1)
            for t in range(TILES):
                turn = nc.tensor.transpose(aux[t // 4][:, (t % 4) * D:(t % 4 + 1) * D], y[:, t, :], core.ident[:])
                if t % 4 == 3:
                    turn.then_inc(y_turned, 1)
            if swiglu:
                pe.wait_ge(gate_loaded, 16)
                pe.wait_ge(yT_ready, 2)
                nc.tensor.transpose(aux[0][:, 0:E], wg_rows[:], core.ident[0:E, 0:E]).then_inc(w_turned, 1)
                pe.wait_ge(w1_loaded, 16)
                pe.wait_ge(w2_loaded, 16)
                blocks = [w1_rows[:, e, c, :] for e in range(E) for c in range(2 * H // P)]
                blocks += [w2_rows[:, e, c * P:(c + 1) * P] for e in range(E) for c in range(C)]
                for k in range(TURNS):
                    pe.wait_ge(w_copied, max(k, 1))
                    for j in range(4):
                        turn = nc.tensor.transpose(aux[k % 2][:, j * P:(j + 1) * P], blocks[4 * k + j], core.ident[:])
                    turn.then_inc(w_turned, 1)
                pe.wait_ge(w_copied, TURNS + 1)
            else:
                pe.wait_ge(gate_loaded, 16 * gate_loads)
                pe.wait_ge(yT_ready, 2)
            for t in range(TILES):
                score = nc.tensor.matmul(aux[0][:, t * E:(t + 1) * E], yT[:, t * P:(t + 1) * P], wg_sb[:],
                                         start=True, stop=True)
            score.then_inc(logits_done, 1)

            hidden = [0]

            def hidden_chunk(e, column):
                k = hidden[0]
                if k >= 2 and not swiglu:
                    pe.wait_ge(h_ready, k - 1)
                elif k >= 2 and k % 2 == 0:
                    pe.wait_ge(silu_done, k // 2)
                elif k >= 2:
                    pe.wait_ge(h_ready, k // 2)
                for half in range(2):
                    nc.tensor.matmul(hid[k % 2][:, half * BANK:(half + 1) * BANK],
                                     w1_sb[:, e, column:column + P], yT[:, half * BANK:(half + 1) * BANK],
                                     start=True, stop=True).then_inc(hid_done, 1)
                hidden[0] += 1

            def expert_hidden(e):
                for c in range(C):
                    hidden_chunk(e, c * P)
                    if swiglu:
                        hidden_chunk(e, H + c * P)

            def expert_out(e):
                pe.wait_ge(h_ready, C * (e + 1))
                if e >= 1:
                    pe.wait_ge(mix_used, e)
                for t in range(TILES):
                    for c in range(C):
                        out = nc.tensor.matmul(mix[:, t, :], hT[:, e % 2, c, t * P:(t + 1) * P], w2_sb[:, e, c, :],
                                               start=(c == 0), stop=(c == C - 1))
                out.then_inc(mix_done, 1)

            if not swiglu:
                pe.wait_ge(w1_loaded, 16 * w1_loads)
            expert_hidden(0)
            for e in range(E):
                if e == 1 and not swiglu:
                    pe.wait_ge(gate_ready, 1)
                    for t in range(TILES):
                        turn = nc.tensor.transpose(aux[t // 4][0:E, (t % 4) * P:(t % 4 + 1) * P], gate[:, t, :],
                                                   core.ident[:])
                    turn.then_inc(gate_turned, 1)
                if e + 1 < E:
                    expert_hidden(e + 1)
                if e == 0 and not swiglu:
                    pe.wait_ge(w2_loaded, 16 * w2_loads)
                expert_out(e)
            if not swiglu:
                pe.wait_ge(gateT_ready, 1)
                pe.wait_ge(mix_used, E)
                for t in range(TILES):
                    out = nc.tensor.matmul(mix[:, t, :], gateT[:, t * P:(t + 1) * P], b2_sb[:], start=True, stop=True)
                out.then_inc(mix_done, 1)

        @block.scalar
        def _(act):
            normalize_act(nc, act, core.eps(EPS_5), TILES, D, stats, var_ready, std_ready, 1)
            for half in range(2):
                act.wait_ge(y_turned, half + 1)
                nc.scalar.copy(yT[:, half * BANK:(half + 1) * BANK], aux[half][:]).then_inc(yT_ready, 1)
            if swiglu:
                act.wait_ge(w_turned, 1)
                nc.scalar.copy(wg_sb[:], aux[0][:, 0:E]).then_inc(w_copied, 1)
                for k in range(TURNS):
                    act.wait_ge(w_turned, k + 2)
                    turned = aux[k % 2][:].rearrange("p (j q) -> p j q", q=P)
                    per = 2 * H // P
                    if 4 * k < E * per:
                        dst = w1_sb[:].rearrange("p e (c q) -> p (e c) q", q=P)[:, 4 * k:4 * k + 4, :]
                    else:
                        j = 4 * k - E * per
                        dst = w2_sb[:].rearrange("p e c d -> p (e c) d")[:, j:j + 4, :]
                    nc.scalar.copy(dst, turned).then_inc(w_copied, 1)
            act.wait_ge(shifted, 1)
            nc.scalar.activation(prob[:], prob[:], ACT.Exp).then_inc(exp_done, 1)

            def hidden_of(e):
                for c in range(C):
                    if swiglu:
                        k = 2 * (e * C + c)
                        act.wait_ge(hid_done, 2 * k + 2)
                        if k >= 2:
                            act.wait_ge(h_ready, e * C + c)
                        nc.scalar.activation(silu[:], hid[0][:], ACT.Silu).then_inc(silu_done, 1)
                    else:
                        k = e * C + c
                        act.wait_ge(hid_done, 2 * k + 2)
                        nc.scalar.activation(hT[:, e % 2, c, :], hid[k % 2][:],
                                             ACT.Relu if kind == "relu" else ACT.Gelu,
                                             bias=b1_sb[:, e, c:c + 1]).then_inc(h_ready, 1)

            if not swiglu:
                act.wait_ge(w1_loaded, 16 * w1_loads)
            for e in range(E):
                hidden_of(e)
                if e == 1 and not swiglu:
                    act.wait_ge(gate_turned, 1)
                    for half in range(2):
                        last = nc.scalar.copy(gateT[:, half * BANK:(half + 1) * BANK], aux[half][0:E, :])
                    last.then_inc(gateT_ready, 1)

        @block.vector
        def _(dve):
            normalize_dve(nc, dve, y[:], lat[:], square[:], stats, var_ready, std_ready, 1).then_inc(y_ready, 1)
            dve.wait_ge(logits_done, 1)
            scores = aux[0][:, 0:TILES * E].rearrange("p (t e) -> p t e", e=E)
            peak, total = norm[:, 0, :], norm[:, 1, :]
            if bg is not None:
                nc.vector.tensor_tensor(gate[:], scores, over_tiles(bg_sb[:], TILES), ALU.add)
            else:
                nc.vector.tensor_copy(gate[:], scores)
            dve.drain()
            if swiglu:
                top2_mask_dve(nc, dve, gate[:], core.rank, -3e38, mask[:], work[:])
            nc.vector.tensor_reduce(peak, gate[:], AX, ALU.max)
            dve.drain()
            nc.vector.tensor_tensor(prob[:], gate[:], over_last(peak, E), ALU.subtract).then_inc(shifted, 1)
            dve.wait_ge(exp_done, 1)
            if swiglu:
                nc.vector.tensor_tensor(prob[:], prob[:], mask[:], ALU.mult)
                dve.drain()
            nc.vector.tensor_reduce(total, prob[:], AX, ALU.add)
            dve.drain()
            nc.vector.reciprocal(total, total)
            dve.drain()
            nc.vector.tensor_tensor(prob[:], prob[:], over_last(total, E), ALU.mult)
            dve.drain()
            if swiglu:
                nc.vector.tensor_copy(gate[:], prob[:])
            else:
                top2_mask_dve(nc, dve, prob[:], core.rank, -4.0, mask[:], work[:])
                if kind == "relu":
                    nc.vector.tensor_tensor(gate[:], prob[:], mask[:], ALU.mult).then_inc(gate_ready, 1)
                else:
                    nc.vector.tensor_tensor(prob[:], prob[:], mask[:], ALU.mult)
                    dve.drain()
                    nc.vector.tensor_reduce(total, prob[:], AX, ALU.add)
                    dve.drain()
                    nc.vector.tensor_scalar(total, total, 1e-12, None, ALU.max)
                    dve.drain()
                    nc.vector.reciprocal(total, total)
                    dve.drain()
                    nc.vector.tensor_tensor(gate[:], prob[:], over_last(total, E), ALU.mult).then_inc(gate_ready, 1)
            dve.drain()

            def gate_products(e):
                for c in range(C):
                    j = e * C + c
                    dve.wait_ge(silu_done, j + 1)
                    dve.wait_ge(hid_done, 4 * (j + 1))
                    nc.vector.tensor_tensor(hT[:, e % 2, c, :], hid[1][:], silu[:], ALU.mult).then_inc(h_ready, 1)

            def mix_in(e):
                dve.wait_ge(mix_done, e + 1)
                if e == E:
                    nc.vector.tensor_tensor(acc[:], mix[:], acc[:], ALU.add)
                    return
                weight = over_last(gate[:, :, e], D)
                if e == 0:
                    nc.vector.tensor_tensor(acc[:], mix[:], weight, ALU.mult).then_inc(mix_used, 1)
                else:
                    nc.vector.tensor_tensor(gated[:], mix[:], weight, ALU.mult).then_inc(mix_used, 1)
                    dve.drain()
                    nc.vector.tensor_tensor(acc[:], acc[:], gated[:], ALU.add)
                dve.drain()

            if swiglu:
                gate_products(0)
            for e in range(E):
                if swiglu and e + 1 < E:
                    gate_products(e + 1)
                mix_in(e)
            if not swiglu:
                mix_in(E)
                dve.drain()
            nc.vector.tensor_tensor(lat[:], lat[:], acc[:], ALU.add)


def turn_tiles_pe(nc, pe, ident, source, banks, ready, ready_at, turned):
    pe.wait_ge(ready, ready_at)
    for t in range(source.shape[1]):
        turn = nc.tensor.transpose(banks[t // 4][:, (t % 4) * P:(t % 4 + 1) * P], source[:, t, :], ident)
        if t % 4 == 3:
            turn.then_inc(turned, 1)


def keep_turned_act(nc, act, out, banks, turned, turned_at, kept, scale=None, bias=None):
    for half in range(len(banks)):
        act.wait_ge(turned, turned_at + half)
        dst = out[:, half * BANK:(half + 1) * BANK]
        if scale is None:
            nc.scalar.copy(dst, banks[half][:]).then_inc(kept, 1)
        else:
            nc.scalar.activation(dst, banks[half][:], ACT.Identity, bias=bias, scale=scale).then_inc(kept, 1)


def column(ap):
    return ap.rearrange("(p a) -> p a", a=1)


def mlstm_stage(core, name, w):
    nc, lat = core.nc, core.lat
    NH, DQK, DV, CAP = 8, 8, 16, 15.0
    HC = 2 * DQK + DV + 2
    Q, K, V, IG, FG = 0, DQK, 2 * DQK, HC - 2, HC - 1
    with ExitStack() as ctx:
        s = Stage(nc, ctx, name)
        y, square, yT = s.sb("y", [P, TILES, D]), s.sb("square", [P, TILES, D]), s.sb("yT", [P, TOKENS])
        stats = s.sb("stats", [P, 4, TILES])
        wq_rows, wk_rows, wv_rows = s.sb("wq_rows", [NH * DQK, D]), s.sb("wk_rows", [NH * DQK, D]), s.sb("wv_rows", [D, D])
        wi_rows, wf_rows = s.sb("wi_rows", [NH, D]), s.sb("wf_rows", [NH, D])
        wog_rows, wout_rows = s.sb("wog_rows", [D, D]), s.sb("wout_rows", [D, D])
        gate_bias = s.sb("gate_bias", [P, 2, NH])
        gain, shift = s.sb("gain", [P, D]), s.sb("shift", [P, D])
        headsT = s.sb("headsT", [D, NH, HC])
        wogT, woutT = s.sb("wogT", [D, D]), s.sb("woutT", [D, D])
        proj = s.sb("proj", [P, TILES, NH, HC])
        out_gate = s.sb("out_gate", [P, TILES, D])
        seq = s.sb("seq", [P, SEQ, HC])
        peak = s.sb("peak", [P, 1 + SEQ])
        decay = s.sb("decay", [P, 3, SEQ])
        decay_v = s.sb("decay_v", [P, DV, SEQ])
        k_in, q_scaled, n_mem = s.sb("k_in", [P, DQK, SEQ]), s.sb("q_scaled", [P, DQK, SEQ]), s.sb("n_mem", [P, DQK, SEQ])
        memory = s.sb("memory", [P, DQK, DV, SEQ])
        num, den = s.sb("num", [P, DV, SEQ]), s.sb("den", [P, 2, SEQ])
        h_seq, h_tok = s.sb("h_seq", [P, SEQ, DV]), s.sb("h_tok", [P, TILES, D])
        hT = s.sb("hT", [P, TOKENS])
        bank = [s.ps(f"bank{i}", [P, BANK]) for i in range(8)]
        seq_dram = nc.dram_tensor(f"{name}_seq_rows", (TOKENS, NH * HC), F32, kind="Internal").ap()
        h_dram = nc.dram_tensor(f"{name}_h_rows", (BATCHES, SEQ, NH, DV), F32, kind="Internal").ap()

        loaded, var_ready, std_ready = s.sem("loaded"), s.sem("var_ready"), s.sem("std_ready")
        y_ready, y_turned, yT_kept = s.sem("y_ready"), s.sem("y_turned"), s.sem("yT_kept")
        w_turned, w_kept = s.sem("w_turned"), s.sem("w_kept")
        proj_done, proj_kept, og_done = s.sem("proj_done"), s.sem("proj_kept"), s.sem("og_done")
        biased, capped, gates_ready = s.sem("biased"), s.sem("capped"), s.sem("gates_ready")
        seq_stored, seq_loaded = s.sem("seq_stored"), s.sem("seq_loaded")
        exponents, exps_done = s.sem("exponents"), s.sem("exps_done")
        h_ready, h_stored, h_loaded = s.sem("h_ready"), s.sem("h_stored"), s.sem("h_loaded")
        og_ready, h_gated, h_turned, hT_kept, out_done = (s.sem("og_ready"), s.sem("h_gated"), s.sem("h_turned"),
                                                          s.sem("hT_kept"), s.sem("out_done"))
        LOADS = 11
        block = s.block()

        @block.sync
        def _(sp):
            for dst, src in ((wq_rows, "Wq"), (wk_rows, "Wk"), (wv_rows, "Wv"), (wi_rows, "Wi"), (wf_rows, "Wf"),
                             (wog_rows, "Wog"), (wout_rows, "Wout")):
                sp.dma_start(dst[:], w[src]).then_inc(loaded, 16)
            sp.dma_start(gate_bias[:, 0, :], w["bi"].partition_broadcast(P)).then_inc(loaded, 16)
            sp.dma_start(gate_bias[:, 1, :], w["bf"].partition_broadcast(P)).then_inc(loaded, 16)
            sp.dma_start(gain[:], w["ln_w"].partition_broadcast(P)).then_inc(loaded, 16)
            sp.dma_start(shift[:], w["ln_b"].partition_broadcast(P)).then_inc(loaded, 16)
            sp.wait_ge(gates_ready, 1)
            sp.dma_start(seq_dram.rearrange("(t p) c -> p t c", p=P), proj[:].rearrange("p t h c -> p t (h c)"))\
                .then_inc(seq_stored, 16)
            sp.wait_ge(seq_stored, 16)
            for b in range(BATCHES):
                sp.dma_start(seq[b * NH:(b + 1) * NH], seq_dram[b * SEQ:(b + 1) * SEQ].rearrange("t (h c) -> h t c", c=HC))\
                    .then_inc(seq_loaded, 16)
            sp.wait_ge(h_ready, 1)
            for b in range(BATCHES):
                sp.dma_start(h_dram[b].rearrange("t h v -> h t v"), h_seq[b * NH:(b + 1) * NH]).then_inc(h_stored, 16)
            sp.wait_ge(h_stored, 16 * BATCHES)
            sp.dma_start(h_tok[:], h_dram.rearrange("(t b) i h v -> (b i) t (h v)", b=2)).then_inc(h_loaded, 16)

        @block.tensor
        def _(pe):
            pe.wait_ge(loaded, 16 * LOADS)
            at = 0
            for rows in (wq_rows, wk_rows, wv_rows, wi_rows, wf_rows):
                n = rows.shape[0]
                turn = nc.tensor.transpose(bank[2][:, at:at + n], rows[:], core.ident[0:n, 0:n])
                at += n
            turn.then_inc(w_turned, 1)
            nc.tensor.transpose(bank[3][:, 0:D], wog_rows[:], core.ident[:])
            nc.tensor.transpose(bank[3][:, D:2 * D], wout_rows[:], core.ident[:]).then_inc(w_turned, 1)
            turn_tiles_pe(nc, pe, core.ident[:], y[:], bank[0:2], y_ready, 1, y_turned)
            pe.wait_ge(w_kept, 2)
            pe.wait_ge(yT_kept, 2)
            heads = headsT[:].rearrange("d h c -> d (h c)")
            for t in range(TILES):
                if t >= 4:
                    pe.wait_ge(proj_kept, t - 3)
                nc.tensor.matmul(bank[4 + t % 4][:, 0:NH * HC], yT[:, t * P:(t + 1) * P], heads, start=True, stop=True)\
                    .then_inc(proj_done, 1)
            for t in range(TILES):
                mm = nc.tensor.matmul(bank[t // 4][:, (t % 4) * D:(t % 4 + 1) * D], yT[:, t * P:(t + 1) * P], wogT[:],
                                      start=True, stop=True)
            mm.then_inc(og_done, 1)
            turn_tiles_pe(nc, pe, core.ident[:], h_tok[:], bank[2:4], h_gated, 1, h_turned)
            pe.wait_ge(hT_kept, 2)
            for t in range(TILES):
                mm = nc.tensor.matmul(bank[4 + t // 4][:, (t % 4) * D:(t % 4 + 1) * D], hT[:, t * P:(t + 1) * P], woutT[:],
                                      start=True, stop=True)
            mm.then_inc(out_done, 1)

        @block.scalar
        def _(act):
            act.wait_ge(w_turned, 2)
            at = 0
            for c, n in ((Q, DQK), (K, DQK), (V, DV), (IG, 1), (FG, 1)):
                last = nc.scalar.copy(headsT[:, :, c:c + n], bank[2][:, at:at + NH * n].rearrange("d (h c) -> d h c", c=n))
                at += NH * n
            last.then_inc(w_kept, 1)
            nc.scalar.copy(wogT[:], bank[3][:, 0:D])
            nc.scalar.copy(woutT[:], bank[3][:, D:2 * D]).then_inc(w_kept, 1)
            normalize_act(nc, act, core.eps(EPS_5), TILES, D, stats, var_ready, std_ready, 1)
            keep_turned_act(nc, act, yT, bank[0:2], y_turned, 1, yT_kept)
            for t in range(TILES):
                act.wait_ge(proj_done, t + 1)
                nc.scalar.copy(proj[:, t].rearrange("p h c -> p (h c)"), bank[4 + t % 4][:, 0:NH * HC])\
                    .then_inc(proj_kept, 1)
            act.wait_ge(biased, 1)
            nc.scalar.activation(proj[:, :, :, IG:HC], proj[:, :, :, IG:HC], ACT.Tanh, scale=1.0 / CAP)\
                .then_inc(capped, 1)
            act.wait_ge(og_done, 1)
            for half in range(2):
                last = nc.scalar.activation(out_gate[:, 4 * half:4 * half + 4, :],
                                            bank[half][:].rearrange("p (t d) -> p t d", d=D), ACT.Sigmoid)
            last.then_inc(og_ready, 1)
            act.wait_ge(exponents, 1)
            nc.scalar.activation(decay[:], decay[:], ACT.Exp).then_inc(exps_done, 1)
            normalize_act(nc, act, core.eps(EPS_6), TILES, D, stats, var_ready, std_ready, 2)
            keep_turned_act(nc, act, hT, bank[2:4], h_turned, 1, hT_kept)

        @block.vector
        def _(dve):
            normalize_dve(nc, dve, y[:], lat[:], square[:], stats, var_ready, std_ready, 1).then_inc(y_ready, 1)
            dve.wait_ge(loaded, 16 * LOADS)
            dve.wait_ge(proj_kept, TILES)
            for n, c in enumerate((IG, FG)):
                last = nc.vector.tensor_tensor(proj[:, :, :, c], proj[:, :, :, c], over_tiles(gate_bias[:, n, :], TILES),
                                               ALU.add)
            last.then_inc(biased, 1)
            dve.wait_ge(capped, 1)
            nc.vector.tensor_scalar(proj[:, :, :, IG:HC], proj[:, :, :, IG:HC], CAP, None, ALU.mult).then_inc(gates_ready, 1)
            dve.wait_ge(seq_loaded, 16 * BATCHES)
            i_gate, f_gate = seq[:, :, IG], seq[:, :, FG]
            nc.vector.memset(peak[:, 0:1], 0.0)
            nc.vector.tensor_tensor_scan(peak[:, 1:], f_gate, i_gate, 0.0, ALU.add, ALU.max)
            dve.drain()
            nc.vector.tensor_tensor(decay[:, 0, :], f_gate, peak[:, 0:SEQ], ALU.add)
            dve.drain()
            nc.vector.tensor_tensor(decay[:, 0, :], decay[:, 0, :], peak[:, 1:], ALU.subtract)
            nc.vector.tensor_tensor(decay[:, 1, :], i_gate, peak[:, 1:], ALU.subtract)
            nc.vector.tensor_scalar(decay[:, 2, :], peak[:, 1:], -1.0, None, ALU.mult).then_inc(exponents, 1)
            by_k = seq[:, :, K:K + DQK].rearrange("p t k -> p k t")
            by_q = seq[:, :, Q:Q + DQK].rearrange("p t k -> p k t")
            by_v = seq[:, :, V:V + DV].rearrange("p t v -> p v t")
            nc.vector.tensor_scalar(q_scaled[:], by_q, DQK ** -0.5, None, ALU.mult)
            dve.wait_ge(exps_done, 1)
            nc.vector.tensor_copy(decay_v[:], over_tiles(decay[:, 0, :], DV))
            nc.vector.tensor_tensor(k_in[:], by_k, over_tiles(decay[:, 1, :], DQK), ALU.mult)
            dve.drain()
            nc.vector.memset(decay_v[:, :, 0:1], 0.0)
            shape = [P, DQK, DV, SEQ]
            nc.vector.tensor_tensor(memory[:], k_in[:].unsqueeze(2).to_broadcast(shape),
                                    by_v.unsqueeze(1).to_broadcast(shape), ALU.mult)
            dve.drain()
            flat = "p a t -> p (a t)"
            nc.vector.tensor_tensor_scan(n_mem[:].rearrange(flat), decay_v[:, 0:DQK, :].rearrange(flat),
                                         k_in[:].rearrange(flat), 0.0, ALU.mult, ALU.add)
            for k in range(DQK):
                nc.vector.tensor_tensor_scan(memory[:, k].rearrange(flat), decay_v[:].rearrange(flat),
                                             memory[:, k].rearrange(flat), 0.0, ALU.mult, ALU.add)
            dve.drain()
            nc.vector.tensor_tensor(n_mem[:], n_mem[:], q_scaled[:], ALU.mult)
            nc.vector.tensor_tensor(memory[:], memory[:], q_scaled[:].unsqueeze(2).to_broadcast(shape), ALU.mult)
            dve.drain()
            nc.vector.tensor_reduce(den[:, 0, :], n_mem[:].rearrange("p k t -> p t k"), AX, ALU.add)
            nc.vector.tensor_reduce(num[:], memory[:].rearrange("p k v t -> p v t k"), AX, ALU.add)
            dve.drain()
            nc.vector.scalar_tensor_tensor(den[:, 1, :], den[:, 0, :], -1.0, den[:, 0, :], ALU.mult, ALU.max)
            dve.drain()
            nc.vector.tensor_tensor(den[:, 0, :], den[:, 1, :], decay[:, 2, :], ALU.max)
            dve.drain()
            nc.vector.tensor_scalar(den[:, 0, :], den[:, 0, :], 1e-6, None, ALU.add)
            dve.drain()
            nc.vector.reciprocal(den[:, 1, :], den[:, 0, :])
            dve.drain()
            nc.vector.tensor_tensor(h_seq[:].rearrange("p t v -> p v t"), num[:], over_tiles(den[:, 1, :], DV), ALU.mult)\
                .then_inc(h_ready, 1)
            dve.wait_ge(h_loaded, 16)
            normalize_dve(nc, dve, h_tok[:], h_tok[:], square[:], stats, var_ready, std_ready, 2)
            dve.drain()
            nc.vector.tensor_tensor(h_tok[:], h_tok[:], over_tiles(gain[:], TILES), ALU.mult)
            dve.drain()
            nc.vector.tensor_tensor(h_tok[:], h_tok[:], over_tiles(shift[:], TILES), ALU.add)
            dve.drain()
            dve.wait_ge(og_ready, 1)
            nc.vector.tensor_tensor(h_tok[:], h_tok[:], out_gate[:], ALU.mult).then_inc(h_gated, 1)
            dve.wait_ge(out_done, 1)
            for half in range(2):
                part = lat[:, 4 * half:4 * half + 4, :]
                nc.vector.tensor_tensor(part, part, bank[4 + half][:].rearrange("p (t d) -> p t d", d=D), ALU.add)


def causal_exp_stage(core, name, w):
    nc, lat = core.nc, core.lat
    INNER = 16
    with ExitStack() as ctx:
        s = Stage(nc, ctx, name)
        y, square, yT = s.sb("y", [P, TILES, D]), s.sb("square", [P, TILES, D]), s.sb("yT", [P, TOKENS])
        stats = s.sb("stats", [P, 4, TILES])
        rows = s.sb("rows", [P, 2, D])
        wT = s.sb("wT", [P, 2 * D])
        angle = s.sb("angle", [P, 2, D])
        turn16 = s.sb("turn16", [P, 2, D], BF16)
        ident16 = s.sb("ident16", [P, P], BF16)
        causal = s.sb("causal", [P, SEQ])
        fc1 = s.sb("fc1", [P, 2, INNER])
        fc2_rows = s.sb("fc2_rows", [D, INNER])
        fc2T = s.sb("fc2T", [INNER, D])
        fc2_b = s.sb("fc2_b", [P, D])
        qk = s.sb("qk", [P, TILES * 2, D], BF16)
        along = s.sb("along", [P, TILES * 2, D], BF16)
        across = s.sb("across", [P, TILES * 2, D], BF16)
        qkT = s.sb("qkT", [P, TILES * 2, P], BF16)
        exps = s.sb("exps", [P, TILES, SEQ])
        total = s.sb("total", [P, TILES])
        hidden = s.sb("hidden", [P, TILES, INNER])
        hiddenT = s.sb("hiddenT", [INNER, TOKENS])
        bank = [s.ps(f"bank{i}", [P, BANK]) for i in range(6)]
        bank16 = [s.ps(f"bank16_{i}", [P, 8 * P], BF16) for i in range(2)]

        loaded, var_ready, std_ready = s.sem("loaded"), s.sem("var_ready"), s.sem("std_ready")
        y_ready, y_turned, yT_kept = s.sem("y_ready"), s.sem("y_turned"), s.sem("yT_kept")
        w_turned, w_kept, consts_ready = s.sem("w_turned"), s.sem("w_kept"), s.sem("consts_ready")
        qk_done, qk_rounded, qk_turned_by_pos = s.sem("qk_done"), s.sem("qk_rounded"), s.sem("qk_turned_by_pos")
        qk_turned, qkT_kept, scores_done, exps_done = (s.sem("qk_turned"), s.sem("qkT_kept"), s.sem("scores_done"),
                                                       s.sem("exps_done"))
        hidden_ready, hidden_turned, hiddenT_kept, out_done = (s.sem("hidden_ready"), s.sem("hidden_turned"),
                                                               s.sem("hiddenT_kept"), s.sem("out_done"))
        LOADS = 8
        block = s.block()

        @block.sync
        def _(sp):
            for dst, src in ((rows[:, 0, :], w["Wq"]), (rows[:, 1, :], w["Wk"]), (fc2_rows[:], w["fc2_w"]),
                             (angle[:], core.w["c_rope32"]), (causal[:], core.w["c_causal"]),
                             (fc1[:, 0, :], w["fc1_w"].rearrange("n a -> (n a)").partition_broadcast(P)),
                             (fc1[:, 1, :], w["fc1_b"].partition_broadcast(P)),
                             (fc2_b[:], w["fc2_b"].partition_broadcast(P))):
                sp.dma_start(dst, src).then_inc(loaded, 16)

        @block.tensor
        def _(pe):
            pe.wait_ge(loaded, 16 * LOADS)
            for n in range(2):
                nc.tensor.transpose(bank[2][:, n * D:(n + 1) * D], rows[:, n, :], core.ident[:])
            nc.tensor.transpose(bank[3][0:INNER, 0:D], fc2_rows[:], core.ident[:]).then_inc(w_turned, 1)
            turn_tiles_pe(nc, pe, core.ident[:], y[:], bank[0:2], y_ready, 1, y_turned)
            pe.wait_ge(w_kept, 1)
            pe.wait_ge(yT_kept, 2)
            for t in range(TILES):
                mm = nc.tensor.matmul(bank[2 + t // 2][:, (t % 2) * 2 * D:(t % 2 + 1) * 2 * D], yT[:, t * P:(t + 1) * P],
                                      wT[:], start=True, stop=True)
                if t % 2:
                    mm.then_inc(qk_done, 1)
            pe.wait_ge(qk_turned_by_pos, 1)
            for n in range(2 * TILES):
                turn = nc.tensor.transpose(bank16[n // 8][:, (n % 8) * P:(n % 8 + 1) * P], qk[:, n, :], ident16[:])
                if n % 8 == 7:
                    turn.then_inc(qk_turned, 1)
            pe.wait_ge(qkT_kept, 2)
            for b in range(BATCHES):
                t, rows_of = b // 2, slice((b % 2) * SEQ, (b % 2 + 1) * SEQ)
                mm = nc.tensor.matmul(bank[0][rows_of, t * SEQ:(t + 1) * SEQ], qkT[:, 2 * t, rows_of],
                                      qkT[:, 2 * t + 1, rows_of], start=True, stop=True)
            mm.then_inc(scores_done, 1)
            pe.wait_ge(hidden_ready, 1)
            for t in range(TILES):
                turn = nc.tensor.transpose(bank[2 + t // 4][0:INNER, (t % 4) * P:(t % 4 + 1) * P], hidden[:, t, :],
                                           core.ident[:])
            turn.then_inc(hidden_turned, 1)
            pe.wait_ge(hiddenT_kept, 2)
            for t in range(TILES):
                mm = nc.tensor.matmul(bank[4 + t // 4][:, (t % 4) * D:(t % 4 + 1) * D], hiddenT[:, t * P:(t + 1) * P],
                                      fc2T[:], start=True, stop=True)
            mm.then_inc(out_done, 1)

        @block.scalar
        def _(act):
            act.wait_ge(w_turned, 1)
            nc.scalar.copy(wT[:], bank[2][:, 0:2 * D])
            nc.scalar.copy(fc2T[:], bank[3][0:INNER, 0:D]).then_inc(w_kept, 1)
            normalize_act(nc, act, core.eps(EPS_5), TILES, D, stats, var_ready, std_ready, 1)
            keep_turned_act(nc, act, yT, bank[0:2], y_turned, 1, yT_kept)
            for k in range(TILES // 2):
                act.wait_ge(qk_done, k + 1)
                nc.scalar.copy(qk[:, 4 * k:4 * k + 4, :], bank[2 + k][:].rearrange("p (n d) -> p n d", d=D))\
                    .then_inc(qk_rounded, 1)
            for half in range(2):
                act.wait_ge(qk_turned, half + 1)
                nc.scalar.copy(qkT[:, 8 * half:8 * half + 8, :], bank16[half][:].rearrange("p (n q) -> p n q", q=P))\
                    .then_inc(qkT_kept, 1)
            act.wait_ge(scores_done, 1)
            nc.scalar.activation(exps[:], bank[0][:].rearrange("p (t j) -> p t j", j=SEQ), ACT.Exp, scale=D ** -0.5)\
                .then_inc(exps_done, 1)
            act.wait_ge(hidden_turned, 1)
            for half in range(2):
                nc.scalar.copy(hiddenT[:, half * BANK:(half + 1) * BANK], bank[2 + half][0:INNER, :])\
                    .then_inc(hiddenT_kept, 1)

        @block.vector
        def _(dve):
            normalize_dve(nc, dve, y[:], lat[:], square[:], stats, var_ready, std_ready, 1).then_inc(y_ready, 1)
            dve.wait_ge(loaded, 16 * LOADS)
            nc.vector.tensor_copy(turn16[:], angle[:])
            nc.vector.tensor_copy(ident16[:], core.ident[:])
            dve.drain()
            half = D // 2
            dve.wait_ge(qk_rounded, TILES // 2)
            nc.vector.tensor_tensor(along[:], qk[:], over_tiles(turn16[:, 0, :], 2 * TILES), ALU.mult)
            nc.vector.tensor_tensor(across[:, :, 0:half], qk[:, :, half:D], over_tiles(turn16[:, 1, 0:half], 2 * TILES),
                                    ALU.mult)
            nc.vector.tensor_tensor(across[:, :, half:D], qk[:, :, 0:half], over_tiles(turn16[:, 1, half:D], 2 * TILES),
                                    ALU.mult)
            dve.drain()
            nc.vector.tensor_tensor(qk[:], along[:], across[:], ALU.add).then_inc(qk_turned_by_pos, 1)
            dve.wait_ge(exps_done, 1)
            nc.vector.tensor_tensor(exps[:], exps[:], over_tiles(causal[:], TILES), ALU.mult)
            dve.drain()
            nc.vector.tensor_reduce(total[:], exps[:], AX, ALU.add)
            dve.drain()
            nc.vector.tensor_tensor(hidden[:], over_last(total[:], INNER), over_tiles(fc1[:, 0, :], TILES), ALU.mult)
            dve.drain()
            nc.vector.tensor_tensor(hidden[:], hidden[:], over_tiles(fc1[:, 1, :], TILES), ALU.add)
            dve.drain()
            nc.vector.tensor_scalar(hidden[:], hidden[:], 0.0, None, ALU.max).then_inc(hidden_ready, 1)
            dve.wait_ge(out_done, 1)
            nc.vector.tensor_tensor(lat[:], lat[:], over_tiles(fc2_b[:], TILES), ALU.add)
            dve.drain()
            for h in range(2):
                part = lat[:, 4 * h:4 * h + 4, :]
                nc.vector.tensor_tensor(part, part, bank[4 + h][:].rearrange("p (t d) -> p t d", d=D), ALU.add)


def projected_mlp_stage(core, name, w):
    nc, lat = core.nc, core.lat
    HID = 512
    C = HID // P
    with ExitStack() as ctx:
        s = Stage(nc, ctx, name)
        x, z, square, zT = (s.sb("x", [P, TILES, D]), s.sb("z", [P, TILES, D]), s.sb("square", [P, TILES, HID]),
                            s.sb("zT", [P, TOKENS]))
        stats = s.sb("stats", [P, 4, TILES])
        proj_rows, fc1_rows, fc2_rows = s.sb("proj_rows", [P, D]), s.sb("fc1_rows", [P, C, D]), s.sb("fc2_rows", [P, HID])
        projT, fc1T, fc2T = s.sb("projT", [P, D]), s.sb("fc1T", [P, HID]), s.sb("fc2T", [P, C, D])
        row = {n: s.sb(n, [P, D]) for n in ("proj_b", "gamma1", "gamma2", "fc2_b")}
        fc1_b = s.sb("fc1_b", [P, HID])
        cols = s.sb("cols", [P, 4 + 2 * C])
        hid = s.sb("hid", [P, TILES, HID])
        hidT = s.sb("hidT", [P, 2, C, P])
        bank = [s.ps(f"bank{i}", [P, BANK]) for i in range(8)]

        loaded, var_ready, std_ready = s.sem("loaded"), s.sem("var_ready"), s.sem("std_ready")
        w_turned, w_kept = s.sem("w_turned"), s.sem("w_kept")
        z_ready, z_turned, zT_kept = s.sem("z_ready"), s.sem("z_turned"), s.sem("zT_kept")
        proj_done, hid_done, hid_biased, gelu_done = s.sem("proj_done"), s.sem("hid_done"), s.sem("hid_biased"), s.sem("gelu_done")
        hid_ready, hid_turned, hidT_kept, out_done = s.sem("hid_ready"), s.sem("hid_turned"), s.sem("hidT_kept"), s.sem("out_done")
        LOADS = 3 + 5 + 4 + 2
        block = s.block()

        @block.sync
        def _(sp):
            sp.dma_start(proj_rows[:], w["proj_w"]).then_inc(loaded, 16)
            sp.dma_start(fc1_rows[:], w["fc1_w"].rearrange("(c p) d -> p c d", p=P)).then_inc(loaded, 16)
            sp.dma_start(fc2_rows[:], w["fc2_w"]).then_inc(loaded, 16)
            for n, dst in row.items():
                sp.dma_start(dst[:], w[n].partition_broadcast(P)).then_inc(loaded, 16)
            sp.dma_start(fc1_b[:], w["fc1_b"].partition_broadcast(P)).then_inc(loaded, 16)
            with nc.allow_non_contiguous_dma("gain columns"):
                for k, n in enumerate(("ln1_g", "ln1_b", "ln2_g", "ln2_b")):
                    sp.dma_start(cols[:, k:k + 1], column(w[n])).then_inc(loaded, 16)
                for k, n in enumerate(("lnh_g", "lnh_b")):
                    sp.dma_start(cols[:, 4 + k * C:4 + (k + 1) * C], w[n].rearrange("(c p) -> p c", p=P)).then_inc(loaded, 16)

        @block.tensor
        def _(pe):
            pe.wait_ge(loaded, 16 * LOADS)
            for c in range(C):
                nc.tensor.transpose(bank[2][:, c * P:(c + 1) * P], fc1_rows[:, c, :], core.ident[:])
            for c in range(C):
                nc.tensor.transpose(bank[3][:, c * P:(c + 1) * P], fc2_rows[:, c * P:(c + 1) * P], core.ident[:])
            nc.tensor.transpose(bank[4][:, 0:D], proj_rows[:], core.ident[:]).then_inc(w_turned, 1)
            turn_tiles_pe(nc, pe, core.ident[:], z[:], bank[0:2], z_ready, 1, z_turned)
            pe.wait_ge(zT_kept, 2)
            pe.wait_ge(w_kept, 1)
            for t in range(TILES):
                mm = nc.tensor.matmul(bank[2 + t // 4][:, (t % 4) * D:(t % 4 + 1) * D], zT[:, t * P:(t + 1) * P], projT[:],
                                      start=True, stop=True)
            mm.then_inc(proj_done, 1)
            turn_tiles_pe(nc, pe, core.ident[:], z[:], bank[0:2], z_ready, 2, z_turned)
            pe.wait_ge(zT_kept, 4)
            for t in range(TILES):
                if t >= 4:
                    pe.wait_ge(hid_biased, t - 3)
                nc.tensor.matmul(bank[4 + t % 4][:], zT[:, t * P:(t + 1) * P], fc1T[:], start=True, stop=True)\
                    .then_inc(hid_done, 1)
            pe.wait_ge(hid_ready, 1)
            for t in range(TILES + 1):
                if t < TILES:
                    if t >= 2:
                        pe.wait_ge(hidT_kept, C * (t - 1))
                    for c in range(C):
                        turn = nc.tensor.transpose(bank[t % 2][:, c * P:(c + 1) * P], hid[:, t, c * P:(c + 1) * P],
                                                   core.ident[:])
                    turn.then_inc(hid_turned, 1)
                if t >= 1:
                    u = t - 1
                    pe.wait_ge(hidT_kept, C * t)
                    for c in range(C):
                        mm = nc.tensor.matmul(bank[2 + u // 4][:, (u % 4) * D:(u % 4 + 1) * D], hidT[:, u % 2, c, :],
                                              fc2T[:, c, :], start=(c == 0), stop=(c == C - 1))
            mm.then_inc(out_done, 1)

        @block.scalar
        def _(act):
            act.wait_ge(w_turned, 1)
            nc.scalar.copy(fc1T[:], bank[2][:])
            nc.scalar.copy(fc2T[:].rearrange("p c d -> p (c d)"), bank[3][:])
            nc.scalar.copy(projT[:], bank[4][:, 0:D]).then_inc(w_kept, 1)
            act.wait_ge(loaded, 16 * LOADS)
            normalize_act(nc, act, core.eps(EPS_5), TILES, D, stats, var_ready, std_ready, 1)
            normalize_act(nc, act, core.eps(EPS_5), TILES, D, stats, var_ready, std_ready, 2)
            keep_turned_act(nc, act, zT, bank[0:2], z_turned, 1, zT_kept, scale=cols[:, 0:1], bias=cols[:, 1:2])
            normalize_act(nc, act, core.eps(EPS_5), TILES, D, stats, var_ready, std_ready, 3)
            keep_turned_act(nc, act, zT, bank[0:2], z_turned, 3, zT_kept, scale=cols[:, 2:3], bias=cols[:, 3:4])
            for t in range(TILES):
                act.wait_ge(hid_biased, t + 1)
                nc.scalar.activation(hid[:, t, :], hid[:, t, :], ACT.Gelu).then_inc(gelu_done, 1)
            normalize_act(nc, act, core.eps(EPS_5), TILES, HID, stats, var_ready, std_ready, 4)
            for t in range(TILES):
                act.wait_ge(hid_turned, t + 1)
                for c in range(C):
                    nc.scalar.activation(hidT[:, t % 2, c, :], bank[t % 2][:, c * P:(c + 1) * P], ACT.Identity,
                                         bias=cols[:, 4 + C + c:5 + C + c], scale=cols[:, 4 + c:5 + c]).then_inc(hidT_kept, 1)

        @block.vector
        def _(dve):
            first = square[:, :, 0:D]
            normalize_dve(nc, dve, x[:], lat[:], first, stats, var_ready, std_ready, 1)
            dve.drain()
            normalize_dve(nc, dve, z[:], x[:], first, stats, var_ready, std_ready, 2).then_inc(z_ready, 1)
            dve.wait_ge(loaded, 16 * LOADS)
            dve.wait_ge(proj_done, 1)
            for half in range(2):
                nc.vector.tensor_tensor(z[:, 4 * half:4 * half + 4, :], bank[2 + half][:].rearrange("p (t d) -> p t d", d=D),
                                        over_tiles(row["proj_b"][:], 4), ALU.add)
            dve.drain()
            nc.vector.tensor_tensor(z[:], z[:], over_tiles(row["gamma1"][:], TILES), ALU.mult)
            dve.drain()
            nc.vector.tensor_tensor(x[:], x[:], z[:], ALU.add)
            dve.drain()
            normalize_dve(nc, dve, z[:], x[:], first, stats, var_ready, std_ready, 3).then_inc(z_ready, 1)
            for t in range(TILES):
                dve.wait_ge(hid_done, t + 1)
                nc.vector.tensor_tensor(hid[:, t, :], bank[4 + t % 4][:], fc1_b[:], ALU.add).then_inc(hid_biased, 1)
            nc.vector.tensor_tensor(lat[:], lat[:], x[:], ALU.add)
            dve.wait_ge(gelu_done, TILES)
            normalize_dve(nc, dve, hid[:], hid[:], square[:], stats, var_ready, std_ready, 4).then_inc(hid_ready, 1)
            dve.wait_ge(out_done, 1)
            for half in range(2):
                nc.vector.tensor_tensor(z[:, 4 * half:4 * half + 4, :], bank[2 + half][:].rearrange("p (t d) -> p t d", d=D),
                                        over_tiles(row["fc2_b"][:], 4), ALU.add)
            dve.drain()
            nc.vector.tensor_tensor(z[:], z[:], over_tiles(row["gamma2"][:], TILES), ALU.mult)
            dve.drain()
            nc.vector.tensor_tensor(lat[:], lat[:], z[:], ALU.add)


def latent_attention_stage(core, name, w):
    nc, lat = core.nc, core.lat
    NH, L, DH, DHE = 16, 64, 8, 4
    KINDS = ("q", "k", "v")
    UP = 3 * DHE
    WIDTH = (UP, UP, DH)
    AT = (0, NH // 2 * UP, NH * UP)
    with ExitStack() as ctx:
        s = Stage(nc, ctx, name)
        y, square, yT = s.sb("y", [P, TILES, D]), s.sb("square", [P, TILES, D]), s.sb("yT", [P, TOKENS])
        stats = s.sb("stats", [P, 4, TILES])
        down = s.sb("down", [P, 3, NH * L])
        downT = s.sb("downT", [P, 3, NH // 2, P])
        up = s.sb("up", [P, 3, UP])
        heads = s.sb("heads", [P, 2, NH, UP])
        headsV = s.sb("headsV", [P, NH, DH])
        wc = s.sb("wc", [P, D])
        angle = s.sb("angle", [P, 2, DHE])
        causal = s.sb("causal", [P, SEQ])
        own_head = s.sb("own_head", [P, NH])
        parity = s.sb("parity", [P, D])
        qk = s.sb("qk", [P, TILES, 2, NH, UP])
        qk_rot = s.sb("qk_rot", [P, TILES, 2, NH, DH])
        turned = s.sb("turned", [P, 2, NH, DHE])
        qT, kT = s.sb("qT", [P, TOKENS]), s.sb("kT", [P, TOKENS])
        y_twice = s.sb("y_twice", [P, BATCHES, 2, SEQ])
        v_diag = s.sb("v_diag", [P, BATCHES, NH, DH])
        k_diag = s.sb("k_diag", [P, 2, NH, SEQ])
        prob = s.sb("prob", [P, 2, NH, SEQ])
        peak, rsum = s.sb("peak", [P, 2, NH]), s.sb("rsum", [P, 2, NH])
        probT = s.sb("probT", [P, 2, NH // 2, P])
        mixed, mixedT = s.sb("mixed", [P, TILES, D]), s.sb("mixedT", [P, TOKENS])
        score = [s.ps(f"score{i}", [P, NH * SEQ]) for i in range(2)]
        bank = [s.ps(f"bank{i}", [P, BANK]) for i in range(4)]

        loaded, var_ready, std_ready = s.sem("loaded"), s.sem("var_ready"), s.sem("std_ready")
        y_ready, y_turned, yT_kept = s.sem("y_ready"), s.sem("y_turned"), s.sem("yT_kept")
        up_ready, down_turned, downT_kept, heads_done, heads_kept = (s.sem("up_ready"), s.sem("down_turned"),
                                                                     s.sem("downT_kept"), s.sem("heads_done"),
                                                                     s.sem("heads_kept"))
        qk_done, qk_kept, rot_ready, rot_turned, rotT_kept = (s.sem("qk_done"), s.sem("qk_kept"), s.sem("rot_ready"),
                                                              s.sem("rot_turned"), s.sem("rotT_kept"))
        twice_ready, v_done, v_kept = s.sem("twice_ready"), s.sem("v_done"), s.sem("v_kept")
        k_spread, score_done, shifted, exp_done, prob_ready = (s.sem("k_spread"), s.sem("score_done"), s.sem("shifted"),
                                                               s.sem("exp_done"), s.sem("prob_ready"))
        prob_turned, probT_kept, mixed_done, mixed_kept = (s.sem("prob_turned"), s.sem("probT_kept"), s.sem("mixed_done"),
                                                           s.sem("mixed_kept"))
        mixed_turned, mixedT_kept, out_done = s.sem("mixed_turned"), s.sem("mixedT_kept"), s.sem("out_done")
        LOADS = 3 + 2 * 5 + 5
        block = s.block()

        @block.sync
        def _(sp):
            for n, kind in enumerate(KINDS):
                sp.dma_start(down[:, n, :], w[f"W{kind}_down"]).then_inc(loaded, 16)
            for half in range(2):
                rows = slice(half * L, (half + 1) * L)
                for n, kind in enumerate("qk"):
                    sp.dma_start(up[rows, n, 0:DHE], w[f"W{kind}_up_c"]).then_inc(loaded, 16)
                    sp.dma_start(up[rows, n, DHE:2 * DHE], w[f"W{kind}_up_e"]).then_inc(loaded, 16)
                sp.dma_start(up[rows, 2, 0:DH], w["Wv_up"]).then_inc(loaded, 16)
            sp.dma_start(wc[:], w["Wc"]).then_inc(loaded, 16)
            sp.dma_start(angle[:], core.w["c_rope4"]).then_inc(loaded, 16)
            sp.dma_start(causal[:], core.w["c_causal_add"]).then_inc(loaded, 16)
            sp.dma_start(own_head[:], core.w["c_own_head"]).then_inc(loaded, 16)
            sp.dma_start(parity[:], core.w["c_parity"]).then_inc(loaded, 16)

        @block.tensor
        def _(pe):
            pe.wait_ge(loaded, 16 * LOADS)
            for j in range(6):
                if j >= 2:
                    pe.wait_ge(downT_kept, j - 1)
                for i in range(4):
                    n, pair = j // 2, (j % 2) * 4 + i
                    turn = nc.tensor.transpose(bank[j % 2][:, i * P:(i + 1) * P], down[:, n, pair * P:(pair + 1) * P],
                                               core.ident[:])
                turn.then_inc(down_turned, 1)
            pe.wait_ge(up_ready, 1)
            pe.wait_ge(downT_kept, 6)
            for parity_of in range(2):
                rows = slice(parity_of * L, (parity_of + 1) * L)
                for n in range(3):
                    for pair in range(NH // 2):
                        mm = nc.tensor.matmul(bank[2 + parity_of][:, AT[n] + pair * WIDTH[n]:AT[n] + (pair + 1) * WIDTH[n]],
                                              downT[rows, n, pair, :], up[rows, n, 0:WIDTH[n]], start=True, stop=True)
                mm.then_inc(heads_done, 1)
            turn_tiles_pe(nc, pe, core.ident[:], y[:], bank[0:2], y_ready, 1, y_turned)
            pe.wait_ge(yT_kept, 2)
            pe.wait_ge(heads_kept, 2)
            for t in range(TILES):
                if t >= 2:
                    pe.wait_ge(qk_kept, t - 1)
                nc.tensor.matmul(bank[2 + t % 2][:, 0:2 * NH * UP], yT[:, t * P:(t + 1) * P],
                                 heads[:].rearrange("p n h c -> p (n h c)"), start=True, stop=True).then_inc(qk_done, 1)
            pe.wait_ge(twice_ready, 1)
            for b in range(BATCHES):
                if b % 4 == 0 and b >= 8:
                    pe.wait_ge(v_kept, b // 4 - 1)
                mm = nc.tensor.matmul(bank[(b // 4) % 2][:, (b % 4) * D:(b % 4 + 1) * D],
                                      y_twice[:, b].rearrange("p n j -> p (n j)"), headsV[:].rearrange("p h d -> p (h d)"),
                                      start=True, stop=True)
                if b % 4 == 3:
                    mm.then_inc(v_done, 1)
            pe.wait_ge(rot_ready, TILES)
            pe.wait_ge(v_kept, 4)
            for j in range(4):
                for i in range(4):
                    t = (j % 2) * 4 + i
                    turn = nc.tensor.transpose(bank[j][:, i * P:(i + 1) * P],
                                               qk_rot[:, t, j // 2].rearrange("p h d -> p (h d)"), core.ident[:])
                turn.then_inc(rot_turned, 1)
            pe.wait_ge(rotT_kept, 4)

            def scores(t):
                if t >= 2:
                    pe.wait_ge(shifted, t - 1)
                for b in (2 * t, 2 * t + 1):
                    pe.wait_ge(k_spread, b + 1)
                    for half in range(2):
                        mm = nc.tensor.matmul(score[t % 2][(b % 2) * SEQ:(b % 2 + 1) * SEQ, half * BANK:(half + 1) * BANK],
                                              qT[:, b * SEQ:(b + 1) * SEQ],
                                              k_diag[:, b % 2].rearrange("p h j -> p (h j)")[:, half * BANK:(half + 1) * BANK],
                                              start=True, stop=True)
                    mm.then_inc(score_done, 1)

            def mix(t):
                pe.wait_ge(prob_ready, t + 1)
                for half in range(2):
                    if t >= 1:
                        pe.wait_ge(probT_kept, 2 * (t - 1) + half + 1)
                    for i in range(4):
                        pair = 4 * half + i
                        turn = nc.tensor.transpose(bank[half][:, i * P:(i + 1) * P],
                                                   prob[:, t % 2].rearrange("p h j -> p (h j)")[:, pair * P:(pair + 1) * P],
                                                   core.ident[:])
                    turn.then_inc(prob_turned, 1)
                pe.wait_ge(probT_kept, 2 * t + 2)
                if t >= 2:
                    pe.wait_ge(mixed_kept, t - 1)
                for b in (2 * t, 2 * t + 1):
                    rows = slice((b % 2) * SEQ, (b % 2 + 1) * SEQ)
                    for pair in range(NH // 2):
                        mm = nc.tensor.matmul(bank[2 + t % 2][rows, pair * 2 * DH:(pair + 1) * 2 * DH],
                                              probT[:, t % 2, pair, rows],
                                              v_diag[:, b, 2 * pair:2 * pair + 2, :].rearrange("p h d -> p (h d)"),
                                              start=True, stop=True)
                mm.then_inc(mixed_done, 1)

            scores(0)
            for t in range(TILES):
                if t + 1 < TILES:
                    scores(t + 1)
                mix(t)
            turn_tiles_pe(nc, pe, core.ident[:], mixed[:], bank[0:2], mixed_kept, TILES, mixed_turned)
            pe.wait_ge(mixedT_kept, 2)
            for t in range(TILES):
                mm = nc.tensor.matmul(bank[2 + t // 4][:, (t % 4) * D:(t % 4 + 1) * D], mixedT[:, t * P:(t + 1) * P], wc[:],
                                      start=True, stop=True)
            mm.then_inc(out_done, 1)

        @block.scalar
        def _(act):
            for j in range(6):
                act.wait_ge(down_turned, j + 1)
                nc.scalar.copy(downT[:, j // 2, (j % 2) * 4:(j % 2) * 4 + 4, :],
                               bank[j % 2][:].rearrange("p (i d) -> p i d", d=P)).then_inc(downT_kept, 1)
            for parity_of in range(2):
                act.wait_ge(heads_done, parity_of + 1)
                for n, dst in enumerate((heads[:, 0], heads[:, 1], headsV[:])):
                    last = nc.scalar.copy(dst.rearrange("p (a r) c -> p r a c", r=2)[:, parity_of],
                                          bank[2 + parity_of][:, AT[n]:AT[n] + NH // 2 * WIDTH[n]]
                                          .rearrange("p (a c) -> p a c", c=WIDTH[n]))
                last.then_inc(heads_kept, 1)
            normalize_act(nc, act, core.eps(EPS_5), TILES, D, stats, var_ready, std_ready, 1)
            keep_turned_act(nc, act, yT, bank[0:2], y_turned, 1, yT_kept)
            act.wait_ge(yT_kept, 2)
            for copy in range(2):
                last = nc.scalar.copy(y_twice[:, :, copy, :], yT[:].rearrange("p (b j) -> p b j", j=SEQ))
            last.then_inc(twice_ready, 1)
            for t in range(TILES):
                act.wait_ge(qk_done, t + 1)
                nc.scalar.copy(qk[:, t].rearrange("p n h c -> p (n h c)"), bank[2 + t % 2][:, 0:2 * NH * UP])\
                    .then_inc(qk_kept, 1)
            for j in range(4):
                act.wait_ge(rot_turned, j + 1)
                nc.scalar.copy((qT if j < 2 else kT)[:, (j % 2) * BANK:(j % 2 + 1) * BANK], bank[j][:]).then_inc(rotT_kept, 1)
            for t in range(TILES):
                act.wait_ge(shifted, t + 1)
                nc.scalar.activation(prob[:, t % 2], prob[:, t % 2], ACT.Exp, scale=DH ** -0.5).then_inc(exp_done, 1)
                for half in range(2):
                    act.wait_ge(prob_turned, 2 * t + half + 1)
                    nc.scalar.copy(probT[:, t % 2, 4 * half:4 * half + 4, :], bank[half][:].rearrange("p (i d) -> p i d", d=P))\
                        .then_inc(probT_kept, 1)
                act.wait_ge(mixed_done, t + 1)
                nc.scalar.copy(mixed[:, t, :], bank[2 + t % 2][:, 0:D]).then_inc(mixed_kept, 1)
            keep_turned_act(nc, act, mixedT, bank[0:2], mixed_turned, 1, mixedT_kept)

        @block.gpsimd
        def _(pool):
            pool.wait_ge(rotT_kept, 4)
            pool.wait_ge(loaded, 16 * LOADS)
            for b in range(BATCHES):
                if b >= 2:
                    pool.wait_ge(score_done, b - 1)
                nc.gpsimd.tensor_tensor(k_diag[:, b % 2], over_tiles(kT[:, b * SEQ:(b + 1) * SEQ], NH),
                                        over_last(own_head[:], SEQ), ALU.mult).then_inc(k_spread, 1)

        @block.vector
        def _(dve):
            dve.wait_ge(loaded, 16 * LOADS)
            pairs = up[:, 0:2, DHE:2 * DHE].rearrange("p n (a b) -> p n a b", b=2)
            partner = up[:, 0:2, 2 * DHE:UP].rearrange("p n (a b) -> p n a b", b=2)
            nc.vector.tensor_scalar(partner[:, :, :, 0], pairs[:, :, :, 1], -1.0, None, ALU.mult)
            nc.vector.tensor_copy(partner[:, :, :, 1], pairs[:, :, :, 0]).then_inc(up_ready, 1)
            normalize_dve(nc, dve, y[:], lat[:], square[:], stats, var_ready, std_ready, 1).then_inc(y_ready, 1)
            for t in range(TILES):
                dve.wait_ge(qk_kept, t + 1)
                cols = qk[:, t].rearrange("p n h c -> p (n h) c")
                out = qk_rot[:, t].rearrange("p n h c -> p (n h) c")
                side = turned[:].rearrange("p n h c -> p (n h) c")
                nc.vector.tensor_copy(out[:, :, 0:DHE], cols[:, :, 0:DHE])
                nc.vector.tensor_tensor(out[:, :, DHE:DH], cols[:, :, DHE:2 * DHE], over_tiles(angle[:, 0, :], 2 * NH), ALU.mult)
                nc.vector.tensor_tensor(side, cols[:, :, 2 * DHE:UP], over_tiles(angle[:, 1, :], 2 * NH), ALU.mult)
                dve.drain()
                nc.vector.tensor_tensor(out[:, :, DHE:DH], out[:, :, DHE:DH], side, ALU.add).then_inc(rot_ready, 1)
                dve.drain()
            for j in range(4):
                dve.wait_ge(v_done, j + 1)
                nc.vector.tensor_tensor(v_diag[:, 4 * j:4 * j + 4].rearrange("p b h d -> p b (h d)"),
                                        bank[j % 2][:].rearrange("p (b c) -> p b c", c=D),
                                        over_tiles(parity[:], 4), ALU.mult).then_inc(v_kept, 1)

            def shift(t):
                dve.wait_ge(score_done, 2 * t + 2)
                rows = prob[:, t % 2]
                nc.vector.tensor_tensor(rows, score[t % 2][:].rearrange("p (h j) -> p h j", j=SEQ),
                                        over_tiles(causal[:], NH), ALU.add)
                dve.drain()
                nc.vector.tensor_reduce(peak[:, t % 2, :], rows, AX, ALU.max)
                dve.drain()
                nc.vector.tensor_tensor(rows, rows, over_last(peak[:, t % 2, :], SEQ), ALU.subtract).then_inc(shifted, 1)

            def normalise(t):
                dve.wait_ge(exp_done, t + 1)
                rows = prob[:, t % 2]
                nc.vector.tensor_reduce(peak[:, t % 2, :], rows, AX, ALU.add)
                dve.drain()
                nc.vector.reciprocal(rsum[:, t % 2, :], peak[:, t % 2, :])
                dve.drain()
                nc.vector.tensor_tensor(rows, rows, over_last(rsum[:, t % 2, :], SEQ), ALU.mult).then_inc(prob_ready, 1)

            shift(0)
            for t in range(TILES):
                normalise(t)
                if t + 1 < TILES:
                    if t >= 1:
                        dve.wait_ge(prob_turned, 2 * t)
                    shift(t + 1)
            dve.wait_ge(out_done, 1)
            for half in range(2):
                part = lat[:, 4 * half:4 * half + 4, :]
                nc.vector.tensor_tensor(part, part, bank[2 + half][:].rearrange("p (t d) -> p t d", d=D), ALU.add)


def gated_recurrence_stage(core, name, w):
    nc, lat = core.nc, core.lat
    STEPS = BATCHES
    NAMES = ("wf", "wi", "wc", "wo", "uf", "ui", "uc", "uo")
    F, I, G = 0, 1, 2
    with ExitStack() as ctx:
        s = Stage(nc, ctx, name)
        y, square, yT = s.sb("y", [P, TILES, D]), s.sb("square", [P, TILES, D]), s.sb("yT", [P, TOKENS])
        stats = s.sb("stats", [P, 4, TILES])
        rows = s.sb("rows", [P, 8, D])
        wT = s.sb("wT", [P, 8, D])
        bias = s.sb("bias", [P, 5])
        state = s.sb("state", [P, SEQ])
        gates = s.sb("gates", [P, 3, SEQ])
        kept, added = s.sb("kept", [P, SEQ]), s.sb("added", [P, SEQ])
        outT = s.sb("outT", [P, TOKENS])
        bank = [s.ps(f"bank{i}", [P, BANK]) for i in range(8)]
        gate_bank = (bank[4:7], (bank[7], bank[2], bank[3]))

        loaded, var_ready, std_ready = s.sem("loaded"), s.sem("var_ready"), s.sem("std_ready")
        y_ready, y_turned, yT_kept = s.sem("y_ready"), s.sem("y_turned"), s.sem("yT_kept")
        w_turned, w_kept = s.sem("w_turned"), s.sem("w_kept")
        pre_done, gates_done, state_ready = s.sem("pre_done"), s.sem("gates_done"), s.sem("state_ready")
        out_done, out_kept, out_turned = s.sem("out_done"), s.sem("out_kept"), s.sem("out_turned")
        LOADS = 13
        block = s.block()

        @block.sync
        def _(sp):
            for n, src in enumerate(NAMES):
                sp.dma_start(rows[:, n, :], w[src]).then_inc(loaded, 16)
            with nc.allow_non_contiguous_dma("bias columns"):
                for n, src in enumerate(("bf", "bi", "bc", "bo", "in_c")):
                    sp.dma_start(bias[:, n:n + 1], column(w[src])).then_inc(loaded, 16)

        @block.tensor
        def _(pe):
            pe.wait_ge(loaded, 16 * LOADS)
            for n in range(8):
                turn = nc.tensor.transpose(bank[2 + n // 4][:, (n % 4) * P:(n % 4 + 1) * P], rows[:, n, :], core.ident[:])
            turn.then_inc(w_turned, 1)
            turn_tiles_pe(nc, pe, core.ident[:], y[:], bank[0:2], y_ready, 1, y_turned)
            pe.wait_ge(w_kept, 2)
            pe.wait_ge(yT_kept, 2)

            def token_part(step):
                if step >= 2:
                    pe.wait_ge(gates_done, 3 * (step - 1))
                for gate in (F, I, G):
                    nc.tensor.matmul(gate_bank[step % 2][gate][:, 0:SEQ], wT[:, gate, :], yT[:, step * SEQ:(step + 1) * SEQ],
                                     start=True, stop=False)

            token_part(0)
            for step in range(STEPS):
                if step + 1 < STEPS:
                    token_part(step + 1)
                pe.wait_ge(state_ready, step + 1)
                for gate in (F, I, G):
                    nc.tensor.matmul(gate_bank[step % 2][gate][:, 0:SEQ], wT[:, 4 + gate, :], state[:], start=False, stop=True)\
                        .then_inc(pre_done, 1)
            for half in range(2):
                nc.tensor.matmul(bank[half][:], wT[:, 3, :], yT[:, half * BANK:(half + 1) * BANK], start=True, stop=False)
            pe.wait_ge(state_ready, STEPS + 1)
            for half in range(2):
                nc.tensor.matmul(bank[half][:].rearrange("p (t j) -> p t j", j=SEQ), wT[:, 7, :],
                                 over_tiles(state[:], STEPS // 2), start=False, stop=True).then_inc(out_done, 1)
            for t in range(TILES):
                if t % 4 == 0:
                    pe.wait_ge(out_kept, t // 4 + 1)
                turn = nc.tensor.transpose(bank[2 + t // 4][:, (t % 4) * P:(t % 4 + 1) * P], outT[:, t * P:(t + 1) * P],
                                           core.ident[:])
                if t % 4 == 3:
                    turn.then_inc(out_turned, 1)

        @block.scalar
        def _(act):
            act.wait_ge(w_turned, 1)
            for half in range(2):
                nc.scalar.copy(wT[:, 4 * half:4 * half + 4, :], bank[2 + half][:].rearrange("p (n d) -> p n d", d=D))\
                    .then_inc(w_kept, 1)
            normalize_act(nc, act, core.eps(EPS_5), TILES, D, stats, var_ready, std_ready, 1)
            keep_turned_act(nc, act, yT, bank[0:2], y_turned, 1, yT_kept)
            act.wait_ge(loaded, 16 * LOADS)
            for step in range(STEPS):
                for gate, func in ((F, ACT.Sigmoid), (I, ACT.Sigmoid), (G, ACT.Tanh)):
                    act.wait_ge(pre_done, 3 * step + gate + 1)
                    if step >= 1 and gate == F:
                        act.wait_ge(state_ready, step + 1)
                    nc.scalar.activation(gates[:, gate, :], gate_bank[step % 2][gate][:, 0:SEQ], func, bias=bias[:, gate:gate + 1])\
                        .then_inc(gates_done, 1)
            for half in range(2):
                act.wait_ge(out_done, half + 1)
                nc.scalar.activation(outT[:, half * BANK:(half + 1) * BANK], bank[half][:], ACT.Tanh, bias=bias[:, 3:4])\
                    .then_inc(out_kept, 1)

        @block.vector
        def _(dve):
            normalize_dve(nc, dve, y[:], lat[:], square[:], stats, var_ready, std_ready, 1).then_inc(y_ready, 1)
            dve.wait_ge(loaded, 16 * LOADS)
            nc.vector.tensor_copy(state[:], bias[:, 4:5].to_broadcast([P, SEQ])).then_inc(state_ready, 1)
            dve.drain()
            for step in range(STEPS):
                dve.wait_ge(gates_done, 3 * step + 1)
                nc.vector.tensor_tensor(kept[:], state[:], gates[:, F, :], ALU.mult)
                dve.wait_ge(gates_done, 3 * step + 3)
                nc.vector.tensor_tensor(added[:], gates[:, I, :], gates[:, G, :], ALU.mult)
                dve.drain()
                nc.vector.tensor_tensor(state[:], kept[:], added[:], ALU.add).then_inc(state_ready, 1)
                dve.drain()
            for half in range(2):
                dve.wait_ge(out_turned, half + 1)
                part = lat[:, 4 * half:4 * half + 4, :]
                nc.vector.tensor_tensor(part, part, bank[2 + half][:].rearrange("p (t d) -> p t d", d=D), ALU.add)


class Core:

    def __init__(self, nc, lat, ident, small):
        self.nc, self.lat, self.ident, self.small = nc, lat, ident, small
        self.rank = small[:, 8:16]

    def eps(self, which):
        return self.small[:, which:which + 1]


def constants():
    small = np.zeros((P, 16), np.float32)
    small[:, EPS_5], small[:, EPS_6] = 1e-5, 1e-6
    small[:, 8:16] = np.arange(8, 0, -1)
    position = np.arange(P, dtype=np.float32) % SEQ
    angle = position[:, None] * np.float32(32.0) ** (-np.arange(0, D, 2, dtype=np.float32) / np.float32(D))
    rope32 = np.stack([np.tile(np.cos(angle), 2), np.concatenate([-np.sin(angle), np.sin(angle)], 1)], 1)
    angle = position[:, None] * (1 / np.float32(10000.0) ** (np.arange(0, 4, 2, dtype=np.float32) / np.float32(4)))
    rope4 = np.stack([np.tile(np.cos(angle), 2), np.tile(np.sin(angle), 2)], 1)
    theta = np.arange(CTX, dtype=np.float32)[None, :] * \
        (1 / np.float32(10000.0) ** (np.arange(0, 64, 2, dtype=np.float32) / np.float32(64)))[np.arange(P) % 32][:, None]
    sign = np.where(np.arange(P) < SEQ, 1, -1)[:, None]
    rope64 = np.stack([np.cos(theta), np.sin(theta) * sign])
    earlier = np.arange(SEQ)[None, :] <= position[:, None]
    feature = np.arange(P)
    return {
        "c_ident": np.eye(P, dtype=np.float32), "c_small": small,
        "c_rope32": rope32.astype(np.float32), "c_rope4": rope4.astype(np.float32),
        "c_causal": earlier.astype(np.float32), "c_causal_add": np.where(earlier, 0, -1e30).astype(np.float32),
        "c_rope64": rope64.astype(np.float32),
        "c_own_head": (feature[:, None] // 8 == np.arange(16)[None, :]).astype(np.float32),
        "c_parity": (feature[:, None] // SEQ == feature[None, :] // 8 % 2).astype(np.float32),
    }


def weights(w, stage):
    return {name[len(stage) + 1:]: ap for name, ap in w.items() if name.startswith(stage + "_")}


STAGES = {
    "L0_xattn": lambda core, w: cross_attention_stage(core, "L0_xattn", weights(w, "L0_xattn"), heads=8, scale=1 / 64,
                                                      normed=True, masked=True, out_norm=True),
    "L0_attn": lambda core, w: mlstm_stage(core, "L0_attn", weights(w, "L0_attn")),
    "L0_ffn": lambda core, w: moe_stage(core, "L0_ffn", "relu", w["L0_ffn_Wg"], w["L0_ffn_W1"], w["L0_ffn_b1"],
                                        w["L0_ffn_W2"], w["L0_ffn_b2"]),
    "L1_xattn": lambda core, w: cross_attention_stage(core, "L1_xattn", weights(w, "L1_xattn"), heads=16, scale=1 / 8),
    "L1_attn": lambda core, w: causal_exp_stage(core, "L1_attn", weights(w, "L1_attn")),
    "L1_ffn": lambda core, w: moe_stage(core, "L1_ffn", "swiglu", w["L1_ffn_gate_w"], w["L1_ffn_w12"], None,
                                        w["L1_ffn_w3"], None),
    "L2_xattn": lambda core, w: cross_attention_stage(core, "L2_xattn", weights(w, "L2_xattn"), heads=1, scale=D ** -0.5,
                                                      single=True),
    "L2_attn": lambda core, w: projected_mlp_stage(core, "L2_attn", weights(w, "L2_attn")),
    "L2_ffn": lambda core, w: moe_stage(core, "L2_ffn", "gelu", w["L2_ffn_Wg"], w["L2_ffn_W1"], w["L2_ffn_b1"],
                                        w["L2_ffn_W2"], w["L2_ffn_b2"], w["L2_ffn_bg"]),
    "L3_xattn": lambda core, w: cross_attention_stage(core, "L3_xattn", weights(w, "L3_xattn"), heads=8, scale=1 / 8,
                                                      normed=True, rotary=True),
    "L3_attn": lambda core, w: latent_attention_stage(core, "L3_attn", weights(w, "L3_attn")),
    "L3_ffn": lambda core, w: gated_recurrence_stage(core, "L3_ffn", weights(w, "L3_ffn")),
}


def build(nc, w, out, stages=tuple(STAGES)):
    with ExitStack() as ctx:
        s = Stage(nc, ctx, "all")
        lat = s.sb("lat", [P, TILES, D])
        ident = s.sb("ident", [P, P])
        small = s.sb("small", [P, 16])
        loaded, stored = s.sem("loaded"), s.sem("stored")
        core = Core(nc, lat, ident, small)
        core.w = w
        with nc.Block() as block:
            @block.sync
            def _(sp):
                sp.dma_start(lat[:], w["x"].rearrange("(t b) i d -> (b i) t d", b=2)).then_inc(loaded, 16)
                sp.dma_start(ident[:], w["c_ident"]).then_inc(loaded, 16)
                sp.dma_start(small[:], w["c_small"]).then_inc(loaded, 16)
                sp.wait_ge(loaded, 48)
        for name in stages:
            STAGES[name](core, w)
        with nc.Block() as block:
            @block.sync
            def _(sp):
                sp.dma_start(out.rearrange("(t b) i d -> (b i) t d", b=2), lat[:]).then_inc(stored, 16)
                sp.wait_ge(stored, 16)


def kernel(**inputs):
    import concourse.bacc as bacc
    from concourse.bass_utils import run_bass_kernel_spmd

    nc = bacc.Bacc("TRN2", target_bir_lowering=False, num_devices=1)
    arrays, w = {}, {}
    for name, value in {**inputs, **constants()}.items():
        value = np.ascontiguousarray(value)
        arrays["in_" + name] = value
        w[name] = nc.dram_tensor("in_" + name, value.shape, mybir.dt.from_np(value.dtype), kind="ExternalInput").ap()
    out = nc.dram_tensor("latents_out", (BATCHES, SEQ, D), F32, kind="ExternalOutput").ap()
    build(nc, w, out)
    result = run_bass_kernel_spmd(nc, [arrays], core_ids=[0])
    return result.results[0]["latents_out"]
```

```python
from contextlib import ExitStack

import numpy as np

import concourse.bass as bass
from concourse import mybir

ALU = mybir.AluOpType
ACT = mybir.ActivationFunctionType
AX = mybir.AxisListType.X
F32 = mybir.dt.float32
BF16 = mybir.dt.bfloat16
U8 = mybir.dt.uint8

P = 128
D = 128
BATCHES = 16
SEQ = 64
TILES = BATCHES * SEQ // P
TOKENS = BATCHES * SEQ
CTX = 1601
BANK = 512
EPS_5, EPS_6 = 0, 1


class Stage:

    def __init__(self, nc, ctx, name):
        self.nc, self.ctx, self.name, self.sems = nc, ctx, name, []
        ctx.callback(self.clear)

    def sb(self, name, shape, dtype=F32):
        return self.ctx.enter_context(self.nc.sbuf_tensor(f"{self.name}_{name}", shape, dtype))

    def ps(self, name, shape, dtype=F32):
        return self.ctx.enter_context(self.nc.psum_tensor(f"{self.name}_{name}", shape, dtype))

    def sem(self, name):
        handle = self.nc.alloc_semaphore(name=f"{self.name}_{name}")
        self.sems.append(handle)
        return handle

    def clear(self):
        self.nc.clear_and_free_semaphores(self.sems)
        self.nc.all_engine_barrier()

    def block(self):
        return self.ctx.enter_context(self.nc.Block())


def over_last(ap, width):
    return ap.unsqueeze(2).to_broadcast([ap.shape[0], ap.shape[1], width])


def over_tiles(ap, tiles):
    return ap.unsqueeze(1).to_broadcast([ap.shape[0], tiles, ap.shape[1]])


def normalize_dve(nc, dve, out, src, square, stats, var_ready, std_ready, use):
    n, width = src.shape[1], src.shape[2]
    mean, var, std, rstd = (stats[:, k, 0:n] for k in range(4))
    nc.vector.tensor_reduce(mean, src, AX, ALU.add)
    dve.drain()
    nc.vector.tensor_scalar(mean, mean, 1.0 / width, None, ALU.mult)
    dve.drain()
    nc.vector.tensor_tensor(out, src, over_last(mean, width), ALU.subtract)
    dve.drain()
    nc.vector.tensor_tensor(square, out, out, ALU.mult)
    dve.drain()
    nc.vector.tensor_reduce(var, square, AX, ALU.add).then_inc(var_ready, 1)
    dve.wait_ge(std_ready, use)
    nc.vector.reciprocal(rstd, std)
    dve.drain()
    return nc.vector.tensor_tensor(out, out, over_last(rstd, width), ALU.mult)


def normalize_act(nc, act, eps, n, width, stats, var_ready, std_ready, use):
    act.wait_ge(var_ready, use)
    nc.scalar.activation(stats[:, 2, 0:n], stats[:, 1, 0:n], ACT.Sqrt, bias=eps, scale=1.0 / width)\
        .then_inc(std_ready, 1)


class Lane:

    def __init__(self, banks, full, free):
        self.banks, self.full, self.free = banks, full, free
        self.at, self.n, self.turn = 0, 0, 0

    def go_to(self, at, turn):
        self.at, self.n, self.turn = at, 0, turn

    def count(self):
        return self.at + self.n

    def bank(self):
        return self.banks[self.turn % len(self.banks)]

    def next(self):
        self.n += 1
        self.turn += 1


def full_tiles(tiles):
    if tiles[0] < CTX // P:
        return [(tiles[0], len(tiles), P)]
    return [(tiles[0], 1, CTX % P)] + [(k, 1, SEQ) for k in tiles[1:]]


def cross_attention_stage(core, name, w, heads, scale, normed=False, masked=False, rotary=False, out_norm=False):
    nc, lat = core.nc, core.lat
    NH, HD = heads, 64
    R = NH // 2
    GROUPS = R // 2
    GCOLS = 2 * P
    CT = -(-CTX // P)
    TAIL = CTX - (CT - 1) * P
    KEYS = CTX + (SEQ if normed else 0)
    tile_of_keys = [(k * P, min(P, CTX - k * P)) for k in range(CT)] + ([(CTX, SEQ)] if normed else [])
    KT = len(tile_of_keys)
    CHUNKS = [(c * BANK, min(BANK, KEYS - c * BANK)) for c in range(-(-KEYS // BANK))]
    CTX_CHUNKS = [(c * BANK, min(BANK, CTX - c * BANK)) for c in range(-(-CTX // BANK))]
    HALVES = [(0, 2 * BANK), (2 * BANK, KEYS - 2 * BANK)]
    QUADS = [list(range(q, min(q + 4, KT))) for q in range(0, KT, 4)]
    PARTS = [range(0, 7), range(7, KT)]
    QJOBS = 1 if rotary else NH // 8
    CTX_SLOT = R - 1 if masked else R - 2
    KEPT_SLOT = 3
    LAST = BATCHES // 2 - 1

    with ExitStack() as ctx:
        s = Stage(nc, ctx, name)
        y, square, yT = s.sb("y", [P, TILES, D]), s.sb("square", [P, TILES, D]), s.sb("yT", [P, TOKENS])
        stats = s.sb("stats", [P, 4, TILES])
        rows = s.sb("rows", [P, 2, KT, D])
        keysT = s.sb("keysT", [P, 2, KEYS])
        prob = s.sb("prob", [P, 2, KEYS])
        probT = s.sb("probT", [P, 2, KT, GCOLS])
        queries = s.sb("queries", [P, 2, R * P])
        peak, neg_peak = s.sb("peak", [P, 2]), s.sb("neg_peak", [P, 2])
        rsum, rinv = s.sb("rsum", [P, 2]), s.sb("rinv", [P, 2])
        mixed = s.sb("mixed", [P, R * P])
        outT = s.sb("outT", [P, TOKENS])
        if normed:
            xhat = s.sb("xhat", [P, CT, D])
            gained = s.sb("gained", [P, CT, D])
            gains = s.sb("gains", [P, 4, D])
        if masked:
            raw = s.sb("raw", [P, CT, D])
            moments, mean_var = s.sb("moments", [P, CT, 6]), s.sb("mean_var", [P, CT, 2])
            cstd, crstd = s.sb("cstd", [P, CT]), s.sb("crstd", [P, CT])
            pick16 = s.sb("pick16", [P, P], BF16)
            mask16 = s.sb("mask16", [P, 2, KEYS], BF16)
            mask_u8, mask_all = s.sb("mask_u8", [BATCHES, CTX], U8), s.sb("mask_all", [BATCHES, KEYS], BF16)
            mask_dram = nc.dram_tensor(f"{name}_mask_rows", (BATCHES, KEYS), BF16, kind="Internal").ap()
        if out_norm:
            out_gains = s.sb("out_gains", [P, 2, D])
        wv_rows, wo_rows = s.sb("wv_rows", [P, NH * HD]), s.sb("wo_rows", [P, R, D])
        wvT = s.sb("wvT", [P, R, D])
        fold_vo = s.sb("fold_vo", [P, NH, D])
        if rotary:
            wq, wk = s.sb("wq", [P, R, P]), s.sb("wk", [P, R, P])
            rot_cos, rot_sin = s.sb("rot_cos", [P, KEYS]), s.sb("rot_sin", [P, KEYS])
            unturned = s.sb("unturned", [P, 2, KEYS])
            projected = s.sb("projected", [P, 2, KEYS])
            crossed = s.sb("crossed", [P, KEYS])
        else:
            wq_rows, wk_rows = s.sb("wq_rows", [P, NH * HD]), s.sb("wk_rows", [P, NH * HD])
            wqT, wkT = s.sb("wqT", [P, R, D]), s.sb("wkT", [P, R, D])
            fold_qk = s.sb("fold_qk", [P, NH, D])
        if "b_o" in w:
            out_bias = s.sb("out_bias", [P, 1])

        score = s.ps("score", [P, 4 * BANK])
        lane_bank = [s.ps(f"lane{i}", [P, BANK]) for i in range(3)]
        sums = s.ps("sums", [P, BANK])

        w_loaded, var_ready, std_ready = s.sem("w_loaded"), s.sem("var_ready"), s.sem("std_ready")
        y_ready, y_turned, yT_kept = s.sem("y_ready"), s.sem("y_turned"), s.sem("yT_kept")
        w_turned, w_kept = s.sem("w_turned"), s.sem("w_kept")
        cleared, ctx_loaded = s.sem("cleared"), s.sem("ctx_loaded")
        if masked:
            mask_ready, mask_stored = s.sem("mask_ready"), s.sem("mask_stored")
            mask_loaded = [s.sem(f"mask_loaded{i}") for i in range(2)]
            raw_used, cvar_ready, cstd_ready, crstd_ready = (s.sem("raw_used"), s.sem("cvar_ready"), s.sem("cstd_ready"),
                                                             s.sem("crstd_ready"))
            xhat_ready, xhat_stored = s.sem("xhat_ready"), s.sem("xhat_stored")
        if normed:
            gained_ready, rows_ready = s.sem("gained_ready"), s.sem("rows_ready")
            own_loaded = [s.sem(f"own_loaded{i}") for i in range(2)]
        else:
            rows_loaded = [s.sem(f"rows_loaded{i}") for i in range(2)]
        if rotary:
            unturned_ready, crossed_ready, keys_turned = s.sem("unturned_ready"), s.sem("crossed_ready"), s.sem("keys_turned")
        score_half, peak_ready, exp_done, prob_ready = (s.sem("score_half"), s.sem("peak_ready"), s.sem("exp_done"),
                                                        s.sem("prob_ready"))
        sums_done, sums_kept = s.sem("sums_done"), s.sem("sums_kept")
        act_full, act_free, dve_full, dve_free = s.sem("act_full"), s.sem("act_free"), s.sem("dve_full"), s.sem("dve_free")
        out_turned = s.sem("out_turned")

        ACT_PROJ = len(CHUNKS) if rotary else 0
        ACT_FIRST, DVE_FIRST = 2 + QJOBS + ACT_PROJ, 2
        ACT_BATCH, DVE_BATCH = (2 + ACT_PROJ) * R + 2 + QJOBS + 1, 2 * R + 2
        ACT_MISSING, DVE_MISSING = 2 + 1, 2

        def lanes():
            return {"A": Lane(lane_bank[0:2], act_full, act_free), "D": Lane(lane_bank[2:3], dve_full, dve_free)}

        def go_to_batch(lane, b, parity, first):
            if first:
                lane["A"].go_to(ACT_FIRST, ACT_FIRST)
                lane["D"].go_to(DVE_FIRST, 0)
            else:
                lane["A"].go_to(ACT_FIRST - ACT_MISSING + ACT_BATCH * b, ACT_FIRST - ACT_MISSING + ACT_BATCH * parity)
                lane["D"].go_to(DVE_FIRST - DVE_MISSING + DVE_BATCH * b, 0)

        def go_to_end(lane):
            for jobs, ln, first, missing, each in ((2 + QJOBS + ACT_PROJ, lane["A"], ACT_FIRST, ACT_MISSING, ACT_BATCH),
                                                   (2, lane["D"], DVE_FIRST, DVE_MISSING, DVE_BATCH)):
                at = first - missing + each * BATCHES - jobs
                ln.go_to(at, at)

        def sums_of_slot(t):
            u = (t - 3) % R
            return (1 if t < 3 else 0), u // 2, u % 2

        def following(pair, parity, t):
            return (pair, parity, t + 1) if t + 1 < R else (pair + parity, 1 - parity, 0)

        def preceding(pair, parity, t):
            return (pair, parity, t - 1) if t else (pair - (1 - parity), 1 - parity, R - 1)

        def tile_number(pair, parity, t):
            return (pair * 2 + parity) * R + t

        loads = [0]
        block = s.block()

        @block.sync
        def _(sp):
            def load(dst, src):
                sp.dma_start(dst, src).then_inc(w_loaded, 16)
                loads[0] += 1

            def move_context(pair, parity, tiles, done, store=False):
                whole = (core.ctx_hat if (rotary or store) else core.w["ctx_1024"])[bass.ds(pair * 2 + parity, 1)]
                whole = whole.rearrange("a n d -> (a n) d")
                for on_chip, in_dram in ((tiles[:, 0:CT - 1, :], whole[0:(CT - 1) * P].rearrange("(k p) d -> p k d", p=P)),
                                         (tiles[0:TAIL, CT - 1, :], whole[(CT - 1) * P:CTX])):
                    if store:
                        sp.dma_start(in_dram, on_chip).then_inc(done, 16)
                    else:
                        sp.dma_start(on_chip, in_dram).then_inc(done, 16)

            def load_own(pair, parity):
                if normed:
                    sp.dma_start(rows[0:SEQ, parity, CT, :], y[parity * SEQ:(parity + 1) * SEQ, bass.ds(pair, 1), :]
                                 .rearrange("p a d -> p (a d)")).then_inc(own_loaded[parity], 16)
                if masked:
                    sp.dma_start(mask16[0:1, parity, :], mask_dram[bass.ds(pair * 2 + parity, 1)]).then_inc(mask_loaded[parity], 16)

            def during(pair, parity, first=False, last=False, no_load=False):
                b = pair * 2 + parity
                after = (pair + parity, 1 - parity)
                if masked:
                    if not no_load:
                        sp.wait_ge(raw_used, b + 2)
                        move_context(pair + 1, parity, raw, ctx_loaded)
                    if not last:
                        sp.wait_ge(xhat_ready, b + 2)
                        move_context(*after, xhat, xhat_stored, store=True)
                if last:
                    return
                if rotary and not no_load:
                    sp.wait_ge(gained_ready, b + 2)
                    move_context(pair + 1, parity, xhat, ctx_loaded)
                if not first:
                    sp.wait_ge(sums_done, GROUPS * b)
                if not normed:
                    move_context(*after, rows[:, 1 - parity], rows_loaded[1 - parity])
                load_own(*after)

            sp.wait_ge(cleared, 1)
            if normed:
                move_context(0, 0, raw if masked else xhat, ctx_loaded)
            else:
                move_context(0, 0, rows[:, 0], rows_loaded[0])
            if masked:
                load(mask_u8[:], core.w["mask_BxS2_bk1"])
            if normed:
                names = ("ln_x_g", "ln_x_b", "ln_l_g", "ln_l_b") if "ln_x_g" in w else ("gamma_x", "beta_x", "gamma_l", "beta_l")
                for n, src in enumerate(names):
                    load(gains[:, n, :], w[src].partition_broadcast(P))
            if "Wkv" in w:
                wk_src, wv_src, wo_src = w["Wkv"][:, 0:NH * HD], w["Wkv"][:, NH * HD:2 * NH * HD], w["Wo"]
            else:
                wk_src, wv_src, wo_src = w["W_k"], w["W_v"], w["W_o"]
            if rotary:
                with nc.allow_non_contiguous_dma("head halves"):
                    for dst, src in ((wq, w["Wq"]), (wk, wk_src)):
                        for t in range(R):
                            for half in range(2):
                                load(dst[:, t, half * SEQ:(half + 1) * SEQ].rearrange("p (h d) -> p h d", h=2),
                                     src[:, t * P:(t + 1) * P].rearrange("p (h a d) -> p a h d", h=2, a=2)[:, half])
                load(rot_cos[:], core.w["c_rope64"][0])
                load(rot_sin[:], core.w["c_rope64"][1])
            else:
                load(wq_rows[:], w["Wq"] if "Wq" in w else w["W_q"])
                load(wk_rows[:], wk_src)
            load(wv_rows[:], wv_src)
            load(wo_rows[:], wo_src.rearrange("(t p) d -> p t d", p=P))
            if out_norm:
                load(out_gains[:, 0, :], w["ln_o_g"].partition_broadcast(P))
                load(out_gains[:, 1, :], w["ln_o_b"].partition_broadcast(P))
            if "b_o" in w:
                with nc.allow_non_contiguous_dma("bias column"):
                    load(out_bias[:], column(w["b_o"]))
            if masked:
                sp.wait_ge(mask_ready, 1)
                sp.dma_start(mask_dram, mask_all[:]).then_inc(mask_stored, 16)
                sp.wait_ge(mask_stored, 16)
                sp.wait_ge(cleared, 2)
                sp.wait_ge(raw_used, 1)
                move_context(0, 1, raw, ctx_loaded)
                sp.wait_ge(xhat_ready, 1)
                move_context(0, 0, xhat, xhat_stored, store=True)
            if rotary:
                sp.wait_ge(gained_ready, 1)
                move_context(0, 1, xhat, ctx_loaded)
            if normed:
                sp.wait_ge(y_ready, 1)
                load_own(0, 0)
            during(0, 0, first=True)
            during(0, 1)
            with sp.Fori(1, LAST) as pair:
                during(pair, 0)
                during(pair, 1)
            during(LAST, 0, no_load=True)
            if masked:
                sp.wait_ge(xhat_stored, 32 * BATCHES)

        LOADS = loads[0]
        QUAD_TURNS = [n for n in (("wv",) if rotary else ("wq", "wk", "wv")) for _ in range(R // 4)]
        TURNS = len(QUAD_TURNS)

        @block.tensor
        def _(pe):
            lane = lanes()
            pe.wait_ge(cleared, 2)
            pe.wait_ge(w_loaded, 16 * LOADS)
            todo = (wv_rows,) if rotary else (wq_rows, wk_rows, wv_rows)
            for j in range(TURNS):
                source, quad = todo[j // (R // 4)], j % (R // 4)
                if j >= 4:
                    pe.wait_ge(w_kept, j - 3)
                for i in range(4):
                    turn = nc.tensor.transpose(score[:, (j % 4) * BANK + i * P:(j % 4) * BANK + (i + 1) * P],
                                               source[:, (4 * quad + i) * P:(4 * quad + i + 1) * P], core.ident[:])
                turn.then_inc(w_turned, 1)
            pe.wait_ge(w_kept, TURNS)
            products = [(wvT, wo_rows)] if rotary else [(wqT, wkT), (wvT, wo_rows)]
            for f in range(len(products) * (R // 4)):
                (left, right), quad = products[f // (R // 4)], f % (R // 4)
                if f >= 2:
                    pe.wait_ge(w_kept, TURNS + f - 1)
                for odd in range(2):
                    part = slice(odd * SEQ, (odd + 1) * SEQ)
                    bank = score[:, (2 * (f % 2) + odd) * BANK:(2 * (f % 2) + odd + 1) * BANK]
                    for i in range(4):
                        mm = nc.tensor.matmul(bank[:, i * P:(i + 1) * P], left[part, 4 * quad + i, :],
                                              right[part, 4 * quad + i, :], start=True, stop=True)
                mm.then_inc(w_turned, 1)
            turn_tiles_pe(nc, pe, core.ident[:], y[:], lane_bank[0:2], y_ready, 1, y_turned)
            pe.wait_ge(yT_kept, 2)
            pe.wait_ge(w_kept, TURNS + len(products) * (R // 4))

            def fill(name):
                ln = lane[name]
                count = ln.count() - len(ln.banks) + 1
                if not isinstance(count, int) or count > 0:
                    pe.wait_ge(ln.free, count)
                return ln.bank()

            def filled(name, ins):
                ins.then_inc(lane[name].full, 1)
                lane[name].next()

            def turn_context(pair, parity, chunks):
                if 0 in chunks:
                    if normed:
                        pe.wait_ge(gained_ready, pair * 2 + parity + 1)
                    else:
                        pe.wait_ge(rows_loaded[parity], 32 * (pair + 1))
                for c in chunks:
                    c0, n = CTX_CHUNKS[c]
                    bank = fill("AD"[c % 2])
                    for k in range(c0 // P, -(-(c0 + n) // P)):
                        size = tile_of_keys[k][1]
                        source = gained[0:size, k, :] if normed else rows[0:size, parity, k, :]
                        turn = nc.tensor.transpose(bank[:, k * P - c0:k * P - c0 + size], source,
                                                   core.ident[0:size, 0:size])
                    filled("AD"[c % 2], turn)

            def make_queries(pair, parity):
                own = yT[:, bass.ds((pair * 2 + parity) * SEQ, SEQ)]
                for job in range(QJOBS):
                    bank = fill("A")
                    for i in range(R if rotary else 8):
                        left = wq[:, i, :] if rotary else fold_qk[:, 8 * job + i, :]
                        mm = nc.tensor.matmul(bank[:, i * SEQ:(i + 1) * SEQ], left, own, start=True, stop=True)
                    filled("A", mm)

            def project(pair, parity, t):
                for c0, n in CHUNKS:
                    filled("A", nc.tensor.matmul(fill("A")[:, 0:n], wk[:, t, :], keysT[:, parity, c0:c0 + n], start=True, stop=True))

            def scores(pair, parity, t, first=False):
                tile = tile_number(pair, parity, t)
                if masked and t == 0:
                    pe.wait_ge(mask_loaded[parity], 16 * (pair + 1))
                if not first:
                    pe.wait_ge(exp_done, tile)
                keys = projected[:, t % 2] if rotary else keysT[:, parity]
                for c, (c0, n) in enumerate(CHUNKS):
                    if rotary and c % 2 == 0:
                        pe.wait_ge(keys_turned, 2 * tile + c // 2 + 1)
                    mm = nc.tensor.matmul(score[:, c0:c0 + n], queries[:, parity, t * P:(t + 1) * P], keys[:, c0:c0 + n],
                                          start=True, stop=not masked)
                    if masked:
                        mm = nc.tensor.matmul(score[:, c0:c0 + n], pick16[:], mask16[:, parity, c0:c0 + n],
                                              start=False, stop=True)
                    if c in (1, len(CHUNKS) - 1):
                        mm.then_inc(score_half, 1)

            def turn_probs(pair, parity, t, quads):
                if 0 in quads:
                    pe.wait_ge(prob_ready, tile_number(pair, parity, t) + 1)
                for j in quads:
                    bank = fill("AD"[j % 2])
                    for i, k in enumerate(QUADS[j]):
                        c0, n = tile_of_keys[k]
                        turn = nc.tensor.transpose(bank[0:n, i * P:(i + 1) * P], prob[:, t % 2, c0:c0 + n], core.ident[:])
                    filled("AD"[j % 2], turn)

            def sum_context(pair, parity, group, part, turned):
                b = pair * 2 + parity
                if part == 0:
                    for name, count in turned.items():
                        pe.wait_ge(lane[name].free, count)
                    if normed:
                        pe.wait_ge(rows_ready, b + 1)
                        pe.wait_ge(own_loaded[parity], 16 * (pair + 1))
                    if not (isinstance(b, int) and b == 0 and group == 0):
                        pe.wait_ge(sums_kept, b * GROUPS + group)
                for k in PARTS[part]:
                    n = tile_of_keys[k][1]
                    mm = nc.tensor.matmul(sums[:, 0:GCOLS], rows[0:n, parity, k, :], probT[0:n, group % 2, k, :],
                                          start=(k == 0), stop=(k == KT - 1))
                if part == 1:
                    mm.then_inc(sums_done, 1)

            def output(pair, parity):
                pe.wait_ge(sums_kept, GROUPS * (pair * 2 + parity + 1))
                bank = fill("A")
                for h in range(NH):
                    mm = nc.tensor.matmul(bank[:, 0:SEQ], fold_vo[:, h, :], mixed[:, h * SEQ:(h + 1) * SEQ],
                                          start=(h == 0), stop=(h == NH - 1))
                filled("A", mm)

            def emptied(counts):
                for name in "AD":
                    pe.wait_ge(lane[name].free, counts[name])

            def prepared(last=False):
                return {name: lane[name].count() for name in "AD"}

            def batch(pair, parity, first=False, last=False):
                go_to_batch(lane, pair * 2 + parity, parity, first)
                before, after = preceding(pair, parity, 0)[0:2], following(pair, parity, R - 1)[0:2]
                turned = prepared()
                for t in range(R):
                    if rotary and not (last and t == R - 1):
                        project(*following(pair, parity, t))
                    scores(pair, parity, t, first and t == 0)
                    if not (first and t == 0):
                        turn_probs(*preceding(pair, parity, t), (0, 1, 2))
                    prepares = t == CTX_SLOT and not last
                    if prepares:
                        turn_context(*after, (0, 1, 2))
                    back, group, part = sums_of_slot(t)
                    if not (first and back):
                        sum_context(*(before if back else (pair, parity)), group, part, turned)
                    if prepares:
                        turn_context(*after, (3,))
                        keys_kept = prepared()
                        make_queries(*after)
                        keys_kept["A"] = lane["A"].count()
                    if not (first and t == 0):
                        turn_probs(*preceding(pair, parity, t), (3,))
                    if t % 2 == 0:
                        turned = prepared()
                    if t == KEPT_SLOT and not first:
                        output(*before)
                    if not last and t == (CTX_SLOT if rotary else R - 1):
                        emptied(keys_kept)

            turn_context(0, 0, range(len(CTX_CHUNKS)))
            make_queries(0, 0)
            emptied(prepared())
            if rotary:
                project(0, 0, 0)
            batch(0, 0, first=True)
            batch(0, 1)
            with pe.Fori(1, LAST) as pair:
                batch(pair, 0)
                batch(pair, 1)
            batch(LAST, 0)
            batch(LAST, 1, last=True)
            go_to_end(lane)
            turned = prepared()
            turn_probs(LAST, 1, R - 1, range(len(QUADS)))
            for t in range(3):
                if t == 1:
                    turned = prepared()
                sum_context(LAST, 1, *sums_of_slot(t)[1:], turned)
            output(LAST, 1)
            emptied(prepared())
            pe.wait_ge(exp_done, BATCHES * R)
            for t in range(TILES):
                turn = nc.tensor.transpose(score[:, t * P:(t + 1) * P], outT[:, t * P:(t + 1) * P], core.ident[:])
            turn.then_inc(out_turned, 1)

        @block.scalar
        def _(act):
            lane = lanes()
            act.wait_ge(cleared, 2)
            act.wait_ge(w_loaded, 16 * LOADS)
            turned_weights = {"wv": wvT} if rotary else {"wq": wqT, "wk": wkT, "wv": wvT}
            for j, n in enumerate(QUAD_TURNS):
                quad = j % (R // 4)
                act.wait_ge(w_turned, j + 1)
                nc.scalar.copy(turned_weights[n][:, 4 * quad:4 * quad + 4, :].rearrange("p i d -> p (i d)"),
                               score[:, (j % 4) * BANK:(j % 4 + 1) * BANK]).then_inc(w_kept, 1)
            folded = [fold_vo] if rotary else [fold_qk, fold_vo]
            for f in range(len(folded) * (R // 4)):
                dst, quad = folded[f // (R // 4)], f % (R // 4)
                act.wait_ge(w_turned, TURNS + f + 1)
                for odd in range(2):
                    bank = score[:, (2 * (f % 2) + odd) * BANK:(2 * (f % 2) + odd + 1) * BANK]
                    kept = nc.scalar.copy(dst[:].rearrange("p (i r) d -> p r i d", r=2)[:, odd, 4 * quad:4 * quad + 4, :],
                                          bank.rearrange("p (i d) -> p i d", d=D))
                kept.then_inc(w_kept, 1)
            normalize_act(nc, act, core.eps(EPS_5), TILES, D, stats, var_ready, std_ready, 1)
            if normed:
                normalize_act(nc, act, core.eps(EPS_5), TILES, D, stats, var_ready, std_ready, 2)
            keep_turned_act(nc, act, yT, lane_bank[0:2], y_turned, 1, yT_kept)
            act.drain()

            def take():
                act.wait_ge(lane["A"].full, lane["A"].count() + 1)
                return lane["A"].bank()

            def emptied(ins):
                ins.then_inc(lane["A"].free, 1)
                lane["A"].next()

            def context_root(b):
                act.wait_ge(cvar_ready, b + 1)
                nc.scalar.activation(cstd[:], mean_var[:, :, 1], ACT.Sqrt, bias=core.eps(EPS_5), scale=1.0)\
                    .then_inc(cstd_ready, 1)

            def keep_context(pair, parity):
                if normed:
                    nc.scalar.copy(keysT[:, parity, CTX:KEYS], yT[:, bass.ds((pair * 2 + parity) * SEQ, SEQ)])
                for c in range(0, len(CTX_CHUNKS), 2):
                    c0, n = CTX_CHUNKS[c]
                    bank = take()
                    emptied(nc.scalar.copy(keysT[:, parity, c0:c0 + n], bank[:, 0:n]))

            def keep_queries(parity):
                for job in range(QJOBS):
                    bank = take()
                    if not rotary:
                        emptied(nc.scalar.copy(queries[:, parity, job * BANK:(job + 1) * BANK], bank[:]))
                        continue
                    for q in range(4):
                        part = slice(32 * q, 32 * q + 32)
                        kept = nc.scalar.copy(queries[part, parity, :].rearrange("p (t h i) -> p t h i", h=2, i=SEQ)[:, :, q % 2, :],
                                              bank[part, 0:R * SEQ].rearrange("p (t i) -> p t i", i=SEQ))
                    emptied(kept)

            def keep_rows(pair, parity):
                act.wait_ge(gained_ready, pair * 2 + parity + 1)
                nc.scalar.copy(rows[:, parity, 0:CT, :], gained[:]).then_inc(rows_ready, 1)

            def keep_projected(t):
                for c, (c0, n) in enumerate(CHUNKS):
                    bank = take()
                    emptied(nc.scalar.copy(unturned[:, t % 2, c0:c0 + n], bank[:, 0:n]))
                    if c in (1, len(CHUNKS) - 1):
                        act.drain().then_inc(unturned_ready, 1)

            def exps(pair, parity, t):
                act.wait_ge(peak_ready, tile_number(pair, parity, t) + 1)
                nc.scalar.activation(prob[:, t % 2, :], score[:, 0:KEYS], ACT.Exp, bias=neg_peak[:, t % 2:t % 2 + 1],
                                     scale=scale, accum_out=rsum[:, t % 2:t % 2 + 1]).then_inc(exp_done, 1)

            def keep_probs(t, quads):
                for j in quads:
                    bank = take()
                    for k0, n, size in full_tiles(QUADS[j]):
                        kept = nc.scalar.copy(probT[0:size, t // 2 % 2, k0:k0 + n, t % 2 * P:t % 2 * P + P],
                                              bank[0:size, (k0 % 4) * P:(k0 % 4 + n) * P].rearrange("p (i r) -> p i r", r=P))
                    emptied(kept)

            def keep_sums(pair, parity, group):
                act.wait_ge(sums_done, (pair * 2 + parity) * GROUPS + group + 1)
                nc.scalar.copy(mixed[:, group * GCOLS:(group + 1) * GCOLS], sums[:, 0:GCOLS]).then_inc(sums_kept, 1)

            def keep_output(pair, parity):
                bank = take()
                dst = outT[:, bass.ds((pair * 2 + parity) * SEQ, SEQ)]
                if "b_o" in w:
                    emptied(nc.scalar.activation(dst, bank[:, 0:SEQ], ACT.Identity, bias=out_bias[:]))
                else:
                    emptied(nc.scalar.copy(dst, bank[:, 0:SEQ]))

            def batch(pair, parity, first=False, last=False, no_stats=False):
                go_to_batch(lane, pair * 2 + parity, parity, first)
                before, after = preceding(pair, parity, 0)[0:2], following(pair, parity, R - 1)[0:2]
                for t in range(R):
                    if t:
                        back, group, part = sums_of_slot(t - 1)
                        if part == 1 and not (first and back):
                            keep_sums(*(before if back else (pair, parity)), group)
                    if masked and t == 3 and not no_stats:
                        context_root(pair * 2 + parity + 2)
                    if rotary and not (last and t == R - 1):
                        keep_projected(following(pair, parity, t)[2])
                    if not (first and t == 0):
                        keep_probs(preceding(pair, parity, t)[2], (0, 2))
                    exps(pair, parity, t)
                    if t == CTX_SLOT and not last:
                        keep_context(*after)
                        keep_queries(1 - parity)
                    if t == KEPT_SLOT and not first:
                        keep_output(*before)
                    if t == KEPT_SLOT and normed and not last:
                        keep_rows(*after)

            if masked:
                context_root(0)
            keep_context(0, 0)
            keep_queries(0)
            if normed:
                keep_rows(0, 0)
            if masked:
                context_root(1)
            if rotary:
                keep_projected(0)
            batch(0, 0, first=True)
            batch(0, 1)
            with act.Fori(1, LAST) as pair:
                batch(pair, 0)
                batch(pair, 1)
            batch(LAST, 0, no_stats=True)
            batch(LAST, 1, last=True, no_stats=True)
            go_to_end(lane)
            keep_probs(R - 1, (0, 2))
            keep_sums(LAST, 1, GROUPS - 2)
            keep_sums(LAST, 1, GROUPS - 1)
            keep_output(LAST, 1)
            if out_norm:
                normalize_act(nc, act, core.eps(EPS_5), TILES, D, stats, var_ready, std_ready, 3)

        @block.gpsimd
        def _(pool):
            if masked:
                nc.gpsimd.memset(raw[:], 0.0)
            elif normed:
                nc.gpsimd.memset(xhat[:], 0.0)
            pool.drain()
            nc.gpsimd.memset(peak[:], 0.0).then_inc(cleared, 1)
            if masked:
                nc.gpsimd.memset(pick16[:], 0.0)
                nc.gpsimd.memset(mask16[:], 0.0)
                pool.drain()
                nc.gpsimd.memset(pick16[0:1, :], 1.0)
            if rotary:
                nc.gpsimd.memset(queries[:], 0.0)
            pool.drain()
            nc.gpsimd.memset(neg_peak[:], 0.0).then_inc(cleared, 1)
            pool.wait_ge(w_loaded, 16 * LOADS)

            def make_xhat(b, first=False):
                pool.wait_ge(crstd_ready, b + 1)
                if not first:
                    pool.wait_ge(xhat_stored, 32 * b)
                nc.gpsimd.tensor_tensor(xhat[:], raw[:], over_last(mean_var[:, :, 0], D), ALU.subtract).then_inc(raw_used, 1)
                pool.drain()
                nc.gpsimd.tensor_tensor(xhat[:], xhat[:], over_last(crstd[:], D), ALU.mult).then_inc(xhat_ready, 1)
                pool.drain()

            def make_gained(b, step, first=False):
                if step == 0:
                    if rotary:
                        pool.wait_ge(ctx_loaded, 32 * (b + 1))
                    if not first:
                        pool.wait_ge(rows_ready, b)
                    nc.gpsimd.tensor_tensor(gained[:], xhat[:], over_tiles(gains[:, 0, :], CT), ALU.mult)
                else:
                    nc.gpsimd.tensor_tensor(gained[:], gained[:], over_tiles(gains[:, 1, :], CT), ALU.add).then_inc(gained_ready, 1)
                pool.drain()

            def turn_keys(pair, parity, t):
                tile = tile_number(pair, parity, t)
                for h, (c0, n) in enumerate(HALVES):
                    pool.wait_ge(unturned_ready, 2 * tile + h + 1)
                    nc.gpsimd.tensor_tensor(projected[:, t % 2, c0:c0 + n], unturned[:, t % 2, c0:c0 + n],
                                            rot_cos[:, c0:c0 + n], ALU.mult)
                pool.drain()
                for h, (c0, n) in enumerate(HALVES):
                    pool.wait_ge(crossed_ready, 2 * tile + h + 1)
                    nc.gpsimd.tensor_tensor(projected[:, t % 2, c0:c0 + n], projected[:, t % 2, c0:c0 + n],
                                            crossed[:, c0:c0 + n], ALU.add).then_inc(keys_turned, 1)

            def batch(pair, parity, first=False, last=False):
                b = pair * 2 + parity
                for t in range(R):
                    if rotary and not (last and t == R - 1):
                        turn_keys(*following(pair, parity, t))
                    if normed and not last:
                        if masked and t == 0:
                            make_xhat(b + 1)
                        if t in (0, 1):
                            make_gained(b + 1, t)

            if masked:
                make_xhat(0, first=True)
            if normed:
                make_gained(0, 0, first=True)
                make_gained(0, 1)
                if rotary:
                    turn_keys(0, 0, 0)
                batch(0, 0, first=True)
                batch(0, 1)
                with pool.Fori(1, LAST) as pair:
                    batch(pair, 0)
                    batch(pair, 1)
                batch(LAST, 0)
                batch(LAST, 1, last=True)

        @block.vector
        def _(dve):
            lane = lanes()
            normalize_dve(nc, dve, y[:], lat[:], square[:], stats, var_ready, std_ready, 1)
            dve.drain()
            dve.wait_ge(w_loaded, 16 * LOADS)
            if normed:
                normalize_dve(nc, dve, y[:], y[:], square[:], stats, var_ready, std_ready, 2)
                dve.drain()
                nc.vector.tensor_tensor(y[:], y[:], over_tiles(gains[:, 2, :], TILES), ALU.mult)
                dve.drain()
                nc.vector.tensor_tensor(y[:], y[:], over_tiles(gains[:, 3, :], TILES), ALU.add).then_inc(y_ready, 1)
            else:
                nc.vector.tensor_copy(square[:, 0, 0:1], y[:, 0, 0:1]).then_inc(y_ready, 1)
            if masked:
                nc.vector.memset(mask_all[:, CTX:KEYS], 0.0)
                nc.vector.tensor_scalar(mask_all[:, 0:CTX], mask_u8[:], -1.0, 1e30, ALU.add, ALU.mult).then_inc(mask_ready, 1)
            dve.wait_ge(cleared, 2)

            def take():
                dve.wait_ge(lane["D"].full, lane["D"].count() + 1)
                return lane["D"].bank()

            def emptied(ins):
                ins.then_inc(lane["D"].free, 1)
                lane["D"].next()

            def measure(b, first=False):
                dve.wait_ge(ctx_loaded, 32 * (b + 1))
                if not first:
                    dve.wait_ge(xhat_ready, b)
                for k in range(CT):
                    nc.vector.bn_stats(moments[:, k, :], raw[:, k, :])
                dve.drain()
                for k in range(CT):
                    ins = nc.vector.bn_aggr(mean_var[:, k, :], moments[:, k, :])
                ins.then_inc(cvar_ready, 1)

            def invert_std(b):
                dve.wait_ge(cstd_ready, b + 1)
                nc.vector.reciprocal(crstd[:], cstd[:]).then_inc(crstd_ready, 1)

            def keep_context(parity):
                for c in range(1, len(CTX_CHUNKS), 2):
                    c0, n = CTX_CHUNKS[c]
                    bank = take()
                    emptied(nc.vector.tensor_copy(keysT[:, parity, c0:c0 + n], bank[:, 0:n]))

            def cross_halves(pair, parity, t):
                tile = tile_number(pair, parity, t)
                for h, (c0, n) in enumerate(HALVES):
                    cols = slice(c0, c0 + n)
                    dve.wait_ge(unturned_ready, 2 * tile + h + 1)
                    if not (isinstance(tile, int) and tile == 0):
                        dve.wait_ge(keys_turned, 2 * tile + h - 1)
                    nc.vector.tensor_tensor(crossed[SEQ:P, cols], unturned[0:SEQ, t % 2, cols], rot_sin[0:SEQ, cols], ALU.mult)
                    nc.vector.tensor_tensor(crossed[0:SEQ, cols], unturned[SEQ:P, t % 2, cols], rot_sin[SEQ:P, cols], ALU.mult)\
                        .then_inc(crossed_ready, 1)

            def maximum(pair, parity, t):
                tile, which = tile_number(pair, parity, t), t % 2
                for h, (c0, n) in enumerate(HALVES):
                    dve.wait_ge(score_half, 2 * tile + h + 1)
                    nc.vector.tensor_reduce(peak[:, h:h + 1], score[:, c0:c0 + n], AX, ALU.max)
                dve.drain()
                nc.vector.tensor_scalar(neg_peak[:, which:which + 1], peak[:, 0:1], peak[:, 1:2], -scale,
                                        ALU.max, ALU.mult).then_inc(peak_ready, 1)

            def normalise(pair, parity, t):
                tile, which = tile_number(pair, parity, t), t % 2
                dve.wait_ge(exp_done, tile + 1)
                nc.vector.reciprocal(rinv[:, which:which + 1], rsum[:, which:which + 1])
                dve.drain()
                nc.vector.tensor_scalar(prob[:, which, :], prob[:, which, :], rinv[:, which:which + 1], None,
                                        ALU.mult).then_inc(prob_ready, 1)

            def keep_probs(t, j):
                bank = take()
                for k0, n, size in full_tiles(QUADS[j]):
                    kept = nc.vector.tensor_copy(probT[0:size, t // 2 % 2, k0:k0 + n, t % 2 * P:t % 2 * P + P],
                                                 bank[0:size, (k0 % 4) * P:(k0 % 4 + n) * P].rearrange("p (i r) -> p i r", r=P))
                emptied(kept)

            def batch(pair, parity, first=False, last=False, no_stats=False):
                b = pair * 2 + parity
                go_to_batch(lane, b, parity, first)
                for t in range(R):
                    turns = not (first and t == 0)
                    rotates = rotary and not (last and t == R - 1)
                    if turns:
                        normalise(*preceding(pair, parity, t))
                    if rotates:
                        cross_halves(*following(pair, parity, t))
                    if masked and t == 3 and not no_stats:
                        invert_std(b + 2)
                    maximum(pair, parity, t)
                    if turns:
                        keep_probs(preceding(pair, parity, t)[2], 1)
                    if t == CTX_SLOT and not last:
                        keep_context(1 - parity)
                    if masked and t == 2 and not no_stats:
                        measure(b + 2)
                    if turns:
                        keep_probs(preceding(pair, parity, t)[2], 3)

            if masked:
                measure(0, first=True)
                invert_std(0)
            keep_context(0)
            if rotary:
                cross_halves(0, 0, 0)
            if masked:
                measure(1)
                invert_std(1)
            batch(0, 0, first=True)
            batch(0, 1)
            with dve.Fori(1, LAST) as pair:
                batch(pair, 0)
                batch(pair, 1)
            batch(LAST, 0, no_stats=True)
            batch(LAST, 1, last=True, no_stats=True)
            go_to_end(lane)
            normalise(LAST, 1, R - 1)
            keep_probs(R - 1, 1)
            keep_probs(R - 1, 3)
            dve.wait_ge(out_turned, 1)
            turned = score[:, 0:TOKENS].rearrange("p (t d) -> p t d", d=D)
            if out_norm:
                nc.vector.tensor_copy(y[:], turned)
                dve.drain()
                normalize_dve(nc, dve, y[:], y[:], square[:], stats, var_ready, std_ready, 3)
                dve.drain()
                nc.vector.tensor_tensor(y[:], y[:], over_tiles(out_gains[:, 0, :], TILES), ALU.mult)
                dve.drain()
                nc.vector.tensor_tensor(y[:], y[:], over_tiles(out_gains[:, 1, :], TILES), ALU.add)
                dve.drain()
                nc.vector.tensor_tensor(lat[:], lat[:], y[:], ALU.add)
            else:
                nc.vector.tensor_tensor(lat[:], lat[:], turned, ALU.add)


def single_head_stage(core, name, w, heads, scale, normed=False, masked=False, rotary=False, single=False,
                          out_norm=False):
    nc, lat = core.nc, core.lat
    absorbed = not (rotary or single)
    NH, HD = heads, D if single else 64
    PAIRS = max(NH // 2, 1)
    ROWS = SEQ if single else P
    R = 1 if single else PAIRS
    TPG = min(R, 4)
    GROUPS = R // TPG
    GROWS = TPG * ROWS
    CT = -(-CTX // P)
    TAIL = CTX - (CT - 1) * P
    KEYS = CTX + (SEQ if normed else 0)
    tile_of_keys = [(k * P, min(P, CTX - k * P)) for k in range(CT)] + ([(CTX, SEQ)] if normed else [])
    KT = len(tile_of_keys)
    CHUNKS = [(c * BANK, min(BANK, KEYS - c * BANK)) for c in range(-(-KEYS // BANK))]
    CTX_CHUNKS = [(c * BANK, min(BANK, CTX - c * BANK)) for c in range(-(-CTX // BANK))]
    QUADS = [list(range(q, min(q + 4, KT))) for q in range(0, KT, 4)]
    T_LANES = "AAAA" if rotary else "ADAD"
    PV_PARTS = [range(0, 5), range(5, 10), range(10, KT)]
    QJOBS = max(NH // 8, 1)
    FOLDS = PAIRS if not single else 0

    with ExitStack() as ctx:
        s = Stage(nc, ctx, name)
        y, square, yT = s.sb("y", [P, TILES, D]), s.sb("square", [P, TILES, D]), s.sb("yT", [P, TOKENS])
        stats = s.sb("stats", [P, 4, TILES])
        staged = s.sb("staged", [P, CT, D]) if normed or single else None
        rows = s.sb("rows", [P, 2, KT, D])
        keysT = s.sb("keysT", [P, 2, KEYS])
        prob = s.sb("prob", [P, 2, KEYS])
        probT = s.sb("probT", [P, 2, KT, GROWS])
        queries = s.sb("queries", [P, 2, R * ROWS])
        peak, neg_peak = s.sb("peak", [P, 2]), s.sb("neg_peak", [P, 2])
        rsum, rinv = s.sb("rsum", [P, 2]), s.sb("rinv", [P, 2])
        mixed = s.sb("mixed", [P, 2, GROWS])
        outT = s.sb("outT", [P, TOKENS])
        if normed:
            raw = s.sb("raw", [P, CT, D])
            csq = s.sb("csq", [P, CT, D])
            cstats = s.sb("cstats", [P, 4, CT])
            gains = s.sb("gains", [P, 4, D])
            cols = s.sb("cols", [P, 2])
        if out_norm:
            out_gains = s.sb("out_gains", [P, 2, D])
            out_rows = s.sb("out_rows", [P, TILES, D])
        if masked:
            pick16 = s.sb("pick16", [P, P], BF16)
            mask16 = s.sb("mask16", [P, 2, KEYS], BF16)
            mask_u8, mask_all = s.sb("mask_u8", [BATCHES, CTX], U8), s.sb("mask_all", [BATCHES, KEYS], BF16)
            mask_dram = nc.dram_tensor(f"{name}_mask_rows", (BATCHES, KEYS), BF16, kind="Internal").ap()
        if single:
            wq, wk, wv, bias = s.sb("wq", [P, D]), s.sb("wk", [P, D]), s.sb("wv", [P, D]), s.sb("bias", [P, 3])
            projected = s.sb("projected", [P, 2, KEYS])
        else:
            wv_rows, wo_rows = s.sb("wv_rows", [P, NH * HD]), s.sb("wo_rows", [P, PAIRS, D])
            wvT = s.sb("wvT", [P, PAIRS, D])
            fold_vo = s.sb("fold_vo", [P, NH, D])
            if absorbed:
                wq_rows, wk_rows = s.sb("wq_rows", [P, NH * HD]), s.sb("wk_rows", [P, NH * HD])
                wqT, wkT = s.sb("wqT", [P, PAIRS, D]), s.sb("wkT", [P, PAIRS, D])
                fold_qk = s.sb("fold_qk", [P, NH, D])
            else:
                wq, wk = s.sb("wq", [P, PAIRS, P]), s.sb("wk", [P, PAIRS, P])
                rot_cos, rot_sin = s.sb("rot_cos", [P, CTX]), s.sb("rot_sin", [P, CTX])
                projected = s.sb("projected", [P, 2, KEYS])
                crossed = s.sb("crossed", [P, 2, BANK])
        if not single and "b_o" in w:
            out_bias = s.sb("out_bias", [P, 1])

        score = s.ps("score", [P, 4 * BANK])
        lane_bank = [s.ps(f"lane{i}", [P, BANK]) for i in range(3)]
        sums = s.ps("sums", [P, BANK])

        w_loaded, var_ready, std_ready = s.sem("w_loaded"), s.sem("var_ready"), s.sem("std_ready")
        y_ready, y_turned, yT_kept = s.sem("y_ready"), s.sem("y_turned"), s.sem("yT_kept")
        w_turned, w_kept = s.sem("w_turned"), s.sem("w_kept")
        mask_ready, mask_stored = s.sem("mask_ready"), s.sem("mask_stored")
        mask_loaded = [s.sem(f"mask_loaded{i}") for i in range(2)]
        cleared = s.sem("cleared")
        ctx_loaded, centred, cvar_ready, cstd_ready, c_ready = (s.sem("ctx_loaded"), s.sem("centred"),
                                                                s.sem("cvar_ready"), s.sem("cstd_ready"), s.sem("c_ready"))
        own_loaded = [s.sem(f"own_loaded{i}") for i in range(2)]
        rows_ready = s.sem("rows_ready")
        rows_loaded = [s.sem(f"rows_loaded{i}") for i in range(2)]
        score_half, peak_ready, exp_done, prob_ready = (s.sem("score_half"), s.sem("peak_ready"), s.sem("exp_done"),
                                                        s.sem("prob_ready"))
        sums_done, sums_kept = s.sem("sums_done"), s.sem("sums_kept")
        crossed_ready, keys_turned = s.sem("crossed_ready"), s.sem("keys_turned")
        act_full, act_free, dve_full, dve_free = s.sem("act_full"), s.sem("act_free"), s.sem("dve_full"), s.sem("dve_free")
        out_turned = s.sem("out_turned")

        ACT_FIRST = 2 + QJOBS + (len(CTX_CHUNKS) if single else 0)
        DVE_FIRST = 2 + (2 * len(CHUNKS) if rotary else 0)
        ACT_BATCH = T_LANES.count("A") * R + ACT_FIRST + 1
        DVE_BATCH = T_LANES.count("D") * R + 2 + (len(CHUNKS) * R if rotary else 0)

        def lanes():
            return {"A": Lane(lane_bank[0:2], act_full, act_free), "D": Lane(lane_bank[2:3], dve_full, dve_free)}

        def go_to_batch(lane, b, parity, first):
            if first:
                lane["A"].go_to(ACT_FIRST, ACT_FIRST)
                lane["D"].go_to(DVE_FIRST, 0)
            else:
                lane["A"].go_to(ACT_FIRST - 1 + ACT_BATCH * b, ACT_FIRST - 1 + ACT_BATCH * parity)
                lane["D"].go_to(DVE_FIRST + DVE_BATCH * b, 0)

        out_slot = 4 if GROUPS > 1 else 0

        def sums_of_slot(t):
            if R == 1:
                return []
            if GROUPS == 1:
                return [(1, 0, t - 1)]
            return [(1, GROUPS - 1, t - 1)] if t <= 3 else [(0, 0, t - 5)] if t >= 5 else []

        loads = [0]
        block = s.block()

        @block.sync
        def _(sp):
            def load(dst, src):
                sp.dma_start(dst, src).then_inc(w_loaded, 16)
                loads[0] += 1

            lane = lanes()

            def load_context(pair, parity, dst, done):
                src = core.w["ctx_1024"][bass.ds(pair * 2 + parity, 1)].rearrange("a n d -> (a n) d")
                sp.dma_start(dst[:, 0:CT - 1, :], src[0:(CT - 1) * P].rearrange("(k p) d -> p k d", p=P)).then_inc(done, 16)
                sp.dma_start(dst[0:TAIL, CT - 1, :], src[(CT - 1) * P:CTX]).then_inc(done, 16)

            def load_staged(pair, parity):
                load_context(pair, parity, raw if normed else staged, ctx_loaded)

            def load_rows(pair, parity):
                load_context(pair, parity, rows[:, parity], rows_loaded[parity])

            def load_own(pair, parity, used=None):
                if used is not None and normed:
                    sp.wait_ge(sums_done, used)
                if normed:
                    sp.dma_start(rows[0:SEQ, parity, CT, :], y[parity * SEQ:(parity + 1) * SEQ, bass.ds(pair, 1), :]
                                 .rearrange("p a d -> p (a d)")).then_inc(own_loaded[parity], 16)
                if masked:
                    sp.dma_start(mask16[0:1, parity, :], mask_dram[bass.ds(pair * 2 + parity, 1)]).then_inc(mask_loaded[parity], 16)

            def during(pair, parity, first=False, last=False):
                b = pair * 2 + parity
                if normed:
                    load_own(pair + parity, 1 - parity, None if first else GROUPS * b)
                    if not last:
                        sp.wait_ge(centred, b + 2)
                        load_staged(pair + 1, parity)
                    return
                if not first:
                    sp.wait_ge(sums_done, GROUPS * b)
                load_rows(pair + parity, 1 - parity)
                if single and not last:
                    go_to_batch(lane, b, parity, first)
                    sp.wait_ge(act_full, lane["A"].count() + 2)
                    sp.wait_ge(dve_full, lane["D"].count() + 2)
                    load_staged(pair + 1, parity)

            sp.wait_ge(cleared, 1)
            if normed or single:
                load_staged(0, 0)
            if not normed:
                load_rows(0, 0)
            if masked:
                load(mask_u8[:], core.w["mask_BxS2_bk1"])
            if normed:
                names = ("ln_x_g", "ln_x_b", "ln_l_g", "ln_l_b") if "ln_x_g" in w else ("gamma_x", "beta_x", "gamma_l", "beta_l")
                for n, src in enumerate(names):
                    load(gains[:, n, :], w[src].partition_broadcast(P))
                with nc.allow_non_contiguous_dma("gain columns"):
                    for n in range(2):
                        load(cols[:, n:n + 1], column(w[names[n]]))
            if "Wkv" in w:
                wk_src, wv_src, wo_src = w["Wkv"][:, 0:NH * HD], w["Wkv"][:, NH * HD:2 * NH * HD], w["Wo"]
            elif not single:
                wk_src, wv_src, wo_src = w["W_k"], w["W_v"], w["W_o"]
            if absorbed:
                load(wq_rows[:], w["Wq"] if "Wq" in w else w["W_q"])
                load(wk_rows[:], wk_src)
            if rotary:
                with nc.allow_non_contiguous_dma("head halves"):
                    for dst, src in ((wq, w["Wq"]), (wk, wk_src)):
                        for t in range(PAIRS):
                            for half in range(2):
                                load(dst[:, t, half * SEQ:(half + 1) * SEQ].rearrange("p (h d) -> p h d", h=2),
                                     src[:, t * P:(t + 1) * P].rearrange("p (h a d) -> p a h d", h=2, a=2)[:, half])
                load(rot_cos[:], core.w["c_rope64"][0])
                load(rot_sin[:], core.w["c_rope64"][1])
            if single:
                for dst, src in ((wq, "Wq"), (wk, "Wk"), (wv, "Wv")):
                    load(dst[:], w[src])
                with nc.allow_non_contiguous_dma("bias columns"):
                    for n, src in enumerate(("bq", "bk", "bv")):
                        load(bias[:, n:n + 1], column(w[src]))
            else:
                load(wv_rows[:], wv_src)
                load(wo_rows[:], wo_src.rearrange("(t p) d -> p t d", p=P))
            if out_norm:
                load(out_gains[:, 0, :], w["ln_o_g"].partition_broadcast(P))
                load(out_gains[:, 1, :], w["ln_o_b"].partition_broadcast(P))
            if "b_o" in w:
                with nc.allow_non_contiguous_dma("bias column"):
                    load(out_bias[:], column(w["b_o"]))
            if masked:
                sp.wait_ge(mask_ready, 1)
                sp.dma_start(mask_dram, mask_all[:]).then_inc(mask_stored, 16)
                sp.wait_ge(mask_stored, 16)
                sp.wait_ge(cleared, 2)
            if normed:
                sp.wait_ge(y_ready, 1)
                sp.wait_ge(centred, 1)
                load_own(0, 0)
                load_staged(0, 1)
            elif single:
                sp.wait_ge(act_full, 2)
                sp.wait_ge(dve_full, 2)
                load_staged(0, 1)
            during(0, 0, first=True)
            during(0, 1)
            with sp.Fori(1, BATCHES // 2 - 1) as pair:
                during(pair, 0)
                during(pair, 1)
            during(BATCHES // 2 - 1, 0, last=True)

        LOADS = loads[0]
        QUAD_TURNS = [n for n in (("wq", "wk", "wv") if absorbed else ("wv",)) for _ in range(PAIRS // 4)] if not single else []
        TURNS = len(QUAD_TURNS)

        @block.tensor
        def _(pe):
            lane = lanes()
            pe.wait_ge(cleared, 2)
            pe.wait_ge(w_loaded, 16 * LOADS)
            if not single:
                todo = ((wq_rows, wk_rows, wv_rows) if absorbed else (wv_rows,))
                for j in range(TURNS):
                    source, quad = todo[j // (PAIRS // 4)], j % (PAIRS // 4)
                    if j >= 4:
                        pe.wait_ge(w_kept, j - 3)
                    for i in range(4):
                        turn = nc.tensor.transpose(score[:, (j % 4) * BANK + i * P:(j % 4) * BANK + (i + 1) * P],
                                                   source[:, (4 * quad + i) * P:(4 * quad + i + 1) * P], core.ident[:])
                    turn.then_inc(w_turned, 1)
                pe.wait_ge(w_kept, TURNS)
                for f, (left, right) in enumerate(([(wqT, wkT)] if absorbed else []) * (PAIRS // 4) + [(wvT, wo_rows)] * (PAIRS // 4)):
                    quad = f % (PAIRS // 4)
                    if f >= 2:
                        pe.wait_ge(w_kept, TURNS + f - 1)
                    for odd in range(2):
                        part = slice(odd * SEQ, (odd + 1) * SEQ)
                        bank = score[:, (2 * (f % 2) + odd) * BANK:(2 * (f % 2) + odd + 1) * BANK]
                        for i in range(4):
                            mm = nc.tensor.matmul(bank[:, i * P:(i + 1) * P], left[part, 4 * quad + i, :],
                                                  right[part, 4 * quad + i, :], start=True, stop=True)
                    mm.then_inc(w_turned, 1)
            turn_tiles_pe(nc, pe, core.ident[:], y[:], lane_bank[0:2], y_ready, 1, y_turned)
            pe.wait_ge(yT_kept, 2)
            if not single:
                pe.wait_ge(w_kept, TURNS + (2 if absorbed else 1) * (PAIRS // 4))

            def fill(name):
                ln = lane[name]
                count = ln.count() - len(ln.banks) + 1
                if not isinstance(count, int) or count > 0:
                    pe.wait_ge(ln.free, count)
                return ln.bank()

            def filled(name, ins):
                ins.then_inc(lane[name].full, 1)
                lane[name].next()

            def emptied(name):
                pe.wait_ge(lane[name].free, lane[name].count())

            def context_turns(pair, parity):
                b = pair * 2 + parity
                if normed:
                    pe.wait_ge(c_ready, b + 1)
                elif single:
                    pe.wait_ge(ctx_loaded, 32 * (b + 1))
                else:
                    pe.wait_ge(rows_loaded[parity], 32 * (pair + 1))
                for c, (c0, n) in enumerate(CTX_CHUNKS):
                    bank = fill("AD"[c % 2])
                    for k in range(c0 // P, -(-(c0 + n) // P)):
                        size = tile_of_keys[k][1]
                        source = rows[0:size, parity, k, :] if staged is None else staged[0:size, k, :]
                        turn = nc.tensor.transpose(bank[:, k * P - c0:k * P - c0 + size], source,
                                                   core.ident[0:size, 0:size])
                    filled("AD"[c % 2], turn)

            def make_queries(pair, parity):
                own = yT[:, bass.ds((pair * 2 + parity) * SEQ, SEQ)]
                if single:
                    filled("A", nc.tensor.matmul(fill("A")[:, 0:SEQ], wq[:], own, start=True, stop=True))
                    return
                for job in range(QJOBS):
                    bank = fill("A")
                    for i in range(8 if absorbed else PAIRS):
                        left = fold_qk[:, 8 * job + i, :] if absorbed else wq[:, i, :]
                        mm = nc.tensor.matmul(bank[:, i * SEQ:(i + 1) * SEQ], left, own, start=True, stop=True)
                    filled("A", mm)

            def project_keys(parity):
                emptied("A")
                emptied("D")
                for c0, n in CHUNKS:
                    filled("A", nc.tensor.matmul(fill("A")[:, 0:n], wk[:], keysT[:, parity, c0:c0 + n], start=True, stop=True))

            def rotary_chunk(pair, parity, t, c):
                if c == 0 and t == 0:
                    emptied("A")
                    emptied("D")
                c0, n = CTX_CHUNKS[c]
                bank = fill("D")
                mm = nc.tensor.matmul(bank[:, 0:n], wk[:, t, :], keysT[:, parity, c0:c0 + n], start=True, stop=True)
                if c == len(CTX_CHUNKS) - 1:
                    mm = nc.tensor.matmul(bank[:, P:P + SEQ], wk[:, t, :], yT[:, bass.ds((pair * 2 + parity) * SEQ, SEQ)],
                                          start=True, stop=True)
                filled("D", mm)

            def scores(pair, parity, t, first=False):
                b = pair * 2 + parity
                tile = b * R + t
                if t == 0 and not rotary:
                    emptied("A")
                    emptied("D")
                if masked and t == 0:
                    pe.wait_ge(mask_loaded[parity], 16 * (pair + 1))
                if rotary:
                    pe.wait_ge(keys_turned, (tile + 1) * len(CTX_CHUNKS))
                if not first:
                    pe.wait_ge(exp_done, tile)
                keys = keysT[:, parity] if absorbed else projected[:, parity] if single else projected[:, t % 2]
                for c, (c0, n) in enumerate(CHUNKS):
                    mm = nc.tensor.matmul(score[0:ROWS, c0:c0 + n], queries[:, parity, t * ROWS:(t + 1) * ROWS],
                                          keys[:, c0:c0 + n], start=True, stop=not masked)
                    if masked:
                        mm = nc.tensor.matmul(score[0:ROWS, c0:c0 + n], pick16[:], mask16[:, parity, c0:c0 + n],
                                              start=False, stop=True)
                    if c in (1, len(CHUNKS) - 1):
                        mm.then_inc(score_half, 1)

            def turn_probs(pair, parity, t, quads):
                if 0 in quads:
                    pe.wait_ge(prob_ready, (pair * 2 + parity) * R + t + 1)
                which = t % 2 if R > 1 else parity
                for j in quads:
                    bank = fill(T_LANES[j])
                    for i, k in enumerate(QUADS[j]):
                        c0, n = tile_of_keys[k]
                        turn = nc.tensor.transpose(bank[0:n, i * P:(i + 1) * P], prob[:, which, c0:c0 + n], core.ident[:])
                    filled(T_LANES[j], turn)

            def sum_context(pair, parity, group, part, turned):
                b = pair * 2 + parity
                if part == 0:
                    for name, count in turned.items():
                        pe.wait_ge(lane[name].free, count)
                    if single:
                        pe.wait_ge(rows_loaded[parity], 32 * (pair + 1))
                    if normed:
                        pe.wait_ge(rows_ready, b + 1)
                        pe.wait_ge(own_loaded[parity], 16 * (pair + 1))
                    if not (isinstance(b, int) and b == 0 and group == 0):
                        pe.wait_ge(sums_kept, b * GROUPS + group)
                which = group if GROUPS > 1 else parity
                for k in PV_PARTS[part]:
                    n = tile_of_keys[k][1]
                    mm = nc.tensor.matmul(sums[:, 0:GROWS], rows[0:n, parity, k, :], probT[0:n, which, k, :],
                                          start=(k == 0), stop=(k == KT - 1))
                if part == len(PV_PARTS) - 1:
                    mm.then_inc(sums_done, 1)

            def output(pair, parity):
                b = pair * 2 + parity
                pe.wait_ge(sums_kept, GROUPS * (b + 1))
                bank = fill("A")
                for h in range(NH):
                    which = h // 8 if GROUPS > 1 else parity
                    col = (h % (2 * TPG)) * SEQ
                    mm = nc.tensor.matmul(bank[:, 0:SEQ], wv[:] if single else fold_vo[:, h, :], mixed[:, which, col:col + SEQ],
                                          start=(h == 0), stop=(h == NH - 1))
                filled("A", mm)

            def prepare(pair, parity, first=False, before=None):
                context_turns(pair, parity)
                make_queries(pair, parity)
                if before is not None:
                    output(*before)
                if single:
                    project_keys(parity)
                if rotary:
                    for c in range(len(CTX_CHUNKS)):
                        rotary_chunk(pair, parity, 0, c)
                scores(pair, parity, 0, first)

            def batch(pair, parity, first=False, last=False):
                b = pair * 2 + parity
                go_to_batch(lane, b, parity, first)
                previous = (pair - (1 - parity), 1 - parity)
                start = {name: lane[name].at for name in "AD"}
                group_turned = start
                for t in range(1, R):
                    scores(pair, parity, t)
                    parts = [(pair, parity, g, p, group_turned) if back == 0 else (*previous, g, p, start)
                             for back, g, p in sums_of_slot(t) if back == 0 or not first]
                    if rotary:
                        chunks = range(len(CTX_CHUNKS)) if t + 1 < R else ()
                        for c in range(4):
                            if c in chunks:
                                rotary_chunk(pair, parity, t + 1, c)
                            if c < 2:
                                turn_probs(pair, parity, t - 1, (2 * c, 2 * c + 1))
                            if c == 2:
                                for part in parts:
                                    sum_context(*part)
                    else:
                        turn_probs(pair, parity, t - 1, (0, 1, 2))
                        for part in parts:
                            sum_context(*part)
                        turn_probs(pair, parity, t - 1, (3,))
                    if t % 4 == 0:
                        group_turned = {name: lane[name].count() for name in "AD"}
                    if t == out_slot and not first:
                        output(*previous)
                if R == 1 and not first:
                    for p in range(len(PV_PARTS)):
                        sum_context(*previous, 0, p, start)
                due = previous if out_slot == 0 and not first else None
                if last:
                    if due is not None:
                        output(*due)
                else:
                    prepare(pair + parity, 1 - parity, before=due)
                    if rotary:
                        for c in range(len(CTX_CHUNKS)):
                            rotary_chunk(pair + parity, 1 - parity, 1, c)
                turn_probs(pair, parity, R - 1, range(len(QUADS)))

            prepare(0, 0, first=True)
            if rotary:
                for c in range(len(CTX_CHUNKS)):
                    rotary_chunk(0, 0, 1, c)
            batch(0, 0, first=True)
            batch(0, 1)
            with pe.Fori(1, BATCHES // 2 - 1) as pair:
                batch(pair, 0)
                batch(pair, 1)
            batch(BATCHES // 2 - 1, 0)
            batch(BATCHES // 2 - 1, 1, last=True)
            for p in range(len(PV_PARTS)):
                sum_context(BATCHES // 2 - 1, 1, GROUPS - 1, p, {name: lane[name].count() for name in "AD"})
            output(BATCHES // 2 - 1, 1)
            emptied("A")
            pe.wait_ge(exp_done, BATCHES * R)
            for t in range(TILES):
                turn = nc.tensor.transpose(score[:, t * P:(t + 1) * P], outT[:, t * P:(t + 1) * P], core.ident[:])
            turn.then_inc(out_turned, 1)

        @block.scalar
        def _(act):
            lane = lanes()
            act.wait_ge(cleared, 2)
            act.wait_ge(w_loaded, 16 * LOADS)
            if not single:
                turned = {"wq": wqT, "wk": wkT, "wv": wvT} if absorbed else {"wv": wvT}
                for j, n in enumerate(QUAD_TURNS):
                    quad = j % (PAIRS // 4)
                    act.wait_ge(w_turned, j + 1)
                    nc.scalar.copy(turned[n][:, 4 * quad:4 * quad + 4, :].rearrange("p i d -> p (i d)"),
                                   score[:, (j % 4) * BANK:(j % 4 + 1) * BANK]).then_inc(w_kept, 1)
                for f, dst in enumerate(([fold_qk] if absorbed else []) * (PAIRS // 4) + [fold_vo] * (PAIRS // 4)):
                    quad = f % (PAIRS // 4)
                    act.wait_ge(w_turned, TURNS + f + 1)
                    for odd in range(2):
                        bank = score[:, (2 * (f % 2) + odd) * BANK:(2 * (f % 2) + odd + 1) * BANK]
                        kept = nc.scalar.copy(dst[:].rearrange("p (i r) d -> p r i d", r=2)[:, odd, 4 * quad:4 * quad + 4, :],
                                              bank.rearrange("p (i d) -> p i d", d=D))
                    kept.then_inc(w_kept, 1)
            normalize_act(nc, act, core.eps(EPS_5), TILES, D, stats, var_ready, std_ready, 1)
            if normed:
                normalize_act(nc, act, core.eps(EPS_5), TILES, D, stats, var_ready, std_ready, 2)
            keep_turned_act(nc, act, yT, lane_bank[0:2], y_turned, 1, yT_kept)

            def take():
                act.wait_ge(lane["A"].full, lane["A"].count() + 1)
                return lane["A"].bank()

            def emptied(ins):
                ins.then_inc(lane["A"].free, 1)
                lane["A"].next()

            def keep_context(pair, parity):
                for c in range(0, len(CTX_CHUNKS), 2):
                    c0, n = CTX_CHUNKS[c]
                    bank = take()
                    if normed:
                        if c == 0:
                            nc.scalar.copy(keysT[:, parity, CTX:KEYS], yT[:, bass.ds((pair * 2 + parity) * SEQ, SEQ)])
                        emptied(nc.scalar.activation(keysT[:, parity, c0:c0 + n], bank[:, 0:n], ACT.Identity,
                                                     bias=cols[:, 1:2], scale=cols[:, 0:1]))
                    else:
                        emptied(nc.scalar.copy(keysT[:, parity, c0:c0 + n], bank[:, 0:n]))

            def keep_queries(parity):
                for job in range(QJOBS):
                    bank = take()
                    if single:
                        emptied(nc.scalar.activation(queries[:, parity, :], bank[:, 0:SEQ], ACT.Identity, bias=bias[:, 0:1]))
                    elif absorbed:
                        emptied(nc.scalar.copy(queries[:, parity, job * BANK:(job + 1) * BANK], bank[:]))
                    else:
                        for q in range(4):
                            part = slice(32 * q, 32 * q + 32)
                            last = nc.scalar.copy(queries[part, parity, :].rearrange("p (t h i) -> p t h i", h=2, i=SEQ)[:, :, q % 2, :],
                                                  bank[part, 0:PAIRS * SEQ].rearrange("p (t i) -> p t i", i=SEQ))
                        emptied(last)

            def exps(pair, parity, t):
                tile = (pair * 2 + parity) * R + t
                which = t % 2 if R > 1 else parity
                act.wait_ge(peak_ready, tile + 1)
                nc.scalar.activation(prob[0:ROWS, which, :], score[0:ROWS, 0:KEYS], ACT.Exp,
                                     bias=neg_peak[0:ROWS, which:which + 1], scale=scale,
                                     accum_out=rsum[0:ROWS, which:which + 1]).then_inc(exp_done, 1)

            def keep_probs(parity, t, quads):
                which, col = (t // TPG if GROUPS > 1 else parity), (t % TPG) * ROWS
                for j in quads:
                    if T_LANES[j] == "A":
                        bank = take()
                        for k0, n, size in full_tiles(QUADS[j]):
                            last = nc.scalar.copy(probT[0:size, which, k0:k0 + n, col:col + ROWS],
                                                  bank[0:size, (k0 % 4) * P:(k0 % 4 + n) * P]
                                                  .rearrange("p (i r) -> p i r", r=P)[:, :, 0:ROWS])
                        emptied(last)

            def keep_sums(pair, parity, group):
                act.wait_ge(sums_done, (pair * 2 + parity) * GROUPS + group + 1)
                which = group if GROUPS > 1 else parity
                nc.scalar.copy(mixed[:, which, :], sums[:, 0:GROWS]).then_inc(sums_kept, 1)

            def keep_output(pair, parity):
                bank = take()
                dst = outT[:, bass.ds((pair * 2 + parity) * SEQ, SEQ)]
                if single:
                    emptied(nc.scalar.activation(dst, bank[:, 0:SEQ], ACT.Identity, bias=bias[:, 2:3]))
                elif "b_o" in w:
                    emptied(nc.scalar.activation(dst, bank[:, 0:SEQ], ACT.Identity, bias=out_bias[:]))
                else:
                    emptied(nc.scalar.copy(dst, bank[:, 0:SEQ]))

            def context_root(b):
                act.wait_ge(cvar_ready, b + 1)
                nc.scalar.activation(cstats[:, 2, :], cstats[:, 1, :], ACT.Sqrt, bias=core.eps(EPS_5), scale=1.0 / D)\
                    .then_inc(cstd_ready, 1)

            def prepare(pair, parity, before=None):
                keep_context(pair, parity)
                keep_queries(parity)
                if before is not None:
                    keep_output(*before)
                if single:
                    for c0, n in CHUNKS:
                        emptied(nc.scalar.activation(projected[:, parity, c0:c0 + n], take()[:, 0:n], ACT.Identity,
                                                     bias=bias[:, 1:2]))

            def batch(pair, parity, first=False, last=False):
                b = pair * 2 + parity
                go_to_batch(lane, b, parity, first)
                previous = (pair - (1 - parity), 1 - parity)
                for t in range(1, R):
                    if GROUPS > 1 and t == 4 and not first:
                        keep_sums(*previous, GROUPS - 1)
                    keep_probs(parity, t - 1, range(len(QUADS)))
                    if t == out_slot and not first:
                        keep_output(*previous)
                    exps(pair, parity, t)
                    if normed and t == 2 and not last:
                        context_root(b + 1)
                if GROUPS > 1:
                    keep_sums(pair, parity, 0)
                elif not first:
                    keep_sums(*previous, 0)
                due = previous if out_slot == 0 and not first else None
                if last:
                    if due is not None:
                        keep_output(*due)
                else:
                    prepare(pair + parity, 1 - parity, due)
                if not last and R == 1:
                    keep_probs(parity, R - 1, range(len(QUADS)))
                    exps(pair + parity, 1 - parity, 0)
                elif not last:
                    keep_probs(parity, R - 1, range(len(QUADS)))
                    exps(pair + parity, 1 - parity, 0)
                else:
                    keep_probs(parity, R - 1, range(len(QUADS)))

            if normed:
                context_root(0)
            prepare(0, 0)
            exps(0, 0, 0)
            batch(0, 0, first=True)
            batch(0, 1)
            with act.Fori(1, BATCHES // 2 - 1) as pair:
                batch(pair, 0)
                batch(pair, 1)
            batch(BATCHES // 2 - 1, 0)
            batch(BATCHES // 2 - 1, 1, last=True)
            keep_sums(BATCHES // 2 - 1, 1, GROUPS - 1)
            keep_output(BATCHES // 2 - 1, 1)
            if out_norm:
                normalize_act(nc, act, core.eps(EPS_5), TILES, D, stats, var_ready, std_ready, 3)

        @block.gpsimd
        def _(pool):
            if normed:
                nc.gpsimd.memset(raw[:], 0.0)
            if single:
                nc.gpsimd.memset(prob[:], 0.0)
            pool.drain()
            nc.gpsimd.memset(neg_peak[:], 0.0).then_inc(cleared, 1)
            if masked:
                nc.gpsimd.memset(pick16[:], 0.0)
                nc.gpsimd.memset(mask16[:], 0.0)
                pool.drain()
                nc.gpsimd.memset(pick16[0:1, :], 1.0)
            if rotary:
                nc.gpsimd.memset(queries[:], 0.0)
            pool.drain()
            nc.gpsimd.memset(peak[:], 0.0).then_inc(cleared, 1)
            pool.wait_ge(w_loaded, 16 * LOADS)

            def add_crossed(tile, t):
                for c, (c0, n) in enumerate(CTX_CHUNKS):
                    pool.wait_ge(crossed_ready, tile * len(CTX_CHUNKS) + c + 1)
                    nc.gpsimd.tensor_tensor(projected[:, t % 2, c0:c0 + n], projected[:, t % 2, c0:c0 + n],
                                            crossed[:, c % 2, 0:n], ALU.add).then_inc(keys_turned, 1)

            def make_rows(pair, parity, free=None):
                b = pair * 2 + parity
                if free is not None:
                    pool.wait_ge(sums_done, free)
                dst = rows[:, parity, 0:CT, :]
                pool.wait_ge(c_ready, b + 1)
                nc.gpsimd.tensor_tensor(dst, staged[:], over_tiles(gains[:, 0, :], CT), ALU.mult)
                pool.drain()
                nc.gpsimd.tensor_tensor(dst, dst, over_tiles(gains[:, 1, :], CT), ALU.add).then_inc(rows_ready, 1)

            def batch(pair, parity, first=False, last=False):
                b = pair * 2 + parity
                for t in range(1, R - 1):
                    if rotary:
                        add_crossed(b * R + t + 1, t + 1)
                if not last:
                    make_rows(pair + parity, 1 - parity, None if first else GROUPS * b)
                    if rotary:
                        add_crossed(b * R + R, 0)
                        add_crossed(b * R + R + 1, 1)

            if normed:
                make_rows(0, 0)
                if rotary:
                    add_crossed(0, 0)
                    add_crossed(1, 1)
                batch(0, 0, first=True)
                batch(0, 1)
                with pool.Fori(1, BATCHES // 2 - 1) as pair:
                    batch(pair, 0)
                    batch(pair, 1)
                batch(BATCHES // 2 - 1, 0)
                batch(BATCHES // 2 - 1, 1, last=True)

        @block.vector
        def _(dve):
            lane = lanes()
            normalize_dve(nc, dve, y[:], lat[:], square[:], stats, var_ready, std_ready, 1)
            dve.drain()
            dve.wait_ge(w_loaded, 16 * LOADS)
            if normed:
                normalize_dve(nc, dve, y[:], y[:], square[:], stats, var_ready, std_ready, 2)
                dve.drain()
                nc.vector.tensor_tensor(y[:], y[:], over_tiles(gains[:, 2, :], TILES), ALU.mult)
                dve.drain()
                nc.vector.tensor_tensor(y[:], y[:], over_tiles(gains[:, 3, :], TILES), ALU.add).then_inc(y_ready, 1)
            else:
                nc.vector.tensor_copy(square[:, 0, 0:1], y[:, 0, 0:1]).then_inc(y_ready, 1)
            if masked:
                nc.vector.memset(mask_all[:, CTX:KEYS], 0.0)
                nc.vector.tensor_scalar(mask_all[:, 0:CTX], mask_u8[:], -1.0, 1e30, ALU.add, ALU.mult).then_inc(mask_ready, 1)
            dve.wait_ge(cleared, 2)

            def take():
                dve.wait_ge(lane["D"].full, lane["D"].count() + 1)
                return lane["D"].bank()

            def emptied(ins):
                ins.then_inc(lane["D"].free, 1)
                lane["D"].next()

            def centre(b, first=False):
                dve.wait_ge(ctx_loaded, 32 * (b + 1))
                nc.vector.tensor_reduce(cstats[:, 0, :], raw[:], AX, ALU.add)
                dve.drain()
                nc.vector.tensor_scalar(cstats[:, 0, :], cstats[:, 0, :], 1.0 / D, None, ALU.mult)
                dve.drain()
                if not first:
                    dve.wait_ge(rows_ready, b)
                nc.vector.tensor_tensor(staged[:], raw[:], over_last(cstats[:, 0, :], D), ALU.subtract).then_inc(centred, 1)
                dve.drain()

            def spread(b):
                nc.vector.tensor_tensor(csq[:], staged[:], staged[:], ALU.mult)
                dve.drain()
                nc.vector.tensor_reduce(cstats[:, 1, :], csq[:], AX, ALU.add).then_inc(cvar_ready, 1)

            def rescale(b):
                dve.wait_ge(cstd_ready, b + 1)
                nc.vector.reciprocal(cstats[:, 3, :], cstats[:, 2, :])
                dve.drain()
                nc.vector.tensor_tensor(staged[:], staged[:], over_last(cstats[:, 3, :], D), ALU.mult).then_inc(c_ready, 1)
                dve.drain()

            def keep_context(parity):
                for c in range(1, len(CTX_CHUNKS), 2):
                    c0, n = CTX_CHUNKS[c]
                    bank = take()
                    if normed:
                        emptied(nc.vector.tensor_scalar(keysT[:, parity, c0:c0 + n], bank[:, 0:n], cols[:, 0:1], cols[:, 1:2],
                                                        ALU.mult, ALU.add))
                    else:
                        emptied(nc.vector.tensor_copy(keysT[:, parity, c0:c0 + n], bank[:, 0:n]))

            def turn_keys(tile, t, start=False):
                for c, (c0, n) in enumerate(CTX_CHUNKS):
                    bank = take()
                    if not (start and c < 2):
                        dve.wait_ge(keys_turned, tile * len(CTX_CHUNKS) + c - 1)
                    if c == len(CTX_CHUNKS) - 1:
                        nc.vector.tensor_copy(projected[:, t % 2, CTX:KEYS], bank[:, P:P + SEQ])
                    nc.vector.tensor_tensor(projected[:, t % 2, c0:c0 + n], bank[:, 0:n], rot_cos[:, c0:c0 + n], ALU.mult)
                    nc.vector.tensor_tensor(crossed[SEQ:P, c % 2, 0:n], bank[0:SEQ, 0:n], rot_sin[0:SEQ, c0:c0 + n], ALU.mult)
                    nc.vector.tensor_tensor(crossed[0:SEQ, c % 2, 0:n], bank[SEQ:P, 0:n], rot_sin[SEQ:P, c0:c0 + n], ALU.mult)\
                        .then_inc(crossed_ready, 1)
                    emptied(dve.drain())

            def maximum(pair, parity, t):
                tile = (pair * 2 + parity) * R + t
                which = t % 2 if R > 1 else parity
                dve.wait_ge(score_half, 2 * tile + 1)
                nc.vector.tensor_reduce(peak[0:ROWS, 0:1], score[0:ROWS, 0:2 * BANK], AX, ALU.max)
                dve.wait_ge(score_half, 2 * tile + 2)
                nc.vector.tensor_reduce(peak[0:ROWS, 1:2], score[0:ROWS, 2 * BANK:KEYS], AX, ALU.max)
                dve.drain()
                nc.vector.tensor_scalar(neg_peak[0:ROWS, which:which + 1], peak[0:ROWS, 0:1], peak[0:ROWS, 1:2], -scale,
                                        ALU.max, ALU.mult).then_inc(peak_ready, 1)

            def normalise(pair, parity, t):
                tile = (pair * 2 + parity) * R + t
                which = t % 2 if R > 1 else parity
                dve.wait_ge(exp_done, tile + 1)
                nc.vector.reciprocal(rinv[0:ROWS, which:which + 1], rsum[0:ROWS, which:which + 1])
                dve.drain()
                nc.vector.tensor_scalar(prob[0:ROWS, which, :], prob[0:ROWS, which, :], rinv[0:ROWS, which:which + 1], None,
                                        ALU.mult).then_inc(prob_ready, 1)

            def keep_probs(parity, t, quads):
                which, col = (t // TPG if GROUPS > 1 else parity), (t % TPG) * ROWS
                for j in quads:
                    if T_LANES[j] == "D":
                        bank = take()
                        for k0, n, size in full_tiles(QUADS[j]):
                            last = nc.vector.tensor_copy(probT[0:size, which, k0:k0 + n, col:col + ROWS],
                                                         bank[0:size, (k0 % 4) * P:(k0 % 4 + n) * P]
                                                         .rearrange("p (i r) -> p i r", r=P)[:, :, 0:ROWS])
                        emptied(last)

            def batch(pair, parity, first=False, last=False):
                b = pair * 2 + parity
                go_to_batch(lane, b, parity, first)
                for t in range(1, R):
                    normalise(pair, parity, t - 1)
                    maximum(pair, parity, t)
                    if rotary and t + 1 < R:
                        turn_keys(b * R + t + 1, t + 1)
                    keep_probs(parity, t - 1, range(len(QUADS)))
                    if normed and not last:
                        if t == 1:
                            centre(b + 1)
                        if t == 2:
                            spread(b + 1)
                        if t == 3:
                            rescale(b + 1)
                normalise(pair, parity, R - 1)
                if not last:
                    keep_context(1 - parity)
                    if rotary:
                        turn_keys(b * R + R, 0)
                    maximum(pair + parity, 1 - parity, 0)
                    if rotary:
                        turn_keys(b * R + R + 1, 1)
                keep_probs(parity, R - 1, range(len(QUADS)))

            if normed:
                centre(0, first=True)
                spread(0)
                rescale(0)
            keep_context(0)
            if rotary:
                turn_keys(0, 0, start=True)
            maximum(0, 0, 0)
            if rotary:
                turn_keys(1, 1)
            batch(0, 0, first=True)
            batch(0, 1)
            with dve.Fori(1, BATCHES // 2 - 1) as pair:
                batch(pair, 0)
                batch(pair, 1)
            batch(BATCHES // 2 - 1, 0)
            batch(BATCHES // 2 - 1, 1, last=True)
            dve.wait_ge(out_turned, 1)
            turned = score[:, 0:TOKENS].rearrange("p (t d) -> p t d", d=D)
            if out_norm:
                nc.vector.tensor_copy(out_rows[:], turned)
                dve.drain()
                normalize_dve(nc, dve, out_rows[:], out_rows[:], square[:], stats, var_ready, std_ready, 3)
                dve.drain()
                nc.vector.tensor_tensor(out_rows[:], out_rows[:], over_tiles(out_gains[:, 0, :], TILES), ALU.mult)
                dve.drain()
                nc.vector.tensor_tensor(out_rows[:], out_rows[:], over_tiles(out_gains[:, 1, :], TILES), ALU.add)
                dve.drain()
                nc.vector.tensor_tensor(lat[:], lat[:], out_rows[:], ALU.add)
            else:
                nc.vector.tensor_tensor(lat[:], lat[:], turned, ALU.add)


def top2_mask_dve(nc, dve, prob, rank, low, mask, work):
    n, experts = prob.shape[1], prob.shape[2]
    first, rest, cand, top = work[:, 0], work[:, 1], work[:, 2], work[:, 3]
    peak = top[:, :, 0]
    for source, chosen in ((prob, first), (rest, mask)):
        nc.vector.tensor_reduce(peak, source, AX, ALU.max)
        dve.drain()
        nc.vector.tensor_tensor(cand, source, over_last(peak, experts), ALU.is_ge)
        dve.drain()
        nc.vector.tensor_tensor(cand, cand, over_tiles(rank, n), ALU.mult)
        dve.drain()
        nc.vector.tensor_reduce(peak, cand, AX, ALU.max)
        dve.drain()
        nc.vector.tensor_tensor(chosen, cand, over_last(peak, experts), ALU.is_equal)
        dve.drain()
        if chosen is first:
            nc.vector.scalar_tensor_tensor(rest, first, low, prob, ALU.mult, ALU.add)
            dve.drain()
    nc.vector.tensor_tensor(mask, mask, first, ALU.add)
    dve.drain()


def moe_stage(core, name, kind, wg, w1, b1, w2, b2, bg=None):
    nc, lat = core.nc, core.lat
    E = 8
    swiglu = kind == "swiglu"
    H = w2.shape[2] if swiglu else w1.shape[2]
    C = H // P
    with ExitStack() as ctx:
        s = Stage(nc, ctx, name)
        y = s.sb("y", [P, TILES, D])
        square = s.sb("square", [P, TILES, D])
        yT = s.sb("yT", [P, TOKENS])
        stats = s.sb("stats", [P, 4, TILES])
        wg_sb = s.sb("wg", [P, E])
        w1_sb = s.sb("w1", [P, E, (2 if swiglu else 1) * H])
        w2_sb = s.sb("w2", [P, E, C, D])
        hT = s.sb("hT", [P, 2, C, TOKENS])
        prob = s.sb("prob", [P, TILES, E])
        gate = s.sb("gate", [P, TILES, E])
        mask = s.sb("mask", [P, TILES, E])
        work = s.sb("work", [P, 4, TILES, E])
        norm = s.sb("norm", [P, 2, TILES])
        gated = s.sb("gated", [P, TILES, D])
        acc = s.sb("acc", [P, TILES, D])
        if swiglu:
            w1_rows = s.sb("w1_rows", [P, E, 2 * H // P, D])
            w2_rows = s.sb("w2_rows", [P, E, H])
            wg_rows = s.sb("wg_rows", [E, D])
            silu = s.sb("silu", [P, TOKENS])
        else:
            b1_sb = s.sb("b1", [P, E, C])
            b2_sb = s.sb("b2", [E, D])
            gateT = s.sb("gateT", [E, TOKENS])
            if bg is not None:
                bg_sb = s.sb("bg", [P, E])
        hid = [s.ps(f"hid{i}", [P, TOKENS]) for i in range(2)]
        mix = s.ps("mix", [P, TILES, D])
        aux = [s.ps(f"aux{i}", [P, BANK]) for i in range(2)]

        gate_loaded, w1_loaded, w2_loaded = s.sem("gate_loaded"), s.sem("w1_loaded"), s.sem("w2_loaded")
        var_ready, std_ready = s.sem("var_ready"), s.sem("std_ready")
        y_ready, y_turned, yT_ready = s.sem("y_ready"), s.sem("y_turned"), s.sem("yT_ready")
        w_turned, w_copied = s.sem("w_turned"), s.sem("w_copied")
        logits_done, shifted, exp_done = s.sem("logits_done"), s.sem("shifted"), s.sem("exp_done")
        gate_ready, gate_turned, gateT_ready = s.sem("gate_ready"), s.sem("gate_turned"), s.sem("gateT_ready")
        hid_done, h_ready, silu_done = s.sem("hid_done"), s.sem("h_ready"), s.sem("silu_done")
        mix_done, mix_used = s.sem("mix_done"), s.sem("mix_used")
        TURNS = E * (2 * H // P) // 4 + E * C // 4
        block = s.block()

        @block.sync
        def _(sp):
            if swiglu:
                sp.dma_start(wg_rows[:], wg).then_inc(gate_loaded, 16)
                sp.dma_start(w1_rows[:], w1.rearrange("e (c p) d -> p e c d", p=P)).then_inc(w1_loaded, 16)
                sp.dma_start(w2_rows[:], w2.rearrange("e d h -> d e h")).then_inc(w2_loaded, 16)
            else:
                sp.dma_start(wg_sb[:], wg).then_inc(gate_loaded, 16)
                if bg is not None:
                    sp.dma_start(bg_sb[:], bg.partition_broadcast(P)).then_inc(gate_loaded, 16)
                sp.dma_start(w1_sb[:], w1.rearrange("e d h -> d e h")).then_inc(w1_loaded, 16)
                with nc.allow_non_contiguous_dma("bias columns"):
                    for e in range(E):
                        sp.dma_start(b1_sb[:, e, :], b1[e].rearrange("(c p) -> p c", p=P)).then_inc(w1_loaded, 16)
                sp.dma_start(b2_sb[:], b2).then_inc(w2_loaded, 16)
                sp.dma_start(w2_sb[:], w2.rearrange("e (c p) d -> p e c d", p=P)).then_inc(w2_loaded, 16)
        gate_loads = 2 if bg is not None else 1
        w1_loads = 1 if swiglu else 1 + E
        w2_loads = 1 if swiglu else 2

        @block.tensor
        def _(pe):
            pe.wait_ge(y_ready, 1)
            for t in range(TILES):
                turn = nc.tensor.transpose(aux[t // 4][:, (t % 4) * D:(t % 4 + 1) * D], y[:, t, :], core.ident[:])
                if t % 4 == 3:
                    turn.then_inc(y_turned, 1)
            if swiglu:
                pe.wait_ge(gate_loaded, 16)
                pe.wait_ge(yT_ready, 2)
                nc.tensor.transpose(aux[0][:, 0:E], wg_rows[:], core.ident[0:E, 0:E]).then_inc(w_turned, 1)
                pe.wait_ge(w1_loaded, 16)
                pe.wait_ge(w2_loaded, 16)
                blocks = [w1_rows[:, e, c, :] for e in range(E) for c in range(2 * H // P)]
                blocks += [w2_rows[:, e, c * P:(c + 1) * P] for e in range(E) for c in range(C)]
                for k in range(TURNS):
                    pe.wait_ge(w_copied, max(k, 1))
                    for j in range(4):
                        turn = nc.tensor.transpose(aux[k % 2][:, j * P:(j + 1) * P], blocks[4 * k + j], core.ident[:])
                    turn.then_inc(w_turned, 1)
                pe.wait_ge(w_copied, TURNS + 1)
            else:
                pe.wait_ge(gate_loaded, 16 * gate_loads)
                pe.wait_ge(yT_ready, 2)
            for t in range(TILES):
                score = nc.tensor.matmul(aux[0][:, t * E:(t + 1) * E], yT[:, t * P:(t + 1) * P], wg_sb[:],
                                         start=True, stop=True)
            score.then_inc(logits_done, 1)

            hidden = [0]

            def hidden_chunk(e, column):
                k = hidden[0]
                if k >= 2 and not swiglu:
                    pe.wait_ge(h_ready, k - 1)
                elif k >= 2 and k % 2 == 0:
                    pe.wait_ge(silu_done, k // 2)
                elif k >= 2:
                    pe.wait_ge(h_ready, k // 2)
                for half in range(2):
                    nc.tensor.matmul(hid[k % 2][:, half * BANK:(half + 1) * BANK],
                                     w1_sb[:, e, column:column + P], yT[:, half * BANK:(half + 1) * BANK],
                                     start=True, stop=True).then_inc(hid_done, 1)
                hidden[0] += 1

            def expert_hidden(e):
                for c in range(C):
                    hidden_chunk(e, c * P)
                    if swiglu:
                        hidden_chunk(e, H + c * P)

            def expert_out(e):
                pe.wait_ge(h_ready, C * (e + 1))
                if e >= 1:
                    pe.wait_ge(mix_used, e)
                for t in range(TILES):
                    for c in range(C):
                        out = nc.tensor.matmul(mix[:, t, :], hT[:, e % 2, c, t * P:(t + 1) * P], w2_sb[:, e, c, :],
                                               start=(c == 0), stop=(c == C - 1))
                out.then_inc(mix_done, 1)

            if not swiglu:
                pe.wait_ge(w1_loaded, 16 * w1_loads)
            expert_hidden(0)
            for e in range(E):
                if e == 1 and not swiglu:
                    pe.wait_ge(gate_ready, 1)
                    for t in range(TILES):
                        turn = nc.tensor.transpose(aux[t // 4][0:E, (t % 4) * P:(t % 4 + 1) * P], gate[:, t, :],
                                                   core.ident[:])
                    turn.then_inc(gate_turned, 1)
                if e + 1 < E:
                    expert_hidden(e + 1)
                if e == 0 and not swiglu:
                    pe.wait_ge(w2_loaded, 16 * w2_loads)
                expert_out(e)
            if not swiglu:
                pe.wait_ge(gateT_ready, 1)
                pe.wait_ge(mix_used, E)
                for t in range(TILES):
                    out = nc.tensor.matmul(mix[:, t, :], gateT[:, t * P:(t + 1) * P], b2_sb[:], start=True, stop=True)
                out.then_inc(mix_done, 1)

        @block.scalar
        def _(act):
            normalize_act(nc, act, core.eps(EPS_5), TILES, D, stats, var_ready, std_ready, 1)
            for half in range(2):
                act.wait_ge(y_turned, half + 1)
                nc.scalar.copy(yT[:, half * BANK:(half + 1) * BANK], aux[half][:]).then_inc(yT_ready, 1)
            if swiglu:
                act.wait_ge(w_turned, 1)
                nc.scalar.copy(wg_sb[:], aux[0][:, 0:E]).then_inc(w_copied, 1)
                for k in range(TURNS):
                    act.wait_ge(w_turned, k + 2)
                    turned = aux[k % 2][:].rearrange("p (j q) -> p j q", q=P)
                    per = 2 * H // P
                    if 4 * k < E * per:
                        dst = w1_sb[:].rearrange("p e (c q) -> p (e c) q", q=P)[:, 4 * k:4 * k + 4, :]
                    else:
                        j = 4 * k - E * per
                        dst = w2_sb[:].rearrange("p e c d -> p (e c) d")[:, j:j + 4, :]
                    nc.scalar.copy(dst, turned).then_inc(w_copied, 1)
            act.wait_ge(shifted, 1)
            nc.scalar.activation(prob[:], prob[:], ACT.Exp).then_inc(exp_done, 1)

            def hidden_of(e):
                for c in range(C):
                    if swiglu:
                        k = 2 * (e * C + c)
                        act.wait_ge(hid_done, 2 * k + 2)
                        if k >= 2:
                            act.wait_ge(h_ready, e * C + c)
                        nc.scalar.activation(silu[:], hid[0][:], ACT.Silu).then_inc(silu_done, 1)
                    else:
                        k = e * C + c
                        act.wait_ge(hid_done, 2 * k + 2)
                        nc.scalar.activation(hT[:, e % 2, c, :], hid[k % 2][:],
                                             ACT.Relu if kind == "relu" else ACT.Gelu,
                                             bias=b1_sb[:, e, c:c + 1]).then_inc(h_ready, 1)

            if not swiglu:
                act.wait_ge(w1_loaded, 16 * w1_loads)
            for e in range(E):
                hidden_of(e)
                if e == 1 and not swiglu:
                    act.wait_ge(gate_turned, 1)
                    for half in range(2):
                        last = nc.scalar.copy(gateT[:, half * BANK:(half + 1) * BANK], aux[half][0:E, :])
                    last.then_inc(gateT_ready, 1)

        @block.vector
        def _(dve):
            normalize_dve(nc, dve, y[:], lat[:], square[:], stats, var_ready, std_ready, 1).then_inc(y_ready, 1)
            dve.wait_ge(logits_done, 1)
            scores = aux[0][:, 0:TILES * E].rearrange("p (t e) -> p t e", e=E)
            peak, total = norm[:, 0, :], norm[:, 1, :]
            if bg is not None:
                nc.vector.tensor_tensor(gate[:], scores, over_tiles(bg_sb[:], TILES), ALU.add)
            else:
                nc.vector.tensor_copy(gate[:], scores)
            dve.drain()
            if swiglu:
                top2_mask_dve(nc, dve, gate[:], core.rank, -3e38, mask[:], work[:])
            nc.vector.tensor_reduce(peak, gate[:], AX, ALU.max)
            dve.drain()
            nc.vector.tensor_tensor(prob[:], gate[:], over_last(peak, E), ALU.subtract).then_inc(shifted, 1)
            dve.wait_ge(exp_done, 1)
            if swiglu:
                nc.vector.tensor_tensor(prob[:], prob[:], mask[:], ALU.mult)
                dve.drain()
            nc.vector.tensor_reduce(total, prob[:], AX, ALU.add)
            dve.drain()
            nc.vector.reciprocal(total, total)
            dve.drain()
            nc.vector.tensor_tensor(prob[:], prob[:], over_last(total, E), ALU.mult)
            dve.drain()
            if swiglu:
                nc.vector.tensor_copy(gate[:], prob[:])
            else:
                top2_mask_dve(nc, dve, prob[:], core.rank, -4.0, mask[:], work[:])
                if kind == "relu":
                    nc.vector.tensor_tensor(gate[:], prob[:], mask[:], ALU.mult).then_inc(gate_ready, 1)
                else:
                    nc.vector.tensor_tensor(prob[:], prob[:], mask[:], ALU.mult)
                    dve.drain()
                    nc.vector.tensor_reduce(total, prob[:], AX, ALU.add)
                    dve.drain()
                    nc.vector.tensor_scalar(total, total, 1e-12, None, ALU.max)
                    dve.drain()
                    nc.vector.reciprocal(total, total)
                    dve.drain()
                    nc.vector.tensor_tensor(gate[:], prob[:], over_last(total, E), ALU.mult).then_inc(gate_ready, 1)
            dve.drain()

            def gate_products(e):
                for c in range(C):
                    j = e * C + c
                    dve.wait_ge(silu_done, j + 1)
                    dve.wait_ge(hid_done, 4 * (j + 1))
                    nc.vector.tensor_tensor(hT[:, e % 2, c, :], hid[1][:], silu[:], ALU.mult).then_inc(h_ready, 1)

            def mix_in(e):
                dve.wait_ge(mix_done, e + 1)
                if e == E:
                    nc.vector.tensor_tensor(acc[:], mix[:], acc[:], ALU.add)
                    return
                weight = over_last(gate[:, :, e], D)
                if e == 0:
                    nc.vector.tensor_tensor(acc[:], mix[:], weight, ALU.mult).then_inc(mix_used, 1)
                else:
                    nc.vector.tensor_tensor(gated[:], mix[:], weight, ALU.mult).then_inc(mix_used, 1)
                    dve.drain()
                    nc.vector.tensor_tensor(acc[:], acc[:], gated[:], ALU.add)
                dve.drain()

            if swiglu:
                gate_products(0)
            for e in range(E):
                if swiglu and e + 1 < E:
                    gate_products(e + 1)
                mix_in(e)
            if not swiglu:
                mix_in(E)
                dve.drain()
            nc.vector.tensor_tensor(lat[:], lat[:], acc[:], ALU.add)


def turn_tiles_pe(nc, pe, ident, source, banks, ready, ready_at, turned):
    pe.wait_ge(ready, ready_at)
    for t in range(source.shape[1]):
        turn = nc.tensor.transpose(banks[t // 4][:, (t % 4) * P:(t % 4 + 1) * P], source[:, t, :], ident)
        if t % 4 == 3:
            turn.then_inc(turned, 1)


def keep_turned_act(nc, act, out, banks, turned, turned_at, kept, scale=None, bias=None):
    for half in range(len(banks)):
        act.wait_ge(turned, turned_at + half)
        dst = out[:, half * BANK:(half + 1) * BANK]
        if scale is None:
            nc.scalar.copy(dst, banks[half][:]).then_inc(kept, 1)
        else:
            nc.scalar.activation(dst, banks[half][:], ACT.Identity, bias=bias, scale=scale).then_inc(kept, 1)


def column(ap):
    return ap.rearrange("(p a) -> p a", a=1)


def mlstm_stage(core, name, w):
    nc, lat = core.nc, core.lat
    NH, DQK, DV, CAP = 8, 8, 16, 15.0
    HC = 2 * DQK + DV + 2
    Q, K, V, IG, FG = 0, DQK, 2 * DQK, HC - 2, HC - 1
    with ExitStack() as ctx:
        s = Stage(nc, ctx, name)
        y, square, yT = s.sb("y", [P, TILES, D]), s.sb("square", [P, TILES, D]), s.sb("yT", [P, TOKENS])
        stats = s.sb("stats", [P, 4, TILES])
        wq_rows, wk_rows, wv_rows = s.sb("wq_rows", [NH * DQK, D]), s.sb("wk_rows", [NH * DQK, D]), s.sb("wv_rows", [D, D])
        wi_rows, wf_rows = s.sb("wi_rows", [NH, D]), s.sb("wf_rows", [NH, D])
        wog_rows, wout_rows = s.sb("wog_rows", [D, D]), s.sb("wout_rows", [D, D])
        gate_bias = s.sb("gate_bias", [P, 2, NH])
        gain, shift = s.sb("gain", [P, D]), s.sb("shift", [P, D])
        headsT = s.sb("headsT", [D, NH, HC])
        wogT, woutT = s.sb("wogT", [D, D]), s.sb("woutT", [D, D])
        proj = s.sb("proj", [P, TILES, NH, HC])
        out_gate = s.sb("out_gate", [P, TILES, D])
        seq = s.sb("seq", [P, SEQ, HC])
        peak = s.sb("peak", [P, 1 + SEQ])
        decay = s.sb("decay", [P, 3, SEQ])
        decay_v = s.sb("decay_v", [P, DV, SEQ])
        k_in, q_scaled, n_mem = s.sb("k_in", [P, DQK, SEQ]), s.sb("q_scaled", [P, DQK, SEQ]), s.sb("n_mem", [P, DQK, SEQ])
        memory = s.sb("memory", [P, DQK, DV, SEQ])
        num, den = s.sb("num", [P, DV, SEQ]), s.sb("den", [P, 2, SEQ])
        h_seq, h_tok = s.sb("h_seq", [P, SEQ, DV]), s.sb("h_tok", [P, TILES, D])
        hT = s.sb("hT", [P, TOKENS])
        bank = [s.ps(f"bank{i}", [P, BANK]) for i in range(8)]
        seq_dram = nc.dram_tensor(f"{name}_seq_rows", (TOKENS, NH * HC), F32, kind="Internal").ap()
        h_dram = nc.dram_tensor(f"{name}_h_rows", (BATCHES, SEQ, NH, DV), F32, kind="Internal").ap()

        loaded, var_ready, std_ready = s.sem("loaded"), s.sem("var_ready"), s.sem("std_ready")
        y_ready, y_turned, yT_kept = s.sem("y_ready"), s.sem("y_turned"), s.sem("yT_kept")
        w_turned, w_kept = s.sem("w_turned"), s.sem("w_kept")
        proj_done, proj_kept, og_done = s.sem("proj_done"), s.sem("proj_kept"), s.sem("og_done")
        biased, capped, gates_ready = s.sem("biased"), s.sem("capped"), s.sem("gates_ready")
        seq_stored, seq_loaded = s.sem("seq_stored"), s.sem("seq_loaded")
        exponents, exps_done = s.sem("exponents"), s.sem("exps_done")
        h_ready, h_stored, h_loaded = s.sem("h_ready"), s.sem("h_stored"), s.sem("h_loaded")
        og_ready, h_gated, h_turned, hT_kept, out_done = (s.sem("og_ready"), s.sem("h_gated"), s.sem("h_turned"),
                                                          s.sem("hT_kept"), s.sem("out_done"))
        LOADS = 11
        block = s.block()

        @block.sync
        def _(sp):
            for dst, src in ((wq_rows, "Wq"), (wk_rows, "Wk"), (wv_rows, "Wv"), (wi_rows, "Wi"), (wf_rows, "Wf"),
                             (wog_rows, "Wog"), (wout_rows, "Wout")):
                sp.dma_start(dst[:], w[src]).then_inc(loaded, 16)
            sp.dma_start(gate_bias[:, 0, :], w["bi"].partition_broadcast(P)).then_inc(loaded, 16)
            sp.dma_start(gate_bias[:, 1, :], w["bf"].partition_broadcast(P)).then_inc(loaded, 16)
            sp.dma_start(gain[:], w["ln_w"].partition_broadcast(P)).then_inc(loaded, 16)
            sp.dma_start(shift[:], w["ln_b"].partition_broadcast(P)).then_inc(loaded, 16)
            sp.wait_ge(gates_ready, 1)
            sp.dma_start(seq_dram.rearrange("(t p) c -> p t c", p=P), proj[:].rearrange("p t h c -> p t (h c)"))\
                .then_inc(seq_stored, 16)
            sp.wait_ge(seq_stored, 16)
            for b in range(BATCHES):
                sp.dma_start(seq[b * NH:(b + 1) * NH], seq_dram[b * SEQ:(b + 1) * SEQ].rearrange("t (h c) -> h t c", c=HC))\
                    .then_inc(seq_loaded, 16)
            sp.wait_ge(h_ready, 1)
            for b in range(BATCHES):
                sp.dma_start(h_dram[b].rearrange("t h v -> h t v"), h_seq[b * NH:(b + 1) * NH]).then_inc(h_stored, 16)
            sp.wait_ge(h_stored, 16 * BATCHES)
            sp.dma_start(h_tok[:], h_dram.rearrange("(t b) i h v -> (b i) t (h v)", b=2)).then_inc(h_loaded, 16)

        @block.tensor
        def _(pe):
            pe.wait_ge(loaded, 16 * LOADS)
            at = 0
            for rows in (wq_rows, wk_rows, wv_rows, wi_rows, wf_rows):
                n = rows.shape[0]
                turn = nc.tensor.transpose(bank[2][:, at:at + n], rows[:], core.ident[0:n, 0:n])
                at += n
            turn.then_inc(w_turned, 1)
            nc.tensor.transpose(bank[3][:, 0:D], wog_rows[:], core.ident[:])
            nc.tensor.transpose(bank[3][:, D:2 * D], wout_rows[:], core.ident[:]).then_inc(w_turned, 1)
            turn_tiles_pe(nc, pe, core.ident[:], y[:], bank[0:2], y_ready, 1, y_turned)
            pe.wait_ge(w_kept, 2)
            pe.wait_ge(yT_kept, 2)
            heads = headsT[:].rearrange("d h c -> d (h c)")
            for t in range(TILES):
                if t >= 4:
                    pe.wait_ge(proj_kept, t - 3)
                nc.tensor.matmul(bank[4 + t % 4][:, 0:NH * HC], yT[:, t * P:(t + 1) * P], heads, start=True, stop=True)\
                    .then_inc(proj_done, 1)
            for t in range(TILES):
                mm = nc.tensor.matmul(bank[t // 4][:, (t % 4) * D:(t % 4 + 1) * D], yT[:, t * P:(t + 1) * P], wogT[:],
                                      start=True, stop=True)
            mm.then_inc(og_done, 1)
            turn_tiles_pe(nc, pe, core.ident[:], h_tok[:], bank[2:4], h_gated, 1, h_turned)
            pe.wait_ge(hT_kept, 2)
            for t in range(TILES):
                mm = nc.tensor.matmul(bank[4 + t // 4][:, (t % 4) * D:(t % 4 + 1) * D], hT[:, t * P:(t + 1) * P], woutT[:],
                                      start=True, stop=True)
            mm.then_inc(out_done, 1)

        @block.scalar
        def _(act):
            act.wait_ge(w_turned, 2)
            at = 0
            for c, n in ((Q, DQK), (K, DQK), (V, DV), (IG, 1), (FG, 1)):
                last = nc.scalar.copy(headsT[:, :, c:c + n], bank[2][:, at:at + NH * n].rearrange("d (h c) -> d h c", c=n))
                at += NH * n
            last.then_inc(w_kept, 1)
            nc.scalar.copy(wogT[:], bank[3][:, 0:D])
            nc.scalar.copy(woutT[:], bank[3][:, D:2 * D]).then_inc(w_kept, 1)
            normalize_act(nc, act, core.eps(EPS_5), TILES, D, stats, var_ready, std_ready, 1)
            keep_turned_act(nc, act, yT, bank[0:2], y_turned, 1, yT_kept)
            for t in range(TILES):
                act.wait_ge(proj_done, t + 1)
                nc.scalar.copy(proj[:, t].rearrange("p h c -> p (h c)"), bank[4 + t % 4][:, 0:NH * HC])\
                    .then_inc(proj_kept, 1)
            act.wait_ge(biased, 1)
            nc.scalar.activation(proj[:, :, :, IG:HC], proj[:, :, :, IG:HC], ACT.Tanh, scale=1.0 / CAP)\
                .then_inc(capped, 1)
            act.wait_ge(og_done, 1)
            for half in range(2):
                last = nc.scalar.activation(out_gate[:, 4 * half:4 * half + 4, :],
                                            bank[half][:].rearrange("p (t d) -> p t d", d=D), ACT.Sigmoid)
            last.then_inc(og_ready, 1)
            act.wait_ge(exponents, 1)
            nc.scalar.activation(decay[:], decay[:], ACT.Exp).then_inc(exps_done, 1)
            normalize_act(nc, act, core.eps(EPS_6), TILES, D, stats, var_ready, std_ready, 2)
            keep_turned_act(nc, act, hT, bank[2:4], h_turned, 1, hT_kept)

        @block.vector
        def _(dve):
            normalize_dve(nc, dve, y[:], lat[:], square[:], stats, var_ready, std_ready, 1).then_inc(y_ready, 1)
            dve.wait_ge(loaded, 16 * LOADS)
            dve.wait_ge(proj_kept, TILES)
            for n, c in enumerate((IG, FG)):
                last = nc.vector.tensor_tensor(proj[:, :, :, c], proj[:, :, :, c], over_tiles(gate_bias[:, n, :], TILES),
                                               ALU.add)
            last.then_inc(biased, 1)
            dve.wait_ge(capped, 1)
            nc.vector.tensor_scalar(proj[:, :, :, IG:HC], proj[:, :, :, IG:HC], CAP, None, ALU.mult).then_inc(gates_ready, 1)
            dve.wait_ge(seq_loaded, 16 * BATCHES)
            i_gate, f_gate = seq[:, :, IG], seq[:, :, FG]
            nc.vector.memset(peak[:, 0:1], 0.0)
            nc.vector.tensor_tensor_scan(peak[:, 1:], f_gate, i_gate, 0.0, ALU.add, ALU.max)
            dve.drain()
            nc.vector.tensor_tensor(decay[:, 0, :], f_gate, peak[:, 0:SEQ], ALU.add)
            dve.drain()
            nc.vector.tensor_tensor(decay[:, 0, :], decay[:, 0, :], peak[:, 1:], ALU.subtract)
            nc.vector.tensor_tensor(decay[:, 1, :], i_gate, peak[:, 1:], ALU.subtract)
            nc.vector.tensor_scalar(decay[:, 2, :], peak[:, 1:], -1.0, None, ALU.mult).then_inc(exponents, 1)
            by_k = seq[:, :, K:K + DQK].rearrange("p t k -> p k t")
            by_q = seq[:, :, Q:Q + DQK].rearrange("p t k -> p k t")
            by_v = seq[:, :, V:V + DV].rearrange("p t v -> p v t")
            nc.vector.tensor_scalar(q_scaled[:], by_q, DQK ** -0.5, None, ALU.mult)
            dve.wait_ge(exps_done, 1)
            nc.vector.tensor_copy(decay_v[:], over_tiles(decay[:, 0, :], DV))
            nc.vector.tensor_tensor(k_in[:], by_k, over_tiles(decay[:, 1, :], DQK), ALU.mult)
            dve.drain()
            nc.vector.memset(decay_v[:, :, 0:1], 0.0)
            shape = [P, DQK, DV, SEQ]
            nc.vector.tensor_tensor(memory[:], k_in[:].unsqueeze(2).to_broadcast(shape),
                                    by_v.unsqueeze(1).to_broadcast(shape), ALU.mult)
            dve.drain()
            flat = "p a t -> p (a t)"
            nc.vector.tensor_tensor_scan(n_mem[:].rearrange(flat), decay_v[:, 0:DQK, :].rearrange(flat),
                                         k_in[:].rearrange(flat), 0.0, ALU.mult, ALU.add)
            for k in range(DQK):
                nc.vector.tensor_tensor_scan(memory[:, k].rearrange(flat), decay_v[:].rearrange(flat),
                                             memory[:, k].rearrange(flat), 0.0, ALU.mult, ALU.add)
            dve.drain()
            nc.vector.tensor_tensor(n_mem[:], n_mem[:], q_scaled[:], ALU.mult)
            nc.vector.tensor_tensor(memory[:], memory[:], q_scaled[:].unsqueeze(2).to_broadcast(shape), ALU.mult)
            dve.drain()
            nc.vector.tensor_reduce(den[:, 0, :], n_mem[:].rearrange("p k t -> p t k"), AX, ALU.add)
            nc.vector.tensor_reduce(num[:], memory[:].rearrange("p k v t -> p v t k"), AX, ALU.add)
            dve.drain()
            nc.vector.scalar_tensor_tensor(den[:, 1, :], den[:, 0, :], -1.0, den[:, 0, :], ALU.mult, ALU.max)
            dve.drain()
            nc.vector.tensor_tensor(den[:, 0, :], den[:, 1, :], decay[:, 2, :], ALU.max)
            dve.drain()
            nc.vector.tensor_scalar(den[:, 0, :], den[:, 0, :], 1e-6, None, ALU.add)
            dve.drain()
            nc.vector.reciprocal(den[:, 1, :], den[:, 0, :])
            dve.drain()
            nc.vector.tensor_tensor(h_seq[:].rearrange("p t v -> p v t"), num[:], over_tiles(den[:, 1, :], DV), ALU.mult)\
                .then_inc(h_ready, 1)
            dve.wait_ge(h_loaded, 16)
            normalize_dve(nc, dve, h_tok[:], h_tok[:], square[:], stats, var_ready, std_ready, 2)
            dve.drain()
            nc.vector.tensor_tensor(h_tok[:], h_tok[:], over_tiles(gain[:], TILES), ALU.mult)
            dve.drain()
            nc.vector.tensor_tensor(h_tok[:], h_tok[:], over_tiles(shift[:], TILES), ALU.add)
            dve.drain()
            dve.wait_ge(og_ready, 1)
            nc.vector.tensor_tensor(h_tok[:], h_tok[:], out_gate[:], ALU.mult).then_inc(h_gated, 1)
            dve.wait_ge(out_done, 1)
            for half in range(2):
                part = lat[:, 4 * half:4 * half + 4, :]
                nc.vector.tensor_tensor(part, part, bank[4 + half][:].rearrange("p (t d) -> p t d", d=D), ALU.add)


def causal_exp_stage(core, name, w):
    nc, lat = core.nc, core.lat
    INNER = 16
    with ExitStack() as ctx:
        s = Stage(nc, ctx, name)
        y, square, yT = s.sb("y", [P, TILES, D]), s.sb("square", [P, TILES, D]), s.sb("yT", [P, TOKENS])
        stats = s.sb("stats", [P, 4, TILES])
        rows = s.sb("rows", [P, 2, D])
        wT = s.sb("wT", [P, 2 * D])
        angle = s.sb("angle", [P, 2, D])
        turn16 = s.sb("turn16", [P, 2, D], BF16)
        ident16 = s.sb("ident16", [P, P], BF16)
        causal = s.sb("causal", [P, SEQ])
        fc1 = s.sb("fc1", [P, 2, INNER])
        fc2_rows = s.sb("fc2_rows", [D, INNER])
        fc2T = s.sb("fc2T", [INNER, D])
        fc2_b = s.sb("fc2_b", [P, D])
        qk = s.sb("qk", [P, TILES * 2, D], BF16)
        along = s.sb("along", [P, TILES * 2, D], BF16)
        across = s.sb("across", [P, TILES * 2, D], BF16)
        qkT = s.sb("qkT", [P, TILES * 2, P], BF16)
        exps = s.sb("exps", [P, TILES, SEQ])
        total = s.sb("total", [P, TILES])
        hidden = s.sb("hidden", [P, TILES, INNER])
        hiddenT = s.sb("hiddenT", [INNER, TOKENS])
        bank = [s.ps(f"bank{i}", [P, BANK]) for i in range(6)]
        bank16 = [s.ps(f"bank16_{i}", [P, 8 * P], BF16) for i in range(2)]

        loaded, var_ready, std_ready = s.sem("loaded"), s.sem("var_ready"), s.sem("std_ready")
        y_ready, y_turned, yT_kept = s.sem("y_ready"), s.sem("y_turned"), s.sem("yT_kept")
        w_turned, w_kept, consts_ready = s.sem("w_turned"), s.sem("w_kept"), s.sem("consts_ready")
        qk_done, qk_rounded, qk_turned_by_pos = s.sem("qk_done"), s.sem("qk_rounded"), s.sem("qk_turned_by_pos")
        qk_turned, qkT_kept, scores_done, exps_done = (s.sem("qk_turned"), s.sem("qkT_kept"), s.sem("scores_done"),
                                                       s.sem("exps_done"))
        hidden_ready, hidden_turned, hiddenT_kept, out_done = (s.sem("hidden_ready"), s.sem("hidden_turned"),
                                                               s.sem("hiddenT_kept"), s.sem("out_done"))
        LOADS = 8
        block = s.block()

        @block.sync
        def _(sp):
            for dst, src in ((rows[:, 0, :], w["Wq"]), (rows[:, 1, :], w["Wk"]), (fc2_rows[:], w["fc2_w"]),
                             (angle[:], core.w["c_rope32"]), (causal[:], core.w["c_causal"]),
                             (fc1[:, 0, :], w["fc1_w"].rearrange("n a -> (n a)").partition_broadcast(P)),
                             (fc1[:, 1, :], w["fc1_b"].partition_broadcast(P)),
                             (fc2_b[:], w["fc2_b"].partition_broadcast(P))):
                sp.dma_start(dst, src).then_inc(loaded, 16)

        @block.tensor
        def _(pe):
            pe.wait_ge(loaded, 16 * LOADS)
            for n in range(2):
                nc.tensor.transpose(bank[2][:, n * D:(n + 1) * D], rows[:, n, :], core.ident[:])
            nc.tensor.transpose(bank[3][0:INNER, 0:D], fc2_rows[:], core.ident[:]).then_inc(w_turned, 1)
            turn_tiles_pe(nc, pe, core.ident[:], y[:], bank[0:2], y_ready, 1, y_turned)
            pe.wait_ge(w_kept, 1)
            pe.wait_ge(yT_kept, 2)
            for t in range(TILES):
                mm = nc.tensor.matmul(bank[2 + t // 2][:, (t % 2) * 2 * D:(t % 2 + 1) * 2 * D], yT[:, t * P:(t + 1) * P],
                                      wT[:], start=True, stop=True)
                if t % 2:
                    mm.then_inc(qk_done, 1)
            pe.wait_ge(qk_turned_by_pos, 1)
            for n in range(2 * TILES):
                turn = nc.tensor.transpose(bank16[n // 8][:, (n % 8) * P:(n % 8 + 1) * P], qk[:, n, :], ident16[:])
                if n % 8 == 7:
                    turn.then_inc(qk_turned, 1)
            pe.wait_ge(qkT_kept, 2)
            for b in range(BATCHES):
                t, rows_of = b // 2, slice((b % 2) * SEQ, (b % 2 + 1) * SEQ)
                mm = nc.tensor.matmul(bank[0][rows_of, t * SEQ:(t + 1) * SEQ], qkT[:, 2 * t, rows_of],
                                      qkT[:, 2 * t + 1, rows_of], start=True, stop=True)
            mm.then_inc(scores_done, 1)
            pe.wait_ge(hidden_ready, 1)
            for t in range(TILES):
                turn = nc.tensor.transpose(bank[2 + t // 4][0:INNER, (t % 4) * P:(t % 4 + 1) * P], hidden[:, t, :],
                                           core.ident[:])
            turn.then_inc(hidden_turned, 1)
            pe.wait_ge(hiddenT_kept, 2)
            for t in range(TILES):
                mm = nc.tensor.matmul(bank[4 + t // 4][:, (t % 4) * D:(t % 4 + 1) * D], hiddenT[:, t * P:(t + 1) * P],
                                      fc2T[:], start=True, stop=True)
            mm.then_inc(out_done, 1)

        @block.scalar
        def _(act):
            act.wait_ge(w_turned, 1)
            nc.scalar.copy(wT[:], bank[2][:, 0:2 * D])
            nc.scalar.copy(fc2T[:], bank[3][0:INNER, 0:D]).then_inc(w_kept, 1)
            normalize_act(nc, act, core.eps(EPS_5), TILES, D, stats, var_ready, std_ready, 1)
            keep_turned_act(nc, act, yT, bank[0:2], y_turned, 1, yT_kept)
            for k in range(TILES // 2):
                act.wait_ge(qk_done, k + 1)
                nc.scalar.copy(qk[:, 4 * k:4 * k + 4, :], bank[2 + k][:].rearrange("p (n d) -> p n d", d=D))\
                    .then_inc(qk_rounded, 1)
            for half in range(2):
                act.wait_ge(qk_turned, half + 1)
                nc.scalar.copy(qkT[:, 8 * half:8 * half + 8, :], bank16[half][:].rearrange("p (n q) -> p n q", q=P))\
                    .then_inc(qkT_kept, 1)
            act.wait_ge(scores_done, 1)
            nc.scalar.activation(exps[:], bank[0][:].rearrange("p (t j) -> p t j", j=SEQ), ACT.Exp, scale=D ** -0.5)\
                .then_inc(exps_done, 1)
            act.wait_ge(hidden_turned, 1)
            for half in range(2):
                nc.scalar.copy(hiddenT[:, half * BANK:(half + 1) * BANK], bank[2 + half][0:INNER, :])\
                    .then_inc(hiddenT_kept, 1)

        @block.vector
        def _(dve):
            normalize_dve(nc, dve, y[:], lat[:], square[:], stats, var_ready, std_ready, 1).then_inc(y_ready, 1)
            dve.wait_ge(loaded, 16 * LOADS)
            nc.vector.tensor_copy(turn16[:], angle[:])
            nc.vector.tensor_copy(ident16[:], core.ident[:])
            dve.drain()
            half = D // 2
            dve.wait_ge(qk_rounded, TILES // 2)
            nc.vector.tensor_tensor(along[:], qk[:], over_tiles(turn16[:, 0, :], 2 * TILES), ALU.mult)
            nc.vector.tensor_tensor(across[:, :, 0:half], qk[:, :, half:D], over_tiles(turn16[:, 1, 0:half], 2 * TILES),
                                    ALU.mult)
            nc.vector.tensor_tensor(across[:, :, half:D], qk[:, :, 0:half], over_tiles(turn16[:, 1, half:D], 2 * TILES),
                                    ALU.mult)
            dve.drain()
            nc.vector.tensor_tensor(qk[:], along[:], across[:], ALU.add).then_inc(qk_turned_by_pos, 1)
            dve.wait_ge(exps_done, 1)
            nc.vector.tensor_tensor(exps[:], exps[:], over_tiles(causal[:], TILES), ALU.mult)
            dve.drain()
            nc.vector.tensor_reduce(total[:], exps[:], AX, ALU.add)
            dve.drain()
            nc.vector.tensor_tensor(hidden[:], over_last(total[:], INNER), over_tiles(fc1[:, 0, :], TILES), ALU.mult)
            dve.drain()
            nc.vector.tensor_tensor(hidden[:], hidden[:], over_tiles(fc1[:, 1, :], TILES), ALU.add)
            dve.drain()
            nc.vector.tensor_scalar(hidden[:], hidden[:], 0.0, None, ALU.max).then_inc(hidden_ready, 1)
            dve.wait_ge(out_done, 1)
            nc.vector.tensor_tensor(lat[:], lat[:], over_tiles(fc2_b[:], TILES), ALU.add)
            dve.drain()
            for h in range(2):
                part = lat[:, 4 * h:4 * h + 4, :]
                nc.vector.tensor_tensor(part, part, bank[4 + h][:].rearrange("p (t d) -> p t d", d=D), ALU.add)


def projected_mlp_stage(core, name, w):
    nc, lat = core.nc, core.lat
    HID = 512
    C = HID // P
    with ExitStack() as ctx:
        s = Stage(nc, ctx, name)
        x, z, square, zT = (s.sb("x", [P, TILES, D]), s.sb("z", [P, TILES, D]), s.sb("square", [P, TILES, HID]),
                            s.sb("zT", [P, TOKENS]))
        stats = s.sb("stats", [P, 4, TILES])
        proj_rows, fc1_rows, fc2_rows = s.sb("proj_rows", [P, D]), s.sb("fc1_rows", [P, C, D]), s.sb("fc2_rows", [P, HID])
        projT, fc1T, fc2T = s.sb("projT", [P, D]), s.sb("fc1T", [P, HID]), s.sb("fc2T", [P, C, D])
        row = {n: s.sb(n, [P, D]) for n in ("proj_b", "gamma1", "gamma2", "fc2_b")}
        fc1_b = s.sb("fc1_b", [P, HID])
        cols = s.sb("cols", [P, 4 + 2 * C])
        hid = s.sb("hid", [P, TILES, HID])
        hidT = s.sb("hidT", [P, 2, C, P])
        bank = [s.ps(f"bank{i}", [P, BANK]) for i in range(8)]

        loaded, var_ready, std_ready = s.sem("loaded"), s.sem("var_ready"), s.sem("std_ready")
        w_turned, w_kept = s.sem("w_turned"), s.sem("w_kept")
        z_ready, z_turned, zT_kept = s.sem("z_ready"), s.sem("z_turned"), s.sem("zT_kept")
        proj_done, hid_done, hid_biased, gelu_done = s.sem("proj_done"), s.sem("hid_done"), s.sem("hid_biased"), s.sem("gelu_done")
        hid_ready, hid_turned, hidT_kept, out_done = s.sem("hid_ready"), s.sem("hid_turned"), s.sem("hidT_kept"), s.sem("out_done")
        LOADS = 3 + 5 + 4 + 2
        block = s.block()

        @block.sync
        def _(sp):
            sp.dma_start(proj_rows[:], w["proj_w"]).then_inc(loaded, 16)
            sp.dma_start(fc1_rows[:], w["fc1_w"].rearrange("(c p) d -> p c d", p=P)).then_inc(loaded, 16)
            sp.dma_start(fc2_rows[:], w["fc2_w"]).then_inc(loaded, 16)
            for n, dst in row.items():
                sp.dma_start(dst[:], w[n].partition_broadcast(P)).then_inc(loaded, 16)
            sp.dma_start(fc1_b[:], w["fc1_b"].partition_broadcast(P)).then_inc(loaded, 16)
            with nc.allow_non_contiguous_dma("gain columns"):
                for k, n in enumerate(("ln1_g", "ln1_b", "ln2_g", "ln2_b")):
                    sp.dma_start(cols[:, k:k + 1], column(w[n])).then_inc(loaded, 16)
                for k, n in enumerate(("lnh_g", "lnh_b")):
                    sp.dma_start(cols[:, 4 + k * C:4 + (k + 1) * C], w[n].rearrange("(c p) -> p c", p=P)).then_inc(loaded, 16)

        @block.tensor
        def _(pe):
            pe.wait_ge(loaded, 16 * LOADS)
            for c in range(C):
                nc.tensor.transpose(bank[2][:, c * P:(c + 1) * P], fc1_rows[:, c, :], core.ident[:])
            for c in range(C):
                nc.tensor.transpose(bank[3][:, c * P:(c + 1) * P], fc2_rows[:, c * P:(c + 1) * P], core.ident[:])
            nc.tensor.transpose(bank[4][:, 0:D], proj_rows[:], core.ident[:]).then_inc(w_turned, 1)
            turn_tiles_pe(nc, pe, core.ident[:], z[:], bank[0:2], z_ready, 1, z_turned)
            pe.wait_ge(zT_kept, 2)
            pe.wait_ge(w_kept, 1)
            for t in range(TILES):
                mm = nc.tensor.matmul(bank[2 + t // 4][:, (t % 4) * D:(t % 4 + 1) * D], zT[:, t * P:(t + 1) * P], projT[:],
                                      start=True, stop=True)
            mm.then_inc(proj_done, 1)
            turn_tiles_pe(nc, pe, core.ident[:], z[:], bank[0:2], z_ready, 2, z_turned)
            pe.wait_ge(zT_kept, 4)
            for t in range(TILES):
                if t >= 4:
                    pe.wait_ge(hid_biased, t - 3)
                nc.tensor.matmul(bank[4 + t % 4][:], zT[:, t * P:(t + 1) * P], fc1T[:], start=True, stop=True)\
                    .then_inc(hid_done, 1)
            pe.wait_ge(hid_ready, 1)
            for t in range(TILES + 1):
                if t < TILES:
                    if t >= 2:
                        pe.wait_ge(hidT_kept, C * (t - 1))
                    for c in range(C):
                        turn = nc.tensor.transpose(bank[t % 2][:, c * P:(c + 1) * P], hid[:, t, c * P:(c + 1) * P],
                                                   core.ident[:])
                    turn.then_inc(hid_turned, 1)
                if t >= 1:
                    u = t - 1
                    pe.wait_ge(hidT_kept, C * t)
                    for c in range(C):
                        mm = nc.tensor.matmul(bank[2 + u // 4][:, (u % 4) * D:(u % 4 + 1) * D], hidT[:, u % 2, c, :],
                                              fc2T[:, c, :], start=(c == 0), stop=(c == C - 1))
            mm.then_inc(out_done, 1)

        @block.scalar
        def _(act):
            act.wait_ge(w_turned, 1)
            nc.scalar.copy(fc1T[:], bank[2][:])
            nc.scalar.copy(fc2T[:].rearrange("p c d -> p (c d)"), bank[3][:])
            nc.scalar.copy(projT[:], bank[4][:, 0:D]).then_inc(w_kept, 1)
            act.wait_ge(loaded, 16 * LOADS)
            normalize_act(nc, act, core.eps(EPS_5), TILES, D, stats, var_ready, std_ready, 1)
            normalize_act(nc, act, core.eps(EPS_5), TILES, D, stats, var_ready, std_ready, 2)
            keep_turned_act(nc, act, zT, bank[0:2], z_turned, 1, zT_kept, scale=cols[:, 0:1], bias=cols[:, 1:2])
            normalize_act(nc, act, core.eps(EPS_5), TILES, D, stats, var_ready, std_ready, 3)
            keep_turned_act(nc, act, zT, bank[0:2], z_turned, 3, zT_kept, scale=cols[:, 2:3], bias=cols[:, 3:4])
            for t in range(TILES):
                act.wait_ge(hid_biased, t + 1)
                nc.scalar.activation(hid[:, t, :], hid[:, t, :], ACT.Gelu).then_inc(gelu_done, 1)
            normalize_act(nc, act, core.eps(EPS_5), TILES, HID, stats, var_ready, std_ready, 4)
            for t in range(TILES):
                act.wait_ge(hid_turned, t + 1)
                for c in range(C):
                    nc.scalar.activation(hidT[:, t % 2, c, :], bank[t % 2][:, c * P:(c + 1) * P], ACT.Identity,
                                         bias=cols[:, 4 + C + c:5 + C + c], scale=cols[:, 4 + c:5 + c]).then_inc(hidT_kept, 1)

        @block.vector
        def _(dve):
            first = square[:, :, 0:D]
            normalize_dve(nc, dve, x[:], lat[:], first, stats, var_ready, std_ready, 1)
            dve.drain()
            normalize_dve(nc, dve, z[:], x[:], first, stats, var_ready, std_ready, 2).then_inc(z_ready, 1)
            dve.wait_ge(loaded, 16 * LOADS)
            dve.wait_ge(proj_done, 1)
            for half in range(2):
                nc.vector.tensor_tensor(z[:, 4 * half:4 * half + 4, :], bank[2 + half][:].rearrange("p (t d) -> p t d", d=D),
                                        over_tiles(row["proj_b"][:], 4), ALU.add)
            dve.drain()
            nc.vector.tensor_tensor(z[:], z[:], over_tiles(row["gamma1"][:], TILES), ALU.mult)
            dve.drain()
            nc.vector.tensor_tensor(x[:], x[:], z[:], ALU.add)
            dve.drain()
            normalize_dve(nc, dve, z[:], x[:], first, stats, var_ready, std_ready, 3).then_inc(z_ready, 1)
            for t in range(TILES):
                dve.wait_ge(hid_done, t + 1)
                nc.vector.tensor_tensor(hid[:, t, :], bank[4 + t % 4][:], fc1_b[:], ALU.add).then_inc(hid_biased, 1)
            nc.vector.tensor_tensor(lat[:], lat[:], x[:], ALU.add)
            dve.wait_ge(gelu_done, TILES)
            normalize_dve(nc, dve, hid[:], hid[:], square[:], stats, var_ready, std_ready, 4).then_inc(hid_ready, 1)
            dve.wait_ge(out_done, 1)
            for half in range(2):
                nc.vector.tensor_tensor(z[:, 4 * half:4 * half + 4, :], bank[2 + half][:].rearrange("p (t d) -> p t d", d=D),
                                        over_tiles(row["fc2_b"][:], 4), ALU.add)
            dve.drain()
            nc.vector.tensor_tensor(z[:], z[:], over_tiles(row["gamma2"][:], TILES), ALU.mult)
            dve.drain()
            nc.vector.tensor_tensor(lat[:], lat[:], z[:], ALU.add)


def latent_attention_stage(core, name, w):
    nc, lat = core.nc, core.lat
    NH, L, DH, DHE = 16, 64, 8, 4
    KINDS = ("q", "k", "v")
    UP = 3 * DHE
    WIDTH = (UP, UP, DH)
    AT = (0, NH // 2 * UP, NH * UP)
    with ExitStack() as ctx:
        s = Stage(nc, ctx, name)
        y, square, yT = s.sb("y", [P, TILES, D]), s.sb("square", [P, TILES, D]), s.sb("yT", [P, TOKENS])
        stats = s.sb("stats", [P, 4, TILES])
        down = s.sb("down", [P, 3, NH * L])
        downT = s.sb("downT", [P, 3, NH // 2, P])
        up = s.sb("up", [P, 3, UP])
        heads = s.sb("heads", [P, 2, NH, UP])
        headsV = s.sb("headsV", [P, NH, DH])
        wc = s.sb("wc", [P, D])
        angle = s.sb("angle", [P, 2, DHE])
        causal = s.sb("causal", [P, SEQ])
        own_head = s.sb("own_head", [P, NH])
        parity = s.sb("parity", [P, D])
        qk = s.sb("qk", [P, TILES, 2, NH, UP])
        qk_rot = s.sb("qk_rot", [P, TILES, 2, NH, DH])
        turned = s.sb("turned", [P, 2, NH, DHE])
        qT, kT = s.sb("qT", [P, TOKENS]), s.sb("kT", [P, TOKENS])
        y_twice = s.sb("y_twice", [P, BATCHES, 2, SEQ])
        v_diag = s.sb("v_diag", [P, BATCHES, NH, DH])
        k_diag = s.sb("k_diag", [P, 2, NH, SEQ])
        prob = s.sb("prob", [P, 2, NH, SEQ])
        peak, rsum = s.sb("peak", [P, 2, NH]), s.sb("rsum", [P, 2, NH])
        probT = s.sb("probT", [P, 2, NH // 2, P])
        mixed, mixedT = s.sb("mixed", [P, TILES, D]), s.sb("mixedT", [P, TOKENS])
        score = [s.ps(f"score{i}", [P, NH * SEQ]) for i in range(2)]
        bank = [s.ps(f"bank{i}", [P, BANK]) for i in range(4)]

        loaded, var_ready, std_ready = s.sem("loaded"), s.sem("var_ready"), s.sem("std_ready")
        y_ready, y_turned, yT_kept = s.sem("y_ready"), s.sem("y_turned"), s.sem("yT_kept")
        up_ready, down_turned, downT_kept, heads_done, heads_kept = (s.sem("up_ready"), s.sem("down_turned"),
                                                                     s.sem("downT_kept"), s.sem("heads_done"),
                                                                     s.sem("heads_kept"))
        qk_done, qk_kept, rot_ready, rot_turned, rotT_kept = (s.sem("qk_done"), s.sem("qk_kept"), s.sem("rot_ready"),
                                                              s.sem("rot_turned"), s.sem("rotT_kept"))
        twice_ready, v_done, v_kept = s.sem("twice_ready"), s.sem("v_done"), s.sem("v_kept")
        k_spread, score_done, shifted, exp_done, prob_ready = (s.sem("k_spread"), s.sem("score_done"), s.sem("shifted"),
                                                               s.sem("exp_done"), s.sem("prob_ready"))
        prob_turned, probT_kept, mixed_done, mixed_kept = (s.sem("prob_turned"), s.sem("probT_kept"), s.sem("mixed_done"),
                                                           s.sem("mixed_kept"))
        mixed_turned, mixedT_kept, out_done = s.sem("mixed_turned"), s.sem("mixedT_kept"), s.sem("out_done")
        LOADS = 3 + 2 * 5 + 5
        block = s.block()

        @block.sync
        def _(sp):
            for n, kind in enumerate(KINDS):
                sp.dma_start(down[:, n, :], w[f"W{kind}_down"]).then_inc(loaded, 16)
            for half in range(2):
                rows = slice(half * L, (half + 1) * L)
                for n, kind in enumerate("qk"):
                    sp.dma_start(up[rows, n, 0:DHE], w[f"W{kind}_up_c"]).then_inc(loaded, 16)
                    sp.dma_start(up[rows, n, DHE:2 * DHE], w[f"W{kind}_up_e"]).then_inc(loaded, 16)
                sp.dma_start(up[rows, 2, 0:DH], w["Wv_up"]).then_inc(loaded, 16)
            sp.dma_start(wc[:], w["Wc"]).then_inc(loaded, 16)
            sp.dma_start(angle[:], core.w["c_rope4"]).then_inc(loaded, 16)
            sp.dma_start(causal[:], core.w["c_causal_add"]).then_inc(loaded, 16)
            sp.dma_start(own_head[:], core.w["c_own_head"]).then_inc(loaded, 16)
            sp.dma_start(parity[:], core.w["c_parity"]).then_inc(loaded, 16)

        @block.tensor
        def _(pe):
            pe.wait_ge(loaded, 16 * LOADS)
            for j in range(6):
                if j >= 2:
                    pe.wait_ge(downT_kept, j - 1)
                for i in range(4):
                    n, pair = j // 2, (j % 2) * 4 + i
                    turn = nc.tensor.transpose(bank[j % 2][:, i * P:(i + 1) * P], down[:, n, pair * P:(pair + 1) * P],
                                               core.ident[:])
                turn.then_inc(down_turned, 1)
            pe.wait_ge(up_ready, 1)
            pe.wait_ge(downT_kept, 6)
            for parity_of in range(2):
                rows = slice(parity_of * L, (parity_of + 1) * L)
                for n in range(3):
                    for pair in range(NH // 2):
                        mm = nc.tensor.matmul(bank[2 + parity_of][:, AT[n] + pair * WIDTH[n]:AT[n] + (pair + 1) * WIDTH[n]],
                                              downT[rows, n, pair, :], up[rows, n, 0:WIDTH[n]], start=True, stop=True)
                mm.then_inc(heads_done, 1)
            turn_tiles_pe(nc, pe, core.ident[:], y[:], bank[0:2], y_ready, 1, y_turned)
            pe.wait_ge(yT_kept, 2)
            pe.wait_ge(heads_kept, 2)
            for t in range(TILES):
                if t >= 2:
                    pe.wait_ge(qk_kept, t - 1)
                nc.tensor.matmul(bank[2 + t % 2][:, 0:2 * NH * UP], yT[:, t * P:(t + 1) * P],
                                 heads[:].rearrange("p n h c -> p (n h c)"), start=True, stop=True).then_inc(qk_done, 1)
            pe.wait_ge(twice_ready, 1)
            for b in range(BATCHES):
                if b % 4 == 0 and b >= 8:
                    pe.wait_ge(v_kept, b // 4 - 1)
                mm = nc.tensor.matmul(bank[(b // 4) % 2][:, (b % 4) * D:(b % 4 + 1) * D],
                                      y_twice[:, b].rearrange("p n j -> p (n j)"), headsV[:].rearrange("p h d -> p (h d)"),
                                      start=True, stop=True)
                if b % 4 == 3:
                    mm.then_inc(v_done, 1)
            pe.wait_ge(rot_ready, TILES)
            pe.wait_ge(v_kept, 4)
            for j in range(4):
                for i in range(4):
                    t = (j % 2) * 4 + i
                    turn = nc.tensor.transpose(bank[j][:, i * P:(i + 1) * P],
                                               qk_rot[:, t, j // 2].rearrange("p h d -> p (h d)"), core.ident[:])
                turn.then_inc(rot_turned, 1)
            pe.wait_ge(rotT_kept, 4)

            def scores(t):
                if t >= 2:
                    pe.wait_ge(shifted, t - 1)
                for b in (2 * t, 2 * t + 1):
                    pe.wait_ge(k_spread, b + 1)
                    for half in range(2):
                        mm = nc.tensor.matmul(score[t % 2][(b % 2) * SEQ:(b % 2 + 1) * SEQ, half * BANK:(half + 1) * BANK],
                                              qT[:, b * SEQ:(b + 1) * SEQ],
                                              k_diag[:, b % 2].rearrange("p h j -> p (h j)")[:, half * BANK:(half + 1) * BANK],
                                              start=True, stop=True)
                    mm.then_inc(score_done, 1)

            def mix(t):
                pe.wait_ge(prob_ready, t + 1)
                for half in range(2):
                    if t >= 1:
                        pe.wait_ge(probT_kept, 2 * (t - 1) + half + 1)
                    for i in range(4):
                        pair = 4 * half + i
                        turn = nc.tensor.transpose(bank[half][:, i * P:(i + 1) * P],
                                                   prob[:, t % 2].rearrange("p h j -> p (h j)")[:, pair * P:(pair + 1) * P],
                                                   core.ident[:])
                    turn.then_inc(prob_turned, 1)
                pe.wait_ge(probT_kept, 2 * t + 2)
                if t >= 2:
                    pe.wait_ge(mixed_kept, t - 1)
                for b in (2 * t, 2 * t + 1):
                    rows = slice((b % 2) * SEQ, (b % 2 + 1) * SEQ)
                    for pair in range(NH // 2):
                        mm = nc.tensor.matmul(bank[2 + t % 2][rows, pair * 2 * DH:(pair + 1) * 2 * DH],
                                              probT[:, t % 2, pair, rows],
                                              v_diag[:, b, 2 * pair:2 * pair + 2, :].rearrange("p h d -> p (h d)"),
                                              start=True, stop=True)
                mm.then_inc(mixed_done, 1)

            scores(0)
            for t in range(TILES):
                if t + 1 < TILES:
                    scores(t + 1)
                mix(t)
            turn_tiles_pe(nc, pe, core.ident[:], mixed[:], bank[0:2], mixed_kept, TILES, mixed_turned)
            pe.wait_ge(mixedT_kept, 2)
            for t in range(TILES):
                mm = nc.tensor.matmul(bank[2 + t // 4][:, (t % 4) * D:(t % 4 + 1) * D], mixedT[:, t * P:(t + 1) * P], wc[:],
                                      start=True, stop=True)
            mm.then_inc(out_done, 1)

        @block.scalar
        def _(act):
            for j in range(6):
                act.wait_ge(down_turned, j + 1)
                nc.scalar.copy(downT[:, j // 2, (j % 2) * 4:(j % 2) * 4 + 4, :],
                               bank[j % 2][:].rearrange("p (i d) -> p i d", d=P)).then_inc(downT_kept, 1)
            for parity_of in range(2):
                act.wait_ge(heads_done, parity_of + 1)
                for n, dst in enumerate((heads[:, 0], heads[:, 1], headsV[:])):
                    last = nc.scalar.copy(dst.rearrange("p (a r) c -> p r a c", r=2)[:, parity_of],
                                          bank[2 + parity_of][:, AT[n]:AT[n] + NH // 2 * WIDTH[n]]
                                          .rearrange("p (a c) -> p a c", c=WIDTH[n]))
                last.then_inc(heads_kept, 1)
            normalize_act(nc, act, core.eps(EPS_5), TILES, D, stats, var_ready, std_ready, 1)
            keep_turned_act(nc, act, yT, bank[0:2], y_turned, 1, yT_kept)
            act.wait_ge(yT_kept, 2)
            for copy in range(2):
                last = nc.scalar.copy(y_twice[:, :, copy, :], yT[:].rearrange("p (b j) -> p b j", j=SEQ))
            last.then_inc(twice_ready, 1)
            for t in range(TILES):
                act.wait_ge(qk_done, t + 1)
                nc.scalar.copy(qk[:, t].rearrange("p n h c -> p (n h c)"), bank[2 + t % 2][:, 0:2 * NH * UP])\
                    .then_inc(qk_kept, 1)
            for j in range(4):
                act.wait_ge(rot_turned, j + 1)
                nc.scalar.copy((qT if j < 2 else kT)[:, (j % 2) * BANK:(j % 2 + 1) * BANK], bank[j][:]).then_inc(rotT_kept, 1)
            for t in range(TILES):
                act.wait_ge(shifted, t + 1)
                nc.scalar.activation(prob[:, t % 2], prob[:, t % 2], ACT.Exp, scale=DH ** -0.5).then_inc(exp_done, 1)
                for half in range(2):
                    act.wait_ge(prob_turned, 2 * t + half + 1)
                    nc.scalar.copy(probT[:, t % 2, 4 * half:4 * half + 4, :], bank[half][:].rearrange("p (i d) -> p i d", d=P))\
                        .then_inc(probT_kept, 1)
                act.wait_ge(mixed_done, t + 1)
                nc.scalar.copy(mixed[:, t, :], bank[2 + t % 2][:, 0:D]).then_inc(mixed_kept, 1)
            keep_turned_act(nc, act, mixedT, bank[0:2], mixed_turned, 1, mixedT_kept)

        @block.gpsimd
        def _(pool):
            pool.wait_ge(rotT_kept, 4)
            pool.wait_ge(loaded, 16 * LOADS)
            for b in range(BATCHES):
                if b >= 2:
                    pool.wait_ge(score_done, b - 1)
                nc.gpsimd.tensor_tensor(k_diag[:, b % 2], over_tiles(kT[:, b * SEQ:(b + 1) * SEQ], NH),
                                        over_last(own_head[:], SEQ), ALU.mult).then_inc(k_spread, 1)

        @block.vector
        def _(dve):
            dve.wait_ge(loaded, 16 * LOADS)
            pairs = up[:, 0:2, DHE:2 * DHE].rearrange("p n (a b) -> p n a b", b=2)
            partner = up[:, 0:2, 2 * DHE:UP].rearrange("p n (a b) -> p n a b", b=2)
            nc.vector.tensor_scalar(partner[:, :, :, 0], pairs[:, :, :, 1], -1.0, None, ALU.mult)
            nc.vector.tensor_copy(partner[:, :, :, 1], pairs[:, :, :, 0]).then_inc(up_ready, 1)
            normalize_dve(nc, dve, y[:], lat[:], square[:], stats, var_ready, std_ready, 1).then_inc(y_ready, 1)
            for t in range(TILES):
                dve.wait_ge(qk_kept, t + 1)
                cols = qk[:, t].rearrange("p n h c -> p (n h) c")
                out = qk_rot[:, t].rearrange("p n h c -> p (n h) c")
                side = turned[:].rearrange("p n h c -> p (n h) c")
                nc.vector.tensor_copy(out[:, :, 0:DHE], cols[:, :, 0:DHE])
                nc.vector.tensor_tensor(out[:, :, DHE:DH], cols[:, :, DHE:2 * DHE], over_tiles(angle[:, 0, :], 2 * NH), ALU.mult)
                nc.vector.tensor_tensor(side, cols[:, :, 2 * DHE:UP], over_tiles(angle[:, 1, :], 2 * NH), ALU.mult)
                dve.drain()
                nc.vector.tensor_tensor(out[:, :, DHE:DH], out[:, :, DHE:DH], side, ALU.add).then_inc(rot_ready, 1)
                dve.drain()
            for j in range(4):
                dve.wait_ge(v_done, j + 1)
                nc.vector.tensor_tensor(v_diag[:, 4 * j:4 * j + 4].rearrange("p b h d -> p b (h d)"),
                                        bank[j % 2][:].rearrange("p (b c) -> p b c", c=D),
                                        over_tiles(parity[:], 4), ALU.mult).then_inc(v_kept, 1)

            def shift(t):
                dve.wait_ge(score_done, 2 * t + 2)
                rows = prob[:, t % 2]
                nc.vector.tensor_tensor(rows, score[t % 2][:].rearrange("p (h j) -> p h j", j=SEQ),
                                        over_tiles(causal[:], NH), ALU.add)
                dve.drain()
                nc.vector.tensor_reduce(peak[:, t % 2, :], rows, AX, ALU.max)
                dve.drain()
                nc.vector.tensor_tensor(rows, rows, over_last(peak[:, t % 2, :], SEQ), ALU.subtract).then_inc(shifted, 1)

            def normalise(t):
                dve.wait_ge(exp_done, t + 1)
                rows = prob[:, t % 2]
                nc.vector.tensor_reduce(peak[:, t % 2, :], rows, AX, ALU.add)
                dve.drain()
                nc.vector.reciprocal(rsum[:, t % 2, :], peak[:, t % 2, :])
                dve.drain()
                nc.vector.tensor_tensor(rows, rows, over_last(rsum[:, t % 2, :], SEQ), ALU.mult).then_inc(prob_ready, 1)

            shift(0)
            for t in range(TILES):
                normalise(t)
                if t + 1 < TILES:
                    if t >= 1:
                        dve.wait_ge(prob_turned, 2 * t)
                    shift(t + 1)
            dve.wait_ge(out_done, 1)
            for half in range(2):
                part = lat[:, 4 * half:4 * half + 4, :]
                nc.vector.tensor_tensor(part, part, bank[2 + half][:].rearrange("p (t d) -> p t d", d=D), ALU.add)


def gated_recurrence_stage(core, name, w):
    nc, lat = core.nc, core.lat
    STEPS = BATCHES
    NAMES = ("wf", "wi", "wc", "wo", "uf", "ui", "uc", "uo")
    F, I, G = 0, 1, 2
    with ExitStack() as ctx:
        s = Stage(nc, ctx, name)
        y, square, yT = s.sb("y", [P, TILES, D]), s.sb("square", [P, TILES, D]), s.sb("yT", [P, TOKENS])
        stats = s.sb("stats", [P, 4, TILES])
        rows = s.sb("rows", [P, 8, D])
        wT = s.sb("wT", [P, 8, D])
        bias = s.sb("bias", [P, 5])
        state = s.sb("state", [P, SEQ])
        gates = s.sb("gates", [P, 3, SEQ])
        kept, added = s.sb("kept", [P, SEQ]), s.sb("added", [P, SEQ])
        outT = s.sb("outT", [P, TOKENS])
        bank = [s.ps(f"bank{i}", [P, BANK]) for i in range(8)]
        gate_bank = (bank[4:7], (bank[7], bank[2], bank[3]))

        loaded, var_ready, std_ready = s.sem("loaded"), s.sem("var_ready"), s.sem("std_ready")
        y_ready, y_turned, yT_kept = s.sem("y_ready"), s.sem("y_turned"), s.sem("yT_kept")
        w_turned, w_kept = s.sem("w_turned"), s.sem("w_kept")
        pre_done, gates_done, state_ready = s.sem("pre_done"), s.sem("gates_done"), s.sem("state_ready")
        out_done, out_kept, out_turned = s.sem("out_done"), s.sem("out_kept"), s.sem("out_turned")
        LOADS = 13
        block = s.block()

        @block.sync
        def _(sp):
            for n, src in enumerate(NAMES):
                sp.dma_start(rows[:, n, :], w[src]).then_inc(loaded, 16)
            with nc.allow_non_contiguous_dma("bias columns"):
                for n, src in enumerate(("bf", "bi", "bc", "bo", "in_c")):
                    sp.dma_start(bias[:, n:n + 1], column(w[src])).then_inc(loaded, 16)

        @block.tensor
        def _(pe):
            pe.wait_ge(loaded, 16 * LOADS)
            for n in range(8):
                turn = nc.tensor.transpose(bank[2 + n // 4][:, (n % 4) * P:(n % 4 + 1) * P], rows[:, n, :], core.ident[:])
            turn.then_inc(w_turned, 1)
            turn_tiles_pe(nc, pe, core.ident[:], y[:], bank[0:2], y_ready, 1, y_turned)
            pe.wait_ge(w_kept, 2)
            pe.wait_ge(yT_kept, 2)

            def token_part(step):
                if step >= 2:
                    pe.wait_ge(gates_done, 3 * (step - 1))
                for gate in (F, I, G):
                    nc.tensor.matmul(gate_bank[step % 2][gate][:, 0:SEQ], wT[:, gate, :], yT[:, step * SEQ:(step + 1) * SEQ],
                                     start=True, stop=False)

            token_part(0)
            for step in range(STEPS):
                if step + 1 < STEPS:
                    token_part(step + 1)
                pe.wait_ge(state_ready, step + 1)
                for gate in (F, I, G):
                    nc.tensor.matmul(gate_bank[step % 2][gate][:, 0:SEQ], wT[:, 4 + gate, :], state[:], start=False, stop=True)\
                        .then_inc(pre_done, 1)
            for half in range(2):
                nc.tensor.matmul(bank[half][:], wT[:, 3, :], yT[:, half * BANK:(half + 1) * BANK], start=True, stop=False)
            pe.wait_ge(state_ready, STEPS + 1)
            for half in range(2):
                nc.tensor.matmul(bank[half][:].rearrange("p (t j) -> p t j", j=SEQ), wT[:, 7, :],
                                 over_tiles(state[:], STEPS // 2), start=False, stop=True).then_inc(out_done, 1)
            for t in range(TILES):
                if t % 4 == 0:
                    pe.wait_ge(out_kept, t // 4 + 1)
                turn = nc.tensor.transpose(bank[2 + t // 4][:, (t % 4) * P:(t % 4 + 1) * P], outT[:, t * P:(t + 1) * P],
                                           core.ident[:])
                if t % 4 == 3:
                    turn.then_inc(out_turned, 1)

        @block.scalar
        def _(act):
            act.wait_ge(w_turned, 1)
            for half in range(2):
                nc.scalar.copy(wT[:, 4 * half:4 * half + 4, :], bank[2 + half][:].rearrange("p (n d) -> p n d", d=D))\
                    .then_inc(w_kept, 1)
            normalize_act(nc, act, core.eps(EPS_5), TILES, D, stats, var_ready, std_ready, 1)
            keep_turned_act(nc, act, yT, bank[0:2], y_turned, 1, yT_kept)
            act.wait_ge(loaded, 16 * LOADS)
            for step in range(STEPS):
                for gate, func in ((F, ACT.Sigmoid), (I, ACT.Sigmoid), (G, ACT.Tanh)):
                    act.wait_ge(pre_done, 3 * step + gate + 1)
                    if step >= 1 and gate == F:
                        act.wait_ge(state_ready, step + 1)
                    nc.scalar.activation(gates[:, gate, :], gate_bank[step % 2][gate][:, 0:SEQ], func, bias=bias[:, gate:gate + 1])\
                        .then_inc(gates_done, 1)
            for half in range(2):
                act.wait_ge(out_done, half + 1)
                nc.scalar.activation(outT[:, half * BANK:(half + 1) * BANK], bank[half][:], ACT.Tanh, bias=bias[:, 3:4])\
                    .then_inc(out_kept, 1)

        @block.vector
        def _(dve):
            normalize_dve(nc, dve, y[:], lat[:], square[:], stats, var_ready, std_ready, 1).then_inc(y_ready, 1)
            dve.wait_ge(loaded, 16 * LOADS)
            nc.vector.tensor_copy(state[:], bias[:, 4:5].to_broadcast([P, SEQ])).then_inc(state_ready, 1)
            dve.drain()
            for step in range(STEPS):
                dve.wait_ge(gates_done, 3 * step + 1)
                nc.vector.tensor_tensor(kept[:], state[:], gates[:, F, :], ALU.mult)
                dve.wait_ge(gates_done, 3 * step + 3)
                nc.vector.tensor_tensor(added[:], gates[:, I, :], gates[:, G, :], ALU.mult)
                dve.drain()
                nc.vector.tensor_tensor(state[:], kept[:], added[:], ALU.add).then_inc(state_ready, 1)
                dve.drain()
            for half in range(2):
                dve.wait_ge(out_turned, half + 1)
                part = lat[:, 4 * half:4 * half + 4, :]
                nc.vector.tensor_tensor(part, part, bank[2 + half][:].rearrange("p (t d) -> p t d", d=D), ALU.add)


class Core:

    def __init__(self, nc, lat, ident, small):
        self.nc, self.lat, self.ident, self.small = nc, lat, ident, small
        self.rank = small[:, 8:16]

    def eps(self, which):
        return self.small[:, which:which + 1]


def constants():
    small = np.zeros((P, 16), np.float32)
    small[:, EPS_5], small[:, EPS_6] = 1e-5, 1e-6
    small[:, 8:16] = np.arange(8, 0, -1)
    position = np.arange(P, dtype=np.float32) % SEQ
    angle = position[:, None] * np.float32(32.0) ** (-np.arange(0, D, 2, dtype=np.float32) / np.float32(D))
    rope32 = np.stack([np.tile(np.cos(angle), 2), np.concatenate([-np.sin(angle), np.sin(angle)], 1)], 1)
    angle = position[:, None] * (1 / np.float32(10000.0) ** (np.arange(0, 4, 2, dtype=np.float32) / np.float32(4)))
    rope4 = np.stack([np.tile(np.cos(angle), 2), np.tile(np.sin(angle), 2)], 1)
    theta = np.arange(CTX, dtype=np.float32)[None, :] * \
        (1 / np.float32(10000.0) ** (np.arange(0, 64, 2, dtype=np.float32) / np.float32(64)))[np.arange(P) % 32][:, None]
    sign = np.where(np.arange(P) < SEQ, 1, -1)[:, None]
    rope64 = np.stack([np.concatenate([np.cos(theta), np.ones((P, SEQ))], 1),
                       np.concatenate([np.sin(theta) * sign, np.zeros((P, SEQ))], 1)])
    earlier = np.arange(SEQ)[None, :] <= position[:, None]
    feature = np.arange(P)
    return {
        "c_ident": np.eye(P, dtype=np.float32), "c_small": small,
        "c_rope32": rope32.astype(np.float32), "c_rope4": rope4.astype(np.float32),
        "c_causal": earlier.astype(np.float32), "c_causal_add": np.where(earlier, 0, -1e30).astype(np.float32),
        "c_rope64": rope64.astype(np.float32),
        "c_own_head": (feature[:, None] // 8 == np.arange(16)[None, :]).astype(np.float32),
        "c_parity": (feature[:, None] // SEQ == feature[None, :] // 8 % 2).astype(np.float32),
    }


def weights(w, stage):
    return {name[len(stage) + 1:]: ap for name, ap in w.items() if name.startswith(stage + "_")}


STAGES = {
    "L0_xattn": lambda core, w: cross_attention_stage(core, "L0_xattn", weights(w, "L0_xattn"), heads=8, scale=1 / 64,
                                                      normed=True, masked=True, out_norm=True),
    "L0_attn": lambda core, w: mlstm_stage(core, "L0_attn", weights(w, "L0_attn")),
    "L0_ffn": lambda core, w: moe_stage(core, "L0_ffn", "relu", w["L0_ffn_Wg"], w["L0_ffn_W1"], w["L0_ffn_b1"],
                                        w["L0_ffn_W2"], w["L0_ffn_b2"]),
    "L1_xattn": lambda core, w: cross_attention_stage(core, "L1_xattn", weights(w, "L1_xattn"), heads=16, scale=1 / 8),
    "L1_attn": lambda core, w: causal_exp_stage(core, "L1_attn", weights(w, "L1_attn")),
    "L1_ffn": lambda core, w: moe_stage(core, "L1_ffn", "swiglu", w["L1_ffn_gate_w"], w["L1_ffn_w12"], None,
                                        w["L1_ffn_w3"], None),
    "L2_xattn": lambda core, w: single_head_stage(core, "L2_xattn", weights(w, "L2_xattn"), heads=1, scale=D ** -0.5,
                                                  single=True),
    "L2_attn": lambda core, w: projected_mlp_stage(core, "L2_attn", weights(w, "L2_attn")),
    "L2_ffn": lambda core, w: moe_stage(core, "L2_ffn", "gelu", w["L2_ffn_Wg"], w["L2_ffn_W1"], w["L2_ffn_b1"],
                                        w["L2_ffn_W2"], w["L2_ffn_b2"], w["L2_ffn_bg"]),
    "L3_xattn": lambda core, w: cross_attention_stage(core, "L3_xattn", weights(w, "L3_xattn"), heads=8, scale=1 / 8,
                                                      normed=True, rotary=True),
    "L3_attn": lambda core, w: latent_attention_stage(core, "L3_attn", weights(w, "L3_attn")),
    "L3_ffn": lambda core, w: gated_recurrence_stage(core, "L3_ffn", weights(w, "L3_ffn")),
}


def build(nc, w, out, stages=tuple(STAGES)):
    with ExitStack() as ctx:
        s = Stage(nc, ctx, "all")
        lat = s.sb("lat", [P, TILES, D])
        ident = s.sb("ident", [P, P])
        small = s.sb("small", [P, 16])
        loaded, stored = s.sem("loaded"), s.sem("stored")
        core = Core(nc, lat, ident, small)
        core.w = w
        core.ctx_hat = nc.dram_tensor("context_normalised", (BATCHES, CTX, D), F32, kind="Internal").ap()
        with nc.Block() as block:
            @block.sync
            def _(sp):
                sp.dma_start(lat[:], w["x"].rearrange("(t b) i d -> (b i) t d", b=2)).then_inc(loaded, 16)
                sp.dma_start(ident[:], w["c_ident"]).then_inc(loaded, 16)
                sp.dma_start(small[:], w["c_small"]).then_inc(loaded, 16)
                sp.wait_ge(loaded, 48)
        for name in stages:
            STAGES[name](core, w)
        with nc.Block() as block:
            @block.sync
            def _(sp):
                sp.dma_start(out.rearrange("(t b) i d -> (b i) t d", b=2), lat[:]).then_inc(stored, 16)
                sp.wait_ge(stored, 16)


def kernel(**inputs):
    import concourse.bacc as bacc
    from concourse.bass_utils import run_bass_kernel_spmd

    nc = bacc.Bacc("TRN2", target_bir_lowering=False, num_devices=1)
    arrays, w = {}, {}
    for name, value in {**inputs, **constants()}.items():
        value = np.ascontiguousarray(value)
        arrays["in_" + name] = value
        w[name] = nc.dram_tensor("in_" + name, value.shape, mybir.dt.from_np(value.dtype), kind="ExternalInput").ap()
    out = nc.dram_tensor("latents_out", (BATCHES, SEQ, D), F32, kind="ExternalOutput").ap()
    build(nc, w, out)
    result = run_bass_kernel_spmd(nc, [arrays], core_ids=[0])
    return result.results[0]["latents_out"]
```

```python
from contextlib import ExitStack

import numpy as np

import concourse.bass as bass
from concourse import mybir

ALU = mybir.AluOpType
ACT = mybir.ActivationFunctionType
AX = mybir.AxisListType.X
F32 = mybir.dt.float32
F32R = mybir.dt.float32r
BF16 = mybir.dt.bfloat16
U8 = mybir.dt.uint8

P = 128
D = 128
BATCHES = 16
SEQ = 64
TILES = BATCHES * SEQ // P
TOKENS = BATCHES * SEQ
CTX = 1601
BANK = 512
EPS_5, EPS_6 = 0, 1


class Stage:

    def __init__(self, nc, ctx, name):
        self.nc, self.ctx, self.name, self.sems = nc, ctx, name, []
        ctx.callback(self.clear)

    def sb(self, name, shape, dtype=F32):
        return self.ctx.enter_context(self.nc.sbuf_tensor(f"{self.name}_{name}", shape, dtype))

    def ps(self, name, shape, dtype=F32):
        return self.ctx.enter_context(self.nc.psum_tensor(f"{self.name}_{name}", shape, dtype))

    def sem(self, name):
        handle = self.nc.alloc_semaphore(name=f"{self.name}_{name}")
        self.sems.append(handle)
        return handle

    def clear(self):
        self.nc.clear_and_free_semaphores(self.sems)
        self.nc.all_engine_barrier()

    def block(self):
        return self.ctx.enter_context(self.nc.Block())


def over_last(ap, width):
    return ap.unsqueeze(2).to_broadcast([ap.shape[0], ap.shape[1], width])


def over_tiles(ap, tiles):
    return ap.unsqueeze(1).to_broadcast([ap.shape[0], tiles, ap.shape[1]])


def normalize_dve(nc, dve, out, src, scratch, stats, var_ready, std_ready, use):
    n = src.shape[1]
    moments, mean_var = scratch[:, :, 0:6], scratch[:, :, 6:8]
    var, std, rstd = (stats[:, k, 0:n] for k in (1, 2, 3))
    for k in range(n):
        nc.vector.bn_stats(moments[:, k, :], src[:, k, :])
    dve.drain()
    for k in range(n):
        nc.vector.bn_aggr(mean_var[:, k, :], moments[:, k, :])
    dve.drain()
    nc.vector.tensor_copy(var, mean_var[:, :, 1]).then_inc(var_ready, 1)
    nc.vector.tensor_tensor(out, src, over_last(mean_var[:, :, 0], src.shape[2]), ALU.subtract)
    dve.wait_ge(std_ready, use)
    nc.vector.reciprocal(rstd, std)
    dve.drain()
    return nc.vector.tensor_tensor(out, out, over_last(rstd, src.shape[2]), ALU.mult)


def normalize_act(nc, act, eps, n, stats, var_ready, std_ready, use):
    act.wait_ge(var_ready, use)
    nc.scalar.activation(stats[:, 2, 0:n], stats[:, 1, 0:n], ACT.Sqrt, bias=eps, scale=1.0).then_inc(std_ready, 1)




class Lane:

    def __init__(self, banks, full, free):
        self.banks, self.full, self.free = banks, full, free
        self.at, self.n, self.turn = 0, 0, 0

    def go_to(self, at, turn):
        self.at, self.n, self.turn = at, 0, turn

    def count(self):
        return self.at + self.n

    def bank(self):
        return self.banks[self.turn % len(self.banks)]

    def next(self):
        self.n += 1
        self.turn += 1


def full_tiles(tiles):
    if tiles[0] < CTX // P:
        return [(tiles[0], len(tiles), P)]
    return [(tiles[0], 1, CTX % P)] + [(k, 1, SEQ) for k in tiles[1:]]


def cross_attention_stage(core, name, w, heads, scale, normed=False, masked=False, rotary=False, out_norm=False):
    nc, lat = core.nc, core.lat
    NH, HD = heads, 64
    R = NH // 2
    GROUPS = R // 2
    GCOLS = 2 * P
    CT = -(-CTX // P)
    TAIL = CTX - (CT - 1) * P
    KEYS = CTX + (SEQ if normed else 0)
    tile_of_keys = [(k * P, min(P, CTX - k * P)) for k in range(CT)] + ([(CTX, SEQ)] if normed else [])
    KT = len(tile_of_keys)
    CHUNKS = [(c * BANK, min(BANK, KEYS - c * BANK)) for c in range(-(-KEYS // BANK))]
    CTX_CHUNKS = [(c * BANK, min(BANK, CTX - c * BANK)) for c in range(-(-CTX // BANK))]
    COLS = KEYS if rotary else KEYS + KEYS % 2
    SCORE_CHUNKS = [(c0, min(BANK, COLS - c0)) for c0, _ in CHUNKS]
    HALVES = [(0, 2 * BANK), (2 * BANK, KEYS - 2 * BANK)]
    QUADS = [list(range(q, min(q + 4, KT))) for q in range(0, KT, 4)]
    PARTS = [range(0, 7), range(7, KT)]
    QJOBS = 1 if rotary else NH // 8
    split_sums = not normed
    CTX_SLOT = R - 2
    QUERY_SLOT = CTX_SLOT - 1 if split_sums else CTX_SLOT
    KEPT_SLOT = 3
    LAST = BATCHES // 2 - 1

    ACT_QUADS, DVE_QUADS = ((0, 2, 3), (1,)) if split_sums else ((0, 2), (1, 3))

    with ExitStack() as ctx, ExitStack() as before_batches:
        s = Stage(nc, ctx, name)
        early_only = Stage(nc, before_batches, name)
        tokens = early_only if split_sums else s
        y, square = tokens.sb("y", [P, TILES, D]), tokens.sb("square", [P, TILES, D])
        wv_rows, wo_rows = early_only.sb("wv_rows", [P, NH * HD]), early_only.sb("wo_rows", [P, R, D])
        wvT = early_only.sb("wvT", [P, R, D])
        if not rotary:
            wq_rows, wk_rows = early_only.sb("wq_rows", [P, NH * HD]), early_only.sb("wk_rows", [P, NH * HD])
            wqT, wkT = early_only.sb("wqT", [P, R, D]), early_only.sb("wkT", [P, R, D])
        before_batches.close()
        if split_sums:
            probT, probT_lo = s.sb("probT", [P, 2, KT, GCOLS], F32R), s.sb("probT_lo", [P, 2, KT, GCOLS], F32R)
            turned_act = s.sb("turned_act", [P, 2, KT, P])
            rows_hi, rows_lo = s.sb("rows_hi", [P, 2, KT, D], F32R), s.sb("rows_lo", [P, 2, KT, D], F32R)
        else:
            probT = s.sb("probT", [P, 2, KT, GCOLS])
        yT = s.sb("yT", [P, TOKENS])
        stats = s.sb("stats", [P, 4, TILES])
        rows = s.sb("rows", [P, 2, KT, D])
        keysT = s.sb("keysT", [P, COLS])
        prob = s.sb("prob", [P, 2, KEYS])
        if rotary:
            queries = s.sb("queries", [P, 2, R * P])
        else:
            queries = s.sb("queries", [P, R * P])
            keys_hi, keys_lo = s.sb("keys_hi", [P, 2, COLS], F32R), s.sb("keys_lo", [P, 2, COLS], F32R)
            queries_hi, queries_lo = s.sb("queries_hi", [P, 2, R * P], F32R), s.sb("queries_lo", [P, 2, R * P], F32R)
        peak, neg_peak = s.sb("peak", [P, 2]), s.sb("neg_peak", [P, 2])
        rsum, rinv = s.sb("rsum", [P, 2]), s.sb("rinv", [P, 2])
        mixed = s.sb("mixed", [P, R * P])
        outT = s.sb("outT", [P, TOKENS])
        if normed:
            xhat = s.sb("xhat", [P, CT, D])
            gained = s.sb("gained", [P, CT, D])
            gains = s.sb("gains", [P, 4, D])
        if masked:
            raw = s.sb("raw", [P, CT, D])
            moments, mean_var = s.sb("moments", [P, CT, 6]), s.sb("mean_var", [P, CT, 2])
            cstd, crstd = s.sb("cstd", [P, CT]), s.sb("crstd", [P, CT])
            mask16 = s.sb("mask16", [P, 2, KEYS], BF16)
            mark = s.sb("mark", [P, 2])
            unmasked = s.sb("unmasked", [P, KEYS])
            mask_u8, mask_all = s.sb("mask_u8", [BATCHES, CTX], U8), s.sb("mask_all", [BATCHES, KEYS], BF16)
            mask_dram = nc.dram_tensor(f"{name}_mask_rows", (BATCHES, KEYS), BF16, kind="Internal").ap()
        if out_norm:
            out_gains = s.sb("out_gains", [P, 2, D])
        fold_vo = s.sb("fold_vo", [P, NH, D])
        if rotary:
            wq, wk = s.sb("wq", [P, R, P]), s.sb("wk", [P, R, P])
            rot_cos, rot_sin = s.sb("rot_cos", [P, KEYS]), s.sb("rot_sin", [P, KEYS])
            unturned = s.sb("unturned", [P, 2, KEYS])
            projected = s.sb("projected", [P, 2, KEYS])
            crossed = s.sb("crossed", [P, KEYS])
        else:
            fold_qk = s.sb("fold_qk", [P, NH, D])
        if "b_o" in w:
            out_bias = s.sb("out_bias", [P, 1])

        score = s.ps("score", [P, 4 * BANK])
        lane_bank = [s.ps(f"lane{i}", [P, BANK]) for i in range(3)]
        sums = s.ps("sums", [P, BANK])

        gains_loaded, w_loaded, late_loaded = s.sem("gains_loaded"), s.sem("w_loaded"), s.sem("late_loaded")
        var_ready, std_ready = s.sem("var_ready"), s.sem("std_ready")
        y_ready, y_turned, yT_kept = s.sem("y_ready"), s.sem("y_turned"), s.sem("yT_kept")
        w_turned, w_kept = s.sem("w_turned"), s.sem("w_kept")
        cleared, ctx_loaded = s.sem("cleared"), s.sem("ctx_loaded")
        if masked:
            mask_ready, mask_stored = s.sem("mask_ready"), s.sem("mask_stored")
            mask_loaded = [s.sem(f"mask_loaded{i}") for i in range(2)]
            raw_used, cvar_ready, cstd_ready, crstd_ready = (s.sem("raw_used"), s.sem("cvar_ready"), s.sem("cstd_ready"),
                                                             s.sem("crstd_ready"))
            xhat_ready, xhat_stored = s.sem("xhat_ready"), s.sem("xhat_stored")
        if normed:
            gained_ready, rows_ready = s.sem("gained_ready"), s.sem("rows_ready")
            own_loaded = [s.sem(f"own_loaded{i}") for i in range(2)]
        else:
            rows_loaded = [s.sem(f"rows_loaded{i}") for i in range(2)]
        if split_sums:
            rows_hi_ready, rows_ready = s.sem("rows_hi_ready"), s.sem("rows_ready")
            probs_hi, probs_lo = s.sem("probs_hi"), s.sem("probs_lo")
        if rotary:
            unturned_ready, crossed_ready, keys_turned = s.sem("unturned_ready"), s.sem("crossed_ready"), s.sem("keys_turned")
        else:
            hi_ready, keys_split, queries_split = s.sem("hi_ready"), s.sem("keys_split"), s.sem("queries_split")
        score_half, peak_ready, exp_done, prob_ready = (s.sem("score_half"), s.sem("peak_ready"), s.sem("exp_done"),
                                                        s.sem("prob_ready"))
        sums_done, sums_kept = s.sem("sums_done"), s.sem("sums_kept")
        act_full, act_free, dve_full, dve_free = s.sem("act_full"), s.sem("act_free"), s.sem("dve_full"), s.sem("dve_free")
        out_turned = s.sem("out_turned")

        ACT_PROJ = len(CHUNKS) if rotary else 0
        ACT_FIRST, DVE_FIRST = 2 + QJOBS + ACT_PROJ, 2
        ACT_BATCH, DVE_BATCH = (len(ACT_QUADS) + ACT_PROJ) * R + 2 + QJOBS + 1, len(DVE_QUADS) * R + 2
        ACT_MISSING, DVE_MISSING = len(ACT_QUADS) + 1, len(DVE_QUADS)

        def lanes():
            return {"A": Lane(lane_bank[0:2], act_full, act_free), "D": Lane(lane_bank[2:3], dve_full, dve_free)}

        def go_to_batch(lane, b, parity, first):
            if first:
                lane["A"].go_to(ACT_FIRST, ACT_FIRST)
                lane["D"].go_to(DVE_FIRST, 0)
            else:
                lane["A"].go_to(ACT_FIRST - ACT_MISSING + ACT_BATCH * b, ACT_FIRST - ACT_MISSING + ACT_BATCH * parity)
                lane["D"].go_to(DVE_FIRST - DVE_MISSING + DVE_BATCH * b, 0)

        def go_to_end(lane):
            for jobs, ln, first, missing, each in ((2 + QJOBS + ACT_PROJ, lane["A"], ACT_FIRST, ACT_MISSING, ACT_BATCH),
                                                   (2, lane["D"], DVE_FIRST, DVE_MISSING, DVE_BATCH)):
                at = first - missing + each * BATCHES - jobs
                ln.go_to(at, at)

        def sums_of_slot(t):
            u = (t - 3) % R
            return (1 if t < 3 else 0), u // 2, u % 2

        def following(pair, parity, t):
            return (pair, parity, t + 1) if t + 1 < R else (pair + parity, 1 - parity, 0)

        def preceding(pair, parity, t):
            return (pair, parity, t - 1) if t else (pair - (1 - parity), 1 - parity, R - 1)

        def tile_number(pair, parity, t):
            return (pair * 2 + parity) * R + t

        loads = {gains_loaded: 0, w_loaded: 0, late_loaded: 0}
        block = s.block()

        def staged(t, j):
            return turned_act[:, t % 2, QUADS[j][0]:QUADS[j][-1] + 1, :]

        @block.sync
        def _(sp):
            def load(dst, src, done):
                sp.dma_start(dst, src).then_inc(done, 16)
                loads[done] += 1

            def move_context(pair, parity, tiles, done, store=False):
                whole = (core.ctx_hat if (rotary or store) else core.w["ctx_1024"])[bass.ds(pair * 2 + parity, 1)]
                whole = whole.rearrange("a n d -> (a n) d")
                for on_chip, in_dram in ((tiles[:, 0:CT - 1, :], whole[0:(CT - 1) * P].rearrange("(k p) d -> p k d", p=P)),
                                         (tiles[0:TAIL, CT - 1, :], whole[(CT - 1) * P:CTX])):
                    if store:
                        sp.dma_start(in_dram, on_chip).then_inc(done, 16)
                    else:
                        sp.dma_start(on_chip, in_dram).then_inc(done, 16)

            def load_own(pair, parity):
                if normed:
                    sp.dma_start(rows[0:SEQ, parity, CT, :], y[parity * SEQ:(parity + 1) * SEQ, bass.ds(pair, 1), :]
                                 .rearrange("p a d -> p (a d)")).then_inc(own_loaded[parity], 16)
                if masked:
                    sp.dma_start(mask16[:, parity, :], mask_dram[bass.ds(pair * 2 + parity, 1)].rearrange("a k -> (a k)")
                                 .partition_broadcast(P)).then_inc(mask_loaded[parity], 16)

            def during(pair, parity, first=False, last=False, no_load=False):
                b = pair * 2 + parity
                after = (pair + parity, 1 - parity)
                if masked:
                    if not no_load:
                        sp.wait_ge(raw_used, b + 2)
                        move_context(pair + 1, parity, raw, ctx_loaded)
                    if not last:
                        sp.wait_ge(xhat_ready, b + 2)
                        move_context(*after, xhat, xhat_stored, store=True)
                if last:
                    return
                if rotary and not no_load:
                    sp.wait_ge(gained_ready, b + 2)
                    move_context(pair + 1, parity, xhat, ctx_loaded)
                if not first:
                    sp.wait_ge(sums_done, GROUPS * b)
                if not normed:
                    move_context(*after, rows[:, 1 - parity], rows_loaded[1 - parity])
                load_own(*after)

            sp.wait_ge(cleared, 1)
            if normed:
                move_context(0, 0, raw if masked else xhat, ctx_loaded)
            else:
                move_context(0, 0, rows[:, 0], rows_loaded[0])
            if masked:
                load(mask_u8[:], core.w["mask_BxS2_bk1"], gains_loaded)
            if normed:
                names = ("ln_x_g", "ln_x_b", "ln_l_g", "ln_l_b") if "ln_x_g" in w else ("gamma_x", "beta_x", "gamma_l", "beta_l")
                for n, src in enumerate(names):
                    load(gains[:, n, :], w[src].partition_broadcast(P), gains_loaded)
            if "Wkv" in w:
                wk_src, wv_src, wo_src = w["Wkv"][:, 0:NH * HD], w["Wkv"][:, NH * HD:2 * NH * HD], w["Wo"]
            else:
                wk_src, wv_src, wo_src = w["W_k"], w["W_v"], w["W_o"]
            if rotary:
                with nc.allow_non_contiguous_dma("head halves"):
                    for dst, src in ((wq, w["Wq"]), (wk, wk_src)):
                        for half in range(2):
                            for h in range(2):
                                at = half * SEQ + h * SEQ // 2
                                load(dst[:, :, at:at + SEQ // 2], src.rearrange("p (t h a d) -> p a h t d", t=R, h=2, a=2)[:, half, h],
                                     w_loaded)
                load(rot_cos[:], core.w["c_rope64"][0], w_loaded)
                load(rot_sin[:], core.w["c_rope64"][1], w_loaded)
            else:
                load(wq_rows[:], w["Wq"] if "Wq" in w else w["W_q"], w_loaded)
                load(wk_rows[:], wk_src, w_loaded)
            load(wv_rows[:], wv_src, late_loaded)
            load(wo_rows[:], wo_src.rearrange("(t p) d -> p t d", p=P), late_loaded)
            if out_norm:
                load(out_gains[:, 0, :], w["ln_o_g"].partition_broadcast(P), late_loaded)
                load(out_gains[:, 1, :], w["ln_o_b"].partition_broadcast(P), late_loaded)
            if "b_o" in w:
                with nc.allow_non_contiguous_dma("bias column"):
                    load(out_bias[:], column(w["b_o"]), late_loaded)
            if masked:
                sp.wait_ge(mask_ready, 1)
                sp.dma_start(mask_dram, mask_all[:]).then_inc(mask_stored, 16)
                sp.wait_ge(mask_stored, 16)
                sp.wait_ge(cleared, 2)
                sp.wait_ge(raw_used, 1)
                move_context(0, 1, raw, ctx_loaded)
                sp.wait_ge(xhat_ready, 1)
                move_context(0, 0, xhat, xhat_stored, store=True)
            if rotary:
                sp.wait_ge(gained_ready, 1)
                move_context(0, 1, xhat, ctx_loaded)
            if normed:
                sp.wait_ge(y_ready, 1)
                load_own(0, 0)
            during(0, 0, first=True)
            during(0, 1)
            with sp.Fori(1, LAST) as pair:
                during(pair, 0)
                during(pair, 1)
            during(LAST, 0, no_load=True)
            if masked:
                sp.wait_ge(xhat_stored, 32 * BATCHES)

        GAINS, LOADS, LATE = (16 * loads[done] for done in (gains_loaded, w_loaded, late_loaded))
        QUADS_OF = R // 4
        QK_JOBS = 0 if rotary else 3 * QUADS_OF
        W_JOBS = QK_JOBS + 2 * QUADS_OF
        early = not masked

        @block.tensor
        def _(pe):
            lane = lanes()

            def turn_weights(sources, before):
                for j in range(len(sources) * QUADS_OF):
                    source, quad = sources[j // QUADS_OF], j % QUADS_OF
                    if j >= 4:
                        pe.wait_ge(w_kept, before + j - 3)
                    for i in range(4):
                        turn = nc.tensor.transpose(score[:, (j % 4) * BANK + i * P:(j % 4) * BANK + (i + 1) * P],
                                                   source[:, (4 * quad + i) * P:(4 * quad + i + 1) * P], core.ident[:])
                    turn.then_inc(w_turned, 1)

            def fold_weights(left, right, before):
                pe.wait_ge(w_kept, before)
                for f in range(QUADS_OF):
                    if f >= 2:
                        pe.wait_ge(w_kept, before + f - 1)
                    for odd in range(2):
                        part = slice(odd * SEQ, (odd + 1) * SEQ)
                        bank = score[:, (2 * (f % 2) + odd) * BANK:(2 * (f % 2) + odd + 1) * BANK]
                        for i in range(4):
                            mm = nc.tensor.matmul(bank[:, i * P:(i + 1) * P], left[part, 4 * f + i, :],
                                                  right[part, 4 * f + i, :], start=True, stop=True)
                    mm.then_inc(w_turned, 1)

            def fill(name):
                ln = lane[name]
                count = ln.count() - len(ln.banks) + 1
                if not isinstance(count, int) or count > 0:
                    pe.wait_ge(ln.free, count)
                return ln.bank()

            def filled(name, ins):
                ins.then_inc(lane[name].full, 1)
                lane[name].next()

            def turn_context(pair, parity, chunks):
                if 0 in chunks:
                    if normed:
                        pe.wait_ge(gained_ready, pair * 2 + parity + 1)
                    else:
                        pe.wait_ge(rows_loaded[parity], 32 * (pair + 1))
                for c in chunks:
                    c0, n = CTX_CHUNKS[c]
                    bank = fill("AD"[c % 2])
                    for k in range(c0 // P, -(-(c0 + n) // P)):
                        size = tile_of_keys[k][1]
                        source = gained[0:size, k, :] if normed else rows[0:size, parity, k, :]
                        turn = nc.tensor.transpose(bank[:, k * P - c0:k * P - c0 + size], source,
                                                   core.ident[0:size, 0:size])
                    filled("AD"[c % 2], turn)

            def make_queries(pair, parity):
                own = yT[:, bass.ds((pair * 2 + parity) * SEQ, SEQ)]
                for job in range(QJOBS):
                    bank = fill("A")
                    for i in range(R if rotary else 8):
                        left = wq[:, i, :] if rotary else fold_qk[:, 8 * job + i, :]
                        mm = nc.tensor.matmul(bank[:, i * SEQ:(i + 1) * SEQ], left, own, start=True, stop=True)
                    filled("A", mm)

            def project(pair, parity, t):
                for c0, n in CHUNKS:
                    filled("A", nc.tensor.matmul(fill("A")[:, 0:n], wk[:, t, :], keysT[:, c0:c0 + n], start=True, stop=True))

            def scores(pair, parity, t, first=False):
                tile = tile_number(pair, parity, t)
                if not first:
                    pe.wait_ge(peak_ready if masked else exp_done, tile)
                own = slice(t * P, (t + 1) * P)
                if not rotary and t == 0:
                    pe.wait_ge(keys_split, pair * 2 + parity + 1)
                    pe.wait_ge(queries_split, pair * 2 + parity + 1)
                for c, (c0, n) in enumerate(SCORE_CHUNKS):
                    cols = slice(c0, c0 + n)
                    if rotary:
                        if c % 2 == 0:
                            pe.wait_ge(keys_turned, 2 * tile + c // 2 + 1)
                        mm = nc.tensor.matmul(score[:, cols], queries[:, parity, own], projected[:, t % 2, cols],
                                              start=True, stop=True)
                    else:
                        nc.tensor.matmul(score[:, cols], queries_hi[:, parity, own], keys_hi[:, parity, cols], start=True, stop=False)
                        nc.tensor.matmul(score[:, cols], queries_hi[:, parity, own], keys_lo[:, parity, cols], start=False, stop=False)
                        mm = nc.tensor.matmul(score[:, cols], queries_lo[:, parity, own], keys_hi[:, parity, cols],
                                              start=False, stop=True)
                    if c in (1, len(CHUNKS) - 1):
                        mm.then_inc(score_half, 1)

            def turn_probs(pair, parity, t, quads):
                if 0 in quads:
                    pe.wait_ge(prob_ready, tile_number(pair, parity, t) + 1)
                for j in quads:
                    name = "A" if j in ACT_QUADS else "D"
                    bank = fill(name)
                    for i, k in enumerate(QUADS[j]):
                        c0, n = tile_of_keys[k]
                        turn = nc.tensor.transpose(bank[0:n, i * P:(i + 1) * P], prob[:, t % 2, c0:c0 + n], core.ident[:])
                    filled(name, turn)

            def sum_context(pair, parity, group, part, turned):
                b = pair * 2 + parity
                if part == 0:
                    for name, count in turned.items():
                        pe.wait_ge(lane[name].free, count)
                    if split_sums:
                        pe.wait_ge(rows_ready, b + 1)
                    if normed:
                        pe.wait_ge(rows_ready, b + 1)
                        pe.wait_ge(own_loaded[parity], 16 * (pair + 1))
                    if not (isinstance(b, int) and b == 0 and group == 0):
                        pe.wait_ge(sums_kept, b * GROUPS + group)
                if split_sums:
                    pe.wait_ge(probs_lo, 3 * tile_number(pair, parity, 2 * group + 1) + (1, 3)[part])
                for k in PARTS[part]:
                    n = tile_of_keys[k][1]
                    probs = probT[0:n, group % 2, k, :]
                    if split_sums:
                        nc.tensor.matmul(sums[:, 0:GCOLS], rows_hi[0:n, parity, k, :], probs, start=(k == 0), stop=False)
                        nc.tensor.matmul(sums[:, 0:GCOLS], rows_lo[0:n, parity, k, :], probs, start=False, stop=False)
                        mm = nc.tensor.matmul(sums[:, 0:GCOLS], rows_hi[0:n, parity, k, :], probT_lo[0:n, group % 2, k, :],
                                              start=False, stop=(k == KT - 1))
                    else:
                        mm = nc.tensor.matmul(sums[:, 0:GCOLS], rows[0:n, parity, k, :], probs,
                                              start=(k == 0), stop=(k == KT - 1))
                if part == 1:
                    mm.then_inc(sums_done, 1)

            def output(pair, parity):
                pe.wait_ge(sums_kept, GROUPS * (pair * 2 + parity + 1))
                bank = fill("A")
                for h in range(NH):
                    mm = nc.tensor.matmul(bank[:, 0:SEQ], fold_vo[:, h, :], mixed[:, h * SEQ:(h + 1) * SEQ],
                                          start=(h == 0), stop=(h == NH - 1))
                filled("A", mm)

            def emptied(counts):
                for name in "AD":
                    pe.wait_ge(lane[name].free, counts[name])

            def prepared(last=False):
                return {name: lane[name].count() for name in "AD"}

            def batch(pair, parity, first=False, last=False):
                go_to_batch(lane, pair * 2 + parity, parity, first)
                before, after = preceding(pair, parity, 0)[0:2], following(pair, parity, R - 1)[0:2]
                turned = prepared()
                for t in range(R):
                    if rotary and t < R - 1:
                        project(*following(pair, parity, t))
                    scores(pair, parity, t, first and t == 0)
                    if rotary and t == R - 1 and not last:
                        emptied(keys_kept)
                        project(*after, 0)
                    if not (first and t == 0):
                        turn_probs(*preceding(pair, parity, t), (0, 1, 2))
                    prepares = t == CTX_SLOT and not last
                    if prepares:
                        turn_context(*after, (0, 2))
                    back, group, part = sums_of_slot(t)
                    if not (first and back):
                        sum_context(*(before if back else (pair, parity)), group, part, turned)
                    if prepares:
                        turn_context(*after, (1,))
                    if t == QUERY_SLOT and not last:
                        make_queries(*after)
                    if prepares:
                        turn_context(*after, (3,))
                        keys_kept = prepared()
                    if not (first and t == 0):
                        turn_probs(*preceding(pair, parity, t), (3,))
                    if t % 2 == 0:
                        turned = prepared()
                    if t == KEPT_SLOT and not first:
                        output(*before)

            pe.wait_ge(cleared, 2)
            if early:
                turn_context(0, 0, (0, 2, 1))
                turn_context(0, 0, (3,))
                emptied(prepared())
            pe.wait_ge(w_loaded, LOADS)
            if not rotary:
                turn_weights((wq_rows, wk_rows), 0)
            turn_tiles_pe(nc, pe, core.ident[:], y[:], lane_bank[0:2], y_ready, 1, y_turned)
            if not rotary:
                fold_weights(wqT, wkT, 2 * QUADS_OF)
                pe.wait_ge(w_kept, QK_JOBS)
            pe.wait_ge(yT_kept, 2)
            if not early:
                turn_context(0, 0, (0, 2, 1))
            make_queries(0, 0)
            if not early:
                turn_context(0, 0, (3,))
            emptied(prepared())
            if rotary:
                project(0, 0, 0)
            pe.wait_ge(late_loaded, LATE)
            turn_weights((wv_rows,), QK_JOBS)
            fold_weights(wvT, wo_rows, QK_JOBS + QUADS_OF)
            pe.wait_ge(w_kept, W_JOBS)
            batch(0, 0, first=True)
            batch(0, 1)
            with pe.Fori(1, LAST) as pair:
                batch(pair, 0)
                batch(pair, 1)
            batch(LAST, 0)
            batch(LAST, 1, last=True)
            go_to_end(lane)
            turned = prepared()
            turn_probs(LAST, 1, R - 1, range(len(QUADS)))
            for t in range(3):
                if t == 1:
                    turned = prepared()
                sum_context(LAST, 1, *sums_of_slot(t)[1:], turned)
            output(LAST, 1)
            emptied(prepared())
            pe.wait_ge(exp_done, BATCHES * R)
            for t in range(TILES):
                turn = nc.tensor.transpose(score[:, t * P:(t + 1) * P], outT[:, t * P:(t + 1) * P], core.ident[:])
            turn.then_inc(out_turned, 1)

        @block.scalar
        def _(act):
            lane = lanes()
            normalize_act(nc, act, core.eps(EPS_5), TILES, stats, var_ready, std_ready, 1)
            if normed:
                normalize_act(nc, act, core.eps(EPS_5), TILES, stats, var_ready, std_ready, 2)
            def context_root(b):
                act.wait_ge(cvar_ready, b + 1)
                nc.scalar.activation(cstd[:], mean_var[:, :, 1], ACT.Sqrt, bias=core.eps(EPS_5), scale=1.0)\
                    .then_inc(cstd_ready, 1)

            act.wait_ge(cleared, 2)
            if masked:
                context_root(0)

            def keep_weights(turned, before):
                for j in range(len(turned) * QUADS_OF):
                    quad = j % QUADS_OF
                    act.wait_ge(w_turned, before + j + 1)
                    nc.scalar.copy(turned[j // QUADS_OF][:, 4 * quad:4 * quad + 4, :].rearrange("p i d -> p (i d)"),
                                   score[:, (j % 4) * BANK:(j % 4 + 1) * BANK]).then_inc(w_kept, 1)

            def keep_folded(dst, before):
                for f in range(QUADS_OF):
                    act.wait_ge(w_turned, before + f + 1)
                    for odd in range(2):
                        bank = score[:, (2 * (f % 2) + odd) * BANK:(2 * (f % 2) + odd + 1) * BANK]
                        kept = nc.scalar.copy(dst[:].rearrange("p (i r) d -> p r i d", r=2)[:, odd, 4 * f:4 * f + 4, :],
                                              bank.rearrange("p (i d) -> p i d", d=D))
                    kept.then_inc(w_kept, 1)

            def take():
                act.wait_ge(lane["A"].full, lane["A"].count() + 1)
                return lane["A"].bank()

            def emptied(ins):
                ins.then_inc(lane["A"].free, 1)
                lane["A"].next()

            def keep_own(pair, parity):
                if normed:
                    nc.scalar.copy(keysT[:, CTX:KEYS], yT[:, bass.ds((pair * 2 + parity) * SEQ, SEQ)])

            def keep_context():
                for c in range(0, len(CTX_CHUNKS), 2):
                    c0, n = CTX_CHUNKS[c]
                    bank = take()
                    emptied(nc.scalar.copy(keysT[:, c0:c0 + n], bank[:, 0:n]))

            def keep_queries(parity):
                for job in range(QJOBS):
                    bank = take()
                    if not rotary:
                        emptied(nc.scalar.copy(queries[:, job * BANK:(job + 1) * BANK], bank[:]))
                        continue
                    for q in range(4):
                        part = slice(32 * q, 32 * q + 32)
                        kept = nc.scalar.copy(queries[part, parity, :].rearrange("p (t h i) -> p t h i", h=2, i=SEQ)[:, :, q % 2, :],
                                              bank[part, 0:R * SEQ].rearrange("p (t i) -> p t i", i=SEQ))
                    emptied(kept)

            def split_queries(parity):
                act.drain()
                nc.scalar.copy(queries_hi[:, parity, :], queries[:]).then_inc(hi_ready, 1)

            def split_keys(parity, dve_jobs):
                act.drain()
                act.wait_ge(dve_free, dve_jobs)
                nc.scalar.copy(keys_hi[:, parity, :], keysT[:]).then_inc(hi_ready, 1)

            def keep_rows(pair, parity):
                if split_sums:
                    act.wait_ge(rows_loaded[parity], 32 * (pair + 1))
                    nc.scalar.copy(rows_hi[:, parity], rows[:, parity]).then_inc(rows_hi_ready, 1)
                    return
                act.wait_ge(gained_ready, pair * 2 + parity + 1)
                nc.scalar.copy(rows[:, parity, 0:CT, :], gained[:]).then_inc(rows_ready, 1)

            def keep_projected(t):
                for c, (c0, n) in enumerate(CHUNKS):
                    bank = take()
                    emptied(nc.scalar.copy(unturned[:, t % 2, c0:c0 + n], bank[:, 0:n]))
                    if c in (1, len(CHUNKS) - 1):
                        act.drain().then_inc(unturned_ready, 1)

            def exps(pair, parity, t):
                act.wait_ge(peak_ready, tile_number(pair, parity, t) + 1)
                nc.scalar.activation(prob[:, t % 2, :], unmasked[:] if masked else score[:, 0:KEYS], ACT.Exp, bias=neg_peak[:, t % 2:t % 2 + 1],
                                     scale=scale, accum_out=rsum[:, t % 2:t % 2 + 1]).then_inc(exp_done, 1)

            def keep_probs(pair, parity, t, quads):
                for j in quads:
                    bank = take()
                    if split_sums:
                        tile, size = tile_number(pair, parity, t), tile_of_keys[QUADS[j][-1]][1]
                        if not isinstance(tile, int) or tile >= 2:
                            act.wait_ge(probs_lo, 3 * (tile - 2) + ACT_QUADS.index(j) + 1)
                        emptied(nc.scalar.copy(staged(t, j)[0:size], bank[0:size, 0:len(QUADS[j]) * P]
                                               .rearrange("p (i r) -> p i r", r=P)))
                        continue
                    for k0, n, size in full_tiles(QUADS[j]):
                        kept = nc.scalar.copy(probT[0:size, t // 2 % 2, k0:k0 + n, t % 2 * P:t % 2 * P + P],
                                              bank[0:size, (k0 % 4) * P:(k0 % 4 + n) * P].rearrange("p (i r) -> p i r", r=P))
                    emptied(kept)

            def split_probs(t, quads):
                act.drain()
                for j in quads:
                    size = tile_of_keys[QUADS[j][-1]][1]
                    nc.scalar.copy(probT[0:size, t // 2 % 2, QUADS[j][0]:QUADS[j][-1] + 1, t % 2 * P:t % 2 * P + P],
                                   staged(t, j)[0:size]).then_inc(probs_hi, 1)

            def keep_sums(pair, parity, group):
                act.wait_ge(sums_done, (pair * 2 + parity) * GROUPS + group + 1)
                nc.scalar.copy(mixed[:, group * GCOLS:(group + 1) * GCOLS], sums[:, 0:GCOLS]).then_inc(sums_kept, 1)

            def keep_output(pair, parity):
                bank = take()
                dst = outT[:, bass.ds((pair * 2 + parity) * SEQ, SEQ)]
                if "b_o" in w:
                    emptied(nc.scalar.activation(dst, bank[:, 0:SEQ], ACT.Identity, bias=out_bias[:]))
                else:
                    emptied(nc.scalar.copy(dst, bank[:, 0:SEQ]))

            def batch(pair, parity, first=False, last=False, no_stats=False):
                go_to_batch(lane, pair * 2 + parity, parity, first)
                before, after = preceding(pair, parity, 0)[0:2], following(pair, parity, R - 1)[0:2]
                for t in range(R):
                    if t:
                        back, group, part = sums_of_slot(t - 1)
                        if part == 1 and not (first and back):
                            keep_sums(*(before if back else (pair, parity)), group)
                    if not (rotary or split_sums) and t == R - 1 and not last:
                        split_queries(1 - parity)
                        split_keys(1 - parity, lane["D"].at + len(DVE_QUADS) * (t - (1 if first else 0)) + 2)
                    if rotary and not (last and t == R - 1):
                        keep_projected(following(pair, parity, t)[2])
                    ready_first = (0,) if split_sums and t != CTX_SLOT else (0, 2)
                    if not (first and t == 0):
                        keep_probs(*preceding(pair, parity, t), ready_first)
                    exps(pair, parity, t)
                    if masked and t == 3 and not no_stats:
                        context_root(pair * 2 + parity + 2)
                    if not (first and t == 0) and 2 not in ready_first:
                        keep_probs(*preceding(pair, parity, t), (2,))
                    prepares = t == CTX_SLOT and not last
                    if split_sums and prepares:
                        split_probs(t - 1, (0, 2))
                    if prepares:
                        keep_own(*after)
                        keep_context()
                    if t == QUERY_SLOT and not last:
                        keep_queries(1 - parity)
                        if split_sums:
                            split_queries(1 - parity)
                    if split_sums and prepares:
                        split_keys(1 - parity, lane["D"].at + len(DVE_QUADS) * (t + 1 - (1 if first else 0)) + 2)
                    if split_sums and not (first and t == 0):
                        keep_probs(*preceding(pair, parity, t), (3,))
                        split_probs(preceding(pair, parity, t)[2], (3,) if prepares else ACT_QUADS)
                    if t == KEPT_SLOT and (normed or split_sums) and not last:
                        keep_rows(*after)
                    if t == KEPT_SLOT and not first:
                        keep_output(*before)

            if early:
                keep_context()
            if not rotary:
                keep_weights((wqT, wkT), 0)
            keep_turned_act(nc, act, yT, lane_bank[0:2], y_turned, 1, yT_kept)
            if not rotary:
                keep_folded(fold_qk, 2 * QUADS_OF)
            act.drain()
            keep_own(0, 0)
            if not early:
                keep_context()
            keep_queries(0)
            if rotary:
                keep_projected(0)
            else:
                split_queries(0)
                split_keys(0, DVE_FIRST)
            act.wait_ge(late_loaded, LATE)
            keep_weights((wvT,), QK_JOBS)
            keep_folded(fold_vo, QK_JOBS + QUADS_OF)
            if normed or split_sums:
                keep_rows(0, 0)
            if masked:
                context_root(1)
            batch(0, 0, first=True)
            batch(0, 1)
            with act.Fori(1, LAST) as pair:
                batch(pair, 0)
                batch(pair, 1)
            batch(LAST, 0, no_stats=True)
            batch(LAST, 1, last=True, no_stats=True)
            go_to_end(lane)
            keep_probs(LAST, 1, R - 1, ACT_QUADS)
            if split_sums:
                split_probs(R - 1, ACT_QUADS)
            keep_sums(LAST, 1, GROUPS - 2)
            keep_sums(LAST, 1, GROUPS - 1)
            keep_output(LAST, 1)
            if out_norm:
                normalize_act(nc, act, core.eps(EPS_5), TILES, stats, var_ready, std_ready, 3)

        @block.gpsimd
        def _(pool):
            if normed:
                nc.gpsimd.memset((raw if masked else xhat)[:, CT - 1, :], 0.0)
            else:
                nc.gpsimd.memset(rows[:, :, CT - 1, :], 0.0)
            pool.drain()
            nc.gpsimd.memset(peak[:], 0.0).then_inc(cleared, 1)
            if masked:
                nc.gpsimd.memset(unmasked[:], 0.0)
            if rotary:
                nc.gpsimd.memset(queries[:], 0.0)
            pool.drain()
            nc.gpsimd.memset(neg_peak[:], 0.0).then_inc(cleared, 1)
            if normed:
                pool.wait_ge(gains_loaded, GAINS)
            pool.wait_ge(w_loaded, LOADS)

            def make_xhat(b):
                pool.wait_ge(crstd_ready, b + 1)
                pool.wait_ge(xhat_stored, 32 * b)
                nc.gpsimd.tensor_tensor(xhat[:], raw[:], over_last(mean_var[:, :, 0], D), ALU.subtract).then_inc(raw_used, 1)
                pool.drain()
                nc.gpsimd.tensor_tensor(xhat[:], xhat[:], over_last(crstd[:], D), ALU.mult).then_inc(xhat_ready, 1)
                pool.drain()

            def make_gained(b, step):
                if step == 0:
                    pool.wait_ge(rows_ready, b)
                    nc.gpsimd.tensor_tensor(gained[:], xhat[:], over_tiles(gains[:, 0, :], CT), ALU.mult)
                else:
                    nc.gpsimd.tensor_tensor(gained[:], gained[:], over_tiles(gains[:, 1, :], CT), ALU.add).then_inc(gained_ready, 1)
                pool.drain()

            def turn_keys(pair, parity, t):
                tile = tile_number(pair, parity, t)
                for h, (c0, n) in enumerate(HALVES):
                    pool.wait_ge(unturned_ready, 2 * tile + h + 1)
                    nc.gpsimd.tensor_tensor(projected[:, t % 2, c0:c0 + n], unturned[:, t % 2, c0:c0 + n],
                                            rot_cos[:, c0:c0 + n], ALU.mult)
                pool.drain()
                for h, (c0, n) in enumerate(HALVES):
                    pool.wait_ge(crossed_ready, 2 * tile + h + 1)
                    nc.gpsimd.tensor_tensor(projected[:, t % 2, c0:c0 + n], projected[:, t % 2, c0:c0 + n],
                                            crossed[:, c0:c0 + n], ALU.add).then_inc(keys_turned, 1)

            def split_keys(b, parity):
                pool.wait_ge(hi_ready, 2 * (b + 1))
                nc.gpsimd.tensor_tensor(keys_lo[:, parity, :], keysT[:], keys_hi[:, parity, :], ALU.subtract).then_inc(keys_split, 1)

            def split_rows(b, parity):
                pool.wait_ge(rows_hi_ready, b + 1)
                nc.gpsimd.tensor_tensor(rows_lo[:, parity], rows[:, parity], rows_hi[:, parity], ALU.subtract)\
                    .then_inc(rows_ready, 1)

            def low_probs(pair, parity, t, quads=ACT_QUADS):
                for j in quads:
                    n = ACT_QUADS.index(j)
                    pool.wait_ge(probs_hi, len(ACT_QUADS) * tile_number(pair, parity, t) + n + 1)
                    size = tile_of_keys[QUADS[j][-1]][1]
                    own = (slice(0, size), t // 2 % 2, slice(QUADS[j][0], QUADS[j][-1] + 1), slice(t % 2 * P, t % 2 * P + P))
                    nc.gpsimd.tensor_tensor(probT_lo[own], staged(t, j)[0:size], probT[own], ALU.subtract).then_inc(probs_lo, 1)

            def batch(pair, parity, first=False, last=False):
                b = pair * 2 + parity
                for t in range(R):
                    if split_sums and t == CTX_SLOT and not last:
                        low_probs(pair, parity, t - 1, (0, 2))
                        split_keys(b + 1, 1 - parity)
                        low_probs(pair, parity, t - 1, (3,))
                    elif split_sums and not (first and t == 0):
                        low_probs(*preceding(pair, parity, t))
                    elif not (rotary or split_sums) and t == R - 1 and not last:
                        split_keys(b + 1, 1 - parity)
                    if split_sums and t == KEPT_SLOT and not last:
                        split_rows(b + 1, 1 - parity)
                    if rotary and not (last and t == R - 1):
                        turn_keys(*following(pair, parity, t))
                    if masked and t == 0 and not last:
                        make_xhat(b + 1)
                        make_gained(b + 1, 0)
                        make_gained(b + 1, 1)

            if rotary:
                turn_keys(0, 0, 0)
            else:
                split_keys(0, 0)
            if split_sums:
                split_rows(0, 0)
            batch(0, 0, first=True)
            batch(0, 1)
            with pool.Fori(1, LAST) as pair:
                batch(pair, 0)
                batch(pair, 1)
            batch(LAST, 0)
            batch(LAST, 1, last=True)
            if split_sums:
                low_probs(LAST, 1, R - 1)

        @block.vector
        def _(dve):
            lane = lanes()

            def measure(b, first=False):
                dve.wait_ge(ctx_loaded, 32 * (b + 1))
                if not first:
                    dve.wait_ge(xhat_ready, b)
                for k in range(CT):
                    nc.vector.bn_stats(moments[:, k, :], raw[:, k, :])
                dve.drain()
                for k in range(CT):
                    ins = nc.vector.bn_aggr(mean_var[:, k, :], moments[:, k, :])
                ins.then_inc(cvar_ready, 1)

            normalize_dve(nc, dve, y[:], lat[:], square[:], stats, var_ready, std_ready, 1)
            dve.drain()
            if normed:
                normalize_dve(nc, dve, y[:], y[:], square[:], stats, var_ready, std_ready, 2)
                dve.drain()
            def take():
                dve.wait_ge(lane["D"].full, lane["D"].count() + 1)
                return lane["D"].bank()

            def emptied(ins):
                ins.then_inc(lane["D"].free, 1)
                lane["D"].next()

            def invert_std(b):
                dve.wait_ge(cstd_ready, b + 1)
                nc.vector.reciprocal(crstd[:], cstd[:]).then_inc(crstd_ready, 1)

            def make_first_xhat():
                dve.drain()
                nc.vector.tensor_tensor(xhat[:], raw[:], over_last(mean_var[:, :, 0], D), ALU.subtract).then_inc(raw_used, 1)
                dve.drain()
                nc.vector.tensor_tensor(xhat[:], xhat[:], over_last(crstd[:], D), ALU.mult).then_inc(xhat_ready, 1)
                dve.drain()

            def make_gained(b, step):
                if step == 0:
                    dve.wait_ge(ctx_loaded, 32 * (b + 1))
                    if not isinstance(b, int) or b > 0:
                        dve.wait_ge(rows_ready, b)
                    nc.vector.tensor_tensor(gained[:], xhat[:], over_tiles(gains[:, 0, :], CT), ALU.mult)
                else:
                    nc.vector.tensor_tensor(gained[:], gained[:], over_tiles(gains[:, 1, :], CT), ALU.add).then_inc(gained_ready, 1)
                dve.drain()

            def keep_context(parity):
                for c in range(1, len(CTX_CHUNKS), 2):
                    c0, n = CTX_CHUNKS[c]
                    bank = take()
                    emptied(nc.vector.tensor_copy(keysT[:, c0:c0 + n], bank[:, 0:n]))

            def cross_halves(pair, parity, t):
                tile = tile_number(pair, parity, t)
                for h, (c0, n) in enumerate(HALVES):
                    cols = slice(c0, c0 + n)
                    dve.wait_ge(unturned_ready, 2 * tile + h + 1)
                    if not (isinstance(tile, int) and tile == 0):
                        dve.wait_ge(keys_turned, 2 * tile + h - 1)
                    nc.vector.tensor_tensor(crossed[SEQ:P, cols], unturned[0:SEQ, t % 2, cols], rot_sin[0:SEQ, cols], ALU.mult)
                    nc.vector.tensor_tensor(crossed[0:SEQ, cols], unturned[SEQ:P, t % 2, cols], rot_sin[SEQ:P, cols], ALU.mult)\
                        .then_inc(crossed_ready, 1)

            def split_queries(b, parity):
                dve.wait_ge(hi_ready, 2 * b + 1)
                nc.vector.tensor_tensor(queries_lo[:, parity, :], queries[:], queries_hi[:, parity, :], ALU.subtract)\
                    .then_inc(queries_split, 1)

            def maximum(pair, parity, t):
                tile, which = tile_number(pair, parity, t), t % 2
                if masked and t == 0:
                    dve.wait_ge(mask_loaded[parity], 16 * (pair + 1))
                for h, (c0, n) in enumerate(HALVES):
                    dve.wait_ge(score_half, 2 * tile + h + 1)
                    if masked:
                        nc.vector.memset(mark[:, h:h + 1], 0.0)
                        nc.vector.tensor_tensor_reduce(unmasked[:, c0:c0 + n], score[:, c0:c0 + n], mask16[:, parity, c0:c0 + n],
                                                       1.0, -3e38, ALU.add, ALU.max, peak[:, h:h + 1])
                        continue
                    nc.vector.tensor_reduce(peak[:, h:h + 1], score[:, c0:c0 + n], AX, ALU.max)
                dve.drain()
                nc.vector.tensor_scalar(neg_peak[:, which:which + 1], peak[:, 0:1], peak[:, 1:2], -scale,
                                        ALU.max, ALU.mult).then_inc(peak_ready, 1)

            def normalise(pair, parity, t):
                tile, which = tile_number(pair, parity, t), t % 2
                dve.wait_ge(exp_done, tile + 1)
                nc.vector.reciprocal(rinv[:, which:which + 1], rsum[:, which:which + 1])
                dve.drain()
                nc.vector.tensor_scalar(prob[:, which, :], prob[:, which, :], rinv[:, which:which + 1], None,
                                        ALU.mult).then_inc(prob_ready, 1)

            def keep_probs(t, j):
                bank = take()
                for k0, n, size in full_tiles(QUADS[j]):
                    own = (slice(0, size), t // 2 % 2, slice(k0, k0 + n), slice(t % 2 * P, t % 2 * P + P))
                    source = bank[0:size, (k0 % 4) * P:(k0 % 4 + n) * P].rearrange("p (i r) -> p i r", r=P)
                    kept = nc.vector.tensor_copy(probT[own], source)
                    if split_sums:
                        dve.drain()
                        kept = nc.vector.tensor_tensor(probT_lo[own], source, probT[own], ALU.subtract)
                emptied(kept)

            def batch(pair, parity, first=False, last=False, no_stats=False):
                b = pair * 2 + parity
                go_to_batch(lane, b, parity, first)
                for t in range(R):
                    turns = not (first and t == 0)
                    rotates = rotary and not (last and t == R - 1)
                    if turns:
                        normalise(*preceding(pair, parity, t))
                    if rotates and t < R - 1:
                        cross_halves(*following(pair, parity, t))
                    if not rotary and t == R - 1 and not last:
                        split_queries(b + 1, 1 - parity)
                    maximum(pair, parity, t)
                    if rotates and t == R - 1:
                        cross_halves(*following(pair, parity, t))
                    if turns:
                        keep_probs(preceding(pair, parity, t)[2], 1)
                    if masked and t == 3 and not no_stats:
                        invert_std(b + 2)
                    if masked and t == CTX_SLOT and not no_stats:
                        measure(b + 2)
                    if t == CTX_SLOT and not last:
                        keep_context(1 - parity)
                    if rotary and t < 2 and not last:
                        make_gained(b + 1, t)
                    if turns and 3 in DVE_QUADS:
                        keep_probs(preceding(pair, parity, t)[2], 3)

            dve.wait_ge(cleared, 2)
            if COLS > KEYS:
                nc.vector.memset(keysT[:, KEYS:COLS], 0.0)
            if masked:
                measure(0, first=True)
            if normed:
                dve.wait_ge(gains_loaded, GAINS)
                if not masked:
                    make_gained(0, 0)
                    make_gained(0, 1)
                nc.vector.tensor_tensor(y[:], y[:], over_tiles(gains[:, 2, :], TILES), ALU.mult)
                dve.drain()
                nc.vector.tensor_tensor(y[:], y[:], over_tiles(gains[:, 3, :], TILES), ALU.add).then_inc(y_ready, 1)
            else:
                nc.vector.tensor_copy(square[:, 0, 0:1], y[:, 0, 0:1]).then_inc(y_ready, 1)
            if masked:
                invert_std(0)
                make_first_xhat()
                make_gained(0, 0)
                make_gained(0, 1)
                nc.vector.memset(mask_all[:, CTX:KEYS], 0.0)
                nc.vector.tensor_scalar(mask_all[:, 0:CTX], mask_u8[:], -1.0, 1e30, ALU.add, ALU.mult).then_inc(mask_ready, 1)
            keep_context(0)
            if rotary:
                dve.wait_ge(w_loaded, LOADS)
                cross_halves(0, 0, 0)
            else:
                split_queries(0, 0)
            if masked:
                measure(1)
                invert_std(1)
            batch(0, 0, first=True)
            batch(0, 1)
            with dve.Fori(1, LAST) as pair:
                batch(pair, 0)
                batch(pair, 1)
            batch(LAST, 0, no_stats=True)
            batch(LAST, 1, last=True, no_stats=True)
            go_to_end(lane)
            normalise(LAST, 1, R - 1)
            for j in DVE_QUADS:
                keep_probs(R - 1, j)
            dve.wait_ge(late_loaded, LATE)
            dve.wait_ge(out_turned, 1)
            turned = score[:, 0:TOKENS].rearrange("p (t d) -> p t d", d=D)
            if out_norm:
                nc.vector.tensor_copy(y[:], turned)
                dve.drain()
                normalize_dve(nc, dve, y[:], y[:], square[:], stats, var_ready, std_ready, 3)
                dve.drain()
                nc.vector.tensor_tensor(y[:], y[:], over_tiles(out_gains[:, 0, :], TILES), ALU.mult)
                dve.drain()
                nc.vector.tensor_tensor(y[:], y[:], over_tiles(out_gains[:, 1, :], TILES), ALU.add)
                dve.drain()
                nc.vector.tensor_tensor(lat[:], lat[:], y[:], ALU.add)
            else:
                nc.vector.tensor_tensor(lat[:], lat[:], turned, ALU.add)


def single_head_stage(core, name, w):
    nc, lat = core.nc, core.lat
    PAIRS = BATCHES // 2
    CT = -(-CTX // P)
    TAIL = CTX - (CT - 1) * P
    tile_of_keys = [(k * P, min(P, CTX - k * P)) for k in range(CT)]
    CHUNKS = [(c * BANK, min(BANK, CTX - c * BANK)) for c in range(-(-CTX // BANK))]
    HALVES = [(0, 2 * BANK), (2 * BANK, CTX - 2 * BANK)]
    QUADS = [list(range(q, min(q + 4, CT))) for q in range(0, CT, 4)]
    SCALE = D ** -0.5

    with ExitStack() as ctx:
        s = Stage(nc, ctx, name)
        y, square, yT = s.sb("y", [P, TILES, D]), s.sb("square", [P, TILES, D]), s.sb("yT", [P, TOKENS])
        stats = s.sb("stats", [P, 4, TILES])
        staged = s.sb("staged", [P, 2, 2, CT, D])
        rows = s.sb("rows", [P, 2, 2, CT, D])
        keysT = s.sb("keysT", [P, 2, CTX])
        prob, probT = s.sb("prob", [P, CTX]), s.sb("probT", [P, CT, P])
        zeros = s.sb("zeros", [P, D])
        queries = s.sb("queries", [P, P])
        mixed, mixedT = s.sb("mixed", [P, TILES, D]), s.sb("mixedT", [P, TOKENS])
        peak, neg_peak = s.sb("peak", [P, 2]), s.sb("neg_peak", [P, 1])
        rsum, rinv = s.sb("rsum", [P, 1]), s.sb("rinv", [P, 1])
        wq, wk, wv = s.sb("wq", [P, D]), s.sb("wk", [P, D]), s.sb("wv", [P, D])
        bq, bv_rows = s.sb("bq", [P, 1]), s.sb("bv_rows", [P, D])
        wT, fold_qk, query_bias = s.sb("wT", [P, 2, D]), s.sb("fold_qk", [P, D]), s.sb("query_bias", [P, 1])

        score = s.ps("score", [P, 4 * BANK])
        lane_bank = [s.ps(f"lane{i}", [P, BANK]) for i in range(3)]
        sums = s.ps("sums", [P, BANK])

        w_loaded, var_ready, std_ready = s.sem("w_loaded"), s.sem("var_ready"), s.sem("std_ready")
        y_ready, y_turned, yT_kept = s.sem("y_ready"), s.sem("y_turned"), s.sem("yT_kept")
        w_turned, w_kept = s.sem("w_turned"), s.sem("w_kept")
        staged_loaded = [s.sem(f"staged_loaded{i}") for i in range(2)]
        rows_ready = s.sem("rows_ready")
        score_half, peak_ready, exp_done, prob_ready = (s.sem("score_half"), s.sem("peak_ready"), s.sem("exp_done"),
                                                        s.sem("prob_ready"))
        sums_done, sums_kept = s.sem("sums_done"), s.sem("sums_kept")
        act_full, act_free, dve_full, dve_free = s.sem("act_full"), s.sem("act_free"), s.sem("dve_full"), s.sem("dve_free")
        mixed_turned, mixedT_kept, out_done = s.sem("mixed_turned"), s.sem("mixedT_kept"), s.sem("out_done")

        ACT_FIRST, ACT_PAIR = 4 + 1, 4 + 1 + 2
        DVE_FIRST, DVE_PAIR = 4, 4 + 2

        def lanes():
            return {"A": Lane(lane_bank[0:2], act_full, act_free), "D": Lane(lane_bank[2:3], dve_full, dve_free)}

        def go_to_pair(lane, pair, turn):
            lane["A"].go_to(ACT_FIRST + ACT_PAIR * pair, ACT_FIRST + ACT_PAIR * turn)
            lane["D"].go_to(DVE_FIRST + DVE_PAIR * pair, 0)

        def jobs_of(*chunks):
            return [(h, c) for h in range(2) for c in chunks]

        ACT_CTX, DVE_CTX, ALL_CTX = jobs_of(0, 2), jobs_of(1, 3), jobs_of(0, 1, 2, 3)

        block = s.block()

        @block.sync
        def _(sp):
            def load_staged(pair, parity):
                for h in range(2):
                    src = core.w["ctx_1024"][bass.ds(pair * 2 + h, 1)].rearrange("a n d -> (a n) d")
                    sp.dma_start(staged[:, parity, h, 0:CT - 1, :], src[0:(CT - 1) * P].rearrange("(k p) d -> p k d", p=P))\
                        .then_inc(staged_loaded[parity], 16)
                    sp.dma_start(staged[0:TAIL, parity, h, CT - 1, :], src[(CT - 1) * P:CTX]).then_inc(staged_loaded[parity], 16)

            def during(pair, parity):
                sp.wait_ge(rows_ready, pair + 1)
                load_staged(pair + 2, parity)

            load_staged(0, 0)
            for dst, src in ((wq, "Wq"), (wk, "Wk"), (wv, "Wv")):
                sp.dma_start(dst[:], w[src]).then_inc(w_loaded, 16)
            with nc.allow_non_contiguous_dma("bias column"):
                sp.dma_start(bq[:], column(w["bq"])).then_inc(w_loaded, 16)
            sp.dma_start(bv_rows[:], w["bv"].partition_broadcast(P)).then_inc(w_loaded, 16)
            load_staged(1, 1)
            during(0, 0)
            with sp.Fori(0, (PAIRS - 2) // 2 - 1) as j:
                during(2 * j + 1, 1)
                during(2 * j + 2, 0)
            during(PAIRS - 3, 1)

        LOADS = 5

        @block.tensor
        def _(pe):
            lane = lanes()
            pe.wait_ge(w_loaded, 16 * LOADS)
            for n, source in enumerate((wq, wk)):
                turn = nc.tensor.transpose(score[:, n * P:(n + 1) * P], source[:], core.ident[:])
            turn.then_inc(w_turned, 1)
            turn_tiles_pe(nc, pe, core.ident[:], y[:], lane_bank[0:2], y_ready, 1, y_turned)
            pe.wait_ge(w_kept, 1)
            nc.tensor.matmul(score[:, BANK:BANK + D], wT[:, 0, :], wT[:, 1, :], start=True, stop=True)
            nc.tensor.matmul(score[:, BANK + D:BANK + D + 1], wT[:, 1, :], bq[:], start=True, stop=True)\
                .then_inc(w_turned, 1)
            pe.wait_ge(yT_kept, 2)
            pe.wait_ge(w_kept, 2)

            def fill(name):
                ln = lane[name]
                count = ln.count() - len(ln.banks) + 1
                if not isinstance(count, int) or count > 0:
                    pe.wait_ge(ln.free, count)
                return ln.bank()

            def filled(name, ins):
                ins.then_inc(lane[name].full, 1)
                lane[name].next()

            def emptied(counts=None):
                for name in "AD":
                    pe.wait_ge(lane[name].free, counts[name] if counts else lane[name].count())

            def turn_context(pair, parity, jobs):
                if jobs[0] == (0, 0):
                    pe.wait_ge(staged_loaded[parity], 64 * (pair + 1))
                for h, c in jobs:
                    c0, n = CHUNKS[c]
                    bank = fill("AD"[c % 2])
                    for k in range(c0 // P, -(-(c0 + n) // P)):
                        size = tile_of_keys[k][1]
                        turn = nc.tensor.transpose(bank[:, k * P - c0:k * P - c0 + size], staged[0:size, parity, h, k, :],
                                                   core.ident[0:size, 0:size])
                    filled("AD"[c % 2], turn)

            def make_queries(pair):
                filled("A", nc.tensor.matmul(fill("A")[:, 0:P], fold_qk[:], yT[:, bass.ds(pair * P, P)], start=True, stop=True))

            def scores(pair, first=False):
                if not first:
                    pe.wait_ge(exp_done, pair)
                for c, (c0, n) in enumerate(CHUNKS):
                    for h in range(2):
                        mm = nc.tensor.matmul(score[h * SEQ:(h + 1) * SEQ, c0:c0 + n], queries[:, h * SEQ:(h + 1) * SEQ],
                                              keysT[:, h, c0:c0 + n], start=True, stop=True)
                    if c % 2:
                        mm.then_inc(score_half, 1)

            def turn_probs(pair):
                pe.wait_ge(prob_ready, pair + 1)
                for j, quad in enumerate(QUADS):
                    bank = fill("AD"[j % 2])
                    for i, k in enumerate(quad):
                        c0, n = tile_of_keys[k]
                        turn = nc.tensor.transpose(bank[0:n, i * P:(i + 1) * P], prob[:, c0:c0 + n], core.ident[:])
                    filled("AD"[j % 2], turn)

            def sum_context(pair, parity, tiles, turned, first=False):
                if 0 in tiles:
                    emptied(turned)
                    pe.wait_ge(rows_ready, pair + 1)
                    if not first:
                        pe.wait_ge(sums_kept, pair)
                for k in tiles:
                    n = tile_of_keys[k][1]
                    for h in range(2):
                        mm = nc.tensor.matmul(sums[h * SEQ:(h + 1) * SEQ, 0:D], probT[0:n, k, h * SEQ:(h + 1) * SEQ],
                                              rows[0:n, parity, h, k, :], start=(k == 0), stop=(k == CT - 1))
                if CT - 1 in tiles:
                    mm.then_inc(sums_done, 1)

            def step(pair, parity, nth, turn, first=False, last=False):
                go_to_pair(lane, pair, turn)
                turned = {name: lane[name].count() for name in "AD"}
                scores(pair, first)
                for jobs, tiles in ((ALL_CTX[0:2], range(0, 6)), (ALL_CTX[2:4], range(6, CT)), (ALL_CTX[4:], ())):
                    if not last:
                        turn_context(nth, 1 - parity, jobs)
                    if not first:
                        sum_context(pair - 1, 1 - parity, tiles, turned, first=isinstance(pair, int) and pair == 1)
                if not last:
                    make_queries(pair + 1)
                    keys_kept = {name: lane[name].count() for name in "AD"}
                turn_probs(pair)
                if not last:
                    emptied(keys_kept)

            turn_context(0, 0, ALL_CTX)
            make_queries(0)
            emptied()
            step(0, 0, 0, 0, first=True)
            with pe.Fori(0, (PAIRS - 2) // 2) as j:
                step(2 * j + 1, 1, j + 1, 1)
                step(2 * j + 2, 0, j + 1, 0)
            step(PAIRS - 1, 1, 0, 1, last=True)
            emptied()
            sum_context(PAIRS - 1, 1, range(CT), {name: lane[name].count() for name in "AD"})
            turn_tiles_pe(nc, pe, core.ident[:], mixed[:], lane_bank[0:2], sums_kept, PAIRS, mixed_turned)
            pe.wait_ge(exp_done, PAIRS)
            pe.wait_ge(mixedT_kept, 2)
            for t in range(TILES):
                mm = nc.tensor.matmul(score[:, t * P:(t + 1) * P], mixedT[:, t * P:(t + 1) * P], wv[:], start=True, stop=True)
            mm.then_inc(out_done, 1)

        @block.scalar
        def _(act):
            lane = lanes()
            normalize_act(nc, act, core.eps(EPS_5), TILES, stats, var_ready, std_ready, 1)
            act.wait_ge(w_turned, 1)
            nc.scalar.copy(wT[:].rearrange("p n d -> p (n d)"), score[:, 0:2 * P]).then_inc(w_kept, 1)
            keep_turned_act(nc, act, yT, lane_bank[0:2], y_turned, 1, yT_kept)
            act.wait_ge(w_turned, 2)
            nc.scalar.copy(fold_qk[:], score[:, BANK:BANK + D])
            nc.scalar.copy(query_bias[:], score[:, BANK + D:BANK + D + 1]).then_inc(w_kept, 1)
            act.drain()

            def take():
                act.wait_ge(lane["A"].full, lane["A"].count() + 1)
                return lane["A"].bank()

            def emptied(ins):
                ins.then_inc(lane["A"].free, 1)
                lane["A"].next()

            def keep_context(jobs):
                for h, c in jobs:
                    c0, n = CHUNKS[c]
                    emptied(nc.scalar.copy(keysT[:, h, c0:c0 + n], take()[:, 0:n]))

            def keep_queries():
                emptied(nc.scalar.activation(queries[:], take()[:, 0:P], ACT.Identity, bias=query_bias[:]))

            def exps(pair):
                act.wait_ge(peak_ready, pair + 1)
                nc.scalar.activation(prob[:], score[:, 0:CTX], ACT.Exp, bias=neg_peak[:], scale=SCALE, accum_out=rsum[:])\
                    .then_inc(exp_done, 1)

            def keep_sums(pair):
                act.wait_ge(sums_done, pair + 1)
                nc.scalar.copy(mixed[:, bass.ds(pair, 1), :].rearrange("p a d -> p (a d)"), sums[:, 0:D]).then_inc(sums_kept, 1)

            def keep_probs():
                for j in (0, 2):
                    bank = take()
                    for k0, n, size in full_tiles(QUADS[j]):
                        kept = nc.scalar.copy(probT[0:size, k0:k0 + n, :].rearrange("p i r -> p (i r)"),
                                              bank[0:size, (k0 % 4) * P:(k0 % 4 + n) * P])
                    emptied(kept)

            def step(pair, turn, first=False, last=False):
                go_to_pair(lane, pair, turn)
                if not last:
                    keep_context(ACT_CTX[0:1])
                exps(pair)
                if not last:
                    keep_context(ACT_CTX[1:])
                    keep_queries()
                if not first:
                    keep_sums(pair - 1)
                keep_probs()

            act.wait_ge(w_loaded, 16 * LOADS)
            keep_context(ACT_CTX)
            keep_queries()
            step(0, 0, first=True)
            with act.Fori(0, (PAIRS - 2) // 2) as j:
                step(2 * j + 1, 1)
                step(2 * j + 2, 0)
            step(PAIRS - 1, 1, last=True)
            keep_sums(PAIRS - 1)
            keep_turned_act(nc, act, mixedT, lane_bank[0:2], mixed_turned, 1, mixedT_kept)

        @block.gpsimd
        def _(pool):
            nc.gpsimd.memset(zeros[:], 0.0)
            pool.drain()

            def copy_rows(pair, parity):
                if isinstance(pair, int) and pair < 2:
                    pool.wait_ge(act_full, ACT_FIRST * (pair + 1))
                else:
                    pool.wait_ge(sums_done, pair - 1)
                    pool.wait_ge(act_full, ACT_FIRST + ACT_PAIR * (pair - 1) + 5)
                for h in range(2):
                    for part in ((slice(0, P), slice(0, CT - 1)), (slice(0, TAIL), slice(CT - 1, CT))):
                        source = staged[part[0], parity, h, part[1], :]
                        copy = nc.gpsimd.tensor_tensor(rows[part[0], parity, h, part[1], :], source,
                                                       over_tiles(zeros[part[0], :], source.shape[1]), ALU.add)
                copy.then_inc(rows_ready, 1)

            copy_rows(0, 0)
            copy_rows(1, 1)
            with pool.Fori(1, PAIRS // 2) as j:
                copy_rows(2 * j, 0)
                copy_rows(2 * j + 1, 1)

        @block.vector
        def _(dve):
            lane = lanes()
            normalize_dve(nc, dve, y[:], lat[:], square[:], stats, var_ready, std_ready, 1).then_inc(y_ready, 1)
            dve.wait_ge(w_loaded, 16 * LOADS)
            nc.vector.tensor_tensor(lat[:], lat[:], over_tiles(bv_rows[:], TILES), ALU.add)

            def take():
                dve.wait_ge(lane["D"].full, lane["D"].count() + 1)
                return lane["D"].bank()

            def emptied(ins):
                ins.then_inc(lane["D"].free, 1)
                lane["D"].next()

            def keep_context(jobs):
                for h, c in jobs:
                    c0, n = CHUNKS[c]
                    emptied(nc.vector.tensor_copy(keysT[:, h, c0:c0 + n], take()[:, 0:n]))

            def maximum(pair):
                for h, (c0, n) in enumerate(HALVES):
                    dve.wait_ge(score_half, 2 * pair + h + 1)
                    nc.vector.tensor_reduce(peak[:, h:h + 1], score[:, c0:c0 + n], AX, ALU.max)
                dve.drain()
                nc.vector.tensor_scalar(neg_peak[:], peak[:, 0:1], peak[:, 1:2], -SCALE, ALU.max, ALU.mult).then_inc(peak_ready, 1)

            def normalise(pair):
                dve.wait_ge(exp_done, pair + 1)
                nc.vector.reciprocal(rinv[:], rsum[:])
                dve.drain()
                nc.vector.tensor_scalar(prob[:], prob[:], rinv[:], None, ALU.mult).then_inc(prob_ready, 1)

            def keep_probs():
                for j in (1, 3):
                    bank = take()
                    for k0, n, size in full_tiles(QUADS[j]):
                        kept = nc.vector.tensor_copy(probT[0:size, k0:k0 + n, :].rearrange("p i r -> p (i r)"),
                                                     bank[0:size, (k0 % 4) * P:(k0 % 4 + n) * P])
                    emptied(kept)

            def step(pair, turn, first=False, last=False):
                go_to_pair(lane, pair, turn)
                maximum(pair)
                if not last:
                    keep_context(DVE_CTX[0:1])
                normalise(pair)
                if not last:
                    keep_context(DVE_CTX[1:])
                keep_probs()

            keep_context(DVE_CTX)
            step(0, 0, first=True)
            with dve.Fori(0, (PAIRS - 2) // 2) as j:
                step(2 * j + 1, 1)
                step(2 * j + 2, 0)
            step(PAIRS - 1, 1, last=True)
            dve.wait_ge(out_done, 1)
            nc.vector.tensor_tensor(lat[:], lat[:], score[:, 0:TOKENS].rearrange("p (t d) -> p t d", d=D), ALU.add)




def top2_mask_dve(nc, dve, prob, rank, low, mask, work):
    n, experts = prob.shape[1], prob.shape[2]
    first, rest, cand, top = work[:, 0], work[:, 1], work[:, 2], work[:, 3]
    peak = top[:, :, 0]
    for source, chosen in ((prob, first), (rest, mask)):
        nc.vector.tensor_reduce(peak, source, AX, ALU.max)
        dve.drain()
        nc.vector.tensor_tensor(cand, source, over_last(peak, experts), ALU.is_ge)
        dve.drain()
        nc.vector.tensor_tensor(cand, cand, over_tiles(rank, n), ALU.mult)
        dve.drain()
        nc.vector.tensor_reduce(peak, cand, AX, ALU.max)
        dve.drain()
        nc.vector.tensor_tensor(chosen, cand, over_last(peak, experts), ALU.is_equal)
        dve.drain()
        if chosen is first:
            nc.vector.scalar_tensor_tensor(rest, first, low, prob, ALU.mult, ALU.add)
            dve.drain()
    nc.vector.tensor_tensor(mask, mask, first, ALU.add)
    dve.drain()


def moe_stage(core, name, kind, wg, w1, b1, w2, b2, bg=None):
    nc, lat = core.nc, core.lat
    E = 8
    swiglu = kind == "swiglu"
    H = w2.shape[2] if swiglu else w1.shape[2]
    C = H // P
    with ExitStack() as ctx:
        s = Stage(nc, ctx, name)
        y = s.sb("y", [P, TILES, D])
        square = s.sb("square", [P, TILES, D])
        yT = s.sb("yT", [P, TOKENS])
        stats = s.sb("stats", [P, 4, TILES])
        wg_sb = s.sb("wg", [P, E])
        w1_sb = s.sb("w1", [P, E, (2 if swiglu else 1) * H])
        w2_sb = s.sb("w2", [P, E, C, D])
        hT = s.sb("hT", [P, 2, C, TOKENS])
        prob = s.sb("prob", [P, TILES, E])
        gate = s.sb("gate", [P, TILES, E])
        mask = s.sb("mask", [P, TILES, E])
        work = s.sb("work", [P, 4, TILES, E])
        norm = s.sb("norm", [P, 2, TILES])
        gated = s.sb("gated", [P, TILES, D])
        acc = s.sb("acc", [P, TILES, D])
        if swiglu:
            w1_rows = s.sb("w1_rows", [P, E, 2 * H // P, D])
            w2_rows = s.sb("w2_rows", [P, E, H])
            wg_rows = s.sb("wg_rows", [E, D])
            silu = s.sb("silu", [P, TOKENS])
        else:
            b1_sb = s.sb("b1", [P, E, C])
            b2_sb = s.sb("b2", [E, D])
            gateT = s.sb("gateT", [E, TOKENS])
            if bg is not None:
                bg_sb = s.sb("bg", [P, E])
        hid = [s.ps(f"hid{i}", [P, TOKENS]) for i in range(2)]
        mix = s.ps("mix", [P, TILES, D])
        aux = [s.ps(f"aux{i}", [P, BANK]) for i in range(2)]

        gate_loaded, w1_loaded, w2_loaded = s.sem("gate_loaded"), s.sem("w1_loaded"), s.sem("w2_loaded")
        var_ready, std_ready = s.sem("var_ready"), s.sem("std_ready")
        y_ready, y_turned, yT_ready = s.sem("y_ready"), s.sem("y_turned"), s.sem("yT_ready")
        w_turned, w_copied = s.sem("w_turned"), s.sem("w_copied")
        logits_done, shifted, exp_done = s.sem("logits_done"), s.sem("shifted"), s.sem("exp_done")
        gate_ready, gate_turned, gateT_ready = s.sem("gate_ready"), s.sem("gate_turned"), s.sem("gateT_ready")
        hid_done, h_ready, silu_done = s.sem("hid_done"), s.sem("h_ready"), s.sem("silu_done")
        mix_done, mix_used = s.sem("mix_done"), s.sem("mix_used")
        TURNS = E * (2 * H // P) // 4 + E * C // 4
        block = s.block()

        @block.sync
        def _(sp):
            if swiglu:
                sp.dma_start(wg_rows[:], wg).then_inc(gate_loaded, 16)
                sp.dma_start(w1_rows[:], w1.rearrange("e (c p) d -> p e c d", p=P)).then_inc(w1_loaded, 16)
                sp.dma_start(w2_rows[:], w2.rearrange("e d h -> d e h")).then_inc(w2_loaded, 16)
            else:
                sp.dma_start(wg_sb[:], wg).then_inc(gate_loaded, 16)
                if bg is not None:
                    sp.dma_start(bg_sb[:], bg.partition_broadcast(P)).then_inc(gate_loaded, 16)
                sp.dma_start(w1_sb[:], w1.rearrange("e d h -> d e h")).then_inc(w1_loaded, 16)
                with nc.allow_non_contiguous_dma("bias columns"):
                    for e in range(E):
                        sp.dma_start(b1_sb[:, e, :], b1[e].rearrange("(c p) -> p c", p=P)).then_inc(w1_loaded, 16)
                sp.dma_start(b2_sb[:], b2).then_inc(w2_loaded, 16)
                sp.dma_start(w2_sb[:], w2.rearrange("e (c p) d -> p e c d", p=P)).then_inc(w2_loaded, 16)
        gate_loads = 2 if bg is not None else 1
        w1_loads = 1 if swiglu else 1 + E
        w2_loads = 1 if swiglu else 2

        @block.tensor
        def _(pe):
            pe.wait_ge(y_ready, 1)
            for t in range(TILES):
                turn = nc.tensor.transpose(aux[t // 4][:, (t % 4) * D:(t % 4 + 1) * D], y[:, t, :], core.ident[:])
                if t % 4 == 3:
                    turn.then_inc(y_turned, 1)
            if swiglu:
                pe.wait_ge(gate_loaded, 16)
                pe.wait_ge(yT_ready, 2)
                nc.tensor.transpose(aux[0][:, 0:E], wg_rows[:], core.ident[0:E, 0:E]).then_inc(w_turned, 1)
                pe.wait_ge(w1_loaded, 16)
                pe.wait_ge(w2_loaded, 16)
                blocks = [w1_rows[:, e, c, :] for e in range(E) for c in range(2 * H // P)]
                blocks += [w2_rows[:, e, c * P:(c + 1) * P] for e in range(E) for c in range(C)]
                for k in range(TURNS):
                    pe.wait_ge(w_copied, max(k, 1))
                    for j in range(4):
                        turn = nc.tensor.transpose(aux[k % 2][:, j * P:(j + 1) * P], blocks[4 * k + j], core.ident[:])
                    turn.then_inc(w_turned, 1)
                pe.wait_ge(w_copied, TURNS + 1)
            else:
                pe.wait_ge(gate_loaded, 16 * gate_loads)
                pe.wait_ge(yT_ready, 2)
            for t in range(TILES):
                score = nc.tensor.matmul(aux[0][:, t * E:(t + 1) * E], yT[:, t * P:(t + 1) * P], wg_sb[:],
                                         start=True, stop=True)
            score.then_inc(logits_done, 1)

            hidden = [0]

            def hidden_chunk(e, column):
                k = hidden[0]
                if k >= 2 and not swiglu:
                    pe.wait_ge(h_ready, k - 1)
                elif k >= 2 and k % 2 == 0:
                    pe.wait_ge(silu_done, k // 2)
                elif k >= 2:
                    pe.wait_ge(h_ready, k // 2)
                for half in range(2):
                    nc.tensor.matmul(hid[k % 2][:, half * BANK:(half + 1) * BANK],
                                     w1_sb[:, e, column:column + P], yT[:, half * BANK:(half + 1) * BANK],
                                     start=True, stop=True).then_inc(hid_done, 1)
                hidden[0] += 1

            def expert_hidden(e):
                for c in range(C):
                    hidden_chunk(e, c * P)
                    if swiglu:
                        hidden_chunk(e, H + c * P)

            def expert_out(e):
                pe.wait_ge(h_ready, C * (e + 1))
                if e >= 1:
                    pe.wait_ge(mix_used, e)
                for t in range(TILES):
                    for c in range(C):
                        out = nc.tensor.matmul(mix[:, t, :], hT[:, e % 2, c, t * P:(t + 1) * P], w2_sb[:, e, c, :],
                                               start=(c == 0), stop=(c == C - 1))
                out.then_inc(mix_done, 1)

            if not swiglu:
                pe.wait_ge(w1_loaded, 16 * w1_loads)
            expert_hidden(0)
            for e in range(E):
                if e == 1 and not swiglu:
                    pe.wait_ge(gate_ready, 1)
                    for t in range(TILES):
                        turn = nc.tensor.transpose(aux[t // 4][0:E, (t % 4) * P:(t % 4 + 1) * P], gate[:, t, :],
                                                   core.ident[:])
                    turn.then_inc(gate_turned, 1)
                if e + 1 < E:
                    expert_hidden(e + 1)
                if e == 0 and not swiglu:
                    pe.wait_ge(w2_loaded, 16 * w2_loads)
                expert_out(e)
            if not swiglu:
                pe.wait_ge(gateT_ready, 1)
                pe.wait_ge(mix_used, E)
                for t in range(TILES):
                    out = nc.tensor.matmul(mix[:, t, :], gateT[:, t * P:(t + 1) * P], b2_sb[:], start=True, stop=True)
                out.then_inc(mix_done, 1)

        @block.scalar
        def _(act):
            normalize_act(nc, act, core.eps(EPS_5), TILES, stats, var_ready, std_ready, 1)
            for half in range(2):
                act.wait_ge(y_turned, half + 1)
                nc.scalar.copy(yT[:, half * BANK:(half + 1) * BANK], aux[half][:]).then_inc(yT_ready, 1)
            if swiglu:
                act.wait_ge(w_turned, 1)
                nc.scalar.copy(wg_sb[:], aux[0][:, 0:E]).then_inc(w_copied, 1)
                for k in range(TURNS):
                    act.wait_ge(w_turned, k + 2)
                    turned = aux[k % 2][:].rearrange("p (j q) -> p j q", q=P)
                    per = 2 * H // P
                    if 4 * k < E * per:
                        dst = w1_sb[:].rearrange("p e (c q) -> p (e c) q", q=P)[:, 4 * k:4 * k + 4, :]
                    else:
                        j = 4 * k - E * per
                        dst = w2_sb[:].rearrange("p e c d -> p (e c) d")[:, j:j + 4, :]
                    nc.scalar.copy(dst, turned).then_inc(w_copied, 1)
            act.wait_ge(shifted, 1)
            nc.scalar.activation(prob[:], prob[:], ACT.Exp).then_inc(exp_done, 1)

            def hidden_of(e):
                for c in range(C):
                    if swiglu:
                        k = 2 * (e * C + c)
                        act.wait_ge(hid_done, 2 * k + 2)
                        if k >= 2:
                            act.wait_ge(h_ready, e * C + c)
                        nc.scalar.activation(silu[:], hid[0][:], ACT.Silu).then_inc(silu_done, 1)
                    else:
                        k = e * C + c
                        act.wait_ge(hid_done, 2 * k + 2)
                        nc.scalar.activation(hT[:, e % 2, c, :], hid[k % 2][:],
                                             ACT.Relu if kind == "relu" else ACT.Gelu,
                                             bias=b1_sb[:, e, c:c + 1]).then_inc(h_ready, 1)

            if not swiglu:
                act.wait_ge(w1_loaded, 16 * w1_loads)
            for e in range(E):
                hidden_of(e)
                if e == 1 and not swiglu:
                    act.wait_ge(gate_turned, 1)
                    for half in range(2):
                        last = nc.scalar.copy(gateT[:, half * BANK:(half + 1) * BANK], aux[half][0:E, :])
                    last.then_inc(gateT_ready, 1)

        @block.vector
        def _(dve):
            normalize_dve(nc, dve, y[:], lat[:], square[:], stats, var_ready, std_ready, 1).then_inc(y_ready, 1)
            dve.wait_ge(logits_done, 1)
            scores = aux[0][:, 0:TILES * E].rearrange("p (t e) -> p t e", e=E)
            peak, total = norm[:, 0, :], norm[:, 1, :]
            if bg is not None:
                nc.vector.tensor_tensor(gate[:], scores, over_tiles(bg_sb[:], TILES), ALU.add)
            else:
                nc.vector.tensor_copy(gate[:], scores)
            dve.drain()
            if swiglu:
                top2_mask_dve(nc, dve, gate[:], core.rank, -3e38, mask[:], work[:])
            nc.vector.tensor_reduce(peak, gate[:], AX, ALU.max)
            dve.drain()
            nc.vector.tensor_tensor(prob[:], gate[:], over_last(peak, E), ALU.subtract).then_inc(shifted, 1)
            dve.wait_ge(exp_done, 1)
            if swiglu:
                nc.vector.tensor_tensor(prob[:], prob[:], mask[:], ALU.mult)
                dve.drain()
            nc.vector.tensor_reduce(total, prob[:], AX, ALU.add)
            dve.drain()
            nc.vector.reciprocal(total, total)
            dve.drain()
            nc.vector.tensor_tensor(prob[:], prob[:], over_last(total, E), ALU.mult)
            dve.drain()
            if swiglu:
                nc.vector.tensor_copy(gate[:], prob[:])
            else:
                top2_mask_dve(nc, dve, prob[:], core.rank, -4.0, mask[:], work[:])
                if kind == "relu":
                    nc.vector.tensor_tensor(gate[:], prob[:], mask[:], ALU.mult).then_inc(gate_ready, 1)
                else:
                    nc.vector.tensor_tensor(prob[:], prob[:], mask[:], ALU.mult)
                    dve.drain()
                    nc.vector.tensor_reduce(total, prob[:], AX, ALU.add)
                    dve.drain()
                    nc.vector.tensor_scalar(total, total, 1e-12, None, ALU.max)
                    dve.drain()
                    nc.vector.reciprocal(total, total)
                    dve.drain()
                    nc.vector.tensor_tensor(gate[:], prob[:], over_last(total, E), ALU.mult).then_inc(gate_ready, 1)
            dve.drain()

            def gate_products(e):
                for c in range(C):
                    j = e * C + c
                    dve.wait_ge(silu_done, j + 1)
                    dve.wait_ge(hid_done, 4 * (j + 1))
                    nc.vector.tensor_tensor(hT[:, e % 2, c, :], hid[1][:], silu[:], ALU.mult).then_inc(h_ready, 1)

            def mix_in(e):
                dve.wait_ge(mix_done, e + 1)
                if e == E:
                    nc.vector.tensor_tensor(acc[:], mix[:], acc[:], ALU.add)
                    return
                weight = over_last(gate[:, :, e], D)
                if e == 0:
                    nc.vector.tensor_tensor(acc[:], mix[:], weight, ALU.mult).then_inc(mix_used, 1)
                else:
                    nc.vector.tensor_tensor(gated[:], mix[:], weight, ALU.mult).then_inc(mix_used, 1)
                    dve.drain()
                    nc.vector.tensor_tensor(acc[:], acc[:], gated[:], ALU.add)
                dve.drain()

            if swiglu:
                gate_products(0)
            for e in range(E):
                if swiglu and e + 1 < E:
                    gate_products(e + 1)
                mix_in(e)
            if not swiglu:
                mix_in(E)
                dve.drain()
            nc.vector.tensor_tensor(lat[:], lat[:], acc[:], ALU.add)


def turn_tiles_pe(nc, pe, ident, source, banks, ready, ready_at, turned):
    pe.wait_ge(ready, ready_at)
    for t in range(source.shape[1]):
        turn = nc.tensor.transpose(banks[t // 4][:, (t % 4) * P:(t % 4 + 1) * P], source[:, t, :], ident)
        if t % 4 == 3:
            turn.then_inc(turned, 1)


def keep_turned_act(nc, act, out, banks, turned, turned_at, kept, scale=None, bias=None):
    for half in range(len(banks)):
        act.wait_ge(turned, turned_at + half)
        dst = out[:, half * BANK:(half + 1) * BANK]
        if scale is None:
            nc.scalar.copy(dst, banks[half][:]).then_inc(kept, 1)
        else:
            nc.scalar.activation(dst, banks[half][:], ACT.Identity, bias=bias, scale=scale).then_inc(kept, 1)


def column(ap):
    return ap.rearrange("(p a) -> p a", a=1)


def mlstm_stage(core, name, w):
    nc, lat = core.nc, core.lat
    NH, DQK, DV, CAP = 8, 8, 16, 15.0
    HC = 2 * DQK + DV + 2
    Q, K, V, IG, FG = 0, DQK, 2 * DQK, HC - 2, HC - 1
    POOL_KEYS, OWN_KEYS = range(5, DQK), range(5)
    with ExitStack() as ctx:
        s = Stage(nc, ctx, name)
        y, square, yT = s.sb("y", [P, TILES, D]), s.sb("square", [P, TILES, D]), s.sb("yT", [P, TOKENS])
        stats = s.sb("stats", [P, 4, TILES])
        wq_rows, wk_rows, wv_rows = s.sb("wq_rows", [NH * DQK, D]), s.sb("wk_rows", [NH * DQK, D]), s.sb("wv_rows", [D, D])
        wi_rows, wf_rows = s.sb("wi_rows", [NH, D]), s.sb("wf_rows", [NH, D])
        wog_rows, wout_rows = s.sb("wog_rows", [D, D]), s.sb("wout_rows", [D, D])
        gate_bias = s.sb("gate_bias", [P, 2, NH])
        gain, shift = s.sb("gain", [P, D]), s.sb("shift", [P, D])
        headsT = s.sb("headsT", [D, NH, HC])
        wogT, woutT = s.sb("wogT", [D, D]), s.sb("woutT", [D, D])
        proj = s.sb("proj", [P, TILES, NH, HC])
        out_gate = s.sb("out_gate", [P, TILES, D])
        seq = s.sb("seq", [P, SEQ, HC])
        peak = s.sb("peak", [P, 1 + SEQ])
        decay = s.sb("decay", [P, 3, SEQ])
        decay_v = s.sb("decay_v", [P, DV, SEQ])
        k_in, q_scaled, n_mem = s.sb("k_in", [P, DQK, SEQ]), s.sb("q_scaled", [P, DQK, SEQ]), s.sb("n_mem", [P, DQK, SEQ])
        memory = s.sb("memory", [P, DQK, DV, SEQ])
        den = s.sb("den", [P, 2, SEQ])
        h_seq, h_tok = s.sb("h_seq", [P, SEQ, DV]), s.sb("h_tok", [P, TILES, D])
        hT = s.sb("hT", [P, TOKENS])
        bank = [s.ps(f"bank{i}", [P, BANK]) for i in range(8)]
        seq_dram = nc.dram_tensor(f"{name}_seq_rows", (TOKENS, NH * HC), F32, kind="Internal").ap()
        h_dram = nc.dram_tensor(f"{name}_h_rows", (BATCHES, SEQ, NH, DV), F32, kind="Internal").ap()

        loaded, var_ready, std_ready = s.sem("loaded"), s.sem("var_ready"), s.sem("std_ready")
        y_ready, y_turned, yT_kept = s.sem("y_ready"), s.sem("y_turned"), s.sem("yT_kept")
        w_turned, w_kept = s.sem("w_turned"), s.sem("w_kept")
        proj_done, proj_kept, og_done = s.sem("proj_done"), s.sem("proj_kept"), s.sem("og_done")
        biased, capped, gates_ready = s.sem("biased"), s.sem("capped"), s.sem("gates_ready")
        seq_stored, seq_loaded = s.sem("seq_stored"), s.sem("seq_loaded")
        exponents, exps_done = s.sem("exponents"), s.sem("exps_done")
        keys_ready, rows_in, scanned = s.sem("keys_ready"), s.sem("rows_in"), s.sem("scanned")
        read_pool, read_own, num_done = s.sem("read_pool"), s.sem("read_own"), s.sem("num_done")
        h_ready, h_stored, h_loaded = s.sem("h_ready"), s.sem("h_stored"), s.sem("h_loaded")
        og_ready, h_gated, h_turned, hT_kept, out_done = (s.sem("og_ready"), s.sem("h_gated"), s.sem("h_turned"),
                                                          s.sem("hT_kept"), s.sem("out_done"))
        LOADS = 11
        block = s.block()

        @block.sync
        def _(sp):
            for dst, src in ((wq_rows, "Wq"), (wk_rows, "Wk"), (wv_rows, "Wv"), (wi_rows, "Wi"), (wf_rows, "Wf"),
                             (wog_rows, "Wog"), (wout_rows, "Wout")):
                sp.dma_start(dst[:], w[src]).then_inc(loaded, 16)
            sp.dma_start(gate_bias[:, 0, :], w["bi"].partition_broadcast(P)).then_inc(loaded, 16)
            sp.dma_start(gate_bias[:, 1, :], w["bf"].partition_broadcast(P)).then_inc(loaded, 16)
            sp.dma_start(gain[:], w["ln_w"].partition_broadcast(P)).then_inc(loaded, 16)
            sp.dma_start(shift[:], w["ln_b"].partition_broadcast(P)).then_inc(loaded, 16)
            sp.wait_ge(gates_ready, 1)
            sp.dma_start(seq_dram.rearrange("(t p) c -> p t c", p=P), proj[:].rearrange("p t h c -> p t (h c)"))\
                .then_inc(seq_stored, 16)
            sp.wait_ge(seq_stored, 16)
            for h in range(NH):
                sp.dma_start(seq[h * BATCHES:(h + 1) * BATCHES], seq_dram.rearrange("(b t) (h c) -> h b t c", t=SEQ, c=HC)[h])\
                    .then_inc(seq_loaded, 16)
            sp.wait_ge(h_ready, 1)
            for h in range(NH):
                sp.dma_start(h_dram[:, :, h, :], h_seq[h * BATCHES:(h + 1) * BATCHES]).then_inc(h_stored, 16)
            sp.wait_ge(h_stored, 16 * NH)
            sp.dma_start(h_tok[:], h_dram.rearrange("(t b) i h v -> (b i) t (h v)", b=2)).then_inc(h_loaded, 16)

        @block.tensor
        def _(pe):
            pe.wait_ge(loaded, 16 * LOADS)
            at = 0
            for rows in (wq_rows, wk_rows, wv_rows, wi_rows, wf_rows):
                n = rows.shape[0]
                turn = nc.tensor.transpose(bank[2][:, at:at + n], rows[:], core.ident[0:n, 0:n])
                at += n
            turn.then_inc(w_turned, 1)
            nc.tensor.transpose(bank[3][:, 0:D], wog_rows[:], core.ident[:])
            nc.tensor.transpose(bank[3][:, D:2 * D], wout_rows[:], core.ident[:]).then_inc(w_turned, 1)
            turn_tiles_pe(nc, pe, core.ident[:], y[:], bank[0:2], y_ready, 1, y_turned)
            pe.wait_ge(w_kept, 2)
            pe.wait_ge(yT_kept, 2)
            heads = headsT[:].rearrange("d h c -> d (h c)")
            for t in range(TILES):
                if t >= 4:
                    pe.wait_ge(proj_kept, t - 3)
                nc.tensor.matmul(bank[4 + t % 4][:, 0:NH * HC], yT[:, t * P:(t + 1) * P], heads, start=True, stop=True)\
                    .then_inc(proj_done, 1)
            for t in range(TILES):
                mm = nc.tensor.matmul(bank[t // 4][:, (t % 4) * D:(t % 4 + 1) * D], yT[:, t * P:(t + 1) * P], wogT[:],
                                      start=True, stop=True)
            mm.then_inc(og_done, 1)
            for n, k in enumerate((*POOL_KEYS, *OWN_KEYS)):
                if k in POOL_KEYS:
                    pe.wait_ge(read_pool, n + 1)
                else:
                    pe.wait_ge(read_own, n + 1 - len(POOL_KEYS))
                for half in range(2):
                    values = memory[:, k, half * DV // 2:(half + 1) * DV // 2, :].rearrange("p v t -> p (v t)")
                    mm = nc.tensor.matmul(bank[6 + half][:], core.ident[:], values, start=(n == 0), stop=(n == DQK - 1))
            mm.then_inc(num_done, 1)
            turn_tiles_pe(nc, pe, core.ident[:], h_tok[:], bank[2:4], h_gated, 1, h_turned)
            pe.wait_ge(hT_kept, 2)
            for t in range(TILES):
                mm = nc.tensor.matmul(bank[4 + t // 4][:, (t % 4) * D:(t % 4 + 1) * D], hT[:, t * P:(t + 1) * P], woutT[:],
                                      start=True, stop=True)
            mm.then_inc(out_done, 1)

        @block.scalar
        def _(act):
            normalize_act(nc, act, core.eps(EPS_5), TILES, stats, var_ready, std_ready, 1)
            act.wait_ge(w_turned, 2)
            at = 0
            for c, n in ((Q, DQK), (K, DQK), (V, DV), (IG, 1), (FG, 1)):
                last = nc.scalar.copy(headsT[:, :, c:c + n], bank[2][:, at:at + NH * n].rearrange("d (h c) -> d h c", c=n))
                at += NH * n
            last.then_inc(w_kept, 1)
            nc.scalar.copy(wogT[:], bank[3][:, 0:D])
            nc.scalar.copy(woutT[:], bank[3][:, D:2 * D]).then_inc(w_kept, 1)
            keep_turned_act(nc, act, yT, bank[0:2], y_turned, 1, yT_kept)
            for t in range(TILES):
                act.wait_ge(proj_done, t + 1)
                nc.scalar.copy(proj[:, t].rearrange("p h c -> p (h c)"), bank[4 + t % 4][:, 0:NH * HC])\
                    .then_inc(proj_kept, 1)
            act.wait_ge(biased, 1)
            nc.scalar.activation(proj[:, :, :, IG:HC], proj[:, :, :, IG:HC], ACT.Tanh, scale=1.0 / CAP)\
                .then_inc(capped, 1)
            act.wait_ge(og_done, 1)
            for half in range(2):
                last = nc.scalar.activation(out_gate[:, 4 * half:4 * half + 4, :],
                                            bank[half][:].rearrange("p (t d) -> p t d", d=D), ACT.Sigmoid)
            last.then_inc(og_ready, 1)
            act.wait_ge(exponents, 1)
            nc.scalar.activation(decay[:], decay[:], ACT.Exp).then_inc(exps_done, 1)
            normalize_act(nc, act, core.eps(EPS_6), TILES, stats, var_ready, std_ready, 2)
            keep_turned_act(nc, act, hT, bank[2:4], h_turned, 1, hT_kept)

        @block.gpsimd
        def _(pool):
            by_v = seq[:, :, V:V + DV].rearrange("p t v -> p v t")
            pool.wait_ge(keys_ready, 1)
            for k in POOL_KEYS:
                nc.gpsimd.tensor_tensor(memory[:, k], over_tiles(k_in[:, k, :], DV), by_v, ALU.mult).then_inc(rows_in, 1)
            for n, k in enumerate(POOL_KEYS):
                pool.wait_ge(scanned, n + 1)
                nc.gpsimd.tensor_tensor(memory[:, k], memory[:, k], over_tiles(q_scaled[:, k, :], DV), ALU.mult)\
                    .then_inc(read_pool, 1)

        @block.vector
        def _(dve):
            normalize_dve(nc, dve, y[:], lat[:], square[:], stats, var_ready, std_ready, 1).then_inc(y_ready, 1)
            dve.wait_ge(loaded, 16 * LOADS)
            dve.wait_ge(proj_kept, TILES)
            for n, c in enumerate((IG, FG)):
                last = nc.vector.tensor_tensor(proj[:, :, :, c], proj[:, :, :, c], over_tiles(gate_bias[:, n, :], TILES),
                                               ALU.add)
            last.then_inc(biased, 1)
            dve.wait_ge(capped, 1)
            nc.vector.tensor_scalar(proj[:, :, :, IG:HC], proj[:, :, :, IG:HC], CAP, None, ALU.mult).then_inc(gates_ready, 1)
            dve.wait_ge(seq_loaded, 16 * NH)
            i_gate, f_gate = seq[:, :, IG], seq[:, :, FG]
            nc.vector.memset(peak[:, 0:1], 0.0)
            nc.vector.tensor_tensor_scan(peak[:, 1:], f_gate, i_gate, 0.0, ALU.add, ALU.max)
            dve.drain()
            nc.vector.tensor_tensor(decay[:, 0, :], f_gate, peak[:, 0:SEQ], ALU.add)
            dve.drain()
            nc.vector.tensor_tensor(decay[:, 0, :], decay[:, 0, :], peak[:, 1:], ALU.subtract)
            nc.vector.tensor_tensor(decay[:, 1, :], i_gate, peak[:, 1:], ALU.subtract)
            nc.vector.tensor_scalar(decay[:, 2, :], peak[:, 1:], -1.0, None, ALU.mult).then_inc(exponents, 1)
            by_k = seq[:, :, K:K + DQK].rearrange("p t k -> p k t")
            by_q = seq[:, :, Q:Q + DQK].rearrange("p t k -> p k t")
            by_v = seq[:, :, V:V + DV].rearrange("p t v -> p v t")
            nc.vector.tensor_scalar(q_scaled[:], by_q, DQK ** -0.5, None, ALU.mult)
            dve.wait_ge(exps_done, 1)
            nc.vector.tensor_tensor(k_in[:], by_k, over_tiles(decay[:, 1, :], DQK), ALU.mult).then_inc(keys_ready, 1)
            nc.vector.tensor_copy(decay_v[:], over_tiles(decay[:, 0, :], DV))
            dve.drain()
            nc.vector.memset(decay_v[:, :, 0:1], 0.0)
            for k in OWN_KEYS:
                nc.vector.tensor_tensor(memory[:, k], over_tiles(k_in[:, k, :], DV), by_v, ALU.mult)
            dve.drain()
            flat = "p a t -> p (a t)"

            def scan(k):
                return nc.vector.tensor_tensor_scan(memory[:, k].rearrange(flat), decay_v[:].rearrange(flat),
                                                    memory[:, k].rearrange(flat), 0.0, ALU.mult, ALU.add)

            for n, k in enumerate(POOL_KEYS):
                dve.wait_ge(rows_in, n + 1)
                scan(k).then_inc(scanned, 1)
            for k in OWN_KEYS:
                scan(k)
                dve.drain()
                nc.vector.tensor_tensor(memory[:, k], memory[:, k], over_tiles(q_scaled[:, k, :], DV), ALU.mult)\
                    .then_inc(read_own, 1)
            nc.vector.tensor_tensor_scan(n_mem[:].rearrange(flat), decay_v[:, 0:DQK, :].rearrange(flat),
                                         k_in[:].rearrange(flat), 0.0, ALU.mult, ALU.add)
            dve.drain()
            nc.vector.tensor_tensor(n_mem[:], n_mem[:], q_scaled[:], ALU.mult)
            dve.drain()
            nc.vector.tensor_reduce(den[:, 0, :], n_mem[:].rearrange("p k t -> p t k"), AX, ALU.add)
            dve.drain()
            nc.vector.scalar_tensor_tensor(den[:, 1, :], den[:, 0, :], -1.0, den[:, 0, :], ALU.mult, ALU.max)
            dve.drain()
            nc.vector.tensor_tensor(den[:, 0, :], den[:, 1, :], decay[:, 2, :], ALU.max)
            dve.drain()
            nc.vector.tensor_scalar(den[:, 0, :], den[:, 0, :], 1e-6, None, ALU.add)
            dve.drain()
            nc.vector.reciprocal(den[:, 1, :], den[:, 0, :])
            dve.drain()
            dve.wait_ge(num_done, 1)
            for half in range(2):
                own = slice(half * DV // 2, (half + 1) * DV // 2)
                last = nc.vector.tensor_tensor(h_seq[:, :, own].rearrange("p t v -> p v t"),
                                               bank[6 + half][:].rearrange("p (v t) -> p v t", t=SEQ),
                                               over_tiles(den[:, 1, :], DV // 2), ALU.mult)
            last.then_inc(h_ready, 1)
            dve.wait_ge(h_loaded, 16)
            normalize_dve(nc, dve, h_tok[:], h_tok[:], square[:], stats, var_ready, std_ready, 2)
            dve.drain()
            nc.vector.tensor_tensor(h_tok[:], h_tok[:], over_tiles(gain[:], TILES), ALU.mult)
            dve.drain()
            nc.vector.tensor_tensor(h_tok[:], h_tok[:], over_tiles(shift[:], TILES), ALU.add)
            dve.drain()
            dve.wait_ge(og_ready, 1)
            nc.vector.tensor_tensor(h_tok[:], h_tok[:], out_gate[:], ALU.mult).then_inc(h_gated, 1)
            dve.wait_ge(out_done, 1)
            for half in range(2):
                part = lat[:, 4 * half:4 * half + 4, :]
                nc.vector.tensor_tensor(part, part, bank[4 + half][:].rearrange("p (t d) -> p t d", d=D), ALU.add)


def causal_exp_stage(core, name, w):
    nc, lat = core.nc, core.lat
    INNER = 16
    with ExitStack() as ctx:
        s = Stage(nc, ctx, name)
        y, square, yT = s.sb("y", [P, TILES, D]), s.sb("square", [P, TILES, D]), s.sb("yT", [P, TOKENS])
        stats = s.sb("stats", [P, 4, TILES])
        rows = s.sb("rows", [P, 2, D])
        wT = s.sb("wT", [P, 2 * D])
        angle = s.sb("angle", [P, 2, D])
        turn16 = s.sb("turn16", [P, 2, D], BF16)
        ident16 = s.sb("ident16", [P, P], BF16)
        causal = s.sb("causal", [P, SEQ])
        fc1 = s.sb("fc1", [P, 2, INNER])
        fc2_rows = s.sb("fc2_rows", [D, INNER])
        fc2T = s.sb("fc2T", [INNER, D])
        fc2_b = s.sb("fc2_b", [P, D])
        qk = s.sb("qk", [P, TILES * 2, D], BF16)
        along = s.sb("along", [P, TILES * 2, D], BF16)
        across = s.sb("across", [P, TILES * 2, D], BF16)
        qkT = s.sb("qkT", [P, TILES * 2, P], BF16)
        exps = s.sb("exps", [P, TILES, SEQ])
        total = s.sb("total", [P, TILES])
        hidden = s.sb("hidden", [P, TILES, INNER])
        hiddenT = s.sb("hiddenT", [INNER, TOKENS])
        bank = [s.ps(f"bank{i}", [P, BANK]) for i in range(6)]
        bank16 = [s.ps(f"bank16_{i}", [P, 8 * P], BF16) for i in range(2)]

        loaded, var_ready, std_ready = s.sem("loaded"), s.sem("var_ready"), s.sem("std_ready")
        y_ready, y_turned, yT_kept = s.sem("y_ready"), s.sem("y_turned"), s.sem("yT_kept")
        w_turned, w_kept, consts_ready = s.sem("w_turned"), s.sem("w_kept"), s.sem("consts_ready")
        qk_done, qk_rounded, qk_turned_by_pos = s.sem("qk_done"), s.sem("qk_rounded"), s.sem("qk_turned_by_pos")
        qk_turned, qkT_kept, scores_done, exps_done = (s.sem("qk_turned"), s.sem("qkT_kept"), s.sem("scores_done"),
                                                       s.sem("exps_done"))
        hidden_ready, hidden_turned, hiddenT_kept, out_done = (s.sem("hidden_ready"), s.sem("hidden_turned"),
                                                               s.sem("hiddenT_kept"), s.sem("out_done"))
        LOADS = 8
        block = s.block()

        @block.sync
        def _(sp):
            for dst, src in ((rows[:, 0, :], w["Wq"]), (rows[:, 1, :], w["Wk"]), (fc2_rows[:], w["fc2_w"]),
                             (angle[:], core.w["c_rope32"]), (causal[:], core.w["c_causal"]),
                             (fc1[:, 0, :], w["fc1_w"].rearrange("n a -> (n a)").partition_broadcast(P)),
                             (fc1[:, 1, :], w["fc1_b"].partition_broadcast(P)),
                             (fc2_b[:], w["fc2_b"].partition_broadcast(P))):
                sp.dma_start(dst, src).then_inc(loaded, 16)

        @block.tensor
        def _(pe):
            pe.wait_ge(loaded, 16 * LOADS)
            for n in range(2):
                nc.tensor.transpose(bank[2][:, n * D:(n + 1) * D], rows[:, n, :], core.ident[:])
            nc.tensor.transpose(bank[3][0:INNER, 0:D], fc2_rows[:], core.ident[:]).then_inc(w_turned, 1)
            turn_tiles_pe(nc, pe, core.ident[:], y[:], bank[0:2], y_ready, 1, y_turned)
            pe.wait_ge(w_kept, 1)
            pe.wait_ge(yT_kept, 2)
            for t in range(TILES):
                mm = nc.tensor.matmul(bank[2 + t // 2][:, (t % 2) * 2 * D:(t % 2 + 1) * 2 * D], yT[:, t * P:(t + 1) * P],
                                      wT[:], start=True, stop=True)
                if t % 2:
                    mm.then_inc(qk_done, 1)
            pe.wait_ge(qk_turned_by_pos, 1)
            for n in range(2 * TILES):
                turn = nc.tensor.transpose(bank16[n // 8][:, (n % 8) * P:(n % 8 + 1) * P], qk[:, n, :], ident16[:])
                if n % 8 == 7:
                    turn.then_inc(qk_turned, 1)
            pe.wait_ge(qkT_kept, 2)
            for b in range(BATCHES):
                t, rows_of = b // 2, slice((b % 2) * SEQ, (b % 2 + 1) * SEQ)
                mm = nc.tensor.matmul(bank[0][rows_of, t * SEQ:(t + 1) * SEQ], qkT[:, 2 * t, rows_of],
                                      qkT[:, 2 * t + 1, rows_of], start=True, stop=True)
            mm.then_inc(scores_done, 1)
            pe.wait_ge(hidden_ready, 1)
            for t in range(TILES):
                turn = nc.tensor.transpose(bank[2 + t // 4][0:INNER, (t % 4) * P:(t % 4 + 1) * P], hidden[:, t, :],
                                           core.ident[:])
            turn.then_inc(hidden_turned, 1)
            pe.wait_ge(hiddenT_kept, 2)
            for t in range(TILES):
                mm = nc.tensor.matmul(bank[4 + t // 4][:, (t % 4) * D:(t % 4 + 1) * D], hiddenT[:, t * P:(t + 1) * P],
                                      fc2T[:], start=True, stop=True)
            mm.then_inc(out_done, 1)

        @block.scalar
        def _(act):
            normalize_act(nc, act, core.eps(EPS_5), TILES, stats, var_ready, std_ready, 1)
            act.wait_ge(w_turned, 1)
            nc.scalar.copy(wT[:], bank[2][:, 0:2 * D])
            nc.scalar.copy(fc2T[:], bank[3][0:INNER, 0:D]).then_inc(w_kept, 1)
            keep_turned_act(nc, act, yT, bank[0:2], y_turned, 1, yT_kept)
            for k in range(TILES // 2):
                act.wait_ge(qk_done, k + 1)
                nc.scalar.copy(qk[:, 4 * k:4 * k + 4, :], bank[2 + k][:].rearrange("p (n d) -> p n d", d=D))\
                    .then_inc(qk_rounded, 1)
            for half in range(2):
                act.wait_ge(qk_turned, half + 1)
                nc.scalar.copy(qkT[:, 8 * half:8 * half + 8, :], bank16[half][:].rearrange("p (n q) -> p n q", q=P))\
                    .then_inc(qkT_kept, 1)
            act.wait_ge(scores_done, 1)
            nc.scalar.activation(exps[:], bank[0][:].rearrange("p (t j) -> p t j", j=SEQ), ACT.Exp, scale=D ** -0.5)\
                .then_inc(exps_done, 1)
            act.wait_ge(hidden_turned, 1)
            for half in range(2):
                nc.scalar.copy(hiddenT[:, half * BANK:(half + 1) * BANK], bank[2 + half][0:INNER, :])\
                    .then_inc(hiddenT_kept, 1)

        @block.vector
        def _(dve):
            normalize_dve(nc, dve, y[:], lat[:], square[:], stats, var_ready, std_ready, 1).then_inc(y_ready, 1)
            dve.wait_ge(loaded, 16 * LOADS)
            nc.vector.tensor_copy(turn16[:], angle[:])
            nc.vector.tensor_copy(ident16[:], core.ident[:])
            dve.drain()
            half = D // 2
            dve.wait_ge(qk_rounded, TILES // 2)
            nc.vector.tensor_tensor(along[:], qk[:], over_tiles(turn16[:, 0, :], 2 * TILES), ALU.mult)
            nc.vector.tensor_tensor(across[:, :, 0:half], qk[:, :, half:D], over_tiles(turn16[:, 1, 0:half], 2 * TILES),
                                    ALU.mult)
            nc.vector.tensor_tensor(across[:, :, half:D], qk[:, :, 0:half], over_tiles(turn16[:, 1, half:D], 2 * TILES),
                                    ALU.mult)
            dve.drain()
            nc.vector.tensor_tensor(qk[:], along[:], across[:], ALU.add).then_inc(qk_turned_by_pos, 1)
            dve.wait_ge(exps_done, 1)
            nc.vector.tensor_tensor(exps[:], exps[:], over_tiles(causal[:], TILES), ALU.mult)
            dve.drain()
            nc.vector.tensor_reduce(total[:], exps[:], AX, ALU.add)
            dve.drain()
            nc.vector.tensor_tensor(hidden[:], over_last(total[:], INNER), over_tiles(fc1[:, 0, :], TILES), ALU.mult)
            dve.drain()
            nc.vector.tensor_tensor(hidden[:], hidden[:], over_tiles(fc1[:, 1, :], TILES), ALU.add)
            dve.drain()
            nc.vector.tensor_scalar(hidden[:], hidden[:], 0.0, None, ALU.max).then_inc(hidden_ready, 1)
            dve.wait_ge(out_done, 1)
            nc.vector.tensor_tensor(lat[:], lat[:], over_tiles(fc2_b[:], TILES), ALU.add)
            dve.drain()
            for h in range(2):
                part = lat[:, 4 * h:4 * h + 4, :]
                nc.vector.tensor_tensor(part, part, bank[4 + h][:].rearrange("p (t d) -> p t d", d=D), ALU.add)


def projected_mlp_stage(core, name, w):
    nc, lat = core.nc, core.lat
    HID = 512
    C = HID // P
    with ExitStack() as ctx:
        s = Stage(nc, ctx, name)
        x, z, square, zT = (s.sb("x", [P, TILES, D]), s.sb("z", [P, TILES, D]), s.sb("square", [P, TILES, HID]),
                            s.sb("zT", [P, TOKENS]))
        stats = s.sb("stats", [P, 4, TILES])
        proj_rows, fc1_rows, fc2_rows = s.sb("proj_rows", [P, D]), s.sb("fc1_rows", [P, C, D]), s.sb("fc2_rows", [P, HID])
        projT, fc1T, fc2T = s.sb("projT", [P, D]), s.sb("fc1T", [P, HID]), s.sb("fc2T", [P, C, D])
        row = {n: s.sb(n, [P, D]) for n in ("proj_b", "gamma1", "gamma2", "fc2_b")}
        fc1_b = s.sb("fc1_b", [P, HID])
        cols = s.sb("cols", [P, 4 + 2 * C])
        hid = s.sb("hid", [P, TILES, HID])
        hidT = s.sb("hidT", [P, 2, C, P])
        bank = [s.ps(f"bank{i}", [P, BANK]) for i in range(8)]

        loaded, var_ready, std_ready = s.sem("loaded"), s.sem("var_ready"), s.sem("std_ready")
        w_turned, w_kept = s.sem("w_turned"), s.sem("w_kept")
        z_ready, z_turned, zT_kept = s.sem("z_ready"), s.sem("z_turned"), s.sem("zT_kept")
        proj_done, hid_done, hid_biased, gelu_done = s.sem("proj_done"), s.sem("hid_done"), s.sem("hid_biased"), s.sem("gelu_done")
        hid_ready, hid_turned, out_done = s.sem("hid_ready"), s.sem("hid_turned"), s.sem("out_done")
        hidT_act, hidT_dve = s.sem("hidT_act"), s.sem("hidT_dve")
        LOADS = 3 + 5 + 4 + 2

        def half_bank(t, c):
            return bank[4 * (c // (C // 2)) + t % 2][:, c % (C // 2) * P:(c % (C // 2) + 1) * P]

        block = s.block()

        @block.sync
        def _(sp):
            sp.dma_start(proj_rows[:], w["proj_w"]).then_inc(loaded, 16)
            sp.dma_start(fc1_rows[:], w["fc1_w"].rearrange("(c p) d -> p c d", p=P)).then_inc(loaded, 16)
            sp.dma_start(fc2_rows[:], w["fc2_w"]).then_inc(loaded, 16)
            for n, dst in row.items():
                sp.dma_start(dst[:], w[n].partition_broadcast(P)).then_inc(loaded, 16)
            sp.dma_start(fc1_b[:], w["fc1_b"].partition_broadcast(P)).then_inc(loaded, 16)
            with nc.allow_non_contiguous_dma("gain columns"):
                for k, n in enumerate(("ln1_g", "ln1_b", "ln2_g", "ln2_b")):
                    sp.dma_start(cols[:, k:k + 1], column(w[n])).then_inc(loaded, 16)
                for k, n in enumerate(("lnh_g", "lnh_b")):
                    sp.dma_start(cols[:, 4 + k * C:4 + (k + 1) * C], w[n].rearrange("(c p) -> p c", p=P)).then_inc(loaded, 16)

        @block.tensor
        def _(pe):
            pe.wait_ge(loaded, 16 * LOADS)
            for c in range(C):
                nc.tensor.transpose(bank[2][:, c * P:(c + 1) * P], fc1_rows[:, c, :], core.ident[:])
            for c in range(C):
                nc.tensor.transpose(bank[3][:, c * P:(c + 1) * P], fc2_rows[:, c * P:(c + 1) * P], core.ident[:])
            nc.tensor.transpose(bank[4][:, 0:D], proj_rows[:], core.ident[:]).then_inc(w_turned, 1)
            turn_tiles_pe(nc, pe, core.ident[:], z[:], bank[0:2], z_ready, 1, z_turned)
            pe.wait_ge(zT_kept, 2)
            pe.wait_ge(w_kept, 1)
            for t in range(TILES):
                mm = nc.tensor.matmul(bank[2 + t // 4][:, (t % 4) * D:(t % 4 + 1) * D], zT[:, t * P:(t + 1) * P], projT[:],
                                      start=True, stop=True)
            mm.then_inc(proj_done, 1)
            turn_tiles_pe(nc, pe, core.ident[:], z[:], bank[0:2], z_ready, 2, z_turned)
            pe.wait_ge(zT_kept, 4)
            for t in range(TILES):
                if t >= 4:
                    pe.wait_ge(hid_biased, t - 3)
                nc.tensor.matmul(bank[4 + t % 4][:], zT[:, t * P:(t + 1) * P], fc1T[:], start=True, stop=True)\
                    .then_inc(hid_done, 1)
            for t in range(TILES + 1):
                if t < TILES:
                    pe.wait_ge(hid_ready, t + 1)
                    if t >= 2:
                        pe.wait_ge(hidT_act, t - 1)
                        pe.wait_ge(hidT_dve, t - 1)
                    for c in range(C):
                        turn = nc.tensor.transpose(half_bank(t, c), hid[:, t, c * P:(c + 1) * P],
                                                   core.ident[:])
                    turn.then_inc(hid_turned, 1)
                if t >= 1:
                    u = t - 1
                    pe.wait_ge(hidT_act, t)
                    pe.wait_ge(hidT_dve, t)
                    for c in range(C):
                        mm = nc.tensor.matmul(bank[2 + u // 4][:, (u % 4) * D:(u % 4 + 1) * D], hidT[:, u % 2, c, :],
                                              fc2T[:, c, :], start=(c == 0), stop=(c == C - 1))
            mm.then_inc(out_done, 1)

        @block.scalar
        def _(act):
            normalize_act(nc, act, core.eps(EPS_5), TILES, stats, var_ready, std_ready, 1)
            normalize_act(nc, act, core.eps(EPS_5), TILES, stats, var_ready, std_ready, 2)
            act.wait_ge(w_turned, 1)
            nc.scalar.copy(fc1T[:], bank[2][:])
            nc.scalar.copy(fc2T[:].rearrange("p c d -> p (c d)"), bank[3][:])
            nc.scalar.copy(projT[:], bank[4][:, 0:D]).then_inc(w_kept, 1)
            act.wait_ge(loaded, 16 * LOADS)
            keep_turned_act(nc, act, zT, bank[0:2], z_turned, 1, zT_kept, scale=cols[:, 0:1], bias=cols[:, 1:2])
            normalize_act(nc, act, core.eps(EPS_5), TILES, stats, var_ready, std_ready, 3)
            keep_turned_act(nc, act, zT, bank[0:2], z_turned, 3, zT_kept, scale=cols[:, 2:3], bias=cols[:, 3:4])
            for t in range(TILES):
                act.wait_ge(hid_biased, t + 1)
                nc.scalar.activation(hid[:, t, :], hid[:, t, :], ACT.Gelu).then_inc(gelu_done, 1)
            normalize_act(nc, act, core.eps(EPS_5), TILES, stats, var_ready, std_ready, 4)
            for t in range(TILES):
                act.wait_ge(hid_turned, t + 1)
                for c in range(C // 2):
                    kept = nc.scalar.activation(hidT[:, t % 2, c, :], half_bank(t, c), ACT.Identity,
                                                bias=cols[:, 4 + C + c:5 + C + c], scale=cols[:, 4 + c:5 + c])
                kept.then_inc(hidT_act, 1)

        @block.vector
        def _(dve):
            first = square[:, :, 0:D]
            normalize_dve(nc, dve, x[:], lat[:], first, stats, var_ready, std_ready, 1)
            dve.drain()
            normalize_dve(nc, dve, z[:], x[:], first, stats, var_ready, std_ready, 2).then_inc(z_ready, 1)
            dve.wait_ge(loaded, 16 * LOADS)
            dve.wait_ge(proj_done, 1)
            for half in range(2):
                nc.vector.tensor_tensor(z[:, 4 * half:4 * half + 4, :], bank[2 + half][:].rearrange("p (t d) -> p t d", d=D),
                                        over_tiles(row["proj_b"][:], 4), ALU.add)
            dve.drain()
            nc.vector.tensor_tensor(z[:], z[:], over_tiles(row["gamma1"][:], TILES), ALU.mult)
            dve.drain()
            nc.vector.tensor_tensor(x[:], x[:], z[:], ALU.add)
            dve.drain()
            normalize_dve(nc, dve, z[:], x[:], first, stats, var_ready, std_ready, 3).then_inc(z_ready, 1)
            moments, mean_var = square[:, :, 0:6], square[:, :, 6:8]
            var, std, rstd = (stats[:, k, :] for k in (1, 2, 3))

            def measure(t):
                dve.wait_ge(gelu_done, t + 1)
                nc.vector.bn_stats(moments[:, t, :], hid[:, t, :])

            for t in range(TILES):
                dve.wait_ge(hid_done, t + 1)
                nc.vector.tensor_tensor(hid[:, t, :], bank[4 + t % 4][:], fc1_b[:], ALU.add).then_inc(hid_biased, 1)
                if t >= 2:
                    measure(t - 2)
            nc.vector.tensor_tensor(lat[:], lat[:], x[:], ALU.add)
            measure(TILES - 2)
            measure(TILES - 1)
            dve.drain()
            for t in range(TILES):
                nc.vector.bn_aggr(mean_var[:, t, :], moments[:, t, :])
            dve.drain()
            nc.vector.tensor_copy(var, mean_var[:, :, 1]).then_inc(var_ready, 1)
            dve.wait_ge(std_ready, 4)
            nc.vector.reciprocal(rstd, std)
            dve.drain()

            def normalise(t):
                nc.vector.tensor_scalar(hid[:, t, :], hid[:, t, :], mean_var[:, t, 0:1], rstd[:, t:t + 1],
                                        ALU.subtract, ALU.mult).then_inc(hid_ready, 1)

            normalise(0)
            normalise(1)
            for t in range(TILES):
                if t + 2 < TILES:
                    normalise(t + 2)
                dve.wait_ge(hid_turned, t + 1)
                for c in range(C // 2, C):
                    kept = nc.vector.tensor_scalar(hidT[:, t % 2, c, :], half_bank(t, c), cols[:, 4 + c:5 + c],
                                                   cols[:, 4 + C + c:5 + C + c], ALU.mult, ALU.add)
                kept.then_inc(hidT_dve, 1)
            dve.wait_ge(out_done, 1)
            for half in range(2):
                nc.vector.tensor_tensor(z[:, 4 * half:4 * half + 4, :], bank[2 + half][:].rearrange("p (t d) -> p t d", d=D),
                                        over_tiles(row["fc2_b"][:], 4), ALU.add)
            dve.drain()
            nc.vector.tensor_tensor(z[:], z[:], over_tiles(row["gamma2"][:], TILES), ALU.mult)
            dve.drain()
            nc.vector.tensor_tensor(lat[:], lat[:], z[:], ALU.add)


def latent_attention_stage(core, name, w):
    nc, lat = core.nc, core.lat
    NH, L, DH, DHE = 16, 64, 8, 4
    KINDS = ("q", "k", "v")
    UP = 3 * DHE
    WIDTH = (UP, UP, DH)
    AT = (0, NH * UP, 2 * NH * UP)
    DV = DH + 1
    with ExitStack() as ctx:
        s = Stage(nc, ctx, name)
        y, square, yT = s.sb("y", [P, TILES, D]), s.sb("square", [P, TILES, D]), s.sb("yT", [P, TOKENS])
        stats = s.sb("stats", [P, 4, TILES])
        down = s.sb("down", [P, 3, NH * L])
        downT = s.sb("downT", [P, 3, NH // 2, P])
        up = s.sb("up", [P, 3, 2, UP])
        heads = s.sb("heads", [P, 2, NH, UP])
        headsV = s.sb("headsV", [P, NH, DH])
        wc = s.sb("wc", [P, D])
        angle = s.sb("angle", [P, 2, DHE])
        causal = s.sb("causal", [P, SEQ])
        own_head = s.sb("own_head", [P, NH])
        parity = s.sb("parity", [P, D])
        qk = s.sb("qk", [P, TILES, 2, NH, UP])
        qk_rot = s.sb("qk_rot", [P, TILES, 2, NH, DH])
        turned = s.sb("turned", [P, 2, NH, DHE])
        qT, kT = s.sb("qT", [P, TOKENS]), s.sb("kT", [P, TOKENS])
        y_twice = s.sb("y_twice", [P, BATCHES, 2, SEQ])
        v_diag = s.sb("v_diag", [P, BATCHES, NH, DV])
        k_diag = s.sb("k_diag", [P, 4, NH, SEQ])
        prob = s.sb("prob", [P, 2, NH, SEQ])
        peak, rsum = s.sb("peak", [P, 2, NH]), s.sb("rsum", [P, 2, NH])
        probT = s.sb("probT", [P, 2, NH // 2, P])
        mixed, mixedT = s.sb("mixed", [P, TILES, D]), s.sb("mixedT", [P, TOKENS])
        score = [s.ps(f"score{i}", [P, NH * SEQ]) for i in range(2)]
        bank = [s.ps(f"bank{i}", [P, BANK]) for i in range(4)]

        down_loaded, up_loaded, loaded = s.sem("down_loaded"), s.sem("up_loaded"), s.sem("loaded")
        cleared, var_ready, std_ready = s.sem("cleared"), s.sem("var_ready"), s.sem("std_ready")
        y_ready, y_turned, yT_kept = s.sem("y_ready"), s.sem("y_turned"), s.sem("yT_kept")
        up_ready, down_turned, downT_kept, heads_done, heads_kept = (s.sem("up_ready"), s.sem("down_turned"),
                                                                     s.sem("downT_kept"), s.sem("heads_done"),
                                                                     s.sem("heads_kept"))
        qk_done, qk_kept, rot_ready, rot_turned, rotT_kept = (s.sem("qk_done"), s.sem("qk_kept"), s.sem("rot_ready"),
                                                              s.sem("rot_turned"), s.sem("rotT_kept"))
        twice_ready, v_done, v_kept = s.sem("twice_ready"), s.sem("v_done"), s.sem("v_kept")
        k_spread, score_done, shifted, exp_done = (s.sem("k_spread"), s.sem("score_done"), s.sem("shifted"),
                                                   s.sem("exp_done"))
        prob_turned, probT_kept, mixed_done, mixed_kept = (s.sem("prob_turned"), s.sem("probT_kept"), s.sem("mixed_done"),
                                                           s.sem("mixed_kept"))
        mixed_turned, mixedT_kept, out_done = s.sem("mixed_turned"), s.sem("mixedT_kept"), s.sem("out_done")
        DOWN_LOADS, UP_LOADS, LOADS = 3, 2 * 5, 5
        block = s.block()

        @block.sync
        def _(sp):
            for n, kind in enumerate(KINDS):
                sp.dma_start(down[:, n, :], w[f"W{kind}_down"]).then_inc(down_loaded, 16)
            sp.wait_ge(cleared, 1)
            for half in range(2):
                rows = slice(half * L, (half + 1) * L)
                for n, kind in enumerate("qk"):
                    sp.dma_start(up[rows, n, half, 0:DHE], w[f"W{kind}_up_c"]).then_inc(up_loaded, 16)
                    sp.dma_start(up[rows, n, half, DHE:2 * DHE], w[f"W{kind}_up_e"]).then_inc(up_loaded, 16)
                sp.dma_start(up[rows, 2, half, 0:DH], w["Wv_up"]).then_inc(up_loaded, 16)
            sp.dma_start(wc[:], w["Wc"]).then_inc(loaded, 16)
            sp.dma_start(angle[:], core.w["c_rope4"]).then_inc(loaded, 16)
            sp.dma_start(causal[:], core.w["c_causal_add"]).then_inc(loaded, 16)
            sp.dma_start(own_head[:], core.w["c_own_head"]).then_inc(loaded, 16)
            sp.dma_start(parity[:], core.w["c_parity"]).then_inc(loaded, 16)

        @block.tensor
        def _(pe):
            pe.wait_ge(down_loaded, 16 * DOWN_LOADS)
            for j in range(6):
                if j >= 2:
                    pe.wait_ge(downT_kept, j - 1)
                for i in range(4):
                    n, pair = j // 2, (j % 2) * 4 + i
                    turn = nc.tensor.transpose(bank[j % 2][:, i * P:(i + 1) * P], down[:, n, pair * P:(pair + 1) * P],
                                               core.ident[:])
                turn.then_inc(down_turned, 1)
            pe.wait_ge(up_ready, 1)
            pe.wait_ge(downT_kept, 6)
            for n in range(3):
                for pair in range(NH // 2):
                    at = AT[n] + pair * 2 * WIDTH[n]
                    mm = nc.tensor.matmul(bank[2][:, at:at + 2 * WIDTH[n]].rearrange("p (r c) -> p r c", r=2),
                                          downT[:, n, pair, :], up[:, n, :, 0:WIDTH[n]], start=True, stop=True)
            mm.then_inc(heads_done, 1)
            turn_tiles_pe(nc, pe, core.ident[:], y[:], bank[0:2], y_ready, 1, y_turned)
            pe.wait_ge(yT_kept, 2)
            pe.wait_ge(heads_kept, 1)
            for t in range(TILES):
                if t >= 2:
                    pe.wait_ge(qk_kept, t - 1)
                nc.tensor.matmul(bank[2 + t % 2][:, 0:2 * NH * UP], yT[:, t * P:(t + 1) * P],
                                 heads[:].rearrange("p n h c -> p (n h c)"), start=True, stop=True).then_inc(qk_done, 1)
            pe.wait_ge(twice_ready, 1)
            for b in range(BATCHES):
                if b % 4 == 0 and b >= 8:
                    pe.wait_ge(v_kept, b // 4 - 1)
                mm = nc.tensor.matmul(bank[(b // 4) % 2][:, (b % 4) * D:(b % 4 + 1) * D],
                                      y_twice[:, b].rearrange("p n j -> p (n j)"), headsV[:].rearrange("p h d -> p (h d)"),
                                      start=True, stop=True)
                if b % 4 == 3:
                    mm.then_inc(v_done, 1)
            pe.wait_ge(rot_ready, TILES)
            pe.wait_ge(v_kept, 4)
            for j in range(4):
                for i in range(4):
                    t = (j % 2) * 4 + i
                    turn = nc.tensor.transpose(bank[j][:, i * P:(i + 1) * P],
                                               qk_rot[:, t, j // 2].rearrange("p h d -> p (h d)"), core.ident[:])
                turn.then_inc(rot_turned, 1)
            pe.wait_ge(rotT_kept, 4)

            def scores(t):
                if t >= 2:
                    pe.wait_ge(shifted, t - 1)
                pe.wait_ge(k_spread, 2 * t + 2)
                for half in range(2):
                    for b in (2 * t, 2 * t + 1):
                        mm = nc.tensor.matmul(score[t % 2][(b % 2) * SEQ:(b % 2 + 1) * SEQ, half * BANK:(half + 1) * BANK],
                                              qT[:, b * SEQ:(b + 1) * SEQ],
                                              k_diag[:, b % 4].rearrange("p h j -> p (h j)")[:, half * BANK:(half + 1) * BANK],
                                              start=True, stop=True)
                        if half == 1:
                            mm.then_inc(score_done, 1)

            def mix(t):
                pe.wait_ge(exp_done, t + 1)
                for half in range(2):
                    if t >= 1:
                        pe.wait_ge(probT_kept, 2 * (t - 1) + half + 1)
                    for i in range(4):
                        pair = 4 * half + i
                        turn = nc.tensor.transpose(bank[half][:, i * P:(i + 1) * P],
                                                   prob[:, t % 2].rearrange("p h j -> p (h j)")[:, pair * P:(pair + 1) * P],
                                                   core.ident[:])
                    turn.then_inc(prob_turned, 1)
                pe.wait_ge(probT_kept, 2 * t + 2)
                if t >= 2:
                    pe.wait_ge(mixed_kept, t - 1)
                for pair in range(NH // 2):
                    for b in (2 * t, 2 * t + 1):
                        rows = slice((b % 2) * SEQ, (b % 2 + 1) * SEQ)
                        mm = nc.tensor.matmul(bank[2 + t % 2][rows, pair * 2 * DV:(pair + 1) * 2 * DV],
                                              probT[:, t % 2, pair, rows],
                                              v_diag[:, b, 2 * pair:2 * pair + 2, :].rearrange("p h d -> p (h d)"),
                                              start=True, stop=True)
                mm.then_inc(mixed_done, 1)

            scores(0)
            for t in range(TILES):
                if t + 1 < TILES:
                    scores(t + 1)
                mix(t)
            pe.wait_ge(loaded, 16 * LOADS)
            turn_tiles_pe(nc, pe, core.ident[:], mixed[:], bank[0:2], mixed_kept, TILES, mixed_turned)
            pe.wait_ge(mixedT_kept, 2)
            for t in range(TILES):
                mm = nc.tensor.matmul(bank[2 + t // 4][:, (t % 4) * D:(t % 4 + 1) * D], mixedT[:, t * P:(t + 1) * P], wc[:],
                                      start=True, stop=True)
            mm.then_inc(out_done, 1)

        @block.scalar
        def _(act):
            normalize_act(nc, act, core.eps(EPS_5), TILES, stats, var_ready, std_ready, 1)
            for j in range(6):
                act.wait_ge(down_turned, j + 1)
                nc.scalar.copy(downT[:, j // 2, (j % 2) * 4:(j % 2) * 4 + 4, :],
                               bank[j % 2][:].rearrange("p (i d) -> p i d", d=P)).then_inc(downT_kept, 1)
            act.wait_ge(heads_done, 1)
            nc.scalar.copy(heads[:].rearrange("p n h c -> p (n h c)"), bank[2][:, 0:AT[2]])
            nc.scalar.copy(headsV[:].rearrange("p h d -> p (h d)"), bank[2][:, AT[2]:AT[2] + NH * DH]).then_inc(heads_kept, 1)
            keep_turned_act(nc, act, yT, bank[0:2], y_turned, 1, yT_kept)
            act.wait_ge(yT_kept, 2)
            for copy in range(2):
                last = nc.scalar.copy(y_twice[:, :, copy, :], yT[:].rearrange("p (b j) -> p b j", j=SEQ))
            last.then_inc(twice_ready, 1)
            for t in range(TILES):
                act.wait_ge(qk_done, t + 1)
                nc.scalar.copy(qk[:, t].rearrange("p n h c -> p (n h c)"), bank[2 + t % 2][:, 0:2 * NH * UP])\
                    .then_inc(qk_kept, 1)
            for j in range(4):
                act.wait_ge(rot_turned, j + 1)
                nc.scalar.copy((qT if j < 2 else kT)[:, (j % 2) * BANK:(j % 2 + 1) * BANK], bank[j][:]).then_inc(rotT_kept, 1)
            for t in range(TILES):
                act.wait_ge(shifted, t + 1)
                nc.scalar.activation(prob[:, t % 2], prob[:, t % 2], ACT.Exp, scale=DH ** -0.5).then_inc(exp_done, 1)
                for half in range(2):
                    act.wait_ge(prob_turned, 2 * t + half + 1)
                    nc.scalar.copy(probT[:, t % 2, 4 * half:4 * half + 4, :], bank[half][:].rearrange("p (i d) -> p i d", d=P))\
                        .then_inc(probT_kept, 1)
            keep_turned_act(nc, act, mixedT, bank[0:2], mixed_turned, 1, mixedT_kept)

        @block.gpsimd
        def _(pool):
            nc.gpsimd.memset(up[:], 0.0).then_inc(cleared, 1)
            pool.wait_ge(rotT_kept, 4)
            pool.wait_ge(loaded, 16 * LOADS)
            for b in range(BATCHES):
                if b >= 4:
                    pool.wait_ge(score_done, b - 3)
                nc.gpsimd.tensor_tensor(k_diag[:, b % 4], over_tiles(kT[:, b * SEQ:(b + 1) * SEQ], NH),
                                        over_last(own_head[:], SEQ), ALU.mult).then_inc(k_spread, 1)

        @block.vector
        def _(dve):
            normalize_dve(nc, dve, y[:], lat[:], square[:], stats, var_ready, std_ready, 1).then_inc(y_ready, 1)
            dve.wait_ge(up_loaded, 16 * UP_LOADS)
            for half in range(2):
                own = up[half * L:(half + 1) * L, 0:2, half]
                pairs = own[:, :, DHE:2 * DHE].rearrange("p n (a b) -> p n a b", b=2)
                partner = own[:, :, 2 * DHE:UP].rearrange("p n (a b) -> p n a b", b=2)
                nc.vector.tensor_scalar(partner[:, :, :, 0], pairs[:, :, :, 1], -1.0, None, ALU.mult)
                last = nc.vector.tensor_copy(partner[:, :, :, 1], pairs[:, :, :, 0])
            last.then_inc(up_ready, 1)
            dve.wait_ge(loaded, 16 * LOADS)
            for t in range(TILES):
                dve.wait_ge(qk_kept, t + 1)
                cols = qk[:, t].rearrange("p n h c -> p (n h) c")
                out = qk_rot[:, t].rearrange("p n h c -> p (n h) c")
                side = turned[:].rearrange("p n h c -> p (n h) c")
                nc.vector.tensor_copy(out[:, :, 0:DHE], cols[:, :, 0:DHE])
                nc.vector.tensor_tensor(out[:, :, DHE:DH], cols[:, :, DHE:2 * DHE], over_tiles(angle[:, 0, :], 2 * NH), ALU.mult)
                nc.vector.tensor_tensor(side, cols[:, :, 2 * DHE:UP], over_tiles(angle[:, 1, :], 2 * NH), ALU.mult)
                dve.drain()
                nc.vector.tensor_tensor(out[:, :, DHE:DH], out[:, :, DHE:DH], side, ALU.add).then_inc(rot_ready, 1)
                dve.drain()
            nc.vector.tensor_copy(v_diag[:, :, :, DH], over_tiles(parity[:].rearrange("p (h d) -> p h d", d=DH)[:, :, 0], BATCHES))
            for j in range(4):
                dve.wait_ge(v_done, j + 1)
                for b in range(4):
                    last = nc.vector.tensor_tensor(v_diag[:, 4 * j + b, :, 0:DH],
                                                   bank[j % 2][:, b * D:(b + 1) * D].rearrange("p (h d) -> p h d", d=DH),
                                                   parity[:].rearrange("p (h d) -> p h d", d=DH), ALU.mult)
                last.then_inc(v_kept, 1)

            def shift(t):
                dve.wait_ge(score_done, 2 * t + 2)
                rows = prob[:, t % 2]
                nc.vector.tensor_tensor(rows, score[t % 2][:].rearrange("p (h j) -> p h j", j=SEQ),
                                        over_tiles(causal[:], NH), ALU.add)
                dve.drain()
                nc.vector.tensor_reduce(peak[:, t % 2, :], rows, AX, ALU.max)
                dve.drain()
                nc.vector.tensor_tensor(rows, rows, over_last(peak[:, t % 2, :], SEQ), ALU.subtract).then_inc(shifted, 1)

            def normalise(t):
                dve.wait_ge(mixed_done, t + 1)
                sums = bank[2 + t % 2][:, 0:NH * DV].rearrange("p (h d) -> p h d", d=DV)
                nc.vector.reciprocal(rsum[:, t % 2, :], sums[:, :, DH])
                dve.drain()
                nc.vector.tensor_tensor(mixed[:, t, :].rearrange("p (h d) -> p h d", d=DH), sums[:, :, 0:DH],
                                        over_last(rsum[:, t % 2, :], DH), ALU.mult).then_inc(mixed_kept, 1)

            shift(0)
            for t in range(TILES):
                if t + 1 < TILES:
                    if t >= 1:
                        dve.wait_ge(prob_turned, 2 * t)
                    shift(t + 1)
                normalise(t)
            dve.wait_ge(out_done, 1)
            for half in range(2):
                part = lat[:, 4 * half:4 * half + 4, :]
                nc.vector.tensor_tensor(part, part, bank[2 + half][:].rearrange("p (t d) -> p t d", d=D), ALU.add)


def gated_recurrence_stage(core, name, w):
    nc, lat = core.nc, core.lat
    STEPS = BATCHES
    NAMES = ("wf", "wi", "wc", "wo", "uf", "ui", "uc", "uo")
    F, I, G = 0, 1, 2
    with ExitStack() as ctx:
        s = Stage(nc, ctx, name)
        y, square, yT = s.sb("y", [P, TILES, D]), s.sb("square", [P, TILES, D]), s.sb("yT", [P, TOKENS])
        stats = s.sb("stats", [P, 4, TILES])
        rows = s.sb("rows", [P, 8, D])
        wT = s.sb("wT", [P, 8, D])
        bias = s.sb("bias", [P, 5])
        state = s.sb("state", [P, SEQ])
        gates = s.sb("gates", [P, 3, SEQ])
        kept, added = s.sb("kept", [P, SEQ]), s.sb("added", [P, SEQ])
        outT = s.sb("outT", [P, TOKENS])
        bank = [s.ps(f"bank{i}", [P, BANK]) for i in range(8)]
        banks_of = {F: (bank[4], bank[7], bank[0]), I: (bank[5], bank[2], bank[1]), G: (bank[6], bank[3])}

        def gate_part(gate, step):
            return banks_of[gate][step % len(banks_of[gate])][:, 0:SEQ]

        loaded, var_ready, std_ready = s.sem("loaded"), s.sem("var_ready"), s.sem("std_ready")
        y_ready, y_turned, yT_kept = s.sem("y_ready"), s.sem("y_turned"), s.sem("yT_kept")
        w_turned, w_kept = s.sem("w_turned"), s.sem("w_kept")
        pre_done, gates_done, state_ready = s.sem("pre_done"), s.sem("gates_done"), s.sem("state_ready")
        out_done, out_kept, out_turned = s.sem("out_done"), s.sem("out_kept"), s.sem("out_turned")
        LOADS = 13
        block = s.block()

        @block.sync
        def _(sp):
            for n, src in enumerate(NAMES):
                sp.dma_start(rows[:, n, :], w[src]).then_inc(loaded, 16)
            with nc.allow_non_contiguous_dma("bias columns"):
                for n, src in enumerate(("bf", "bi", "bc", "bo", "in_c")):
                    sp.dma_start(bias[:, n:n + 1], column(w[src])).then_inc(loaded, 16)

        @block.tensor
        def _(pe):
            pe.wait_ge(loaded, 16 * LOADS)
            for n in range(8):
                turn = nc.tensor.transpose(bank[2 + n // 4][:, (n % 4) * P:(n % 4 + 1) * P], rows[:, n, :], core.ident[:])
            turn.then_inc(w_turned, 1)
            turn_tiles_pe(nc, pe, core.ident[:], y[:], bank[0:2], y_ready, 1, y_turned)
            pe.wait_ge(w_kept, 2)
            pe.wait_ge(yT_kept, 2)

            def token_part(step):
                for gate in (F, I, G):
                    before = step - len(banks_of[gate])
                    if before >= 0:
                        pe.wait_ge(gates_done, 3 * before + gate + 1)
                    nc.tensor.matmul(gate_part(gate, step), wT[:, gate, :], yT[:, step * SEQ:(step + 1) * SEQ],
                                     start=True, stop=False)

            token_part(0)
            for step in range(STEPS):
                if step + 1 < STEPS:
                    token_part(step + 1)
                pe.wait_ge(state_ready, step + 1)
                for gate in (F, I, G):
                    nc.tensor.matmul(gate_part(gate, step), wT[:, 4 + gate, :], state[:], start=False, stop=True)\
                        .then_inc(pre_done, 1)
            pe.wait_ge(gates_done, 3 * (STEPS - 1))
            for half in range(2):
                nc.tensor.matmul(bank[half][:], wT[:, 3, :], yT[:, half * BANK:(half + 1) * BANK], start=True, stop=False)
            pe.wait_ge(state_ready, STEPS + 1)
            for half in range(2):
                nc.tensor.matmul(bank[half][:].rearrange("p (t j) -> p t j", j=SEQ), wT[:, 7, :],
                                 over_tiles(state[:], STEPS // 2), start=False, stop=True).then_inc(out_done, 1)
            for t in range(TILES):
                if t % 4 == 0:
                    pe.wait_ge(out_kept, t // 4 + 1)
                turn = nc.tensor.transpose(bank[2 + t // 4][:, (t % 4) * P:(t % 4 + 1) * P], outT[:, t * P:(t + 1) * P],
                                           core.ident[:])
                if t % 4 == 3:
                    turn.then_inc(out_turned, 1)

        @block.scalar
        def _(act):
            normalize_act(nc, act, core.eps(EPS_5), TILES, stats, var_ready, std_ready, 1)
            act.wait_ge(w_turned, 1)
            for half in range(2):
                nc.scalar.copy(wT[:, 4 * half:4 * half + 4, :], bank[2 + half][:].rearrange("p (n d) -> p n d", d=D))\
                    .then_inc(w_kept, 1)
            keep_turned_act(nc, act, yT, bank[0:2], y_turned, 1, yT_kept)
            act.wait_ge(loaded, 16 * LOADS)
            for step in range(STEPS):
                for gate, func in ((F, ACT.Sigmoid), (I, ACT.Sigmoid), (G, ACT.Tanh)):
                    act.wait_ge(pre_done, 3 * step + gate + 1)
                    if step >= 1 and gate == F:
                        act.wait_ge(state_ready, step + 1)
                    nc.scalar.activation(gates[:, gate, :], gate_part(gate, step), func, bias=bias[:, gate:gate + 1])\
                        .then_inc(gates_done, 1)
            for half in range(2):
                act.wait_ge(out_done, half + 1)
                nc.scalar.activation(outT[:, half * BANK:(half + 1) * BANK], bank[half][:], ACT.Tanh, bias=bias[:, 3:4])\
                    .then_inc(out_kept, 1)

        @block.vector
        def _(dve):
            normalize_dve(nc, dve, y[:], lat[:], square[:], stats, var_ready, std_ready, 1).then_inc(y_ready, 1)
            dve.wait_ge(loaded, 16 * LOADS)
            nc.vector.tensor_copy(state[:], bias[:, 4:5].to_broadcast([P, SEQ])).then_inc(state_ready, 1)
            dve.drain()
            for step in range(STEPS):
                dve.wait_ge(gates_done, 3 * step + 1)
                nc.vector.tensor_tensor(kept[:], state[:], gates[:, F, :], ALU.mult)
                dve.wait_ge(gates_done, 3 * step + 3)
                nc.vector.tensor_tensor(added[:], gates[:, I, :], gates[:, G, :], ALU.mult)
                dve.drain()
                nc.vector.tensor_tensor(state[:], kept[:], added[:], ALU.add).then_inc(state_ready, 1)
                dve.drain()
            for half in range(2):
                dve.wait_ge(out_turned, half + 1)
                part = lat[:, 4 * half:4 * half + 4, :]
                nc.vector.tensor_tensor(part, part, bank[2 + half][:].rearrange("p (t d) -> p t d", d=D), ALU.add)


class Core:

    def __init__(self, nc, lat, ident, small):
        self.nc, self.lat, self.ident, self.small = nc, lat, ident, small
        self.rank = small[:, 8:16]

    def eps(self, which):
        return self.small[:, which:which + 1]


def constants():
    small = np.zeros((P, 16), np.float32)
    small[:, EPS_5], small[:, EPS_6] = 1e-5, 1e-6
    small[:, 8:16] = np.arange(8, 0, -1)
    position = np.arange(P, dtype=np.float32) % SEQ
    angle = position[:, None] * np.float32(32.0) ** (-np.arange(0, D, 2, dtype=np.float32) / np.float32(D))
    rope32 = np.stack([np.tile(np.cos(angle), 2), np.concatenate([-np.sin(angle), np.sin(angle)], 1)], 1)
    angle = position[:, None] * (1 / np.float32(10000.0) ** (np.arange(0, 4, 2, dtype=np.float32) / np.float32(4)))
    rope4 = np.stack([np.tile(np.cos(angle), 2), np.tile(np.sin(angle), 2)], 1)
    theta = np.arange(CTX, dtype=np.float32)[None, :] * \
        (1 / np.float32(10000.0) ** (np.arange(0, 64, 2, dtype=np.float32) / np.float32(64)))[np.arange(P) % 32][:, None]
    sign = np.where(np.arange(P) < SEQ, 1, -1)[:, None]
    rope64 = np.stack([np.concatenate([np.cos(theta), np.ones((P, SEQ))], 1),
                       np.concatenate([np.sin(theta) * sign, np.zeros((P, SEQ))], 1)])
    earlier = np.arange(SEQ)[None, :] <= position[:, None]
    feature = np.arange(P)
    return {
        "c_ident": np.eye(P, dtype=np.float32), "c_small": small,
        "c_rope32": rope32.astype(np.float32), "c_rope4": rope4.astype(np.float32),
        "c_causal": earlier.astype(np.float32), "c_causal_add": np.where(earlier, 0, -1e30).astype(np.float32),
        "c_rope64": rope64.astype(np.float32),
        "c_own_head": (feature[:, None] // 8 == np.arange(16)[None, :]).astype(np.float32),
        "c_parity": (feature[:, None] // SEQ == feature[None, :] // 8 % 2).astype(np.float32),
    }


def weights(w, stage):
    return {name[len(stage) + 1:]: ap for name, ap in w.items() if name.startswith(stage + "_")}


STAGES = {
    "L0_xattn": lambda core, w: cross_attention_stage(core, "L0_xattn", weights(w, "L0_xattn"), heads=8, scale=1 / 64,
                                                      normed=True, masked=True, out_norm=True),
    "L0_attn": lambda core, w: mlstm_stage(core, "L0_attn", weights(w, "L0_attn")),
    "L0_ffn": lambda core, w: moe_stage(core, "L0_ffn", "relu", w["L0_ffn_Wg"], w["L0_ffn_W1"], w["L0_ffn_b1"],
                                        w["L0_ffn_W2"], w["L0_ffn_b2"]),
    "L1_xattn": lambda core, w: cross_attention_stage(core, "L1_xattn", weights(w, "L1_xattn"), heads=16, scale=1 / 8),
    "L1_attn": lambda core, w: causal_exp_stage(core, "L1_attn", weights(w, "L1_attn")),
    "L1_ffn": lambda core, w: moe_stage(core, "L1_ffn", "swiglu", w["L1_ffn_gate_w"], w["L1_ffn_w12"], None,
                                        w["L1_ffn_w3"], None),
    "L2_xattn": lambda core, w: single_head_stage(core, "L2_xattn", weights(w, "L2_xattn")),
    "L2_attn": lambda core, w: projected_mlp_stage(core, "L2_attn", weights(w, "L2_attn")),
    "L2_ffn": lambda core, w: moe_stage(core, "L2_ffn", "gelu", w["L2_ffn_Wg"], w["L2_ffn_W1"], w["L2_ffn_b1"],
                                        w["L2_ffn_W2"], w["L2_ffn_b2"], w["L2_ffn_bg"]),
    "L3_xattn": lambda core, w: cross_attention_stage(core, "L3_xattn", weights(w, "L3_xattn"), heads=8, scale=1 / 8,
                                                      normed=True, rotary=True),
    "L3_attn": lambda core, w: latent_attention_stage(core, "L3_attn", weights(w, "L3_attn")),
    "L3_ffn": lambda core, w: gated_recurrence_stage(core, "L3_ffn", weights(w, "L3_ffn")),
}


def build(nc, w, out, stages=tuple(STAGES)):
    with ExitStack() as ctx:
        s = Stage(nc, ctx, "all")
        lat = s.sb("lat", [P, TILES, D])
        ident = s.sb("ident", [P, P])
        small = s.sb("small", [P, 16])
        loaded, stored = s.sem("loaded"), s.sem("stored")
        core = Core(nc, lat, ident, small)
        core.w = w
        core.ctx_hat = nc.dram_tensor("context_normalised", (BATCHES, CTX, D), F32, kind="Internal").ap()
        with nc.Block() as block:
            @block.sync
            def _(sp):
                sp.dma_start(lat[:], w["x"].rearrange("(t b) i d -> (b i) t d", b=2)).then_inc(loaded, 16)
                sp.dma_start(ident[:], w["c_ident"]).then_inc(loaded, 16)
                sp.dma_start(small[:], w["c_small"]).then_inc(loaded, 16)
                sp.wait_ge(loaded, 48)
        for name in stages:
            STAGES[name](core, w)
        with nc.Block() as block:
            @block.sync
            def _(sp):
                sp.dma_start(out.rearrange("(t b) i d -> (b i) t d", b=2), lat[:]).then_inc(stored, 16)
                sp.wait_ge(stored, 16)


def kernel(**inputs):
    import concourse.bacc as bacc
    from concourse.bass_utils import run_bass_kernel_spmd

    nc = bacc.Bacc("TRN2", target_bir_lowering=False, num_devices=1)
    arrays, w = {}, {}
    for name, value in {**inputs, **constants()}.items():
        value = np.ascontiguousarray(value)
        arrays["in_" + name] = value
        w[name] = nc.dram_tensor("in_" + name, value.shape, mybir.dt.from_np(value.dtype), kind="ExternalInput").ap()
    out = nc.dram_tensor("latents_out", (BATCHES, SEQ, D), F32, kind="ExternalOutput").ap()
    build(nc, w, out)
    result = run_bass_kernel_spmd(nc, [arrays], core_ids=[0])
    return result.results[0]["latents_out"]
```
